# Optimizing a Trainium2 kernel written in Bass

```python
import numpy as np
import jax
import jax.numpy as jnp

def _softmax(x, axis=-1):
    return jax.nn.softmax(x, axis=axis)

def _gelu(x):
    return jax.nn.gelu(x, approximate=True)

def _silu(x):
    return jax.nn.silu(x)

def _sigmoid(x):
    return jax.nn.sigmoid(x)

def _layernorm(x, axis=-1, eps=1e-05):
    m = jnp.mean(x, axis=axis, keepdims=True)
    v = jnp.var(x, axis=axis, keepdims=True)
    return (x - m) / jnp.sqrt(v + eps)

def _scatter_add(tgt, idx, src, axis=0):
    return tgt.at[idx].add(src)

def _segment_sum(src, seg, n):
    return jax.ops.segment_sum(src, seg, n)
kernel_name = 'mk_gnn_ffn_d2_gnn_r16_7f3113'

def setup_inputs(seed: int=0):
    np.random.seed(seed)
    _w = jnp.asarray

    def _rec_inputs():
        import jax
        import jax.numpy as jnp
        _gk = jax.random.key(seed)
        x = -0.0003713 + 1 * jax.random.normal(jax.random.fold_in(_gk, 1), (6250, 256), jnp.float32)
        _s = jax.random.randint(jax.random.fold_in(_gk, 2), (50000,), 0, 6250, jnp.int32)
        _d = jax.random.randint(jax.random.fold_in(_gk, 3), (50000,), 0, 6250, jnp.int32)
        _loop = jnp.arange(6250, dtype=jnp.int32)
        src = jnp.concatenate([_s, _d, _loop])
        dst = jnp.concatenate([_d, _s, _loop])
        _o = jnp.argsort(dst, stable=True)
        src = src[_o]
        dst = dst[_o]
        edge_attr_64 = 0.000189758 + 1.00013 * jax.random.normal(jax.random.fold_in(_gk, 12), (106250, 64), jnp.float32)
        return (x, src, dst, edge_attr_64)
    x, src, dst, edge_attr_64 = _rec_inputs()

    def _L0_gnn_setup():
        import jax, jax.numpy as jnp
        import numpy as np
        N = 3125
        E = 50000
        F = 256
        H = 4
        D = 64
        key = jax.random.key(seed)
        ks = jax.random.split(key, 10)
        s = 0.02
        HD = H * D
        return {'feat': jax.random.normal(ks[0], (N, F), jnp.float32), 'src': jax.random.randint(ks[1], (E,), 0, N), 'dst': jax.random.randint(ks[2], (E,), 0, N), 'Wq': jax.random.normal(ks[3], (HD, F), jnp.float32) * s, 'bq': jnp.zeros((HD,), jnp.float32), 'Wk': jax.random.normal(ks[4], (HD, F), jnp.float32) * s, 'bk': jnp.zeros((HD,), jnp.float32), 'Wv': jax.random.normal(ks[5], (HD, F), jnp.float32) * s, 'bv': jnp.zeros((HD,), jnp.float32), 'Wskip': jax.random.normal(ks[6], (HD, F), jnp.float32) * s, 'bskip': jnp.zeros((HD,), jnp.float32), 'Wgate': jax.random.normal(ks[7], (1, 3 * HD), jnp.float32) * s, 'bgate': jnp.zeros((1,), jnp.float32), 'ln_w': jnp.ones((HD,), jnp.float32), 'ln_b': jnp.zeros((HD,), jnp.float32), 'prelu_a': jnp.float32(0.25)}
    _L0_gnn_all = _L0_gnn_setup()
    _L0_gnn_in = {k: v for k, v in _L0_gnn_all.items() if k in ('Wq', 'bq', 'Wk', 'bk', 'Wv', 'bv', 'Wskip', 'bskip', 'Wgate', 'bgate', 'ln_w', 'ln_b', 'prelu_a')}
    del _L0_gnn_all

    def _L0_ffn_setup():
        import jax, jax.numpy as jnp
        import numpy as np
        B, N, D = (16, 256, 256)
        NUM_EXPERTS, TOP_K, HEADS = (4, 2, 4)
        N_EDGES = 65536
        LN_EPS = 1e-05

        def _layernorm(x, g, b):
            mu = x.mean(-1, keepdims=True)
            var = ((x - mu) ** 2).mean(-1, keepdims=True)
            return (x - mu) * jax.lax.rsqrt(var + LN_EPS) * g + b

        def _forward(x, edge_index, W_gat, att_src, att_dst, b_gat, ln_gamma, ln_beta, W1, b1, W2, b2):
            Bc, Nc, Dc = x.shape
            M = Bc * Nc
            x_flat = x.reshape(M, Dc)
            h = (x_flat @ W_gat).reshape(M, HEADS, NUM_EXPERTS)
            loops = jnp.arange(M, dtype=edge_index.dtype)
            src = jnp.concatenate([edge_index[0], loops])
            dst = jnp.concatenate([edge_index[1], loops])
            a_src = (h * att_src).sum(-1)
            a_dst = (h * att_dst).sum(-1)
            e = jax.nn.leaky_relu(a_src[src] + a_dst[dst], negative_slope=0.2)
            e_max = jax.ops.segment_max(e, dst, num_segments=M)
            ee = jnp.exp(e - e_max[dst])
            denom = jax.ops.segment_sum(ee, dst, num_segments=M)
            alpha = ee / (denom[dst] + 1e-16)
            msg = h[src] * alpha[:, :, None]
            agg = jax.ops.segment_sum(msg, dst, num_segments=M).reshape(M, HEADS * NUM_EXPERTS) + b_gat
            scores = _layernorm(agg, ln_gamma, ln_beta).reshape(M, HEADS, NUM_EXPERTS).mean(1)
            scores = scores.reshape(Bc, Nc, NUM_EXPERTS)
            topk_s, topk_i = jax.lax.top_k(scores, TOP_K)
            w = jax.nn.softmax(topk_s, axis=-1)
            out = jnp.zeros_like(x)
            for ei in range(NUM_EXPERTS):
                g = jnp.where(topk_i == ei, w, 0.0).sum(-1)
                hh = jax.nn.gelu(x @ W1[ei] + b1[ei], approximate=False)
                out = out + g[..., None] * (hh @ W2[ei] + b2[ei])
            return out
        key = jax.random.key(seed)
        ks = jax.random.split(key, 8)
        s = 0.05
        return {'x': jax.random.normal(ks[0], (B, N, D), jnp.float32), 'W_gat': jax.random.normal(ks[1], (D, HEADS * NUM_EXPERTS), jnp.float32) * s, 'att_src': jax.random.normal(ks[2], (HEADS, NUM_EXPERTS), jnp.float32) * s, 'att_dst': jax.random.normal(ks[3], (HEADS, NUM_EXPERTS), jnp.float32) * s, 'b_gat': jnp.zeros((HEADS * NUM_EXPERTS,), jnp.float32), 'ln_gamma': jnp.ones((HEADS * NUM_EXPERTS,), jnp.float32), 'ln_beta': jnp.zeros((HEADS * NUM_EXPERTS,), jnp.float32), 'W1': jax.random.normal(ks[4], (NUM_EXPERTS, D, 2 * D), jnp.float32) * s, 'b1': jnp.zeros((NUM_EXPERTS, 2 * D), jnp.float32), 'W2': jax.random.normal(ks[5], (NUM_EXPERTS, 2 * D, D), jnp.float32) * s, 'b2': jnp.zeros((NUM_EXPERTS, D), jnp.float32), 'edge_index': jax.random.randint(ks[6], (2, N_EDGES), 0, B * N, jnp.int32)}
    _L0_ffn_all = _L0_ffn_setup()
    _L0_ffn_in = {k: v for k, v in _L0_ffn_all.items() if k in ('W_gat', 'att_src', 'att_dst', 'b_gat', 'ln_gamma', 'ln_beta', 'W1', 'b1', 'W2', 'b2', 'edge_index')}
    del _L0_ffn_all

    def _L1_gnn_setup():
        import jax, jax.numpy as jnp
        import numpy as np
        N, E = (3125, 50000)
        HID, EDIM, HEADS = (256, 64, 8)
        C = HID // HEADS
        NEG_SLOPE = 0.2
        LN_EPS = 1e-05

        def _gat_block(x, edge_index, edge_attr, W, W_e, att_src, att_dst, att_edge, bias, gamma, beta):
            n = x.shape[0]
            src, dst = (edge_index[0], edge_index[1])
            xp = (x @ W).reshape(n, HEADS, C)
            a_src = jnp.einsum('nhc,hc->nh', xp, att_src)
            a_dst = jnp.einsum('nhc,hc->nh', xp, att_dst)
            ep = (edge_attr @ W_e).reshape(-1, HEADS, C)
            a_edge = jnp.einsum('ehc,hc->eh', ep, att_edge)
            alpha = a_src[src] + a_dst[dst] + a_edge
            alpha = jax.nn.leaky_relu(alpha, NEG_SLOPE)
            m = jax.ops.segment_max(alpha, dst, num_segments=n)
            m = jnp.where(jnp.isfinite(m), m, 0.0)
            ea = jnp.exp(alpha - m[dst])
            den = jax.ops.segment_sum(ea, dst, num_segments=n)
            attn = ea / (den[dst] + 1e-16)
            msg = xp[src] * attn[:, :, None]
            out = jax.ops.segment_sum(msg, dst, num_segments=n)
            h = out.reshape(n, HEADS * C) + bias
            y = x + h
            mu = jnp.mean(y, axis=-1, keepdims=True)
            var = jnp.var(y, axis=-1, keepdims=True)
            return (y - mu) * jax.lax.rsqrt(var + LN_EPS) * gamma + beta
        key = jax.random.key(seed)
        ks = jax.random.split(key, 12)
        s = 1.0 / np.sqrt(HID)
        se = 1.0 / np.sqrt(EDIM)
        return {'x': jax.random.normal(ks[0], (N, HID), jnp.float32), 'edge_index': jax.random.randint(ks[1], (2, E), 0, N, jnp.int32), 'edge_attr': jax.random.normal(ks[2], (E, EDIM), jnp.float32), 'W': jax.random.uniform(ks[3], (HID, HEADS * C), jnp.float32, -s, s), 'W_e': jax.random.uniform(ks[4], (EDIM, HEADS * C), jnp.float32, -se, se), 'att_src': jax.random.normal(ks[5], (HEADS, C), jnp.float32) * 0.1, 'att_dst': jax.random.normal(ks[6], (HEADS, C), jnp.float32) * 0.1, 'att_edge': jax.random.normal(ks[7], (HEADS, C), jnp.float32) * 0.1, 'bias': jnp.zeros((HEADS * C,), jnp.float32), 'gamma': jnp.ones((HID,), jnp.float32), 'beta': jnp.zeros((HID,), jnp.float32)}
    _L1_gnn_all = _L1_gnn_setup()
    _L1_gnn_in = {k: v for k, v in _L1_gnn_all.items() if k in ('W', 'W_e', 'att_src', 'att_dst', 'att_edge', 'bias', 'gamma', 'beta')}
    del _L1_gnn_all

    def _L1_ffn_setup():
        import jax, jax.numpy as jnp
        import numpy as np
        BN_EPS = 0.001

        def _bn(h, g, b, m, v):
            return g * (h - m) * jax.lax.rsqrt(v + BN_EPS) + b
        key = jax.random.key(seed)
        ks = jax.random.split(key, 8)
        B, F, Df = (256, 64, 256)
        E, H, D = (8, 256, 256)
        s1 = 1.0 / np.sqrt(Df)
        s2 = 1.0 / np.sqrt(H)
        return {'x': jax.random.normal(ks[0], (B, F, Df), jnp.float32), 'Wr': jax.random.normal(ks[1], (Df, E), jnp.float32) * s1, 'br': jnp.zeros((E,), jnp.float32), 'W1': jax.random.normal(ks[2], (E, Df, H), jnp.float32) * s1, 'b1': jnp.zeros((E, H), jnp.float32), 'g1': jnp.ones((E, H), jnp.float32), 'be1': jnp.zeros((E, H), jnp.float32), 'm1': jnp.zeros((E, H), jnp.float32), 'v1': jnp.ones((E, H), jnp.float32), 'W2': jax.random.normal(ks[3], (E, H, H), jnp.float32) * s2, 'b2': jnp.zeros((E, H), jnp.float32), 'g2': jnp.ones((E, H), jnp.float32), 'be2': jnp.zeros((E, H), jnp.float32), 'm2': jnp.zeros((E, H), jnp.float32), 'v2': jnp.ones((E, H), jnp.float32), 'Wo': jax.random.normal(ks[4], (E, H, D), jnp.float32) * s2, 'bo': jnp.zeros((E, D), jnp.float32)}
    _L1_ffn_all = _L1_ffn_setup()
    _L1_ffn_in = {k: v for k, v in _L1_ffn_all.items() if k in ('Wr', 'br', 'W1', 'b1', 'g1', 'be1', 'm1', 'v1', 'W2', 'b2', 'g2', 'be2', 'm2', 'v2', 'Wo', 'bo')}
    del _L1_ffn_all
    return {'x': x, 'src': src, 'dst': dst, 'edge_attr_64': edge_attr_64, 'L0_gnn_Wq': _L0_gnn_in['Wq'], 'L0_gnn_bq': _L0_gnn_in['bq'], 'L0_gnn_Wk': _L0_gnn_in['Wk'], 'L0_gnn_bk': _L0_gnn_in['bk'], 'L0_gnn_Wv': _L0_gnn_in['Wv'], 'L0_gnn_bv': _L0_gnn_in['bv'], 'L0_gnn_Wskip': _L0_gnn_in['Wskip'], 'L0_gnn_bskip': _L0_gnn_in['bskip'], 'L0_gnn_Wgate': _L0_gnn_in['Wgate'], 'L0_gnn_bgate': _L0_gnn_in['bgate'], 'L0_gnn_ln_w': _L0_gnn_in['ln_w'], 'L0_gnn_ln_b': _L0_gnn_in['ln_b'], 'L0_gnn_prelu_a': _L0_gnn_in['prelu_a'], 'L0_ffn_W_gat': _L0_ffn_in['W_gat'], 'L0_ffn_att_src': _L0_ffn_in['att_src'], 'L0_ffn_att_dst': _L0_ffn_in['att_dst'], 'L0_ffn_b_gat': _L0_ffn_in['b_gat'], 'L0_ffn_ln_gamma': _L0_ffn_in['ln_gamma'], 'L0_ffn_ln_beta': _L0_ffn_in['ln_beta'], 'L0_ffn_W1': _L0_ffn_in['W1'], 'L0_ffn_b1': _L0_ffn_in['b1'], 'L0_ffn_W2': _L0_ffn_in['W2'], 'L0_ffn_b2': _L0_ffn_in['b2'], 'L0_ffn_edge_index': _L0_ffn_in['edge_index'], 'L1_gnn_W': _L1_gnn_in['W'], 'L1_gnn_W_e': _L1_gnn_in['W_e'], 'L1_gnn_att_src': _L1_gnn_in['att_src'], 'L1_gnn_att_dst': _L1_gnn_in['att_dst'], 'L1_gnn_att_edge': _L1_gnn_in['att_edge'], 'L1_gnn_bias': _L1_gnn_in['bias'], 'L1_gnn_gamma': _L1_gnn_in['gamma'], 'L1_gnn_beta': _L1_gnn_in['beta'], 'L1_ffn_Wr': _L1_ffn_in['Wr'], 'L1_ffn_br': _L1_ffn_in['br'], 'L1_ffn_W1': _L1_ffn_in['W1'], 'L1_ffn_b1': _L1_ffn_in['b1'], 'L1_ffn_g1': _L1_ffn_in['g1'], 'L1_ffn_be1': _L1_ffn_in['be1'], 'L1_ffn_m1': _L1_ffn_in['m1'], 'L1_ffn_v1': _L1_ffn_in['v1'], 'L1_ffn_W2': _L1_ffn_in['W2'], 'L1_ffn_b2': _L1_ffn_in['b2'], 'L1_ffn_g2': _L1_ffn_in['g2'], 'L1_ffn_be2': _L1_ffn_in['be2'], 'L1_ffn_m2': _L1_ffn_in['m2'], 'L1_ffn_v2': _L1_ffn_in['v2'], 'L1_ffn_Wo': _L1_ffn_in['Wo'], 'L1_ffn_bo': _L1_ffn_in['bo']}

def reference(x, src, dst, edge_attr_64, L0_gnn_Wq, L0_gnn_bq, L0_gnn_Wk, L0_gnn_bk, L0_gnn_Wv, L0_gnn_bv, L0_gnn_Wskip, L0_gnn_bskip, L0_gnn_Wgate, L0_gnn_bgate, L0_gnn_ln_w, L0_gnn_ln_b, L0_gnn_prelu_a, L0_ffn_W_gat, L0_ffn_att_src, L0_ffn_att_dst, L0_ffn_b_gat, L0_ffn_ln_gamma, L0_ffn_ln_beta, L0_ffn_W1, L0_ffn_b1, L0_ffn_W2, L0_ffn_b2, L0_ffn_edge_index, L1_gnn_W, L1_gnn_W_e, L1_gnn_att_src, L1_gnn_att_dst, L1_gnn_att_edge, L1_gnn_bias, L1_gnn_gamma, L1_gnn_beta, L1_ffn_Wr, L1_ffn_br, L1_ffn_W1, L1_ffn_b1, L1_ffn_g1, L1_ffn_be1, L1_ffn_m1, L1_ffn_v1, L1_ffn_W2, L1_ffn_b2, L1_ffn_g2, L1_ffn_be2, L1_ffn_m2, L1_ffn_v2, L1_ffn_Wo, L1_ffn_bo):
    import jax
    import jax.numpy as jnp

    def _L0_gnn_ref(feat, src, dst, Wq, bq, Wk, bk, Wv, bv, Wskip, bskip, Wgate, bgate, ln_w, ln_b, prelu_a):
        import jax, jax.numpy as jnp
        import numpy as np
        N = 3125
        E = 50000
        F = 256
        H = 4
        D = 64
        n = feat.shape[0]
        scale = 1.0 / np.sqrt(D).astype(np.float32)
        q = (feat @ Wq.T + bq).reshape(n, H, D)
        k = (feat @ Wk.T + bk).reshape(n, H, D)
        v = (feat @ Wv.T + bv).reshape(n, H, D)
        e = jnp.einsum('ehd,ehd->eh', q[src], k[dst]) * scale
        m = jax.ops.segment_max(e, dst, num_segments=n)
        ex = jnp.exp(e - m[dst])
        denom = jax.ops.segment_sum(ex, dst, num_segments=n)
        sa = ex / denom[dst]
        agg = jax.ops.segment_sum(sa[:, :, None] * v[src], dst, num_segments=n)
        rst = agg.reshape(n, H * D)
        skip = feat @ Wskip.T + bskip
        g = jax.nn.sigmoid(jnp.concatenate([skip, rst, skip - rst], axis=-1) @ Wgate.T + bgate)
        rst = g * skip + (1.0 - g) * rst
        mu = rst.mean(-1, keepdims=True)
        var = rst.var(-1, keepdims=True)
        rst = (rst - mu) * jax.lax.rsqrt(var + 1e-05) * ln_w + ln_b
        return jnp.where(rst >= 0, rst, prelu_a * rst)

    def _L0_ffn_ref(x, W_gat, att_src, att_dst, b_gat, ln_gamma, ln_beta, W1, b1, W2, b2, edge_index):
        import jax, jax.numpy as jnp
        import numpy as np
        B, N, D = (16, 256, 256)
        NUM_EXPERTS, TOP_K, HEADS = (4, 2, 4)
        N_EDGES = 65536
        LN_EPS = 1e-05

        def _layernorm(x, g, b):
            mu = x.mean(-1, keepdims=True)
            var = ((x - mu) ** 2).mean(-1, keepdims=True)
            return (x - mu) * jax.lax.rsqrt(var + LN_EPS) * g + b

        def _forward(x, edge_index, W_gat, att_src, att_dst, b_gat, ln_gamma, ln_beta, W1, b1, W2, b2):
            Bc, Nc, Dc = x.shape
            M = Bc * Nc
            x_flat = x.reshape(M, Dc)
            h = (x_flat @ W_gat).reshape(M, HEADS, NUM_EXPERTS)
            loops = jnp.arange(M, dtype=edge_index.dtype)
            src = jnp.concatenate([edge_index[0], loops])
            dst = jnp.concatenate([edge_index[1], loops])
            a_src = (h * att_src).sum(-1)
            a_dst = (h * att_dst).sum(-1)
            e = jax.nn.leaky_relu(a_src[src] + a_dst[dst], negative_slope=0.2)
            e_max = jax.ops.segment_max(e, dst, num_segments=M)
            ee = jnp.exp(e - e_max[dst])
            denom = jax.ops.segment_sum(ee, dst, num_segments=M)
            alpha = ee / (denom[dst] + 1e-16)
            msg = h[src] * alpha[:, :, None]
            agg = jax.ops.segment_sum(msg, dst, num_segments=M).reshape(M, HEADS * NUM_EXPERTS) + b_gat
            scores = _layernorm(agg, ln_gamma, ln_beta).reshape(M, HEADS, NUM_EXPERTS).mean(1)
            scores = scores.reshape(Bc, Nc, NUM_EXPERTS)
            topk_s, topk_i = jax.lax.top_k(scores, TOP_K)
            w = jax.nn.softmax(topk_s, axis=-1)
            out = jnp.zeros_like(x)
            for ei in range(NUM_EXPERTS):
                g = jnp.where(topk_i == ei, w, 0.0).sum(-1)
                hh = jax.nn.gelu(x @ W1[ei] + b1[ei], approximate=False)
                out = out + g[..., None] * (hh @ W2[ei] + b2[ei])
            return out
        return _forward(x, edge_index, W_gat, att_src, att_dst, b_gat, ln_gamma, ln_beta, W1, b1, W2, b2)

    def _L1_gnn_ref(x, edge_index, edge_attr, W, W_e, att_src, att_dst, att_edge, bias, gamma, beta):
        import jax, jax.numpy as jnp
        import numpy as np
        N, E = (3125, 50000)
        HID, EDIM, HEADS = (256, 64, 8)
        C = HID // HEADS
        NEG_SLOPE = 0.2
        LN_EPS = 1e-05

        def _gat_block(x, edge_index, edge_attr, W, W_e, att_src, att_dst, att_edge, bias, gamma, beta):
            n = x.shape[0]
            src, dst = (edge_index[0], edge_index[1])
            xp = (x @ W).reshape(n, HEADS, C)
            a_src = jnp.einsum('nhc,hc->nh', xp, att_src)
            a_dst = jnp.einsum('nhc,hc->nh', xp, att_dst)
            ep = (edge_attr @ W_e).reshape(-1, HEADS, C)
            a_edge = jnp.einsum('ehc,hc->eh', ep, att_edge)
            alpha = a_src[src] + a_dst[dst] + a_edge
            alpha = jax.nn.leaky_relu(alpha, NEG_SLOPE)
            m = jax.ops.segment_max(alpha, dst, num_segments=n)
            m = jnp.where(jnp.isfinite(m), m, 0.0)
            ea = jnp.exp(alpha - m[dst])
            den = jax.ops.segment_sum(ea, dst, num_segments=n)
            attn = ea / (den[dst] + 1e-16)
            msg = xp[src] * attn[:, :, None]
            out = jax.ops.segment_sum(msg, dst, num_segments=n)
            h = out.reshape(n, HEADS * C) + bias
            y = x + h
            mu = jnp.mean(y, axis=-1, keepdims=True)
            var = jnp.var(y, axis=-1, keepdims=True)
            return (y - mu) * jax.lax.rsqrt(var + LN_EPS) * gamma + beta
        return _gat_block(x, edge_index, edge_attr, W, W_e, att_src, att_dst, att_edge, bias, gamma, beta)

    def _L1_ffn_ref(x, Wr, br, W1, b1, g1, be1, m1, v1, W2, b2, g2, be2, m2, v2, Wo, bo):
        import jax, jax.numpy as jnp
        import numpy as np
        BN_EPS = 0.001

        def _bn(h, g, b, m, v):
            return g * (h - m) * jax.lax.rsqrt(v + BN_EPS) + b
        feat = jnp.mean(x, axis=0)
        w = jax.nn.softmax(feat @ Wr + br, axis=-1)
        h = jnp.einsum('bfd,edh->bfeh', x, W1) + b1
        h = jax.nn.relu(_bn(h, g1, be1, m1, v1))
        h = jnp.einsum('bfeh,ehk->bfek', h, W2) + b2
        h = jax.nn.relu(_bn(h, g2, be2, m2, v2))
        y = jnp.einsum('bfeh,ehd->bfed', h, Wo) + bo
        return jnp.einsum('bfed,fe->bfd', y, w)
    edge_index = jnp.stack([src, dst])
    x = x + _L0_gnn_ref(_layernorm(x, axis=-1), src, dst, L0_gnn_Wq, L0_gnn_bq, L0_gnn_Wk, L0_gnn_bk, L0_gnn_Wv, L0_gnn_bv, L0_gnn_Wskip, L0_gnn_bskip, L0_gnn_Wgate, L0_gnn_bgate, L0_gnn_ln_w, L0_gnn_ln_b, L0_gnn_prelu_a)
    x = x + _L0_ffn_ref(_layernorm(x, axis=-1)[None], L0_ffn_W_gat, L0_ffn_att_src, L0_ffn_att_dst, L0_ffn_b_gat, L0_ffn_ln_gamma, L0_ffn_ln_beta, L0_ffn_W1, L0_ffn_b1, L0_ffn_W2, L0_ffn_b2, L0_ffn_edge_index)[0]
    x = x + _L1_gnn_ref(_layernorm(x, axis=-1), edge_index, edge_attr_64, L1_gnn_W, L1_gnn_W_e, L1_gnn_att_src, L1_gnn_att_dst, L1_gnn_att_edge, L1_gnn_bias, L1_gnn_gamma, L1_gnn_beta)
    x = x + _L1_ffn_ref(_layernorm(x, axis=-1)[None], L1_ffn_Wr, L1_ffn_br, L1_ffn_W1, L1_ffn_b1, L1_ffn_g1, L1_ffn_be1, L1_ffn_m1, L1_ffn_v1, L1_ffn_W2, L1_ffn_b2, L1_ffn_g2, L1_ffn_be2, L1_ffn_m2, L1_ffn_v2, L1_ffn_Wo, L1_ffn_bo)[0]
    return x

_drawn_inputs = setup_inputs


def setup_inputs(seed=0):
    import zlib

    import numpy as np

    out = dict(_drawn_inputs(seed))
    spreads = {'L0_gnn_bq': (0.0, 2.0),
     'L0_gnn_bk': (0.0, 0.527),
     'L0_gnn_bv': (0.0, 0.1),
     'L0_gnn_bskip': (0.0, 0.1),
     'L0_gnn_ln_w': (1.0, 0.2),
     'L0_gnn_ln_b': (0.0, 0.1),
     'L0_ffn_b_gat': (0.0, 0.1),
     'L0_ffn_ln_gamma': (1.0, 0.2),
     'L0_ffn_ln_beta': (0.0, 0.1),
     'L0_ffn_b1': (0.0, 0.1),
     'L0_ffn_b2': (0.0, 0.1),
     'L1_gnn_bias': (0.0, 0.1),
     'L1_gnn_gamma': (1.0, 0.2),
     'L1_gnn_beta': (0.0, 0.1),
     'L1_ffn_br': (0.0, 0.8),
     'L1_ffn_b1': (0.0, 0.696),
     'L1_ffn_g1': (1.0, 0.6),
     'L1_ffn_be1': (0.0, 0.758),
     'L1_ffn_m1': (0.0, 0.717),
     'L1_ffn_v1': (1.0, 0.6),
     'L1_ffn_b2': (0.0, 0.514),
     'L1_ffn_g2': (1.0, 0.6),
     'L1_ffn_be2': (0.0, 0.563),
     'L1_ffn_m2': (0.0, 0.503),
     'L1_ffn_v2': (1.0, 0.6),
     'L1_ffn_bo': (0.0, 0.382)}
    factors = {'edge_attr_64': 3.616,
     'L1_gnn_W_e': 3.551,
     'L1_gnn_att_src': 2.848,
     'L1_gnn_att_dst': 64.0,
     'L1_gnn_att_edge': 3.47}
    for name, (base, spread) in spreads.items():
        noise = np.random.default_rng([zlib.crc32(name.encode()), seed]).standard_normal(out[name].shape)
        drawn = base * np.exp(spread * noise) if base else spread * noise
        out[name] = jnp.asarray(drawn.astype(out[name].dtype))
    for name, factor in factors.items():
        out[name] = (out[name] * factor).astype(out[name].dtype)
    return out
```

```python
from contextlib import ExitStack

import numpy as np

import concourse.bass as bass
from concourse import mybir

F32 = mybir.dt.float32
BF16 = mybir.dt.bfloat16
I32 = mybir.dt.int32
ALU = mybir.AluOpType
ACT = mybir.ActivationFunctionType
AX = mybir.AxisListType.X

P = 128
N = 6250
D = 256
NODE_TILES = -(-N // P)
NP = NODE_TILES * P
CHUNKS = 7
TPC = NODE_TILES // CHUNKS
ROWS = TPC * P
HALF = ROWS // 2
BIG = 1.0e30
FAR = 1.0e6
EPS = 1e-5
HOPS = 65536
HOP_TILES = HOPS // P


class EdgeList:

    def __init__(self, name, edges):
        self.name = name
        self.edges = edges
        self.tiles = -(-edges // P)
        self.real_steps = self.tiles + NODE_TILES - 1
        self.steps = -(-self.real_steps // 8) * 8
        self.blocks = -(-self.steps // P)
        self.tile_blocks = -(-self.tiles // P)


GRAPH = EdgeList("g", 106250)
HOP = EdgeList("f", HOPS + NP)


class Tally:

    def __init__(self, eng, sem):
        self.eng, self.sem = eng, sem
        self.before, self.per, self.turn, self.here = 0, 0, 0, 0

    def loop(self, turn, per):
        self.before += self.here
        self.turn, self.per, self.here = turn, per, 0

    def leave(self, turns):
        assert self.here == self.per, (self.here, self.per)
        self.before += turns * self.per
        self.turn, self.per, self.here = 0, 0, 0

    def done(self, ins):
        self.here += 1
        ins.then_inc(self.sem, 1)
        self.eng.wait_ge(self.sem, self.before + self.per * self.turn + self.here)


class Scope:

    def __init__(self, nc, ctx, name):
        self.nc, self.ctx, self.name, self.sems = nc, ctx, name, []
        ctx.callback(self.release)

    def release(self):
        for sem in self.sems:
            self.nc.gpsimd.sem_clear(sem)
            self.nc.release_semaphore(sem)

    def sb(self, name, shape, dt=F32):
        return self.ctx.enter_context(self.nc.sbuf_tensor(f"{self.name}_{name}", shape, dt))

    def ps(self, name, shape, dt=F32):
        return self.ctx.enter_context(self.nc.psum_tensor(f"{self.name}_{name}", shape, dt))

    def gather_sem(self, name):
        return self.nc.alloc_semaphore(f"{self.name}_{name}")

    def sem(self, name):
        self.sems.append(self.nc.alloc_semaphore(f"{self.name}_{name}"))
        return self.sems[-1]


def bcast_rows(ap, n):
    return ap.partition_broadcast(n)


def stage_constants(nc, T, K):
    with ExitStack() as ctx:
        s = Scope(nc, ctx, "c")
        frow_i = s.sb("frow_i", [P, P], I32)
        pcol_i = s.sb("pcol_i", [P, 1], I32)
        zero = s.sb("zero", [P, D])
        pad_dst = s.sb("pad_dst", [P, 1], I32)
        made = s.sem("made")
        filled = s.sem("filled")
        moved = s.sem("moved")
        block = ctx.enter_context(nc.Block())
        tail = NP - N
        epad = GRAPH.tiles * P - GRAPH.edges

        @block.gpsimd
        def _(pool):
            pool.iota(frow_i[:, :], pattern=[[1, P]], base=0, channel_multiplier=0).then_inc(made, 1)
            pool.iota(pcol_i[:, :], pattern=[[1, 1]], base=0, channel_multiplier=1).then_inc(made, 1)

        @block.vector
        def _(dve):
            link = Tally(dve, s.sem("dve"))
            dve.memset(zero[:, :], 0.0).then_inc(filled, 1)
            dve.memset(pad_dst[:, :], NP - 1).then_inc(filled, 1)
            dve.wait_ge(made, 2)
            dve.tensor_copy(K["frow"][:, :], frow_i[:, :]).then_inc(link.sem, 1)
            link.here += 1
            link.done(dve.tensor_copy(K["pcol"][:, :], pcol_i[:, :]))
            dve.tensor_scalar(K["ident"][:, :], K["frow"][:, :], K["pcol"][:, 0:1], None, ALU.is_equal)
            dve.tensor_scalar(K["below"][:, :], K["frow"][:, :], K["pcol"][:, 0:1], None, ALU.is_gt)
            dve.memset(K["ones"][:, :], 1.0)
            dve.memset(K["eps"][:, :], EPS)

        @block.sync
        def _(sp):
            sp.dma_start(T["x0"][0:N, :], T["x"]).then_inc(moved, 16)
            sp.dma_start(T["g_src"][0:GRAPH.edges].rearrange("(a n) -> a n", a=50),
                         T["src"].rearrange("(a n) -> a n", a=50)).then_inc(moved, 16)
            sp.dma_start(T["g_dst"][0:GRAPH.edges].rearrange("(a n) -> a n", a=50),
                         T["dst"].rearrange("(a n) -> a n", a=50)).then_inc(moved, 16)
            sp.wait_ge(filled, 2)
            sp.dma_start(T["x0"][N:NP, :], zero[0:tail, :]).then_inc(moved, 16)
            sp.dma_start(T["g_src"][GRAPH.edges:].rearrange("(p a) -> p a", a=1),
                         pad_dst[0:epad, :]).then_inc(moved, 16)
            sp.dma_start(T["g_dst"][GRAPH.edges:].rearrange("(p a) -> p a", a=1),
                         pad_dst[0:epad, :]).then_inc(moved, 16)
            sp.wait_ge(moved, 96)


def stage_sort(nc, T, K):
    U = 8
    G = 4
    TURNS = HOP_TILES // U
    with ExitStack() as ctx:
        s = Scope(nc, ctx, "s")
        ends = s.sb("ends", [P, 2, HOP_TILES], I32)
        hi_i = s.sb("hi_i", [P, HOP_TILES], I32)
        lo_i = s.sb("lo_i", [P, HOP_TILES], I32)
        hi = s.sb("hi", [P, HOP_TILES])
        lo = s.sb("lo", [P, HOP_TILES])
        one_lo = s.sb("one_lo", [P, 2, U, P], BF16)
        one_hi = s.sb("one_hi", [P, 2, U, NODE_TILES], BF16)
        seen = s.sb("seen", [P, (HOP_TILES + 1) * NODE_TILES])
        seen_t = seen[:, :].rearrange("p (t c) -> p t c", c=NODE_TILES)
        base1 = s.sb("base1", [P, NODE_TILES])
        total = s.sb("total", [P, NODE_TILES])
        upto = s.sb("upto", [P, NODE_TILES])
        loop_i = s.sb("loop_i", [P, NODE_TILES], I32)
        loop_pos = s.sb("loop_pos", [P, NODE_TILES], I32)
        loop_pair = s.sb("loop_pair", [P, NODE_TILES, 2], I32)
        zeros = s.sb("zeros", [P, NODE_TILES])
        lo32 = s.sb("lo32", [P, U, P])
        hi32 = s.sb("hi32", [P, U, NODE_TILES])
        lo_t = s.sb("lo_t", [P, U, P])
        same = s.sb("same", [P, U, P])
        picked = s.sb("picked", [P, U, NODE_TILES])
        pos = s.sb("pos", [P, U])
        pos_i = s.sb("pos_i", [P, 2, U], I32)
        pair = s.sb("pair", [P, 2, U, 2], I32)
        pp = s.ps("pp", [P, 8, 512])
        loaded = s.sem("loaded")
        hot = s.sem("hot")
        counted = s.sem("counted")
        summed = s.sem("summed")
        tot_ready = s.sem("tot_ready")
        tot_summed = s.sem("tot_summed")
        base_ready = s.sem("base_ready")
        loops_ready = s.sem("loops_ready")
        hot32 = s.sem("hot32")
        turned = s.sem("turned")
        turned_sb = s.sem("turned_sb")
        eq_ready = s.sem("eq_ready")
        eq_masked = s.sem("eq_masked")
        ranked = s.sem("ranked")
        placed = s.sem("placed")
        iota_done = s.sem("iota_done")
        put = [s.gather_sem("put0"), s.gather_sem("put1")]
        put_loop = s.gather_sem("put_loop")
        block = ctx.enter_context(nc.Block())
        C8 = U * NODE_TILES

        @block.sync
        def _(sp):
            for k in range(2):
                sp.dma_start(ends[:, k, :], T["L0_ffn_edge_index"][k].rearrange("(p t) -> p t", p=P)).then_inc(loaded, 16)

        @block.vector
        def _(dve):
            link = Tally(dve, s.sem("dve"))

            def build(h, t0):
                dve.tensor_tensor(one_lo[:, h, :, :], K["frow"][:, :].unsqueeze(1).broadcast_to((P, U, P)),
                                  lo[:, bass.ds(t0, U)].unsqueeze(2).broadcast_to((P, U, P)), ALU.is_equal)
                dve.tensor_tensor(one_hi[:, h, :, :],
                                  K["frow"][:, 0:NODE_TILES].unsqueeze(1).broadcast_to((P, U, NODE_TILES)),
                                  hi[:, bass.ds(t0, U)].unsqueeze(2).broadcast_to((P, U, NODE_TILES)),
                                  ALU.is_equal).then_inc(hot, 1)

            def add(h, t0):
                for u in range(U):
                    link.done(dve.tensor_tensor(seen_t[:, bass.ds(t0 + u + 1, 1), :], seen_t[:, bass.ds(t0 + u, 1), :],
                                                pp[:, h:h + 1, u * NODE_TILES:(u + 1) * NODE_TILES], ALU.add))

            dve.memset(zeros[:, :], 0.0)
            link.done(dve.memset(seen_t[:, 0, :], 0.0))
            dve.wait_ge(loaded, 32)
            dve.tensor_scalar(hi_i[:, :], ends[:, 1, :], 7, None, ALU.arith_shift_right)
            link.done(dve.tensor_scalar(lo_i[:, :], ends[:, 1, :], P - 1, None, ALU.bitwise_and))
            dve.tensor_copy(hi[:, :], hi_i[:, :])
            link.done(dve.tensor_copy(lo[:, :], lo_i[:, :]))
            with dve.Fori(0, TURNS // 2) as i:
                link.loop(i, 2 * U)
                for h in range(2):
                    dve.wait_ge(counted, 2 * i + h)
                    build(h, (2 * i + h) * U)
                for h in range(2):
                    dve.wait_ge(counted, 2 * i + h + 1)
                    add(h, (2 * i + h) * U)
                    dve.sem_inc(summed, 1)
            link.leave(TURNS // 2)
            link.done(dve.tensor_scalar(total[:, :], seen_t[:, HOP_TILES, :], 1.0, None, ALU.add))
            dve.sem_inc(tot_ready, 1)
            dve.wait_ge(tot_summed, 1)
            link.done(dve.tensor_copy(base1[:, :], pp[:, 2, 0:NODE_TILES]))
            link.done(dve.tensor_tensor_scan(upto[:, :], zeros[:, :], base1[:, :], 0.0, ALU.add, ALU.add))
            link.done(dve.tensor_tensor(upto[:, :], upto[:, :], base1[:, :], ALU.subtract))
            link.done(dve.tensor_tensor(upto[:, :], upto[:, :], pp[:, 3, 0:NODE_TILES], ALU.add))
            link.done(dve.tensor_copy(loop_pos[:, :], upto[:, :]))
            link.done(dve.tensor_scalar(base1[:, :], upto[:, :], 1.0, None, ALU.add))
            dve.sem_inc(base_ready, 1)
            dve.wait_ge(iota_done, 1)
            dve.tensor_copy(loop_pair[:, :, 0], loop_i[:, :])
            link.done(dve.tensor_copy(loop_pair[:, :, 1], loop_i[:, :]))
            dve.sem_inc(loops_ready, 1)
            with dve.Fori(0, TURNS // 2) as i:
                link.loop(i, 12)
                for h in range(2):
                    g = 2 * i + h
                    t0 = g * U
                    dve.tensor_tensor(lo32[:, :, :], K["frow"][:, :].unsqueeze(1).broadcast_to((P, U, P)),
                                      lo[:, bass.ds(t0, U)].unsqueeze(2).broadcast_to((P, U, P)), ALU.is_equal)
                    link.done(dve.tensor_tensor(hi32[:, :, :],
                                                K["frow"][:, 0:NODE_TILES].unsqueeze(1).broadcast_to((P, U, NODE_TILES)),
                                                hi[:, bass.ds(t0, U)].unsqueeze(2).broadcast_to((P, U, NODE_TILES)),
                                                ALU.is_equal))
                    dve.sem_inc(hot32, 1)
                    dve.wait_ge(eq_ready, g + 1)
                    for q in range(2):
                        link.done(dve.tensor_tensor(same[:, q * G:(q + 1) * G, :],
                                                    pp[:, 2 + q, :].rearrange("p (g c) -> p g c", g=G),
                                                    K["below"][:, :].unsqueeze(1).broadcast_to((P, G, P)), ALU.mult))
                    dve.sem_inc(eq_masked, 1)
                    dve.wait_ge(ranked, g + 1)
                    link.done(dve.tensor_tensor(picked[:, :, :], pp[:, 4, 0:C8].rearrange("p (u c) -> p u c", u=U),
                                                hi32[:, :, :], ALU.mult))
                    link.done(dve.tensor_reduce(pos[:, :], picked[:, :, :], AX, ALU.add))
                    dve.wait_ge(put[h], 16 * U * i)
                    dve.tensor_copy(pos_i[:, h, :], pos[:, :])
                    dve.tensor_copy(pair[:, h, :, 0], ends[:, 0, bass.ds(t0, U)])
                    link.done(dve.tensor_copy(pair[:, h, :, 1], ends[:, 1, bass.ds(t0, U)]))
                    dve.sem_inc(placed, 1)
            link.leave(TURNS // 2)

        @block.tensor
        def _(pe):
            with pe.Fori(0, TURNS // 2) as i:
                for h in range(2):
                    pe.wait_ge(hot, 2 * i + h + 1)
                    pe.wait_ge(summed, 2 * i + h)
                    for u in range(U):
                        mm = pe.matmul(pp[:, h, u * NODE_TILES:(u + 1) * NODE_TILES], one_lo[:, h, u, :],
                                       one_hi[:, h, u, :], start=True, stop=True)
                    mm.then_inc(counted, 1)
            pe.wait_ge(tot_ready, 1)
            pe.matmul(pp[:, 2, 0:NODE_TILES], K["ones"][:, :], total[:, :], start=True, stop=True)
            pe.matmul(pp[:, 3, 0:NODE_TILES], K["below"][:, :], total[:, :], start=True, stop=True).then_inc(tot_summed, 1)
            pe.wait_ge(base_ready, 1)
            with pe.Fori(0, TURNS) as g:
                pe.wait_ge(hot32, g + 1)
                for u in range(U):
                    mm = pe.transpose(pp[:, u // G, (u % G) * P:(u % G + 1) * P], lo32[:, u, :], K["ident"][:, :])
                mm.then_inc(turned, 1)
                pe.wait_ge(turned_sb, g + 1)
                for u in range(U):
                    mm = pe.matmul(pp[:, 2 + u // G, (u % G) * P:(u % G + 1) * P], lo_t[:, u, :], lo_t[:, u, :],
                                   start=True, stop=True)
                mm.then_inc(eq_ready, 1)
                pe.wait_ge(eq_masked, g + 1)
                for u in range(U):
                    rank = pp[:, 4, u * NODE_TILES:(u + 1) * NODE_TILES]
                    pe.matmul(rank, lo_t[:, u, :], seen_t[:, bass.ds(g * U + u, 1), :], start=True, stop=False)
                    pe.matmul(rank, lo_t[:, u, :], base1[:, :], start=False, stop=False)
                    mm = pe.matmul(rank, same[:, u, :], hi32[:, u, :], start=False, stop=True)
                mm.then_inc(ranked, 1)

        @block.scalar
        def _(act):
            with act.Fori(0, TURNS) as g:
                act.wait_ge(turned, g + 1)
                act.activation(lo_t[:, 0:G, :], pp[:, 0, :].rearrange("p (g c) -> p g c", g=G), ACT.Copy)
                act.activation(lo_t[:, G:U, :], pp[:, 1, :].rearrange("p (g c) -> p g c", g=G),
                               ACT.Copy).then_inc(turned_sb, 1)

        @block.gpsimd
        def _(pool):
            pool.iota(loop_i[:, :], pattern=[[P, NODE_TILES]], base=0, channel_multiplier=1).then_inc(iota_done, 1)
            pool.wait_ge(loops_ready, 1)
            for c in range(NODE_TILES):
                pool.indirect_dma_start(out=T["f_pairs"], out_offset=bass.IndirectOffsetOnAxis(ap=loop_pos[:, c:c + 1], axis=0),
                                        in_=loop_pair[:, c, :], in_offset=None).then_inc(put_loop, 16)
            with pool.Fori(0, TURNS // 2) as i:
                for h in range(2):
                    pool.wait_ge(placed, 2 * i + h + 1)
                    pool.nop(nofuse=True)
                    for u in range(U):
                        pool.indirect_dma_start(out=T["f_pairs"],
                                                out_offset=bass.IndirectOffsetOnAxis(ap=pos_i[:, h, u:u + 1], axis=0),
                                                in_=pair[:, h, u, :], in_offset=None).then_inc(put[h], 16)
            pool.wait_ge(put[0], 16 * U * (TURNS // 2))
            pool.wait_ge(put[1], 16 * U * (TURNS // 2))
            pool.wait_ge(put_loop, 16 * NODE_TILES)


def stage_split(nc, T, K):
    n = HOP.tiles
    with ExitStack() as ctx:
        s = Scope(nc, ctx, "p")
        pairs = s.sb("pairs", [P, n, 2], I32)
        ends = s.sb("ends", [P, 2, n], I32)
        loaded = s.sem("loaded")
        split = s.sem("split")
        stored = s.sem("stored")
        block = ctx.enter_context(nc.Block())

        @block.sync
        def _(sp):
            sp.dma_start(pairs[:, :, :], T["f_pairs"].rearrange("(p n) c -> p n c", p=P)).then_inc(loaded, 16)
            sp.wait_ge(split, 2)
            sp.dma_start(T["f_src"].rearrange("(p n) -> p n", p=P), ends[:, 0, :]).then_inc(stored, 16)
            sp.dma_start(T["f_dst"].rearrange("(p n) -> p n", p=P), ends[:, 1, :]).then_inc(stored, 16)
            sp.wait_ge(stored, 32)

        @block.vector
        def _(dve):
            dve.wait_ge(loaded, 16)
            for k in range(2):
                dve.tensor_copy(ends[:, k, :], pairs[:, :, k]).then_inc(split, 1)


def stage_schedule(nc, T, K, L):
    B, W = L.blocks, L.blocks * P
    with ExitStack() as ctx:
        s = Scope(nc, ctx, "m" + L.name)
        last_i = s.sb("last_i", [P, L.tile_blocks], I32)
        last = s.sb("last", [P, L.tile_blocks])
        num_i = s.sb("num_i", [P, max(B, L.tile_blocks)], I32)
        num = s.sb("num", [P, max(B, L.tile_blocks)])
        srow_i = s.sb("srow_i", [P, W], I32)
        srow = s.sb("srow", [P, W])
        left = s.sb("left", [P, L.tile_blocks, W], BF16)
        ones = s.sb("ones", [P, 1], BF16)
        j_of = s.sb("j_of", [P, B])
        i_of = s.sb("i_of", [P, B])
        far = s.sb("far", [P, B])
        j_idx = s.sb("j_idx", [P, B], I32)
        i_row = s.sb("i_row", [1, W])
        i_row_i = s.sb("i_row_i", [1, W], I32)
        j_row_i = s.sb("j_row_i", [1, W], I32)
        got = s.sb("got", [P, 2, B, P], I32)
        val = s.sb("val", [P, 2, B, P])
        rel = s.sb("rel", [P, B, P])
        src_t = s.sb("src_t", [P, W], I32)
        rel_t = s.sb("rel_t", [P, W])
        pj = s.ps("pj", [P, 512])
        prow = s.ps("prow", [1, 2, 512])
        pt = s.ps("pt", [P, 4, 512])
        loaded = s.sem("loaded")
        iotas = s.sem("iotas")
        filled = s.sem("filled")
        marked = s.sem("marked")
        placed = s.sem("placed")
        j_ready = s.sem("j_ready")
        got_rows = s.gather_sem("got_rows")
        rel_ready = s.sem("rel_ready")
        turned = s.sem("turned")
        stored = s.sem("stored")
        t_ready = s.sem("t_ready")
        block = ctx.enter_context(nc.Block())
        full = L.tiles // P * P
        rest = L.tiles - full
        dst_rows = T[L.name + "_dst"].rearrange("(j e) -> j e", e=P)
        src_rows = T[L.name + "_src"].rearrange("(j e) -> j e", e=P)
        HW = W // 2

        @block.gpsimd
        def _(pool):
            pool.iota(num_i[:, :], pattern=[[P, num_i.shape[1]]], base=0, channel_multiplier=1).then_inc(iotas, 1)
            pool.iota(srow_i[:, :], pattern=[[1, W]], base=0, channel_multiplier=0).then_inc(iotas, 1)
            pool.wait_ge(j_ready, 1)
            for b in range(B):
                for k, rows in enumerate((src_rows, dst_rows)):
                    pool.indirect_dma_start(out=got[:, k, b, :], out_offset=None, in_=rows,
                                            in_offset=bass.IndirectOffsetOnAxis(ap=j_idx[:, b:b + 1], axis=0)
                                            ).then_inc(got_rows, 16)

        @block.sync
        def _(sp):
            sp.wait_ge(filled, 1)
            with nc.allow_non_contiguous_dma(reason="one destination of each edge tile"):
                sp.dma_start(last_i[:, 0:full // P], dst_rows[0:full, P - 1:P].rearrange("(b p) a -> p (b a)", p=P)
                             ).then_inc(loaded, 16)
                sp.dma_start(last_i[0:rest, full // P:full // P + 1], dst_rows[full:L.tiles, P - 1:P]).then_inc(loaded, 16)
            sp.wait_ge(rel_ready, 1)
            sp.dma_start(T[L.name + "_rel_rows"].rearrange("(b s) e -> s b e", s=P), rel[:, :, :]).then_inc(stored, 16)
            sp.dma_start(T[L.name + "_key_rows"].rearrange("(b s) e -> s b e", s=P), val[:, 1, :, :]).then_inc(stored, 16)
            sp.dma_start(T[L.name + "_i_row"].rearrange("(a s) -> a s", a=1), i_row_i[:, :]).then_inc(stored, 16)
            sp.dma_start(T[L.name + "_j_row"].rearrange("(a s) -> a s", a=1), j_row_i[:, :]).then_inc(stored, 16)
            sp.wait_ge(t_ready, 1)
            sp.dma_start(T[L.name + "_src_t"], src_t[:, 0:L.steps]).then_inc(stored, 16)
            sp.dma_start(T[L.name + "_rel_t"], rel_t[:, 0:L.steps]).then_inc(stored, 16)
            sp.wait_ge(stored, 96)

        @block.vector
        def _(dve):
            link = Tally(dve, s.sem("dve"))
            dve.memset(ones[:, :], 1.0)
            dve.memset(last_i[:, :], 1 << 28).then_inc(filled, 1)
            dve.wait_ge(iotas, 2)
            dve.tensor_copy(num[:, :], num_i[:, :])
            link.done(dve.tensor_copy(srow[:, :], srow_i[:, :]))
            dve.wait_ge(loaded, 32)
            link.done(dve.tensor_scalar(last_i[:, :], last_i[:, :], 7, None, ALU.arith_shift_right))
            link.done(dve.tensor_copy(last[:, :], last_i[:, :]))
            link.done(dve.tensor_tensor(last[:, :], last[:, :], num[:, 0:L.tile_blocks], ALU.add))
            for b in range(L.tile_blocks):
                link.done(dve.tensor_scalar(left[:, b, :], srow[:, :], last[:, b:b + 1], None, ALU.is_gt))
            dve.sem_inc(marked, 1)
            dve.wait_ge(placed, 1)
            link.done(dve.tensor_copy(j_of[:, :], pj[:, 0:B]))
            for h in range(2):
                link.done(dve.tensor_tensor(i_row[:, h * HW:(h + 1) * HW], srow[0:1, h * HW:(h + 1) * HW],
                                            prow[:, h, 0:HW], ALU.subtract))
            link.done(dve.tensor_scalar(i_row[:, :], i_row[:, :], float(NODE_TILES - 1), None, ALU.min))
            dve.tensor_copy(i_row_i[:, :], i_row[:, :])
            dve.tensor_tensor(j_row_i[:, :], srow[0:1, :], i_row[:, :], ALU.subtract)
            link.done(dve.tensor_tensor(i_of[:, :], num[:, 0:B], j_of[:, :], ALU.subtract))
            link.done(dve.tensor_scalar(j_of[:, :], j_of[:, :], float(L.tiles - 1), None, ALU.min))
            link.done(dve.tensor_copy(j_idx[:, :], j_of[:, :]))
            dve.sem_inc(j_ready, 1)
            dve.tensor_scalar(far[:, :], num[:, 0:B], float(L.real_steps) - 0.5, FAR, ALU.is_gt, ALU.mult)
            link.done(dve.tensor_scalar(i_of[:, :], i_of[:, :], float(P), None, ALU.mult))
            link.done(dve.tensor_tensor(i_of[:, :], i_of[:, :], far[:, :], ALU.add))
            dve.wait_ge(got_rows, 32 * B)
            link.done(dve.tensor_copy(val[:, :, :, :], got[:, :, :, :]))
            link.done(dve.tensor_tensor(rel[:, :, :], val[:, 1, :, :], i_of[:, :].unsqueeze(2).broadcast_to((P, B, P)),
                                        ALU.subtract))
            dve.sem_inc(rel_ready, 1)
            dve.wait_ge(turned, 1)
            for k, to in enumerate((src_t, rel_t)):
                for h in range(2):
                    w = min(512, W - h * 512)
                    link.done(dve.tensor_copy(to[:, h * 512:h * 512 + w], pt[:, 2 * k + h, 0:w]))
            dve.sem_inc(t_ready, 1)

        @block.tensor
        def _(pe):
            pe.wait_ge(marked, 1)
            for b in range(B):
                for c in range(L.tile_blocks):
                    pe.matmul(pj[:, b:b + 1], left[:, c, b * P:(b + 1) * P], ones[:, :],
                              start=(c == 0), stop=(c == L.tile_blocks - 1))
            for h in range(2):
                for c in range(L.tile_blocks):
                    mm = pe.matmul(prow[:, h, 0:HW], ones[:, :], left[:, c, h * HW:(h + 1) * HW],
                                   start=(c == 0), stop=(c == L.tile_blocks - 1))
            mm.then_inc(placed, 1)
            pe.wait_ge(rel_ready, 1)
            for k in range(2):
                for b in range(B):
                    of = val[:, 0, b, :] if k == 0 else rel[:, b, :]
                    mm = pe.transpose(pt[:, 2 * k + b // 4, (b % 4) * P:(b % 4 + 1) * P], of, K["ident"][:, :])
            mm.then_inc(turned, 1)


def rows_of(ap):
    return ap.rearrange("(t p) f -> p t f", p=P)


class Norm:

    def __init__(self, s, turn=True):
        self.x = s.sb("x", [P, TPC, D])
        self.xn = s.sb("xn", [P, TPC, D])
        self.stat = s.sb("stat", [P, TPC, 6])
        self.mv = s.sb("mv", [P, TPC, 2])
        self.sd = s.sb("sd", [P, TPC])
        self.rstd = s.sb("rstd", [P, TPC])
        self.x_loaded = s.sem("x_loaded")
        self.var_ready = s.sem("var_ready")
        self.sd_ready = s.sem("sd_ready")
        self.xn_ready = s.sem("xn_ready")
        if turn:
            self.xt = s.sb("xt", [P, 2, ROWS])
            self.pt = s.ps("pt", [P, 4, 512])
            self.turned = s.sem("turned")
            self.xt_ready = s.sem("xt_ready")

    def load(self, sp, table, c):
        sp.dma_start(self.x[:, :, :], table[bass.ds(c * ROWS, ROWS), :].rearrange("(t p) f -> p t f", p=P)
                     ).then_inc(self.x_loaded, 16)

    def vector(self, dve, link, c, x=None, out=None):
        x = self.x if x is None else x
        out = self.xn if out is None else out
        for t in range(TPC):
            ins = dve.bn_stats(self.stat[:, t, :], x[:, t, :])
        link.done(ins)
        dve.nop(nofuse=True)
        for t in range(TPC):
            ins = dve.bn_aggr(self.mv[:, t, :], self.stat[:, t, :])
        ins.then_inc(self.var_ready, 1)
        dve.wait_ge(self.sd_ready, c + 1)
        link.done(dve.reciprocal(self.rstd[:, :], self.sd[:, :]))
        for t in range(TPC):
            ins = dve.tensor_scalar(out[:, t, :], x[:, t, :], self.mv[:, t, 0:1], self.rstd[:, t:t + 1],
                                    ALU.subtract, ALU.mult)
        return ins

    def scalar(self, act, K, c):
        act.wait_ge(self.var_ready, c + 1)
        act.activation(self.sd[:, :], self.mv[:, :, 1], ACT.Sqrt, bias=K["eps"][:, 0:1]).then_inc(self.sd_ready, 1)

    def tensor(self, pe, K, c):
        pe.wait_ge(self.xn_ready, c + 1)
        for f in range(2):
            for t in range(TPC):
                ins = pe.transpose(self.pt[:, 2 * f + t // 4, (t % 4) * P:(t % 4 + 1) * P],
                                   self.xn[:, t, f * P:(f + 1) * P], K["ident"][:, :])
        ins.then_inc(self.turned, 1)

    def scalar_turned(self, act, c):
        act.wait_ge(self.turned, c + 1)
        for f in range(2):
            for h in range(2):
                w = min(512, ROWS - h * 512)
                ins = act.activation(self.xt[:, f, h * 512:h * 512 + w], self.pt[:, 2 * f + h, 0:w], ACT.Copy)
        ins.then_inc(self.xt_ready, 1)


def stage_l0_project(nc, T, K):
    with ExitStack() as ctx:
        s = Scope(nc, ctx, "q")
        n = Norm(s)
        w = s.sb("w", [P, 4, 2, D])
        wt = s.sb("wt", [P, 2, 4 * D])
        bias = s.sb("bias", [P, 4 * D])
        out = s.sb("out", [P, TPC, 4 * D])
        pq = s.ps("pq", [P, 2, 2 * 512])
        loaded = s.sem("loaded")
        w_turned = s.sem("w_turned")
        wt_ready = s.sem("wt_ready")
        projected = s.sem("projected")
        biased = s.sem("biased")
        stored = s.sem("stored")
        block = ctx.enter_context(nc.Block())
        names = ("q", "k", "v", "skip")

        @block.sync
        def _(sp):
            n.load(sp, T["x0"], 0)
            for k, m in enumerate(names):
                sp.dma_start(w[:, k, :, :], T["L0_gnn_W" + m].rearrange("(a p) f -> p a f", p=P)).then_inc(loaded, 16)
                sp.dma_start(bias[:, k * D:(k + 1) * D], bcast_rows(T["L0_gnn_b" + m], P)).then_inc(loaded, 16)
            with sp.Fori(0, CHUNKS) as c:
                sp.wait_ge(n.xn_ready, c + 1)
                n.load(sp, T["x0"], (c + 1) % CHUNKS)
                sp.wait_ge(biased, TPC * (c + 1))
                for k, m in enumerate(names):
                    sp.dma_start(T["l0_" + m][bass.ds(c * ROWS, ROWS), :].rearrange("(t p) f -> p t f", p=P),
                                 out[:, :, k * D:(k + 1) * D]).then_inc(stored, 16)
            sp.wait_ge(stored, 64 * CHUNKS)
            sp.wait_ge(n.x_loaded, 16 * (CHUNKS + 1))

        @block.vector
        def _(dve):
            link = Tally(dve, s.sem("dve"))
            with dve.Fori(0, CHUNKS) as c:
                link.loop(c, 2)
                dve.wait_ge(n.x_loaded, 16 * c + 16)
                n.vector(dve, link, c).then_inc(n.xn_ready, 1)
                dve.wait_ge(loaded, 128)
                dve.wait_ge(stored, 64 * c)
                for t in range(TPC):
                    dve.wait_ge(projected, TPC * c + t + 1)
                    dve.tensor_tensor(out[:, t, :], pq[:, t % 2, :], bias[:, :], ALU.add).then_inc(biased, 1)
            link.leave(CHUNKS)

        @block.scalar
        def _(act):
            act.wait_ge(w_turned, 1)
            for k in range(4):
                for f in range(2):
                    ins = act.activation(wt[:, f, k * D:(k + 1) * D], n.pt[:, k, f * D:(f + 1) * D], ACT.Copy)
            ins.then_inc(wt_ready, 1)
            with act.Fori(0, CHUNKS) as c:
                n.scalar(act, K, c)
                n.scalar_turned(act, c)

        @block.tensor
        def _(pe):
            pe.wait_ge(loaded, 128)
            for k in range(4):
                for f in range(2):
                    for a in range(2):
                        ins = pe.transpose(n.pt[:, k, f * D + a * P:f * D + (a + 1) * P],
                                           w[:, k, a, f * P:(f + 1) * P], K["ident"][:, :])
            ins.then_inc(w_turned, 1)
            pe.wait_ge(wt_ready, 1)
            with pe.Fori(0, CHUNKS) as c:
                n.tensor(pe, K, c)
                pe.wait_ge(n.xt_ready, c + 1)
                for t in range(TPC):
                    g = TPC * c + t
                    pe.wait_ge(biased, g if t < 2 else g - 1)
                    for h in range(2):
                        for f in range(2):
                            ins = pe.matmul(pq[:, t % 2, h * 512:(h + 1) * 512], n.xt[:, f, t * P:(t + 1) * P],
                                            wt[:, f, h * 512:(h + 1) * 512], start=(f == 0), stop=(f == 1))
                    ins.then_inc(projected, 1)


def stage_dot(nc, T, K, L):
    H, U = 4, 4
    TURNS = L.steps // (2 * U)
    with ExitStack() as ctx:
        s = Scope(nc, ctx, "d")
        keys = s.sb("keys", [P, NODE_TILES, D])
        src = s.sb("src", [P, L.steps], I32)
        i_row = s.sb("i_row", [1, L.steps], I32)
        spread = s.sb("spread", [P, 2, U * P])
        hot = s.sb("hot", [P, 2, U, P])
        idx = s.sb("idx", [P, 2, U], I32)
        q = s.sb("q", [P, 2, U, D])
        prod = s.sb("prod", [P, 2, U * D])
        score = s.sb("score", [P, L.steps, H])
        pk = s.ps("pk", [P, 2, U * D])
        loaded = s.sem("loaded")
        spread_in = [s.sem(f"spread_in{h}") for h in range(2)]
        hot_ready = s.sem("hot_ready")
        idx_ready = s.sem("idx_ready")
        q_in = [s.gather_sem(f"q_in{k}") for k in range(2)]
        keys_out = s.sem("keys_out")
        multiplied = s.sem("multiplied")
        scored = s.sem("scored")
        stored = s.sem("stored")
        block = ctx.enter_context(nc.Block())
        rel_flat = T[L.name + "_rel_rows"].rearrange("s e -> (s e)")

        @block.sync
        def _(sp):
            sp.dma_start(src[:, :], T[L.name + "_src_t"]).then_inc(loaded, 16)
            sp.dma_start(i_row[:, :], T[L.name + "_i_row"][0:L.steps].rearrange("(a s) -> a s", a=1)).then_inc(loaded, 16)
            sp.dma_start(keys[:, :, :], rows_of(T["l0_k"])).then_inc(loaded, 16)
            with sp.Fori(0, TURNS) as i:
                for h in range(2):
                    sp.wait_ge(hot_ready, 2 * i)
                    sp.dma_start(spread[:, h, :], rel_flat[bass.ds((2 * i + h) * U * P, U * P)].partition_broadcast(P)
                                 ).then_inc(spread_in[h], 16)
            sp.wait_ge(scored, 2 * TURNS)
            sp.dma_start(T["score"][:, 0:L.steps * H], score[:, :, :].rearrange("p s h -> p (s h)")).then_inc(stored, 16)
            sp.wait_ge(stored, 16)

        @block.gpsimd
        def _(pool):
            with pool.Fori(0, TURNS) as i:
                for h in range(2):
                    pool.wait_ge(idx_ready, 2 * i + h + 1)
                    pool.nop(nofuse=True)
                    for u in range(U):
                        pool.indirect_dma_start(out=q[:, h, u, :], out_offset=None, in_=T["l0_q"],
                                                in_offset=bass.IndirectOffsetOnAxis(ap=idx[:, h, u:u + 1], axis=0)
                                                ).then_inc(q_in[h], 16)

        @block.vector
        def _(dve):
            dve.wait_ge(loaded, 48)
            for h in range(2):
                dve.tensor_copy(idx[:, h, :], src[:, h * U:(h + 1) * U]).then_inc(idx_ready, 1)
            with dve.Fori(0, TURNS) as i:
                for h in range(2):
                    dve.wait_ge(spread_in[h], 16 * (i + 1))
                    dve.wait_ge(keys_out, 2 * i)
                    dve.tensor_scalar(hot[:, h, :, :].rearrange("p u e -> p (u e)"), spread[:, h, :], K["pcol"][:, 0:1],
                                      None, ALU.is_equal).then_inc(hot_ready, 1)
                for h in range(2):
                    g = 2 * i + h
                    dve.wait_ge(keys_out, g + 1)
                    dve.wait_ge(q_in[h], 16 * U * (i + 1))
                    dve.tensor_tensor(prod[:, h, :], pk[:, h, :], q[:, h, :, :].rearrange("p u d -> p (u d)"),
                                      ALU.mult).then_inc(multiplied, 1)
                    dve.wait_ge(multiplied, g + 1)
                    dve.tensor_copy(idx[:, h, :], src[:, bass.ds((g + 2) % (2 * TURNS) * U, U)]).then_inc(idx_ready, 1)
                    dve.tensor_reduce(score[:, bass.ds(g * U, U), :].rearrange("p u h -> p (u h)"),
                                      prod[:, h, :].rearrange("p (a c) -> p a c", c=D // H), AX, ALU.add).then_inc(scored, 1)

        @block.tensor
        def _(pe):
            pe.wait_ge(loaded, 48)
            with pe.Fori(0, TURNS) as i:
                for h in range(2):
                    g = 2 * i + h
                    tiles = [pe.value_load(i_row[0:1, bass.ds(g * U + u, 1)], min_val=0, max_val=NODE_TILES - 1)
                             for u in range(U)]
                    pe.wait_ge(hot_ready, g + 1)
                    pe.wait_ge(multiplied, 2 * i)
                    for u in range(U):
                        mm = pe.matmul(pk[:, h, u * D:(u + 1) * D], hot[:, h, u, :],
                                       keys[:, bass.ds(tiles[u], 1), :], start=True, stop=True)
                    mm.then_inc(keys_out, 1)


def stage_softmax(nc, T, K, L, H, scale):
    B, S = L.blocks, L.steps
    W = B * P
    last = S - (B - 1) * P
    with ExitStack() as ctx:
        s = Scope(nc, ctx, "x" + L.name + str(H))
        score = s.sb("score", [P, S, H])
        one = s.sb("one", [P, W])
        rows = s.sb("rows", [P, B, P])
        lane = s.sb("lane", [P, S])
        key = s.sb("key", [P, S + 2])
        rel = s.sb("rel", [P, S])
        off = s.sb("off", [P, S])
        from_left = s.sb("from_left", [P, S])
        from_right = s.sb("from_right", [P, S])
        in_first = s.sb("in_first", [P, S])
        in_last = s.sb("in_last", [P, S])
        val = s.sb("val", [P, S])
        fwd = s.sb("fwd", [P, S])
        bwd = s.sb("bwd", [P, S])
        edge = s.sb("edge", [P, 2])
        spread = s.sb("spread", [P, 2, P])
        match = s.sb("match", [P, 2, 2, P])
        cand = s.sb("cand", [P, 2, 2, P])
        top = s.sb("top", [P, 2])
        weight = s.sb("weight", [P, S, H])
        pt = s.ps("pt", [P, 2, 512])
        pb = s.ps("pb", [P, 2, 512])
        pw = s.ps("pw", [P, 2, 512])
        loaded = s.sem("loaded")
        one_ready = s.sem("one_ready")
        turned = s.sem("turned")
        rows_ready = s.sem("rows_ready")
        rows_out = s.sem("rows_out")
        lane_in = s.sem("lane_in")
        spread_ready = s.sem("spread_ready")
        spread_out = s.sem("spread_out")
        diff_ready = s.sem("diff_ready")
        exp_ready = s.sem("exp_ready")
        back_out = s.sem("back_out")
        back_in = s.sem("back_in")
        back_turned = s.sem("back_turned")
        weighted = s.sem("weighted")
        stored = s.sem("stored")
        block = ctx.enter_context(nc.Block())
        flat = T["lanes"]
        by_lane = flat[0:P * S].rearrange("(p s) -> p s", p=P)
        head_rows = flat[0:(B - 1) * P * P].rearrange("(b s e) -> s b e", s=P, e=P)
        tail_rows = flat[(B - 1) * P * P:S * P].rearrange("(s e) -> s e", e=P)

        @block.sync
        def _(sp):
            sp.dma_start(score[:, :, :].rearrange("p s h -> p (s h)"), T["score"][:, 0:S * H]).then_inc(loaded, 16)
            for to, of in ((key[:, 1:S + 1], "_key_rows"), (rel[:, :], "_rel_rows")):
                sp.dma_start(to, T[L.name + of].rearrange("s e -> (s e)")[0:P * S].rearrange("(p s) -> p s", p=P)
                             ).then_inc(loaded, 16)
            with sp.Fori(0, H) as h:
                sp.wait_ge(rows_ready, h + 1)
                sp.dma_start(head_rows, rows[:, 0:B - 1, :]).then_inc(rows_out, 16)
                sp.dma_start(tail_rows, rows[0:last, B - 1, :]).then_inc(rows_out, 16)
                sp.wait_ge(rows_out, 32 * (h + 1))
                sp.dma_start(lane[:, :], by_lane).then_inc(lane_in, 16)
                sp.wait_ge(exp_ready, h + 1)
                sp.dma_start(by_lane, val[:, :]).then_inc(back_out, 16)
                sp.wait_ge(back_out, 16 * (h + 1))
                sp.dma_start(rows[:, 0:B - 1, :], head_rows).then_inc(back_in, 16)
                sp.dma_start(rows[0:last, B - 1, :], tail_rows).then_inc(back_in, 16)
            sp.wait_ge(weighted, H)
            sp.dma_start(T["weight"][:, 0:S * H], weight[:, :, :].rearrange("p s h -> p (s h)")).then_inc(stored, 16)
            sp.wait_ge(stored, 16)

        @block.vector
        def _(dve):
            link = Tally(dve, s.sem("dve"))
            dve.memset(one[:, :], 0.0)
            dve.memset(rows[:, :, :], 0.0)
            dve.wait_ge(loaded, 48)
            dve.tensor_scalar(off[:, :], rel[:, :], 0.0, -BIG, ALU.is_lt, ALU.mult)
            link.done(dve.tensor_scalar(lane[:, :], rel[:, :], float(P - 1), -BIG, ALU.is_gt, ALU.mult))
            link.done(dve.tensor_tensor(off[:, :], off[:, :], lane[:, :], ALU.add))
            dve.memset(key[:, 0:1], -1.0)
            link.done(dve.memset(key[:, S + 1:S + 2], -1.0))
            link.done(dve.tensor_tensor(from_left[:, :], key[:, 1:S + 1], key[:, 0:S], ALU.not_equal))
            link.done(dve.tensor_tensor(from_right[:, :], key[:, 1:S + 1], key[:, 2:S + 2], ALU.not_equal))
            dve.tensor_scalar(from_left[:, :], from_left[:, :], -BIG, None, ALU.mult)
            dve.tensor_scalar(from_right[:, :], from_right[:, :], -BIG, None, ALU.mult)
            dve.tensor_scalar(in_first[:, :], key[:, 1:S + 1], key[:, 1:2], -BIG, ALU.not_equal, ALU.mult)
            link.done(dve.tensor_scalar(in_last[:, :], key[:, 1:S + 1], key[:, S:S + 1], -BIG, ALU.not_equal, ALU.mult))
            ends = (key[:, 1:2], key[:, S:S + 1])
            for k in range(2):
                dve.tensor_copy(spread[:, k, :], ends[k].broadcast_to((P, P))).then_inc(spread_ready, 1)
            dve.wait_ge(spread_out, 1)
            for a in range(2):
                for k in range(2):
                    ins = dve.tensor_scalar(match[:, a, k, :], pb[:, k, 0:P], ends[a], -BIG, ALU.not_equal, ALU.mult)
            link.done(ins)
            with dve.Fori(0, H) as h:
                link.loop(h, 11)
                dve.tensor_copy(one[:, 0:S], score[:, :, bass.ds(h, 1)].rearrange("p s a -> p (s a)")).then_inc(one_ready, 1)
                dve.wait_ge(turned, h + 1)
                dve.wait_ge(weighted, h)
                full = min(B - 1, 4)
                dve.tensor_copy(rows[:, 0:full, :], pt[:, 0, 0:full * P].rearrange("p (b e) -> p b e", e=P))
                if B - 1 > 4:
                    dve.tensor_copy(rows[:, 4:B - 1, :], pt[:, 1, 0:(B - 5) * P].rearrange("p (b e) -> p b e", e=P))
                dve.tensor_copy(rows[0:last, B - 1, :], pt[0:last, (B - 1) // 4, (B - 1) % 4 * P:((B - 1) % 4 + 1) * P]
                                ).then_inc(rows_ready, 1)
                dve.wait_ge(lane_in, 16 * (h + 1))
                link.done(dve.tensor_tensor(val[:, :], lane[:, :], off[:, :], ALU.add))
                dve.tensor_tensor_scan(fwd[:, :], from_left[:, :], val[:, :], -BIG, ALU.add, ALU.max)
                link.done(dve.tensor_tensor_scan(bwd[:, ::-1], from_right[:, ::-1], val[:, ::-1], -BIG, ALU.add, ALU.max))
                dve.tensor_copy(spread[:, 0, :], bwd[:, 0:1].broadcast_to((P, P))).then_inc(spread_ready, 1)
                dve.tensor_copy(spread[:, 1, :], fwd[:, S - 1:S].broadcast_to((P, P))).then_inc(spread_ready, 1)
                link.done(dve.tensor_tensor(val[:, :], fwd[:, :], bwd[:, :], ALU.max))
                dve.wait_ge(spread_out, h + 2)
                for a in range(2):
                    ins = dve.tensor_tensor(cand[:, a, :, :], pb[:, :, 0:P], match[:, a, :, :], ALU.add)
                link.done(ins)
                link.done(dve.tensor_reduce(top[:, :], cand[:, :, :, :].rearrange("p a k c -> p a (k c)"), AX, ALU.max))
                link.done(dve.scalar_tensor_tensor(val[:, :], in_first[:, :], top[:, 0:1], val[:, :], ALU.add, ALU.max))
                link.done(dve.scalar_tensor_tensor(val[:, :], in_last[:, :], top[:, 1:2], val[:, :], ALU.add, ALU.max))
                link.done(dve.tensor_tensor(val[:, :], lane[:, :], val[:, :], ALU.subtract))
                link.done(dve.tensor_scalar(val[:, :], val[:, :], 0.0, None, ALU.min))
                dve.sem_inc(diff_ready, 1)
                dve.wait_ge(back_turned, h + 1)
                for b in range(0, B, 4):
                    w = min(512, S - b * P)
                    ins = dve.tensor_copy(weight[:, b * P:b * P + w, bass.ds(h, 1)].rearrange("p s a -> p (s a)"),
                                          pw[:, b // 4, 0:w])
                    link.done(ins)
                dve.sem_inc(weighted, 1)
            link.leave(H)

        @block.scalar
        def _(act):
            with act.Fori(0, H) as h:
                act.wait_ge(diff_ready, h + 1)
                act.activation(val[:, :], val[:, :], ACT.Exp, scale=scale).then_inc(exp_ready, 1)

        @block.tensor
        def _(pe):
            pe.wait_ge(spread_ready, 2)
            for k in range(2):
                mm = pe.transpose(pb[:, k, 0:P], spread[:, k, :], K["ident"][:, :])
            mm.then_inc(spread_out, 1)
            with pe.Fori(0, H) as h:
                pe.wait_ge(one_ready, h + 1)
                for b in range(B):
                    mm = pe.transpose(pt[:, b // 4, (b % 4) * P:(b % 4 + 1) * P], one[:, b * P:(b + 1) * P], K["ident"][:, :])
                mm.then_inc(turned, 1)
                pe.wait_ge(spread_ready, 2 * h + 4)
                for k in range(2):
                    mm = pe.transpose(pb[:, k, 0:P], spread[:, k, :], K["ident"][:, :])
                mm.then_inc(spread_out, 1)
                pe.wait_ge(back_in, 32 * (h + 1))
                for b in range(B):
                    mm = pe.transpose(pw[:, b // 4, (b % 4) * P:(b % 4 + 1) * P], rows[:, b, :], K["ident"][:, :])
                mm.then_inc(back_turned, 1)


def stage_sum(nc, T, K, L, H, W, table=None):
    U = 4
    TURNS = L.steps // (2 * U)
    C = W // H
    with ExitStack() as ctx:
        s = Scope(nc, ctx, "a" + L.name + str(H))
        acc = s.sb("acc", [P, NODE_TILES, W + H])
        weight = s.sb("weight", [P, L.steps, H])
        rel = s.sb("rel", [P, L.steps])
        i_row = s.sb("i_row", [1, L.steps], I32)
        hot = s.sb("hot", [P, 2, U, P])
        rhs = s.sb("rhs", [P, 2, U, W + H])
        BANK = 512
        pa = s.ps("pa", [P, 2, U, BANK])
        loaded = s.sem("loaded")
        cleared = s.sem("cleared")
        hot_ready = s.sem("hot_ready")
        rhs_ready = s.sem("rhs_ready")
        summed = s.sem("summed")
        added = s.sem("added")
        stored = s.sem("stored")
        n_loads = 4
        if table is not None:
            src = s.sb("src", [P, L.steps], I32)
            idx = s.sb("idx", [P, 2, U], I32)
            got = s.sb("got", [P, 2, U, W])
            idx_ready = s.sem("idx_ready")
            got_in = [s.gather_sem(f"got_in{h}") for h in range(2)]
        else:
            every = s.sb("every", [P, L.steps, W])
        block = ctx.enter_context(nc.Block())

        @block.sync
        def _(sp):
            if table is not None:
                sp.dma_start(src[:, :], T[L.name + "_src_t"]).then_inc(loaded, 16)
            else:
                sp.dma_start(every[:, :, :], T["f_rows"]).then_inc(loaded, 16)
            sp.dma_start(i_row[:, :], T[L.name + "_i_row"][0:L.steps].rearrange("(a s) -> a s", a=1)).then_inc(loaded, 16)
            sp.dma_start(rel[:, :], T[L.name + "_rel_t"]).then_inc(loaded, 16)
            sp.dma_start(weight[:, :, :].rearrange("p s h -> p (s h)"), T["weight"][:, 0:L.steps * H]).then_inc(loaded, 16)
            sp.wait_ge(added, L.steps)
            sp.dma_start(T["acc"][:, 0:NODE_TILES * (W + H)], acc[:, :, :].rearrange("p t w -> p (t w)")).then_inc(stored, 16)
            sp.wait_ge(stored, 16)

        if table is not None:
            @block.gpsimd
            def _(pool):
                with pool.Fori(0, TURNS) as i:
                    for h in range(2):
                        pool.wait_ge(idx_ready, 2 * i + h + 1)
                        pool.nop(nofuse=True)
                        for u in range(U):
                            pool.indirect_dma_start(out=got[:, h, u, :], out_offset=None, in_=table,
                                                    in_offset=bass.IndirectOffsetOnAxis(ap=idx[:, h, u:u + 1], axis=0)
                                                    ).then_inc(got_in[h], 16)

        @block.vector
        def _(dve):
            dve.memset(acc[:, :, :], 0.0).then_inc(cleared, 1)
            dve.wait_ge(loaded, 16 * n_loads)
            dve.wait_ge(cleared, 1)
            if table is not None:
                for h in range(2):
                    dve.tensor_copy(idx[:, h, :], src[:, h * U:(h + 1) * U]).then_inc(idx_ready, 1)
            with dve.Fori(0, TURNS) as i:
                for h in range(2):
                    g = 2 * i + h
                    dve.wait_ge(summed, 2 * i)
                    dve.tensor_tensor(hot[:, h, :, :], K["frow"][:, :].unsqueeze(1).broadcast_to((P, U, P)),
                                      rel[:, bass.ds(g * U, U)].unsqueeze(2).broadcast_to((P, U, P)),
                                      ALU.is_equal).then_inc(hot_ready, 1)
                    w = weight[:, bass.ds(g * U, U), :]
                    dve.tensor_copy(rhs[:, h, :, W:W + H], w).then_inc(rhs_ready, 1)
                    if table is not None:
                        dve.wait_ge(got_in[h], 16 * U * (i + 1))
                        rows = got[:, h, :, :]
                    else:
                        rows = every[:, bass.ds(g * U, U), :]
                    dve.tensor_tensor(rhs[:, h, :, 0:W].rearrange("p u (h c) -> p u h c", h=H),
                                      rows.rearrange("p u (h c) -> p u h c", h=H),
                                      w.unsqueeze(3).broadcast_to((P, U, H, C)), ALU.mult).then_inc(rhs_ready, 1)
                    if table is not None:
                        dve.wait_ge(rhs_ready, 2 * g + 2)
                        dve.tensor_copy(idx[:, h, :], src[:, bass.ds((g + 2) % (2 * TURNS) * U, U)]).then_inc(idx_ready, 1)
                for h in range(2):
                    g = 2 * i + h
                    tiles = [dve.value_load(i_row[0:1, bass.ds(g * U + u, 1)], min_val=0, max_val=NODE_TILES - 1)
                             for u in range(U)]
                    dve.wait_ge(summed, g + 1)
                    for u in range(U):
                        dve.wait_ge(added, g * U + u)
                        to = acc[:, bass.ds(tiles[u], 1), :].rearrange("p a w -> p (a w)")
                        dve.tensor_tensor(to, to, pa[:, h, u, 0:W + H], ALU.add).then_inc(added, 1)

        @block.tensor
        def _(pe):
            with pe.Fori(0, TURNS) as i:
                for h in range(2):
                    g = 2 * i + h
                    pe.wait_ge(hot_ready, g + 1)
                    pe.wait_ge(rhs_ready, 2 * g + 2)
                    pe.wait_ge(added, 2 * U * i)
                    for u in range(U):
                        mm = pe.matmul(pa[:, h, u, 0:W + H], hot[:, h, u, :], rhs[:, h, u, :], start=True, stop=True)
                    mm.then_inc(summed, 1)


PAIRS = -(-TPC // 2)


def chunk_of(ap, c):
    return ap[bass.ds(c * ROWS, ROWS), :].rearrange("(t p) f -> p t f", p=P)


def over_tiles(ap, tiles=TPC):
    return ap.unsqueeze(1).broadcast_to((P, tiles, ap.shape[1]))


def stage_l0_finish(nc, T, K):
    H, W = 4, D
    with ExitStack() as ctx:
        s = Scope(nc, ctx, "e")
        n = Norm(s, turn=False)
        acc = s.sb("acc", [P, TPC, W + H])
        skip = s.sb("skip", [P, TPC, D])
        x0 = s.sb("x0", [P, TPC, D])
        gates = s.sb("gates", [P, 3, D])
        w_skip = s.sb("w_skip", [P, D])
        w_rst = s.sb("w_rst", [P, D])
        gain = s.sb("gain", [P, D])
        shift = s.sb("shift", [P, D])
        slope = s.sb("slope", [P, 1])
        g_bias = s.sb("g_bias", [P, 1])
        rden = s.sb("rden", [P, TPC, H])
        rst = s.sb("rst", [P, TPC, D])
        t1 = s.sb("t1", [P, TPC, D])
        t2 = s.sb("t2", [P, TPC, D])
        z = s.sb("z", [P, TPC])
        gate = s.sb("gate", [P, TPC])
        out = s.sb("out", [P, TPC, D])
        params = s.sem("params")
        loaded = s.sem("loaded")
        z_ready = s.sem("z_ready")
        gate_ready = s.sem("gate_ready")
        out_ready = s.sem("out_ready")
        stored = s.sem("stored")
        block = ctx.enter_context(nc.Block())
        acc_all = T["acc"][:, 0:NODE_TILES * (W + H)]

        @block.sync
        def _(sp):
            sp.dma_start(gates[:, :, :].rearrange("p a d -> p (a d)"), bcast_rows(T["L0_gnn_Wgate"].rearrange("a n -> (a n)"), P)
                         ).then_inc(params, 16)
            sp.dma_start(gain[:, :], bcast_rows(T["L0_gnn_ln_w"], P)).then_inc(params, 16)
            sp.dma_start(shift[:, :], bcast_rows(T["L0_gnn_ln_b"], P)).then_inc(params, 16)
            sp.dma_start(slope[:, :], bcast_rows(T["L0_gnn_prelu_a"], P)).then_inc(params, 16)
            sp.dma_start(g_bias[:, :], bcast_rows(T["L0_gnn_bgate"], P)).then_inc(params, 16)
            with sp.Fori(0, CHUNKS) as c:
                sp.wait_ge(out_ready, c)
                sp.dma_start(acc[:, :, :].rearrange("p t w -> p (t w)"),
                             acc_all[:, bass.ds(c * (TPC * (W + H)), TPC * (W + H))]).then_inc(loaded, 16)
                sp.dma_start(skip[:, :, :], chunk_of(T["l0_skip"], c)).then_inc(loaded, 16)
                sp.dma_start(x0[:, :, :], chunk_of(T["x0"], c)).then_inc(loaded, 16)
                sp.wait_ge(out_ready, c + 1)
                sp.dma_start(chunk_of(T["x1"], c), out[:, :, :]).then_inc(stored, 16)
            sp.wait_ge(stored, 16 * CHUNKS)

        @block.vector
        def _(dve):
            link = Tally(dve, s.sem("dve"))
            dve.wait_ge(params, 80)
            dve.tensor_tensor(w_skip[:, :], gates[:, 0, :], gates[:, 2, :], ALU.add)
            link.done(dve.tensor_tensor(w_rst[:, :], gates[:, 1, :], gates[:, 2, :], ALU.subtract))
            with dve.Fori(0, CHUNKS) as c:
                link.loop(c, 13)
                dve.wait_ge(loaded, 48 * c + 48)
                link.done(dve.tensor_scalar(rden[:, :, :], acc[:, :, W:W + H], 1e-16, 0.5, ALU.add, ALU.max))
                link.done(dve.reciprocal(rden[:, :, :], rden[:, :, :]))
                dve.tensor_tensor(t1[:, :, :], skip[:, :, :], over_tiles(w_skip[:, :]), ALU.mult)
                link.done(dve.tensor_tensor(rst[:, :, :].rearrange("p t (h c) -> p t h c", h=H),
                                            acc[:, :, 0:W].rearrange("p t (h c) -> p t h c", h=H),
                                            rden[:, :, :].unsqueeze(3).broadcast_to((P, TPC, H, W // H)), ALU.mult))
                link.done(dve.tensor_tensor(t2[:, :, :], rst[:, :, :], over_tiles(w_rst[:, :]), ALU.mult))
                link.done(dve.tensor_tensor(t1[:, :, :], t1[:, :, :], t2[:, :, :], ALU.add))
                dve.tensor_reduce(z[:, :], t1[:, :, :], AX, ALU.add).then_inc(z_ready, 1)
                link.done(dve.tensor_tensor(t2[:, :, :], skip[:, :, :], rst[:, :, :], ALU.subtract))
                dve.wait_ge(gate_ready, c + 1)
                for t in range(TPC):
                    ins = dve.scalar_tensor_tensor(rst[:, t, :], t2[:, t, :], gate[:, t:t + 1], rst[:, t, :],
                                                   ALU.mult, ALU.add)
                link.done(ins)
                link.done(n.vector(dve, link, c, x=rst, out=t1))
                link.done(dve.tensor_tensor(t1[:, :, :], t1[:, :, :], over_tiles(gain[:, :]), ALU.mult))
                link.done(dve.tensor_tensor(t1[:, :, :], t1[:, :, :], over_tiles(shift[:, :]), ALU.add))
                dve.tensor_scalar(t2[:, :, :], t1[:, :, :], 0.0, slope[:, 0:1], ALU.min, ALU.mult)
                link.done(dve.scalar_tensor_tensor(rst[:, :, :].rearrange("p t d -> p (t d)"),
                                                   t1[:, :, :].rearrange("p t d -> p (t d)"), 0.0,
                                                   x0[:, :, :].rearrange("p t d -> p (t d)"), ALU.max, ALU.add))
                dve.wait_ge(stored, 16 * c)
                dve.tensor_tensor(out[:, :, :], rst[:, :, :], t2[:, :, :], ALU.add).then_inc(out_ready, 1)
            link.leave(CHUNKS)

        @block.scalar
        def _(act):
            with act.Fori(0, CHUNKS) as c:
                act.wait_ge(params, 80)
                act.wait_ge(z_ready, c + 1)
                act.activation(gate[:, :], z[:, :], ACT.Sigmoid, bias=g_bias[:, 0:1]).then_inc(gate_ready, 1)
                n.scalar(act, K, c)


def stage_hop_project(nc, T, K):
    H, E = 4, 4
    W = H * E
    with ExitStack() as ctx:
        s = Scope(nc, ctx, "h")
        n = Norm(s)
        w = s.sb("w", [P, 2, W])
        att = s.sb("att", [P, 2, W])
        row = s.sb("row", [P, TPC, W + H])
        t1 = s.sb("t1", [P, 2, TPC * H, E])
        to_dst = s.sb("to_dst", [P, NODE_TILES, H])
        ph = s.ps("ph", [P, 512])
        loaded = s.sem("loaded")
        projected = s.sem("projected")
        row_ready = s.sem("row_ready")
        dst_ready = s.sem("dst_ready")
        stored = s.sem("stored")
        block = ctx.enter_context(nc.Block())

        @block.sync
        def _(sp):
            n.load(sp, T["x1"], 0)
            sp.dma_start(w[:, :, :], T["L0_ffn_W_gat"].rearrange("(a p) n -> p a n", p=P)).then_inc(loaded, 16)
            for k, m in enumerate(("src", "dst")):
                sp.dma_start(att[:, k, :], bcast_rows(T["L0_ffn_att_" + m].rearrange("h e -> (h e)"), P)).then_inc(loaded, 16)
            with sp.Fori(0, CHUNKS) as c:
                sp.wait_ge(n.xn_ready, c + 1)
                n.load(sp, T["x1"], (c + 1) % CHUNKS)
                sp.wait_ge(row_ready, c + 1)
                sp.dma_start(chunk_of(T["f_table"], c), row[:, :, :]).then_inc(stored, 16)
            sp.wait_ge(dst_ready, CHUNKS)
            sp.dma_start(T["f_adst"], to_dst[:, :, :]).then_inc(stored, 16)
            sp.wait_ge(stored, 16 * (CHUNKS + 1))
            sp.wait_ge(n.x_loaded, 16 * (CHUNKS + 1))

        @block.vector
        def _(dve):
            link = Tally(dve, s.sem("dve"))
            dve.wait_ge(loaded, 48)
            with dve.Fori(0, CHUNKS) as c:
                link.loop(c, 4)
                dve.wait_ge(n.x_loaded, 16 * c + 16)
                n.vector(dve, link, c).then_inc(n.xn_ready, 1)
                dve.wait_ge(stored, 16 * c)
                dve.wait_ge(projected, c + 1)
                link.done(dve.tensor_copy(row[:, :, 0:W], ph[:, 0:TPC * W].rearrange("p (t w) -> p t w", w=W)))
                for k in range(2):
                    ins = dve.tensor_tensor(t1[:, k, :, :].rearrange("p (t h) e -> p t (h e)", t=TPC), row[:, :, 0:W],
                                            over_tiles(att[:, k, :]), ALU.mult)
                link.done(ins)
                dve.tensor_reduce(to_dst[:, bass.ds(c * TPC, TPC), :].rearrange("p t h -> p (t h)"), t1[:, 1, :, :],
                                  AX, ALU.add).then_inc(dst_ready, 1)
                dve.tensor_reduce(row[:, :, W:W + H], t1[:, 0, :, :].rearrange("p (t h) e -> p t h e", t=TPC), AX, ALU.add
                                  ).then_inc(row_ready, 1)
            link.leave(CHUNKS)

        @block.scalar
        def _(act):
            with act.Fori(0, CHUNKS) as c:
                n.scalar(act, K, c)
                n.scalar_turned(act, c)

        @block.tensor
        def _(pe):
            pe.wait_ge(loaded, 48)
            with pe.Fori(0, CHUNKS) as c:
                n.tensor(pe, K, c)
                pe.wait_ge(n.xt_ready, c + 1)
                pe.wait_ge(row_ready, c)
                for t in range(TPC):
                    for f in range(2):
                        mm = pe.matmul(ph[:, t * W:(t + 1) * W], n.xt[:, f, t * P:(t + 1) * P], w[:, f, :],
                                       start=(f == 0), stop=(f == 1))
                mm.then_inc(projected, 1)


def stage_pair(nc, T, K, L, H, table, W, at, dst_name, edge_name=None, keep=0):
    U = 4
    TURNS = L.steps // (2 * U)
    with ExitStack() as ctx:
        s = Scope(nc, ctx, "w" + L.name)
        to_dst = s.sb("to_dst", [P, NODE_TILES, H])
        src = s.sb("src", [P, L.steps], I32)
        i_row = s.sb("i_row", [1, L.steps], I32)
        j_row = s.sb("j_row", [1, L.steps], I32)
        spread = s.sb("spread", [P, 2, U * P])
        hot = s.sb("hot", [P, 2, U, P])
        idx = s.sb("idx", [P, 2, U], I32)
        got = s.sb("got", [P, 2, U, W])
        sums = s.sb("sums", [P, 2, U, H])
        score = s.sb("score", [P, L.steps, H])
        pd = s.ps("pd", [P, 2, 512])
        loaded = s.sem("loaded")
        spread_in = [s.sem(f"spread_in{h}") for h in range(2)]
        hot_ready = s.sem("hot_ready")
        idx_ready = s.sem("idx_ready")
        got_in = [s.gather_sem(f"got_in{k}") for k in range(2)]
        dst_out = s.sem("dst_out")
        summed = s.sem("summed")
        scored = s.sem("scored")
        stored = s.sem("stored")
        loads = 4
        if keep:
            kept = s.sb("kept", [P, L.steps, keep])
            was_kept = s.sem("was_kept")
        if edge_name:
            edge = s.sb("edge", [P, L.tiles + 1, H])
            edge_added = s.sem("edge_added")
            loads += 1
        block = ctx.enter_context(nc.Block())
        rel_flat = T[L.name + "_rel_rows"].rearrange("s e -> (s e)")

        @block.sync
        def _(sp):
            sp.dma_start(src[:, :], T[L.name + "_src_t"]).then_inc(loaded, 16)
            for row, name in ((i_row, "_i_row"), (j_row, "_j_row")):
                sp.dma_start(row[:, :], T[L.name + name][0:L.steps].rearrange("(a s) -> a s", a=1)).then_inc(loaded, 16)
            sp.dma_start(to_dst[:, :, :], T[dst_name]).then_inc(loaded, 16)
            if edge_name:
                sp.dma_start(edge[:, :, :], T[edge_name]).then_inc(loaded, 16)
            with sp.Fori(0, TURNS) as i:
                for h in range(2):
                    sp.wait_ge(hot_ready, 2 * i)
                    sp.dma_start(spread[:, h, :], rel_flat[bass.ds((2 * i + h) * U * P, U * P)].partition_broadcast(P)
                                 ).then_inc(spread_in[h], 16)
            sp.wait_ge(scored, 2 * TURNS)
            sp.dma_start(T["score"][:, 0:L.steps * H], score[:, :, :].rearrange("p s h -> p (s h)")).then_inc(stored, 16)
            sp.wait_ge(stored, 16)
            if keep:
                sp.wait_ge(was_kept, 2 * TURNS)
                sp.dma_start(T["f_rows"], kept[:, :, :]).then_inc(stored, 16)
                sp.wait_ge(stored, 32)

        @block.gpsimd
        def _(pool):
            with pool.Fori(0, TURNS) as i:
                for h in range(2):
                    pool.wait_ge(idx_ready, 2 * i + h + 1)
                    pool.nop(nofuse=True)
                    for u in range(U):
                        pool.indirect_dma_start(out=got[:, h, u, :], out_offset=None, in_=table,
                                                in_offset=bass.IndirectOffsetOnAxis(ap=idx[:, h, u:u + 1], axis=0)
                                                ).then_inc(got_in[h], 16)

        @block.vector
        def _(dve):
            dve.wait_ge(loaded, 16 * loads)
            for h in range(2):
                dve.tensor_copy(idx[:, h, :], src[:, h * U:(h + 1) * U]).then_inc(idx_ready, 1)
            with dve.Fori(0, TURNS) as i:
                for h in range(2):
                    dve.wait_ge(spread_in[h], 16 * (i + 1))
                    dve.wait_ge(dst_out, 2 * i)
                    dve.tensor_scalar(hot[:, h, :, :].rearrange("p u e -> p (u e)"), spread[:, h, :], K["pcol"][:, 0:1],
                                      None, ALU.is_equal).then_inc(hot_ready, 1)
                for h in range(2):
                    g = 2 * i + h
                    if edge_name:
                        tiles = [dve.value_load(j_row[0:1, bass.ds(g * U + u, 1)], min_val=0, max_val=L.tiles)
                                 for u in range(U)]
                    dve.wait_ge(dst_out, g + 1)
                    dve.wait_ge(got_in[h], 16 * U * (i + 1))
                    if keep:
                        dve.tensor_copy(kept[:, bass.ds(g * U, U), :], got[:, h, :, 0:keep]).then_inc(was_kept, 1)
                        dve.wait_ge(was_kept, g + 1)
                    dve.tensor_tensor(sums[:, h, :, :], got[:, h, :, at:at + H],
                                      pd[:, h, 0:U * H].rearrange("p (u h) -> p u h", h=H), ALU.add).then_inc(summed, 1)
                    dve.wait_ge(summed, g + 1)
                    dve.tensor_copy(idx[:, h, :], src[:, bass.ds((g + 2) % (2 * TURNS) * U, U)]).then_inc(idx_ready, 1)
                    if edge_name:
                        for u in range(U):
                            ins = dve.tensor_tensor(sums[:, h, u, :], sums[:, h, u, :],
                                                    edge[:, bass.ds(tiles[u], 1), :].rearrange("p a h -> p (a h)"), ALU.add)
                        ins.then_inc(edge_added, 1)
                        dve.wait_ge(edge_added, g + 1)
                    flat = sums[:, h, :, :].rearrange("p u h -> p (u h)")
                    dve.scalar_tensor_tensor(score[:, bass.ds(g * U, U), :].rearrange("p u h -> p (u h)"), flat, 0.2, flat,
                                             ALU.mult, ALU.max).then_inc(scored, 1)

        @block.tensor
        def _(pe):
            pe.wait_ge(loaded, 16 * loads)
            with pe.Fori(0, TURNS) as i:
                for h in range(2):
                    g = 2 * i + h
                    tiles = [pe.value_load(i_row[0:1, bass.ds(g * U + u, 1)], min_val=0, max_val=NODE_TILES - 1)
                             for u in range(U)]
                    pe.wait_ge(hot_ready, g + 1)
                    pe.wait_ge(summed, 2 * i)
                    for u in range(U):
                        mm = pe.matmul(pd[:, h, u * H:(u + 1) * H], hot[:, h, u, :], to_dst[:, bass.ds(tiles[u], 1), :],
                                       start=True, stop=True)
                    mm.then_inc(dst_out, 1)


def stage_hop_gate(nc, T, K):
    H, E, NT = 4, 4, NODE_TILES
    W = H * E
    with ExitStack() as ctx:
        s = Scope(nc, ctx, "r")
        acc = s.sb("acc", [P, NT, W + H])
        rows = s.sb("rows", [P, 3, W])
        rden = s.sb("rden", [P, NT, H])
        a = s.sb("a", [P, NT, W])
        b = s.sb("b", [P, NT, W])
        m = s.sb("m", [P, NT])
        v = s.sb("v", [P, NT])
        sd = s.sb("sd", [P, NT])
        rs = s.sb("rs", [P, NT])
        sc = s.sb("sc", [P, NT, E])
        order = s.sb("order", [P, E])
        best = s.sb("best", [P, 2, NT])
        at = s.sb("at", [P, NT, E])
        first = s.sb("first", [P, NT])
        one = s.sb("one", [P, 2, NT, E])
        ex = s.sb("ex", [P, NT])
        ws = s.sb("ws", [P, 2, NT])
        gate = s.sb("gate", [P, NT, E])
        loaded = s.sem("loaded")
        var_ready = s.sem("var_ready")
        sd_ready = s.sem("sd_ready")
        diff_ready = s.sem("diff_ready")
        ex_ready = s.sem("ex_ready")
        gate_ready = s.sem("gate_ready")
        stored = s.sem("stored")
        block = ctx.enter_context(nc.Block())

        def per_tile(ap, n):
            return ap.unsqueeze(2).broadcast_to((P, NT, n))

        @block.sync
        def _(sp):
            sp.dma_start(acc[:, :, :].rearrange("p t w -> p (t w)"), T["acc"][:, 0:NT * (W + H)]).then_inc(loaded, 16)
            for k, name in enumerate(("b_gat", "ln_gamma", "ln_beta")):
                sp.dma_start(rows[:, k, :], bcast_rows(T["L0_ffn_" + name], P)).then_inc(loaded, 16)
            sp.wait_ge(gate_ready, 1)
            sp.dma_start(T["f_gate"], gate[:, :, :]).then_inc(stored, 16)
            sp.wait_ge(stored, 16)

        @block.vector
        def _(dve):
            link = Tally(dve, s.sem("dve"))
            dve.wait_ge(loaded, 64)
            link.done(dve.tensor_scalar(rden[:, :, :], acc[:, :, W:W + H], 1e-16, 0.5, ALU.add, ALU.max))
            link.done(dve.reciprocal(rden[:, :, :], rden[:, :, :]))
            link.done(dve.tensor_tensor(a[:, :, :].rearrange("p t (h c) -> p t h c", h=H),
                                        acc[:, :, 0:W].rearrange("p t (h c) -> p t h c", h=H),
                                        rden[:, :, :].unsqueeze(3).broadcast_to((P, NT, H, E)), ALU.mult))
            link.done(dve.tensor_tensor(a[:, :, :], a[:, :, :], over_tiles(rows[:, 0, :], NT), ALU.add))
            link.done(dve.tensor_reduce(m[:, :], a[:, :, :], AX, ALU.add))
            link.done(dve.tensor_scalar(m[:, :], m[:, :], 1.0 / W, None, ALU.mult))
            link.done(dve.tensor_tensor(a[:, :, :], a[:, :, :], per_tile(m[:, :], W), ALU.subtract))
            link.done(dve.tensor_tensor(b[:, :, :], a[:, :, :], a[:, :, :], ALU.mult))
            link.done(dve.tensor_reduce(v[:, :], b[:, :, :], AX, ALU.add))
            link.done(dve.tensor_scalar(v[:, :], v[:, :], 1.0 / W, EPS, ALU.mult, ALU.add))
            dve.sem_inc(var_ready, 1)
            dve.wait_ge(sd_ready, 1)
            link.done(dve.reciprocal(rs[:, :], sd[:, :]))
            link.done(dve.tensor_tensor(a[:, :, :], a[:, :, :], per_tile(rs[:, :], W), ALU.mult))
            link.done(dve.tensor_tensor(a[:, :, :], a[:, :, :], over_tiles(rows[:, 1, :], NT), ALU.mult))
            link.done(dve.tensor_tensor(a[:, :, :], a[:, :, :], over_tiles(rows[:, 2, :], NT), ALU.add))
            link.done(dve.tensor_reduce(sc[:, :, :], a[:, :, :].rearrange("p t (h e) -> p t e h", h=H), AX, ALU.add))
            link.done(dve.tensor_scalar(sc[:, :, :], sc[:, :, :], 1.0 / H, None, ALU.mult))
            dve.tensor_copy(order[:, :], K["frow"][:, 0:E])
            for k in range(2):
                link.done(dve.tensor_reduce(best[:, k, :], sc[:, :, :], AX, ALU.max))
                link.done(dve.tensor_tensor(at[:, :, :], sc[:, :, :], per_tile(best[:, k, :], E), ALU.is_lt))
                link.done(dve.scalar_tensor_tensor(at[:, :, :], at[:, :, :], float(E), over_tiles(order[:, :], NT),
                                                   ALU.mult, ALU.add))
                link.done(dve.tensor_reduce(first[:, :], at[:, :, :], AX, ALU.min))
                link.done(dve.tensor_tensor(one[:, k, :, :], over_tiles(order[:, :], NT), per_tile(first[:, :], E),
                                            ALU.is_equal))
                if k == 0:
                    link.done(dve.scalar_tensor_tensor(sc[:, :, :], one[:, 0, :, :], -BIG, sc[:, :, :], ALU.mult, ALU.add))
            link.done(dve.tensor_tensor(m[:, :], best[:, 1, :], best[:, 0, :], ALU.subtract))
            dve.sem_inc(diff_ready, 1)
            dve.wait_ge(ex_ready, 1)
            link.done(dve.tensor_scalar(v[:, :], ex[:, :], 1.0, None, ALU.add))
            link.done(dve.reciprocal(ws[:, 0, :], v[:, :]))
            link.done(dve.tensor_tensor(ws[:, 1, :], ws[:, 0, :], ex[:, :], ALU.mult))
            for k in range(2):
                ins = dve.tensor_tensor(one[:, k, :, :], one[:, k, :, :], per_tile(ws[:, k, :], E), ALU.mult)
            link.done(ins)
            dve.tensor_tensor(gate[:, :, :], one[:, 0, :, :], one[:, 1, :, :], ALU.add).then_inc(gate_ready, 1)

        @block.scalar
        def _(act):
            act.wait_ge(var_ready, 1)
            act.activation(sd[:, :], v[:, :], ACT.Sqrt).then_inc(sd_ready, 1)
            act.wait_ge(diff_ready, 1)
            act.activation(ex[:, :], m[:, :], ACT.Exp).then_inc(ex_ready, 1)


def stage_experts2(nc, T, K):
    E, F = 4, 2 * D
    FC = F // P
    with ExitStack() as ctx:
        s = Scope(nc, ctx, "t")
        n = Norm(s, turn=False)
        n.xt = s.sb("xt", [P, 2, ROWS])
        n.turned = s.sem("turned")
        n.xt_ready = s.sem("xt_ready")
        w1 = s.sb("w1", [P, E, 2, F])
        w2 = s.sb("w2", [P, E, FC, D])
        b1r = s.sb("b1r", [E * FC, P])
        b1 = s.sb("b1", [P, E * FC])
        b2 = s.sb("b2", [P, E, D])
        gate = s.sb("gate", [P, NODE_TILES, E])
        gc = s.sb("gc", [P, TPC, E])
        hid = s.sb("hid", [P, 2, FC, ROWS])
        acc = s.sb("acc", [P, TPC, D])
        ph = s.ps("ph", [P, 2, 2, 512])
        po = s.ps("po", [P, 4, 512])
        n.pt = po
        loaded = s.sem("loaded")
        b1_turned = s.sem("b1_turned")
        b1_ready = s.sem("b1_ready")
        up = s.sem("up")
        act_done = s.sem("act_done")
        down = s.sem("down")
        acc_done = s.sem("acc_done")
        stored = s.sem("stored")
        block = ctx.enter_context(nc.Block())

        def slot(t):
            return po[:, t // 2, t % 2 * D:(t % 2 + 1) * D]

        @block.sync
        def _(sp):
            n.load(sp, T["x1"], 0)
            sp.dma_start(b1r[:, :], T["L0_ffn_b1"].rearrange("e (a p) -> (e a) p", p=P)).then_inc(loaded, 16)
            sp.dma_start(gate[:, :, :], T["f_gate"]).then_inc(loaded, 16)
            for e in range(E):
                sp.dma_start(w1[:, e, :, :], T["L0_ffn_W1"][e].rearrange("(a p) f -> p a f", p=P)).then_inc(loaded, 16)
                sp.dma_start(w2[:, e, :, :], T["L0_ffn_W2"][e].rearrange("(a p) d -> p a d", p=P)).then_inc(loaded, 16)
                sp.dma_start(b2[:, e, :], bcast_rows(T["L0_ffn_b2"][e], P)).then_inc(loaded, 16)
            with sp.Fori(0, CHUNKS) as c:
                sp.wait_ge(acc_done, PAIRS * E * (c + 1))
                sp.dma_start(chunk_of(T["x2"], c), acc[:, :, :]).then_inc(stored, 16)
                n.load(sp, T["x1"], (c + 1) % CHUNKS)
            sp.wait_ge(stored, 16 * CHUNKS)
            sp.wait_ge(n.x_loaded, 16 * (CHUNKS + 1))

        @block.vector
        def _(dve):
            link = Tally(dve, s.sem("dve"))
            dve.wait_ge(loaded, 16 * (2 + 3 * E))
            with dve.Fori(0, CHUNKS) as c:
                link.loop(c, 2 + 1 + E)
                dve.wait_ge(n.x_loaded, 16 * c + 16)
                n.vector(dve, link, c).then_inc(n.xn_ready, 1)
                link.done(dve.tensor_copy(gc[:, :, :], gate[:, bass.ds(c * TPC, TPC), :]))
                dve.wait_ge(stored, 16 * c)
                for e in range(E):
                    for t in range(TPC):
                        ins = dve.scalar_tensor_tensor(acc[:, t, :], b2[:, e, :], gc[:, t, e:e + 1],
                                                       n.x[:, t, :] if e == 0 else acc[:, t, :], ALU.mult, ALU.add)
                    link.done(ins)
                for e in range(E):
                    for b in range(PAIRS):
                        g = (c * E + e) * PAIRS + b
                        dve.wait_ge(down, g + 1)
                        if e:
                            dve.wait_ge(acc_done, g - PAIRS + 1)
                        for t in range(2 * b, min(2 * b + 2, TPC)):
                            ins = dve.scalar_tensor_tensor(acc[:, t, :], slot(t), gc[:, t, e:e + 1], acc[:, t, :],
                                                           ALU.mult, ALU.add)
                        ins.then_inc(acc_done, 1)
            link.leave(CHUNKS)

        @block.scalar
        def _(act):
            act.wait_ge(b1_turned, 1)
            act.activation(b1[:, :], ph[:, 0, 0, 0:E * FC], ACT.Copy).then_inc(b1_ready, 1)
            act.wait_ge(b1_ready, 1)
            with act.Fori(0, CHUNKS) as c:
                n.scalar(act, K, c)
                n.scalar_turned(act, c)
                for e in range(E):
                    for f in range(FC):
                        g = (c * E + e) * FC + f
                        act.wait_ge(up, g + 1)
                        act.activation(hid[:, e % 2, f, :].rearrange("p (h r) -> p h r", h=2), ph[:, f % 2, :, 0:HALF], ACT.Gelu,
                                       bias=b1[:, e * FC + f:e * FC + f + 1]).then_inc(act_done, 1)

        @block.tensor
        def _(pe):
            def layer1(c, e):
                for f in range(FC):
                    g = (c * E + e) * FC + f
                    pe.wait_ge(act_done, g - 1 if (e or f) else g)
                    for a in range(2):
                        for h in range(2):
                            mm = pe.matmul(ph[:, f % 2, h, 0:HALF], w1[:, e, a, f * P:(f + 1) * P],
                                           n.xt[:, a, h * HALF:(h + 1) * HALF], start=(a == 0), stop=(a == 1))
                    mm.then_inc(up, 1)

            def layer2(c, e):
                pe.wait_ge(act_done, (c * E + e + 1) * FC)
                for b in range(PAIRS):
                    g = (c * E + e) * PAIRS + b
                    pe.wait_ge(acc_done, g - PAIRS + 1 if e else g - b)
                    for t in range(2 * b, min(2 * b + 2, TPC)):
                        for f in range(FC):
                            mm = pe.matmul(slot(t), hid[:, e % 2, f, t * P:(t + 1) * P], w2[:, e, f, :],
                                           start=(f == 0), stop=(f == FC - 1))
                    mm.then_inc(down, 1)

            pe.wait_ge(loaded, 16 * (2 + 3 * E))
            pe.transpose(ph[:, 0, 0, 0:E * FC], b1r[:, :], K["ident"][0:E * FC, 0:E * FC]).then_inc(b1_turned, 1)
            pe.wait_ge(b1_ready, 1)
            with pe.Fori(0, CHUNKS) as c:
                n.tensor(pe, K, c)
                pe.wait_ge(n.xt_ready, c + 1)
                layer1(c, 0)
                for e in range(1, E):
                    layer1(c, e)
                    layer2(c, e - 1)
                layer2(c, E - 1)


def stage_edge_scores(nc, T, K):
    H, A, U = 8, 64, 8
    TURNS = GRAPH.tiles // (2 * U)
    rest = GRAPH.tiles - TURNS * 2 * U - U
    odd = GRAPH.edges - (GRAPH.tiles - 1) * P
    with ExitStack() as ctx:
        s = Scope(nc, ctx, "g")
        we = s.sb("we", [P, D])
        att = s.sb("att", [P, D])
        ve = s.sb("ve", [P, 2 * H])
        attr = s.sb("attr", [P, 2, U, A])
        attr_t = s.sb("attr_t", [P, 2, U // 2, P])
        out = s.sb("out", [P, GRAPH.tiles + 1, H])
        pt = s.ps("pt", [P, 2, 512])
        pv = s.ps("pv", [P, 2, 512])
        params = s.sem("params")
        ve_ready = s.sem("ve_ready")
        cleared = s.sem("cleared")
        attr_in = [s.sem(f"attr_in{h}") for h in range(2)]
        turned = s.sem("turned")
        turned_sb = s.sem("turned_sb")
        scored = s.sem("scored")
        kept = s.sem("kept")
        stored = s.sem("stored")
        block = ctx.enter_context(nc.Block())
        src = T["edge_attr_64"]

        @block.sync
        def _(sp):
            for k in range(2):
                sp.dma_start(we[k * A:(k + 1) * A, :], T["L1_gnn_W_e"]).then_inc(params, 16)
            sp.dma_start(att[:, :], bcast_rows(T["L1_gnn_att_edge"].rearrange("h c -> (h c)"), P)).then_inc(params, 16)
            with sp.Fori(0, TURNS) as i:
                for h in range(2):
                    sp.wait_ge(turned, 2 * i)
                    sp.dma_start(attr[:, h, :, :], src[bass.ds((2 * i + h) * U * P, U * P), :].rearrange("(u p) a -> p u a", p=P)
                                 ).then_inc(attr_in[h], 16)
            sp.wait_ge(turned, 2 * TURNS)
            at = TURNS * 2 * U * P
            sp.dma_start(attr[:, 0, :, :], src[at:at + U * P, :].rearrange("(u p) a -> p u a", p=P)).then_inc(attr_in[0], 16)
            at += U * P
            sp.wait_ge(cleared, 2)
            sp.dma_start(attr[:, 1, 0:rest - 1, :], src[at:at + (rest - 1) * P, :].rearrange("(u p) a -> p u a", p=P)
                         ).then_inc(attr_in[1], 16)
            at += (rest - 1) * P
            sp.dma_start(attr[0:odd, 1, rest - 1, :], src[at:at + odd, :]).then_inc(attr_in[1], 16)
            sp.wait_ge(kept, 2 * TURNS + 2)
            sp.dma_start(T["l1_aedge"], out[:, :, :]).then_inc(stored, 16)
            sp.wait_ge(stored, 16)

        @block.vector
        def _(dve):
            link = Tally(dve, s.sem("dve"))
            dve.memset(out[:, GRAPH.tiles:GRAPH.tiles + 1, :], 0.0).then_inc(cleared, 1)
            link.done(dve.memset(ve[:, :], 0.0))
            dve.wait_ge(params, 48)
            link.done(dve.tensor_tensor(we[:, :], we[:, :], att[:, :], ALU.mult))
            for k in range(2):
                dve.tensor_reduce(ve[k * A:(k + 1) * A, k * H:(k + 1) * H],
                                  we[k * A:(k + 1) * A, :].rearrange("p (h c) -> p h c", h=H), AX, ALU.add).then_inc(ve_ready, 1)

            def keep(g, h, n):
                dve.wait_ge(scored, g + 1)
                dve.tensor_copy(out[:, bass.ds(g * U, n), :] if not isinstance(g, int) else out[:, g * U:g * U + n, :],
                                pv[:, h, 0:n * H].rearrange("p (u h) -> p u h", h=H)).then_inc(kept, 1)

            with dve.Fori(0, TURNS) as i:
                for h in range(2):
                    keep(2 * i + h, h, U)
            dve.wait_ge(turned, 2 * TURNS)
            dve.memset(attr[:, 1, :, :], 0.0).then_inc(cleared, 1)
            keep(2 * TURNS, 0, U)
            keep(2 * TURNS + 1, 1, rest)

        @block.scalar
        def _(act):
            def copy(g, h):
                act.wait_ge(turned, g + 1)
                act.activation(attr_t[:, h, :, :], pt[:, h, :].rearrange("p (u e) -> p u e", e=P), ACT.Copy
                               ).then_inc(turned_sb, 1)

            with act.Fori(0, TURNS) as i:
                for h in range(2):
                    copy(2 * i + h, h)
            for h in range(2):
                copy(2 * TURNS + h, h)

        @block.tensor
        def _(pe):
            def turn(g, h, landed):
                pe.wait_ge(attr_in[h], landed)
                for u in range(U // 2):
                    mm = pe.transpose(pt[:, h, u * P:(u + 1) * P], attr[:, h, 2 * u:2 * u + 2, :].rearrange("p u a -> p (u a)"),
                                      K["ident"][:, :])
                mm.then_inc(turned, 1)

            def score(g, h):
                pe.wait_ge(turned_sb, g + 1)
                for u in range(U // 2):
                    mm = pe.matmul(pv[:, h, u * 2 * H:(u + 1) * 2 * H], attr_t[:, h, u, :], ve[:, :], start=True, stop=True)
                mm.then_inc(scored, 1)

            pe.wait_ge(ve_ready, 2)
            with pe.Fori(0, TURNS) as i:
                pe.wait_ge(kept, 2 * i)
                for h in range(2):
                    turn(2 * i + h, h, 16 * (i + 1))
                for h in range(2):
                    score(2 * i + h, h)
            pe.wait_ge(kept, 2 * TURNS)
            turn(2 * TURNS, 0, 16 * (TURNS + 1))
            turn(2 * TURNS + 1, 1, 16 * (TURNS + 2))
            score(2 * TURNS, 0)
            score(2 * TURNS + 1, 1)


def stage_l1_project(nc, T, K):
    H = 8
    with ExitStack() as ctx:
        s = Scope(nc, ctx, "y")
        n = Norm(s)
        w = s.sb("w", [P, 2, D])
        att = s.sb("att", [P, 2, D])
        row = s.sb("row", [P, TPC, D])
        t1 = s.sb("t1", [P, 2, TPC, D])
        to_src = s.sb("to_src", [P, TPC, H])
        to_dst = s.sb("to_dst", [P, NODE_TILES, H])
        pq = s.ps("pq", [P, 4, 512])
        loaded = s.sem("loaded")
        projected = s.sem("projected")
        row_ready = s.sem("row_ready")
        src_ready = s.sem("src_ready")
        dst_ready = s.sem("dst_ready")
        stored = s.sem("stored")
        block = ctx.enter_context(nc.Block())

        @block.sync
        def _(sp):
            n.load(sp, T["x2"], 0)
            sp.dma_start(w[:, :, :], T["L1_gnn_W"].rearrange("(a p) n -> p a n", p=P)).then_inc(loaded, 16)
            for k, m in enumerate(("src", "dst")):
                sp.dma_start(att[:, k, :], bcast_rows(T["L1_gnn_att_" + m].rearrange("h c -> (h c)"), P)).then_inc(loaded, 16)
            with sp.Fori(0, CHUNKS) as c:
                sp.wait_ge(n.xn_ready, c + 1)
                n.load(sp, T["x2"], (c + 1) % CHUNKS)
                sp.dma_start(chunk_of(T["l1_xn"], c), n.xn[:, :, :]).then_inc(stored, 16)
                sp.wait_ge(row_ready, c + 1)
                sp.dma_start(chunk_of(T["l1_table"], c), row[:, :, :]).then_inc(stored, 16)
                sp.wait_ge(src_ready, c + 1)
                sp.dma_start(chunk_of(T["l1_asrc"], c), to_src[:, :, :]).then_inc(stored, 16)
            sp.wait_ge(dst_ready, CHUNKS)
            sp.dma_start(T["l1_adst"], to_dst[:, :, :]).then_inc(stored, 16)
            sp.wait_ge(stored, 48 * CHUNKS + 16)
            sp.wait_ge(n.x_loaded, 16 * (CHUNKS + 1))

        @block.vector
        def _(dve):
            link = Tally(dve, s.sem("dve"))
            dve.wait_ge(loaded, 48)
            with dve.Fori(0, CHUNKS) as c:
                link.loop(c, 4)
                dve.wait_ge(n.x_loaded, 16 * c + 16)
                dve.wait_ge(stored, 48 * c)
                n.vector(dve, link, c).then_inc(n.xn_ready, 1)
                dve.wait_ge(projected, c + 1)
                for t in range(TPC):
                    ins = dve.tensor_copy(row[:, t, :], pq[:, t // 2, t % 2 * D:(t % 2 + 1) * D])
                ins.then_inc(row_ready, 1)
                dve.wait_ge(row_ready, c + 1)
                for k in range(2):
                    link.done(dve.tensor_tensor(t1[:, k, :, :], row[:, :, :], over_tiles(att[:, k, :]), ALU.mult))
                dve.tensor_reduce(to_src[:, :, :].rearrange("p t h -> p (t h)"),
                                  t1[:, 0, :, :].rearrange("p t (h c) -> p (t h) c", h=H), AX, ALU.add).then_inc(src_ready, 1)
                dve.tensor_reduce(to_dst[:, bass.ds(c * TPC, TPC), :].rearrange("p t h -> p (t h)"),
                                  t1[:, 1, :, :].rearrange("p t (h c) -> p (t h) c", h=H), AX, ALU.add).then_inc(dst_ready, 1)
            link.leave(CHUNKS)

        @block.scalar
        def _(act):
            with act.Fori(0, CHUNKS) as c:
                n.scalar(act, K, c)
                n.scalar_turned(act, c)

        @block.tensor
        def _(pe):
            pe.wait_ge(loaded, 48)
            with pe.Fori(0, CHUNKS) as c:
                n.tensor(pe, K, c)
                pe.wait_ge(n.xt_ready, c + 1)
                pe.wait_ge(row_ready, c)
                for t in range(TPC):
                    for f in range(2):
                        mm = pe.matmul(pq[:, t // 2, t % 2 * D:(t % 2 + 1) * D], n.xt[:, f, t * P:(t + 1) * P], w[:, f, :],
                                       start=(f == 0), stop=(f == 1))
                mm.then_inc(projected, 1)


def stage_l1_finish(nc, T, K):
    H, W = 8, D
    with ExitStack() as ctx:
        s = Scope(nc, ctx, "z")
        n = Norm(s, turn=False)
        acc = s.sb("acc", [P, TPC, W + H])
        xn = s.sb("xn1", [P, TPC, D])
        x2 = s.sb("x2", [P, TPC, D])
        bias = s.sb("bias", [P, D])
        gain = s.sb("gain", [P, D])
        shift = s.sb("shift", [P, D])
        rden = s.sb("rden", [P, TPC, H])
        t1 = s.sb("t1", [P, TPC, D])
        t2 = s.sb("t2", [P, TPC, D])
        out = s.sb("out", [P, TPC, D])
        params = s.sem("params")
        loaded = s.sem("loaded")
        out_ready = s.sem("out_ready")
        stored = s.sem("stored")
        block = ctx.enter_context(nc.Block())
        acc_all = T["acc"][:, 0:NODE_TILES * (W + H)]

        @block.sync
        def _(sp):
            for to, name in ((bias, "bias"), (gain, "gamma"), (shift, "beta")):
                sp.dma_start(to[:, :], bcast_rows(T["L1_gnn_" + name], P)).then_inc(params, 16)
            with sp.Fori(0, CHUNKS) as c:
                sp.wait_ge(out_ready, c)
                sp.dma_start(acc[:, :, :].rearrange("p t w -> p (t w)"),
                             acc_all[:, bass.ds(c * (TPC * (W + H)), TPC * (W + H))]).then_inc(loaded, 16)
                sp.dma_start(xn[:, :, :], chunk_of(T["l1_xn"], c)).then_inc(loaded, 16)
                sp.dma_start(x2[:, :, :], chunk_of(T["x2"], c)).then_inc(loaded, 16)
                sp.wait_ge(out_ready, c + 1)
                sp.dma_start(chunk_of(T["x3"], c), out[:, :, :]).then_inc(stored, 16)
            sp.wait_ge(stored, 16 * CHUNKS)

        @block.vector
        def _(dve):
            link = Tally(dve, s.sem("dve"))
            dve.wait_ge(params, 48)
            with dve.Fori(0, CHUNKS) as c:
                link.loop(c, 10)
                dve.wait_ge(loaded, 48 * c + 48)
                link.done(dve.tensor_scalar(rden[:, :, :], acc[:, :, W:W + H], 1e-16, 0.5, ALU.add, ALU.max))
                link.done(dve.reciprocal(rden[:, :, :], rden[:, :, :]))
                link.done(dve.tensor_tensor(t1[:, :, :].rearrange("p t (h c) -> p t h c", h=H),
                                            acc[:, :, 0:W].rearrange("p t (h c) -> p t h c", h=H),
                                            rden[:, :, :].unsqueeze(3).broadcast_to((P, TPC, H, W // H)), ALU.mult))
                link.done(dve.tensor_tensor(t1[:, :, :], t1[:, :, :], over_tiles(bias[:, :]), ALU.add))
                link.done(dve.tensor_tensor(t1[:, :, :], t1[:, :, :], xn[:, :, :], ALU.add))
                link.done(n.vector(dve, link, c, x=t1, out=t2))
                link.done(dve.tensor_tensor(t2[:, :, :], t2[:, :, :], over_tiles(gain[:, :]), ALU.mult))
                link.done(dve.tensor_tensor(t2[:, :, :], t2[:, :, :], over_tiles(shift[:, :]), ALU.add))
                dve.wait_ge(stored, 16 * c)
                dve.tensor_tensor(out[:, :, :], t2[:, :, :], x2[:, :, :], ALU.add).then_inc(out_ready, 1)
            link.leave(CHUNKS)

        @block.scalar
        def _(act):
            with act.Fori(0, CHUNKS) as c:
                n.scalar(act, K, c)


def stage_experts3(nc, T, K):
    E = 8
    BN_EPS = 0.001
    with ExitStack() as ctx:
        s = Scope(nc, ctx, "l")
        n = Norm(s, turn=False)
        n.xt = s.sb("xt", [P, 2, ROWS])
        n.turned = s.sem("turned")
        n.xt_ready = s.sem("xt_ready")
        wm = [s.sb(f"wm{k}", [P, E, 2, D]) for k in range(3)]
        wr = s.sb("wr", [P, 2, E])
        br = s.sb("br", [P, E])
        raw = s.sb("raw", [5 * 2 * E, 2, P])
        par = s.sb("par", [P, 2, 5, 2 * E])
        bn = s.sb("bn", [P, 2, 2, 2 * E])
        bn_eps = s.sb("bn_eps", [P, 1])
        sdv = s.sb("sdv", [P, 2, 2 * E])
        bo = s.sb("bo", [P, E, D])
        logit = s.sb("logit", [P, TPC, E])
        mx = s.sb("mx", [P, TPC])
        prob = s.sb("prob", [P, TPC, E])
        den = s.sb("den", [P, TPC])
        h1 = s.sb("h1", [P, 2, 2, ROWS])
        h2 = s.sb("h2", [P, 2, 2, ROWS])
        acc = s.sb("acc", [P, TPC, D])
        ph = s.ps("ph", [P, 2, 2, 512])
        po = s.ps("po", [P, 4, 512])
        n.pt = po
        loaded = s.sem("loaded")
        par_turned = s.sem("par_turned")
        var_ready = s.sem("bn_var")
        bn_sd = s.sem("bn_sd")
        bn_ready = s.sem("bn_ready")
        routed = s.sem("routed")
        route_read = s.sem("route_read")
        diff_ready = s.sem("diff_ready")
        exp_ready = s.sem("exp_ready")
        up = s.sem("up")
        act_done = s.sem("act_done")
        down = s.sem("down")
        acc_done = s.sem("acc_done")
        stored = s.sem("stored")
        block = ctx.enter_context(nc.Block())
        n_loads = 3 * E + 2 + 10 + 1
        order = []
        for e in range(E + 1):
            order += [(0, e)] * (e < E) + [(1, e - 1)] * (e > 0)
        place = {what: k for k, what in enumerate(order)}
        PER = 2 * len(order)

        def slot(t):
            return po[:, t // 2, t % 2 * D:(t % 2 + 1) * D]

        @block.sync
        def _(sp):
            n.load(sp, T["x3"], 0)
            for k in range(2):
                for a, name in enumerate(("b", "g", "be", "m", "v")):
                    sp.dma_start(raw[a * 2 * E:(a + 1) * 2 * E, k, :],
                                 T[f"L1_ffn_{name}{k + 1}"].rearrange("e (a p) -> (e a) p", p=P)).then_inc(loaded, 16)
            sp.dma_start(wr[:, :, :], T["L1_ffn_Wr"].rearrange("(a p) e -> p a e", p=P)).then_inc(loaded, 16)
            sp.dma_start(br[:, :], bcast_rows(T["L1_ffn_br"], P)).then_inc(loaded, 16)
            sp.dma_start(bo[:, :, :].rearrange("p e d -> p (e d)"), bcast_rows(T["L1_ffn_bo"].rearrange("e d -> (e d)"), P)
                         ).then_inc(loaded, 16)
            for e in range(E):
                for k, name in enumerate(("W1", "W2", "Wo")):
                    sp.dma_start(wm[k][:, e, :, :], T["L1_ffn_" + name][e].rearrange("(a p) f -> p a f", p=P)).then_inc(loaded, 16)
            with sp.Fori(0, CHUNKS - 1) as c:
                sp.wait_ge(acc_done, PAIRS * E * (c + 1))
                sp.dma_start(T["out"][bass.ds(c * ROWS, ROWS), :].rearrange("(t p) f -> p t f", p=P), acc[:, :, :]
                             ).then_inc(stored, 16)
                n.load(sp, T["x3"], c + 1)
            sp.wait_ge(acc_done, PAIRS * E * CHUNKS)
            at = (CHUNKS - 1) * ROWS
            full = (N - at) // P
            sp.dma_start(T["out"][at:at + full * P, :].rearrange("(t p) f -> p t f", p=P), acc[:, 0:full, :]).then_inc(stored, 16)
            at += full * P
            sp.dma_start(T["out"][at:N, :], acc[0:N - at, full, :]).then_inc(stored, 16)
            sp.wait_ge(stored, 16 * (CHUNKS + 1))

        @block.vector
        def _(dve):
            link = Tally(dve, s.sem("dve"))
            dve.memset(bn_eps[:, :], BN_EPS)
            dve.wait_ge(par_turned, 1)
            for k in range(2):
                ins = dve.tensor_copy(par[:, k, :, :], po[:, k, 0:5 * 2 * E].rearrange("p (a n) -> p a n", a=5))
            link.done(ins)
            dve.sem_inc(var_ready, 1)
            dve.wait_ge(bn_sd, 1)
            link.done(dve.reciprocal(sdv[:, :, :], sdv[:, :, :]))
            link.done(dve.tensor_tensor(bn[:, :, 0, :], sdv[:, :, :], par[:, :, 1, :], ALU.mult))
            link.done(dve.tensor_tensor(sdv[:, :, :], par[:, :, 0, :], par[:, :, 3, :], ALU.subtract))
            link.done(dve.tensor_tensor(sdv[:, :, :], sdv[:, :, :], bn[:, :, 0, :], ALU.mult))
            dve.tensor_tensor(bn[:, :, 1, :], sdv[:, :, :], par[:, :, 2, :], ALU.add).then_inc(bn_ready, 1)
            dve.wait_ge(loaded, 16 * n_loads)
            with dve.Fori(0, CHUNKS) as c:
                link.loop(c, 2 + 4 + E)
                dve.wait_ge(n.x_loaded, 16 * c + 16)
                n.vector(dve, link, c).then_inc(n.xn_ready, 1)
                dve.wait_ge(routed, c + 1)
                dve.tensor_tensor(logit[:, :, :], po[:, 0, 0:TPC * E].rearrange("p (t e) -> p t e", e=E), over_tiles(br[:, :]),
                                  ALU.add).then_inc(route_read, 1)
                dve.wait_ge(route_read, c + 1)
                link.done(dve.tensor_reduce(mx[:, :], logit[:, :, :], AX, ALU.max))
                dve.tensor_tensor(logit[:, :, :], logit[:, :, :], mx[:, :].unsqueeze(2).broadcast_to((P, TPC, E)), ALU.subtract
                                  ).then_inc(diff_ready, 1)
                dve.wait_ge(exp_ready, c + 1)
                link.done(dve.tensor_reduce(den[:, :], prob[:, :, :], AX, ALU.add))
                link.done(dve.reciprocal(den[:, :], den[:, :]))
                link.done(dve.tensor_tensor(prob[:, :, :], prob[:, :, :], den[:, :].unsqueeze(2).broadcast_to((P, TPC, E)), ALU.mult))
                dve.wait_ge(stored, 16 * c)
                for e in range(E):
                    for t in range(TPC):
                        ins = dve.scalar_tensor_tensor(acc[:, t, :], bo[:, e, :], prob[:, t, e:e + 1],
                                                       n.x[:, t, :] if e == 0 else acc[:, t, :], ALU.mult, ALU.add)
                    link.done(ins)
                for e in range(E):
                    for b in range(PAIRS):
                        g = (c * E + e) * PAIRS + b
                        dve.wait_ge(down, g + 1)
                        if e:
                            dve.wait_ge(acc_done, g - PAIRS + 1)
                        for t in range(2 * b, min(2 * b + 2, TPC)):
                            ins = dve.scalar_tensor_tensor(acc[:, t, :], slot(t), prob[:, t, e:e + 1], acc[:, t, :],
                                                           ALU.mult, ALU.add)
                        ins.then_inc(acc_done, 1)
            link.leave(CHUNKS)

        @block.scalar
        def _(act):
            act.wait_ge(var_ready, 1)
            act.activation(sdv[:, :, :], par[:, :, 4, :], ACT.Sqrt, bias=bn_eps[:, 0:1]).then_inc(bn_sd, 1)
            act.wait_ge(bn_ready, 1)
            with act.Fori(0, CHUNKS) as c:
                n.scalar(act, K, c)
                n.scalar_turned(act, c)
                act.wait_ge(diff_ready, c + 1)
                act.activation(prob[:, :, :], logit[:, :, :], ACT.Exp).then_inc(exp_ready, 1)
                for k, (layer, e) in enumerate(order):
                    to = (h1, h2)[layer]
                    for f in range(2):
                        act.wait_ge(up, c * PER + 2 * k + f + 1)
                        act.activation(to[:, e % 2, f, :].rearrange("p (h r) -> p h r", h=2), ph[:, f, :, 0:HALF], ACT.Relu,
                                       scale=bn[:, layer, 0, 2 * e + f:2 * e + f + 1],
                                       bias=bn[:, layer, 1, 2 * e + f:2 * e + f + 1]).then_inc(act_done, 1)

        @block.tensor
        def _(pe):
            def layer(c, which, e):
                k = place[which, e]
                if which:
                    pe.wait_ge(act_done, c * PER + 2 * place[0, e] + 2)
                of = (n.xt[:, :, :], h1[:, e % 2, :, :])[which]
                for f in range(2):
                    pe.wait_ge(act_done, c * PER + 2 * k + f - (1 if k else f))
                    for a in range(2):
                        for h in range(2):
                            mm = pe.matmul(ph[:, f, h, 0:HALF], wm[which][:, e, a, f * P:(f + 1) * P],
                                           of[:, a, h * HALF:(h + 1) * HALF], start=(a == 0), stop=(a == 1))
                    mm.then_inc(up, 1)

            def last(c, e):
                pe.wait_ge(act_done, c * PER + 2 * place[1, e] + 2)
                for b in range(PAIRS):
                    g = (c * E + e) * PAIRS + b
                    pe.wait_ge(acc_done, g - PAIRS + 1 if e else g - b)
                    for t in range(2 * b, min(2 * b + 2, TPC)):
                        for f in range(2):
                            mm = pe.matmul(slot(t), h2[:, e % 2, f, t * P:(t + 1) * P], wm[2][:, e, f, :],
                                           start=(f == 0), stop=(f == 1))
                    mm.then_inc(down, 1)

            pe.wait_ge(loaded, 16 * n_loads)
            for k in range(2):
                mm = pe.transpose(po[:, k, 0:5 * 2 * E], raw[:, k, :], K["ident"][0:5 * 2 * E, 0:5 * 2 * E])
            mm.then_inc(par_turned, 1)
            pe.wait_ge(bn_ready, 1)
            with pe.Fori(0, CHUNKS) as c:
                n.tensor(pe, K, c)
                pe.wait_ge(n.xt_ready, c + 1)
                for t in range(TPC):
                    for f in range(2):
                        mm = pe.matmul(po[:, 0, t * E:(t + 1) * E], n.xt[:, f, t * P:(t + 1) * P], wr[:, f, :],
                                       start=(f == 0), stop=(f == 1))
                mm.then_inc(routed, 1)
                for e in range(E + 2):
                    if e < E:
                        layer(c, 0, e)
                    if 0 < e <= E:
                        layer(c, 1, e - 1)
                    if e > 1:
                        if e == 2:
                            pe.wait_ge(route_read, c + 1)
                        last(c, e - 2)


def scratch_shapes():
    shapes = {"x0": ([NP, D], F32)}
    for L in (GRAPH, HOP):
        n = L.name
        shapes.update({
            n + "_src": ([L.tiles * P], I32), n + "_dst": ([L.tiles * P], I32),
            n + "_rel_rows": ([L.blocks * P, P], F32), n + "_key_rows": ([L.blocks * P, P], F32),
            n + "_i_row": ([L.blocks * P], I32), n + "_j_row": ([L.blocks * P], I32),
            n + "_src_t": ([P, L.steps], I32), n + "_rel_t": ([P, L.steps], F32),
        })
    shapes["f_pairs"] = ([HOP.tiles * P, 2], I32)
    for k in ("q", "k", "v", "skip"):
        shapes["l0_" + k] = ([NP, D], F32)
    shapes.update({
        "score": ([P, GRAPH.steps * 8], F32), "weight": ([P, GRAPH.steps * 8], F32), "lanes": ([P * GRAPH.steps], F32),
        "acc": ([P, NODE_TILES * (D + 8)], F32), "x1": ([NP, D], F32), "x2": ([NP, D], F32), "x3": ([NP, D], F32),
        "f_table": ([NP, 20], F32), "f_rows": ([P, HOP.steps, 16], F32), "f_gate": ([P, NODE_TILES, 4], F32),
        "f_adst": ([P, NODE_TILES, 4], F32),
        "l1_table": ([NP, D], F32), "l1_asrc": ([NP, 8], F32), "l1_adst": ([P, NODE_TILES, 8], F32),
        "l1_aedge": ([P, GRAPH.tiles + 1, 8], F32), "l1_xn": ([NP, D], F32),
    })
    return shapes


def two_layers(nc, T):
    for name, (shape, dt) in scratch_shapes().items():
        T[name] = nc.dram_tensor("tmp_" + name, shape, dt).ap()
    with ExitStack() as ctx:
        K = {name: ctx.enter_context(nc.sbuf_tensor("const_" + name, shape, F32)) for name, shape in
             (("frow", [P, P]), ("pcol", [P, 1]), ("ident", [P, P]), ("below", [P, P]), ("ones", [P, P]), ("eps", [P, 1]))}
        stage_constants(nc, T, K)
        stage_sort(nc, T, K)
        stage_split(nc, T, K)
        for edges in (GRAPH, HOP):
            stage_schedule(nc, T, K, edges)
        stage_l0_project(nc, T, K)
        stage_dot(nc, T, K, GRAPH)
        stage_softmax(nc, T, K, GRAPH, 4, 64 ** -0.5)
        stage_sum(nc, T, K, GRAPH, 4, D, T["l0_v"])
        stage_l0_finish(nc, T, K)
        stage_hop_project(nc, T, K)
        stage_pair(nc, T, K, HOP, 4, T["f_table"], 20, 16, "f_adst", keep=16)
        stage_softmax(nc, T, K, HOP, 4, 1.0)
        stage_sum(nc, T, K, HOP, 4, 16)
        stage_hop_gate(nc, T, K)
        stage_experts2(nc, T, K)
        stage_edge_scores(nc, T, K)
        stage_l1_project(nc, T, K)
        stage_pair(nc, T, K, GRAPH, 8, T["l1_asrc"], 8, 0, "l1_adst", edge_name="l1_aedge")
        stage_softmax(nc, T, K, GRAPH, 8, 1.0)
        stage_sum(nc, T, K, GRAPH, 8, D, T["l1_table"])
        stage_l1_finish(nc, T, K)
        stage_experts3(nc, T, K)


def kernel(**inputs):
    import numpy as _np
    import concourse.bacc as _bacc
    from concourse import mybir as _mybir
    from concourse.bass_utils import run_bass_kernel_spmd as _run

    nc = _bacc.Bacc("TRN2", target_bir_lowering=False, num_devices=1)
    arrays, tables = {}, {}
    for name in inputs:
        a = _np.ascontiguousarray(inputs[name])
        a = a.reshape(a.shape or (1,))
        arrays["in_" + name] = a
        tables[name] = nc.dram_tensor("in_" + name, a.shape, _mybir.dt.from_np(a.dtype), kind="ExternalInput").ap()
    tables["out"] = nc.dram_tensor("out", (N, D), _mybir.dt.float32, kind="ExternalOutput").ap()
    two_layers(nc, tables)
    return _run(nc, [arrays], core_ids=[0]).results[0]["out"]
```

```python
from contextlib import ExitStack

import numpy as np

import concourse.bass as bass
from concourse import mybir

F32 = mybir.dt.float32
BF16 = mybir.dt.bfloat16
I32 = mybir.dt.int32
ALU = mybir.AluOpType
ACT = mybir.ActivationFunctionType
AX = mybir.AxisListType.X

P = 128
N = 6250
D = 256
NODE_TILES = -(-N // P)
NP = NODE_TILES * P
CHUNKS = 7
TPC = NODE_TILES // CHUNKS
ROWS = TPC * P
HALF = ROWS // 2
BIG = 1.0e30
FAR = 1.0e6
EPS = 1e-5
HOPS = 65536
HOP_TILES = HOPS // P
U = 4
DEPTH = 4


class EdgeList:

    def __init__(self, name, edges):
        self.name = name
        self.edges = edges
        self.edge_tiles = -(-edges // P)
        self.pairs = -(-self.edge_tiles // 2)
        self.tiles = 2 * self.pairs
        self.real_stops = self.pairs + NODE_TILES - 1
        self.stops = -(-self.real_stops // 8) * 8
        self.steps = 2 * self.stops
        self.blocks = -(-self.steps // P)
        self.pair_blocks = -(-self.pairs // P)
        self.turns = self.steps // (U * DEPTH)
        self.pad = self.tiles * P - edges


GRAPH = EdgeList("g", 106250)
HOP = EdgeList("f", HOPS + NP)


class Tally:

    def __init__(self, eng, sem):
        self.eng, self.sem = eng, sem
        self.before, self.per, self.turn, self.here = 0, 0, 0, 0

    def loop(self, turn, per):
        self.before += self.here
        self.turn, self.per, self.here = turn, per, 0

    def leave(self, turns):
        assert self.here == self.per, (self.here, self.per)
        self.before += turns * self.per
        self.turn, self.per, self.here = 0, 0, 0

    def done(self, ins):
        self.here += 1
        ins.then_inc(self.sem, 1)
        self.eng.wait_ge(self.sem, self.before + self.per * self.turn + self.here)


class Scope:

    def __init__(self, nc, ctx, name):
        self.nc, self.ctx, self.name, self.sems = nc, ctx, name, []
        ctx.callback(self.release)

    def release(self):
        for sem in self.sems:
            self.nc.gpsimd.sem_clear(sem)
            self.nc.release_semaphore(sem)

    def sb(self, name, shape, dt=F32):
        return self.ctx.enter_context(self.nc.sbuf_tensor(f"{self.name}_{name}", shape, dt))

    def ps(self, name, shape, dt=F32):
        return self.ctx.enter_context(self.nc.psum_tensor(f"{self.name}_{name}", shape, dt))

    def gather_sem(self, name):
        return self.nc.alloc_semaphore(f"{self.name}_{name}")

    def sem(self, name):
        self.sems.append(self.nc.alloc_semaphore(f"{self.name}_{name}"))
        return self.sems[-1]


def bcast_rows(ap, n):
    return ap.partition_broadcast(n)


def stage_constants(nc, T, K):
    with ExitStack() as ctx:
        s = Scope(nc, ctx, "c")
        frow_i = s.sb("frow_i", [P, P], I32)
        pcol_i = s.sb("pcol_i", [P, 1], I32)
        zero = s.sb("zero", [P, D])
        pad_dst = s.sb("pad_dst", [P, 2], I32)
        made = s.sem("made")
        filled = s.sem("filled")
        moved = s.sem("moved")
        block = ctx.enter_context(nc.Block())
        tail = NP - N

        @block.gpsimd
        def _(pool):
            pool.iota(frow_i[:, :], pattern=[[1, P]], base=0, channel_multiplier=0).then_inc(made, 1)
            pool.iota(pcol_i[:, :], pattern=[[1, 1]], base=0, channel_multiplier=1).then_inc(made, 1)

        @block.vector
        def _(dve):
            link = Tally(dve, s.sem("dve"))
            dve.memset(zero[:, :], 0.0).then_inc(filled, 1)
            dve.memset(pad_dst[:, :], NP - 1).then_inc(filled, 1)
            dve.wait_ge(made, 2)
            dve.tensor_copy(K["frow"][:, :], frow_i[:, :]).then_inc(link.sem, 1)
            link.here += 1
            link.done(dve.tensor_copy(K["pcol"][:, :], pcol_i[:, :]))
            dve.tensor_scalar(K["ident"][:, :], K["frow"][:, :], K["pcol"][:, 0:1], None, ALU.is_equal)
            dve.tensor_scalar(K["below"][:, :], K["frow"][:, :], K["pcol"][:, 0:1], None, ALU.is_gt)
            dve.tensor_scalar(K["minus_col"][:, :], K["pcol"][:, :], -1.0, None, ALU.mult)
            dve.memset(K["ones"][:, :], 1.0)
            dve.memset(K["eps"][:, :], EPS)

        @block.sync
        def _(sp):
            sp.dma_start(T["x0"][0:N, :], T["x"]).then_inc(moved, 16)
            sp.dma_start(T["g_src"][0:GRAPH.edges].rearrange("(a n) -> a n", a=50),
                         T["src"].rearrange("(a n) -> a n", a=50)).then_inc(moved, 16)
            sp.dma_start(T["g_dst"][0:GRAPH.edges].rearrange("(a n) -> a n", a=50),
                         T["dst"].rearrange("(a n) -> a n", a=50)).then_inc(moved, 16)
            sp.wait_ge(filled, 2)
            sp.dma_start(T["x0"][N:NP, :], zero[0:tail, :]).then_inc(moved, 16)
            for L in (GRAPH, HOP):
                for end in ("_src", "_dst"):
                    sp.dma_start(T[L.name + end][L.edges:].rearrange("(p a) -> p a", a=2),
                                 pad_dst[0:L.pad // 2, :]).then_inc(moved, 16)
            sp.wait_ge(moved, 128)


def stage_sort(nc, T, K):
    B = 8
    TURNS = HOP_TILES // B
    NT = NODE_TILES
    with ExitStack() as ctx:
        s = Scope(nc, ctx, "s")
        ends = s.sb("ends", [P, 2, HOP_TILES], I32)
        hi_i = s.sb("hi_i", [P, HOP_TILES], I32)
        lo_i = s.sb("lo_i", [P, HOP_TILES], I32)
        hi = s.sb("hi", [P, HOP_TILES])
        lo = s.sb("lo", [P, HOP_TILES])
        ident = s.sb("ident", [P, P], BF16)
        zeros = s.sb("zeros", [P, P], BF16)
        one_lo = s.sb("one_lo", [P, 2, B, P], BF16)
        one_hi = s.sb("one_hi", [P, 2, B, NT], BF16)
        total = s.sb("total", [P, NT])
        below = s.sb("below", [P, NT])
        upto = s.sb("upto", [P, NT])
        none = s.sb("none", [P, NT])
        loop_i = s.sb("loop_i", [P, NT], I32)
        loop_pos = s.sb("loop_pos", [P, NT], I32)
        loop_pair = s.sb("loop_pair", [P, NT, 2], I32)
        taken = s.sb("taken", [P, NT])
        taken_by_tile = s.sb("taken_by_tile", [P, B, NT])
        lo_t = s.sb("lo_t", [P, 2, B, P])
        lo_t16 = s.sb("lo_t16", [P, 2, B, P], BF16)
        earlier = s.sb("earlier", [P, B, P], BF16)
        picked = s.sb("picked", [P, B, NT])
        pos = s.sb("pos", [P, B])
        pos_i = s.sb("pos_i", [P, 2, B], I32)
        pair = s.sb("pair", [P, 2, B, 2], I32)
        pt = s.ps("pt", [P, B, P])
        pc = s.ps("pc", [P, 2, 512])
        pq = s.ps("pq", [P, B, P])
        pr = s.ps("pr", [P, 512])
        loaded = s.sem("loaded")
        made = s.sem("made")
        hot = s.sem("hot")
        counted = s.sem("counted")
        all_counted = s.sem("all_counted")
        total_ready = s.sem("total_ready")
        total_summed = s.sem("total_summed")
        loops_ready = s.sem("loops_ready")
        hot2 = s.sem("hot2")
        turned = s.sem("turned")
        lo_t_ready = s.sem("lo_t_ready")
        taken_ready = s.sem("taken_ready")
        same_ready = s.sem("same_ready")
        masked = s.sem("masked")
        ranked = s.sem("ranked")
        placed = s.sem("placed")
        iota_done = s.sem("iota_done")
        put = [s.gather_sem("put0"), s.gather_sem("put1")]
        put_loop = s.gather_sem("put_loop")
        block = ctx.enter_context(nc.Block())

        def by_tile(ap):
            return ap[:, 0:B * NT].rearrange("p (u c) -> p u c", u=B)

        @block.sync
        def _(sp):
            for k in range(2):
                sp.dma_start(ends[:, k, :], T["L0_ffn_edge_index"][k].rearrange("(p t) -> p t", p=P)).then_inc(loaded, 16)

        @block.vector
        def _(dve):
            link = Tally(dve, s.sem("dve"))

            def build(h, t0):
                dve.tensor_tensor(one_lo[:, h, :, :], K["frow"][:, :].unsqueeze(1).broadcast_to((P, B, P)),
                                  lo[:, bass.ds(t0, B)].unsqueeze(2).broadcast_to((P, B, P)), ALU.is_equal)
                return dve.tensor_tensor(one_hi[:, h, :, :], K["frow"][:, 0:NT].unsqueeze(1).broadcast_to((P, B, NT)),
                                         hi[:, bass.ds(t0, B)].unsqueeze(2).broadcast_to((P, B, NT)), ALU.is_equal)

            dve.tensor_copy(ident[:, :], K["ident"][:, :]).then_inc(made, 1)
            dve.memset(zeros[:, :], 0.0).then_inc(made, 1)
            dve.memset(none[:, :], 0.0)
            dve.wait_ge(loaded, 32)
            dve.tensor_scalar(hi_i[:, :], ends[:, 1, :], 7, None, ALU.arith_shift_right)
            link.done(dve.tensor_scalar(lo_i[:, :], ends[:, 1, :], P - 1, None, ALU.bitwise_and))
            dve.tensor_copy(hi[:, :], hi_i[:, :])
            link.done(dve.tensor_copy(lo[:, :], lo_i[:, :]))
            with dve.Fori(0, TURNS // 2) as i:
                for h in range(2):
                    g = 2 * i + h
                    dve.wait_ge(counted, g + 1)
                    build(h, g * B).then_inc(hot, 1)
            dve.wait_ge(all_counted, 1)
            dve.tensor_scalar(total[:, :], pr[:, 0:NT], 1.0, None, ALU.add).then_inc(total_ready, 1)
            dve.wait_ge(total_summed, 1)
            link.done(dve.tensor_copy(below[:, :], pc[:, 0, 0:NT]))
            link.done(dve.tensor_tensor_scan(upto[:, :], none[:, :], below[:, :], 0.0, ALU.add, ALU.add))
            link.done(dve.tensor_tensor(upto[:, :], upto[:, :], below[:, :], ALU.subtract))
            link.done(dve.tensor_tensor(upto[:, :], upto[:, :], pc[:, 1, 0:NT], ALU.add))
            dve.tensor_copy(loop_pos[:, :], upto[:, :])
            link.done(dve.tensor_scalar(taken[:, :], upto[:, :], 1.0, None, ALU.add))
            dve.wait_ge(iota_done, 1)
            dve.tensor_copy(loop_pair[:, :, 0], loop_i[:, :])
            dve.tensor_copy(loop_pair[:, :, 1], loop_i[:, :]).then_inc(loops_ready, 1)
            link.done(build(0, 0))
            dve.sem_inc(hot2, 1)
            with dve.Fori(0, TURNS // 2) as i:
                link.loop(i, 2 * 6)
                for h in range(2):
                    g = 2 * i + h
                    link.done(build(1 - h, (g + 1) % TURNS * B))
                    dve.sem_inc(hot2, 1)
                    dve.wait_ge(turned, g + 1)
                    link.done(dve.tensor_tensor(taken_by_tile[:, :, :], by_tile(pc[:, h, :]),
                                                taken[:, :].unsqueeze(1).broadcast_to((P, B, NT)), ALU.add))
                    link.done(dve.tensor_tensor(taken[:, :], taken[:, :], pc[:, h, B * NT:(B + 1) * NT], ALU.add))
                    dve.sem_inc(taken_ready, 1)
                    dve.wait_ge(same_ready, g + 1)
                    dve.tensor_tensor(earlier[:, :, :], pq[:, :, :], K["below"][:, :].unsqueeze(1).broadcast_to((P, B, P)),
                                      ALU.mult).then_inc(masked, 1)
                    dve.wait_ge(ranked, g + 1)
                    link.done(dve.tensor_tensor(picked[:, :, :], by_tile(pr[:, :]), one_hi[:, h, :, :], ALU.mult))
                    link.done(dve.tensor_reduce(pos[:, :], picked[:, :, :], AX, ALU.add))
                    dve.wait_ge(put[h], 16 * B * i)
                    dve.tensor_copy(pair[:, h, :, 0], ends[:, 0, bass.ds(g * B, B)])
                    dve.tensor_copy(pair[:, h, :, 1], ends[:, 1, bass.ds(g * B, B)])
                    link.done(dve.tensor_copy(pos_i[:, h, :], pos[:, :]))
                    dve.sem_inc(placed, 1)
            link.leave(TURNS // 2)

        @block.tensor
        def _(pe):
            def turn(h):
                for u in range(B):
                    pe.matmul(pt[:, u, :], one_lo[:, h, u, :], ident[:, :], start=True, stop=True)
                pe.matmul(pc[:, h, 0:NT], zeros[:, :], zeros[:, 0:NT], start=True, stop=True)
                for u in range(1, B + 1):
                    for v in range(u):
                        mm = pe.matmul(pc[:, h, u * NT:(u + 1) * NT], one_lo[:, h, v, :], one_hi[:, h, v, :],
                                       start=(v == 0), stop=(v == u - 1))
                return mm

            pe.wait_ge(made, 2)
            pe.sem_inc(counted, 2)
            pe.matmul(pr[:, 0:NT], zeros[:, :], zeros[:, 0:NT], start=True, stop=False)
            with pe.Fori(0, TURNS // 2) as i:
                for h in range(2):
                    pe.wait_ge(hot, 2 * i + h + 1)
                    for u in range(B):
                        mm = pe.matmul(pr[:, 0:NT], one_lo[:, h, u, :], one_hi[:, h, u, :], start=False, stop=False)
                    mm.then_inc(counted, 1)
            pe.matmul(pr[:, 0:NT], zeros[:, :], zeros[:, 0:NT], start=False, stop=True).then_inc(all_counted, 1)
            pe.wait_ge(total_ready, 1)
            pe.matmul(pc[:, 0, 0:NT], K["ones"][:, :], total[:, :], start=True, stop=True)
            pe.matmul(pc[:, 1, 0:NT], K["below"][:, :], total[:, :], start=True, stop=True).then_inc(total_summed, 1)
            pe.wait_ge(hot2, 1)
            turn(0).then_inc(turned, 1)
            with pe.Fori(0, TURNS // 2) as i:
                for h in range(2):
                    g = 2 * i + h
                    pe.wait_ge(lo_t_ready, g + 1)
                    pe.wait_ge(masked, g)
                    for u in range(B):
                        mm = pe.matmul(pq[:, u, :], lo_t16[:, h, u, :], lo_t16[:, h, u, :], start=True, stop=True)
                    mm.then_inc(same_ready, 1)
                    pe.wait_ge(hot2, g + 2)
                    turn(1 - h).then_inc(turned, 1)
                    pe.wait_ge(taken_ready, g + 1)
                    pe.wait_ge(masked, g + 1)
                    for u in range(B):
                        rank = pr[:, u * NT:(u + 1) * NT]
                        pe.matmul(rank, lo_t[:, h, u, :], taken_by_tile[:, u, :], start=True, stop=False)
                        mm = pe.matmul(rank, earlier[:, u, :], one_hi[:, h, u, :], start=False, stop=True)
                    mm.then_inc(ranked, 1)

        @block.scalar
        def _(act):
            def copy(h):
                act.activation(lo_t[:, h, :, :], pt[:, :, :], ACT.Copy)
                return act.activation(lo_t16[:, h, :, :], pt[:, :, :], ACT.Copy)

            act.wait_ge(turned, 1)
            copy(0).then_inc(lo_t_ready, 1)
            with act.Fori(0, TURNS // 2) as i:
                for h in range(2):
                    g = 2 * i + h
                    act.wait_ge(turned, g + 2)
                    act.wait_ge(ranked, g)
                    copy(1 - h).then_inc(lo_t_ready, 1)

        @block.gpsimd
        def _(pool):
            pool.iota(loop_i[:, :], pattern=[[P, NT]], base=0, channel_multiplier=1).then_inc(iota_done, 1)
            pool.wait_ge(loops_ready, 1)
            for c in range(NT):
                pool.indirect_dma_start(out=T["f_pairs"], out_offset=bass.IndirectOffsetOnAxis(ap=loop_pos[:, c:c + 1], axis=0),
                                        in_=loop_pair[:, c, :], in_offset=None).then_inc(put_loop, 16)
            with pool.Fori(0, TURNS // 2) as i:
                for h in range(2):
                    pool.wait_ge(placed, 2 * i + h + 1)
                    pool.nop(nofuse=True)
                    for u in range(B):
                        pool.indirect_dma_start(out=T["f_pairs"],
                                                out_offset=bass.IndirectOffsetOnAxis(ap=pos_i[:, h, u:u + 1], axis=0),
                                                in_=pair[:, h, u, :], in_offset=None).then_inc(put[h], 16)
            pool.wait_ge(put[0], 16 * B * (TURNS // 2))
            pool.wait_ge(put[1], 16 * B * (TURNS // 2))
            pool.wait_ge(put_loop, 16 * NT)


def stage_split(nc, T, K):
    n = HOP.edge_tiles
    with ExitStack() as ctx:
        s = Scope(nc, ctx, "p")
        pairs = s.sb("pairs", [P, n, 2], I32)
        ends = s.sb("ends", [P, 2, n], I32)
        loaded = s.sem("loaded")
        split = s.sem("split")
        stored = s.sem("stored")
        block = ctx.enter_context(nc.Block())

        @block.sync
        def _(sp):
            sp.dma_start(pairs[:, :, :], T["f_pairs"].rearrange("(p n) c -> p n c", p=P)).then_inc(loaded, 16)
            sp.wait_ge(split, 2)
            sp.dma_start(T["f_src"][0:HOP.edges].rearrange("(p n) -> p n", p=P), ends[:, 0, :]).then_inc(stored, 16)
            sp.dma_start(T["f_dst"][0:HOP.edges].rearrange("(p n) -> p n", p=P), ends[:, 1, :]).then_inc(stored, 16)
            sp.wait_ge(stored, 32)

        @block.vector
        def _(dve):
            dve.wait_ge(loaded, 16)
            for k in range(2):
                dve.tensor_copy(ends[:, k, :], pairs[:, :, k]).then_inc(split, 1)


def stage_schedule(nc, T, K, L):
    B, W = L.blocks, L.blocks * P
    with ExitStack() as ctx:
        s = Scope(nc, ctx, "m" + L.name)
        last_i = s.sb("last_i", [P, L.pair_blocks], I32)
        last = s.sb("last", [P, L.pair_blocks])
        num_i = s.sb("num_i", [P, max(B, L.pair_blocks)], I32)
        num = s.sb("num", [P, max(B, L.pair_blocks)])
        stop_i = s.sb("stop_i", [P, B], I32)
        stop = s.sb("stop", [P, B])
        second_i = s.sb("second_i", [P, B], I32)
        second = s.sb("second", [P, B])
        srow_i = s.sb("srow_i", [P, W], I32)
        srow = s.sb("srow", [P, W])
        left = s.sb("left", [P, L.pair_blocks, W], BF16)
        ones = s.sb("ones", [P, 1], BF16)
        j_of = s.sb("j_of", [P, B])
        i_of = s.sb("i_of", [P, B])
        far = s.sb("far", [P, B])
        j_idx = s.sb("j_idx", [P, B], I32)
        i_row = s.sb("i_row", [1, W])
        j_row = s.sb("j_row", [1, W // 2])
        i_row_i = s.sb("i_row_i", [1, W // 2], I32)
        j_row_i = s.sb("j_row_i", [1, W // 2], I32)
        got = s.sb("got", [P, 2, B, P], I32)
        val = s.sb("val", [P, 2, B, P])
        rel = s.sb("rel", [P, B, P])
        src_t = s.sb("src_t", [P, W], I32)
        rel_t = s.sb("rel_t", [P, W])
        pj = s.ps("pj", [P, 512])
        prow = s.ps("prow", [1, 2, 512])
        pt = s.ps("pt", [P, 4, 512])
        loaded = s.sem("loaded")
        iotas = s.sem("iotas")
        filled = s.sem("filled")
        marked = s.sem("marked")
        placed = s.sem("placed")
        j_ready = s.sem("j_ready")
        got_rows = s.gather_sem("got_rows")
        rel_ready = s.sem("rel_ready")
        turned = s.sem("turned")
        stored = s.sem("stored")
        t_ready = s.sem("t_ready")
        block = ctx.enter_context(nc.Block())
        full = L.pairs // P * P
        rest = L.pairs - full
        pair_rows = T[L.name + "_dst"].rearrange("(j e) -> j e", e=2 * P)
        dst_rows = T[L.name + "_dst"].rearrange("(j e) -> j e", e=P)
        src_rows = T[L.name + "_src"].rearrange("(j e) -> j e", e=P)
        HW = W // 2

        @block.gpsimd
        def _(pool):
            pool.iota(num_i[:, :], pattern=[[P, num_i.shape[1]]], base=0, channel_multiplier=1).then_inc(iotas, 1)
            pool.iota(srow_i[:, :].rearrange("p (r k) -> p r k", k=2), pattern=[[1, W // 2], [0, 2]], base=0, channel_multiplier=0).then_inc(iotas, 1)
            pool.wait_ge(j_ready, 1)
            for b in range(B):
                for k, rows in enumerate((src_rows, dst_rows)):
                    pool.indirect_dma_start(out=got[:, k, b, :], out_offset=None, in_=rows,
                                            in_offset=bass.IndirectOffsetOnAxis(ap=j_idx[:, b:b + 1], axis=0)
                                            ).then_inc(got_rows, 16)

        @block.sync
        def _(sp):
            sp.wait_ge(filled, 1)
            with nc.allow_non_contiguous_dma(reason="one destination of each pair of tiles"):
                sp.dma_start(last_i[:, 0:full // P], pair_rows[0:full, 2 * P - 1:2 * P].rearrange("(b p) a -> p (b a)", p=P)
                             ).then_inc(loaded, 16)
                sp.dma_start(last_i[0:rest, full // P:full // P + 1], pair_rows[full:L.pairs, 2 * P - 1:2 * P]).then_inc(loaded, 16)
            sp.wait_ge(rel_ready, 1)
            sp.dma_start(T[L.name + "_rel_rows"].rearrange("(b s) e -> s b e", s=P), rel[:, :, :]).then_inc(stored, 16)
            sp.dma_start(T[L.name + "_key_rows"].rearrange("(b s) e -> s b e", s=P), val[:, 1, :, :]).then_inc(stored, 16)
            sp.dma_start(T[L.name + "_i_row"].rearrange("(a s) -> a s", a=1), i_row_i[:, :]).then_inc(stored, 16)
            sp.dma_start(T[L.name + "_j_row"].rearrange("(a s) -> a s", a=1), j_row_i[:, :]).then_inc(stored, 16)
            sp.wait_ge(t_ready, 1)
            sp.dma_start(T[L.name + "_src_t"], src_t[:, 0:L.steps]).then_inc(stored, 16)
            sp.dma_start(T[L.name + "_rel_t"], rel_t[:, 0:L.steps]).then_inc(stored, 16)
            sp.wait_ge(stored, 96)

        @block.vector
        def _(dve):
            link = Tally(dve, s.sem("dve"))
            dve.memset(ones[:, :], 1.0)
            dve.memset(last_i[:, :], 1 << 28).then_inc(filled, 1)
            dve.wait_ge(iotas, 2)
            dve.tensor_copy(num[:, :], num_i[:, :])
            dve.tensor_copy(srow[:, :], srow_i[:, :])
            dve.tensor_scalar(stop_i[:, :], num_i[:, 0:B], 1, None, ALU.arith_shift_right)
            link.done(dve.tensor_scalar(second_i[:, :], num_i[:, 0:B], 1, None, ALU.bitwise_and))
            dve.tensor_copy(stop[:, :], stop_i[:, :])
            link.done(dve.tensor_copy(second[:, :], second_i[:, :]))
            dve.wait_ge(loaded, 32)
            link.done(dve.tensor_scalar(last_i[:, :], last_i[:, :], 7, None, ALU.arith_shift_right))
            link.done(dve.tensor_copy(last[:, :], last_i[:, :]))
            link.done(dve.tensor_tensor(last[:, :], last[:, :], num[:, 0:L.pair_blocks], ALU.add))
            for b in range(L.pair_blocks):
                link.done(dve.tensor_scalar(left[:, b, :], srow[:, :], last[:, b:b + 1], None, ALU.is_gt))
            dve.sem_inc(marked, 1)
            dve.wait_ge(placed, 1)
            link.done(dve.tensor_copy(j_of[:, :], pj[:, 0:B]))
            for h in range(2):
                link.done(dve.tensor_tensor(i_row[:, h * HW:(h + 1) * HW], srow[0:1, h * HW:(h + 1) * HW],
                                            prow[:, h, 0:HW], ALU.subtract))
            link.done(dve.tensor_scalar(i_row[:, :], i_row[:, :], float(NODE_TILES - 1), None, ALU.min))
            dve.tensor_copy(i_row_i[:, :], i_row[:, 0:W:2])
            link.done(dve.tensor_tensor(j_row[:, :], srow[0:1, 0:W:2], i_row[:, 0:W:2], ALU.subtract))
            dve.tensor_scalar(j_row_i[:, :], j_row[:, :], float(L.pairs - 1), None, ALU.min)
            link.done(dve.tensor_tensor(i_of[:, :], stop[:, :], j_of[:, :], ALU.subtract))
            link.done(dve.tensor_scalar(j_of[:, :], j_of[:, :], float(L.pairs - 1), 2.0, ALU.min, ALU.mult))
            link.done(dve.tensor_tensor(j_of[:, :], j_of[:, :], second[:, :], ALU.add))
            link.done(dve.tensor_copy(j_idx[:, :], j_of[:, :]))
            dve.sem_inc(j_ready, 1)
            dve.tensor_scalar(far[:, :], stop[:, :], float(L.real_stops) - 0.5, FAR, ALU.is_gt, ALU.mult)
            link.done(dve.tensor_scalar(i_of[:, :], i_of[:, :], float(P), None, ALU.mult))
            link.done(dve.tensor_tensor(i_of[:, :], i_of[:, :], far[:, :], ALU.add))
            dve.wait_ge(got_rows, 32 * B)
            link.done(dve.tensor_copy(val[:, :, :, :], got[:, :, :, :]))
            link.done(dve.tensor_tensor(rel[:, :, :], val[:, 1, :, :], i_of[:, :].unsqueeze(2).broadcast_to((P, B, P)),
                                        ALU.subtract))
            dve.sem_inc(rel_ready, 1)
            dve.wait_ge(turned, 1)
            for k, to in enumerate((src_t, rel_t)):
                for h in range(2):
                    w = min(512, W - h * 512)
                    link.done(dve.tensor_copy(to[:, h * 512:h * 512 + w], pt[:, 2 * k + h, 0:w]))
            dve.sem_inc(t_ready, 1)

        @block.tensor
        def _(pe):
            pe.wait_ge(marked, 1)
            for b in range(B):
                for c in range(L.pair_blocks):
                    pe.matmul(pj[:, b:b + 1], left[:, c, b * P:(b + 1) * P], ones[:, :],
                              start=(c == 0), stop=(c == L.pair_blocks - 1))
            for h in range(2):
                for c in range(L.pair_blocks):
                    mm = pe.matmul(prow[:, h, 0:HW], ones[:, :], left[:, c, h * HW:(h + 1) * HW],
                                   start=(c == 0), stop=(c == L.pair_blocks - 1))
            mm.then_inc(placed, 1)
            pe.wait_ge(rel_ready, 1)
            for k in range(2):
                for b in range(B):
                    of = val[:, 0, b, :] if k == 0 else rel[:, b, :]
                    mm = pe.transpose(pt[:, 2 * k + b // 4, (b % 4) * P:(b % 4 + 1) * P], of, K["ident"][:, :])
            mm.then_inc(turned, 1)


def rows_of(ap):
    return ap.rearrange("(t p) f -> p t f", p=P)


class Norm:

    def __init__(self, s, turn=True):
        self.x = s.sb("x", [P, TPC, D])
        self.xn = s.sb("xn", [P, TPC, D])
        self.stat = s.sb("stat", [P, TPC, 6])
        self.mv = s.sb("mv", [P, TPC, 2])
        self.sd = s.sb("sd", [P, TPC])
        self.rstd = s.sb("rstd", [P, TPC])
        self.x_loaded = s.sem("x_loaded")
        self.var_ready = s.sem("var_ready")
        self.sd_ready = s.sem("sd_ready")
        self.xn_ready = s.sem("xn_ready")
        if turn:
            self.xt = s.sb("xt", [P, 2, ROWS])
            self.pt = s.ps("pt", [P, 4, 512])
            self.turned = s.sem("turned")
            self.xt_ready = s.sem("xt_ready")

    def load(self, sp, table, c):
        sp.dma_start(self.x[:, :, :], table[bass.ds(c * ROWS, ROWS), :].rearrange("(t p) f -> p t f", p=P)
                     ).then_inc(self.x_loaded, 16)

    def vector(self, dve, link, c, x=None, out=None):
        x = self.x if x is None else x
        out = self.xn if out is None else out
        for t in range(TPC):
            ins = dve.bn_stats(self.stat[:, t, :], x[:, t, :])
        link.done(ins)
        dve.nop(nofuse=True)
        for t in range(TPC):
            ins = dve.bn_aggr(self.mv[:, t, :], self.stat[:, t, :])
        ins.then_inc(self.var_ready, 1)
        dve.wait_ge(self.sd_ready, c + 1)
        link.done(dve.reciprocal(self.rstd[:, :], self.sd[:, :]))
        for t in range(TPC):
            ins = dve.tensor_scalar(out[:, t, :], x[:, t, :], self.mv[:, t, 0:1], self.rstd[:, t:t + 1],
                                    ALU.subtract, ALU.mult)
        return ins

    def scalar(self, act, K, c):
        act.wait_ge(self.var_ready, c + 1)
        act.activation(self.sd[:, :], self.mv[:, :, 1], ACT.Sqrt, bias=K["eps"][:, 0:1]).then_inc(self.sd_ready, 1)

    def tensor(self, pe, K, c):
        pe.wait_ge(self.xn_ready, c + 1)
        for f in range(2):
            for t in range(TPC):
                ins = pe.transpose(self.pt[:, 2 * f + t // 4, (t % 4) * P:(t % 4 + 1) * P],
                                   self.xn[:, t, f * P:(f + 1) * P], K["ident"][:, :])
        ins.then_inc(self.turned, 1)

    def scalar_turned(self, act, c):
        act.wait_ge(self.turned, c + 1)
        for f in range(2):
            for h in range(2):
                w = min(512, ROWS - h * 512)
                ins = act.activation(self.xt[:, f, h * 512:h * 512 + w], self.pt[:, 2 * f + h, 0:w], ACT.Copy)
        ins.then_inc(self.xt_ready, 1)


def stage_l0_project(nc, T, K):
    with ExitStack() as ctx:
        s = Scope(nc, ctx, "q")
        n = Norm(s)
        w = s.sb("w", [P, 4, 2, D])
        wt = s.sb("wt", [P, 2, 4 * D])
        bias = s.sb("bias", [P, 4 * D])
        out = s.sb("out", [P, TPC, 4 * D])
        pq = s.ps("pq", [P, 2, 2 * 512])
        loaded = s.sem("loaded")
        w_turned = s.sem("w_turned")
        wt_ready = s.sem("wt_ready")
        projected = s.sem("projected")
        biased = s.sem("biased")
        stored = s.sem("stored")
        block = ctx.enter_context(nc.Block())
        names = ("q", "k", "v", "skip")

        @block.sync
        def _(sp):
            n.load(sp, T["x0"], 0)
            for k, m in enumerate(names):
                sp.dma_start(w[:, k, :, :], T["L0_gnn_W" + m].rearrange("(a p) f -> p a f", p=P)).then_inc(loaded, 16)
                sp.dma_start(bias[:, k * D:(k + 1) * D], bcast_rows(T["L0_gnn_b" + m], P)).then_inc(loaded, 16)
            with sp.Fori(0, CHUNKS) as c:
                sp.wait_ge(n.xn_ready, c + 1)
                n.load(sp, T["x0"], (c + 1) % CHUNKS)
                sp.wait_ge(biased, TPC * (c + 1))
                for k, m in enumerate(names):
                    sp.dma_start(T["l0_" + m][bass.ds(c * ROWS, ROWS), :].rearrange("(t p) f -> p t f", p=P),
                                 out[:, :, k * D:(k + 1) * D]).then_inc(stored, 16)
            sp.wait_ge(stored, 64 * CHUNKS)
            sp.wait_ge(n.x_loaded, 16 * (CHUNKS + 1))

        @block.vector
        def _(dve):
            link = Tally(dve, s.sem("dve"))
            with dve.Fori(0, CHUNKS) as c:
                link.loop(c, 2)
                dve.wait_ge(n.x_loaded, 16 * c + 16)
                n.vector(dve, link, c).then_inc(n.xn_ready, 1)
                dve.wait_ge(loaded, 128)
                dve.wait_ge(stored, 64 * c)
                for t in range(TPC):
                    dve.wait_ge(projected, TPC * c + t + 1)
                    dve.tensor_tensor(out[:, t, :], pq[:, t % 2, :], bias[:, :], ALU.add).then_inc(biased, 1)
            link.leave(CHUNKS)

        @block.scalar
        def _(act):
            act.wait_ge(w_turned, 1)
            for k in range(4):
                for f in range(2):
                    ins = act.activation(wt[:, f, k * D:(k + 1) * D], n.pt[:, k, f * D:(f + 1) * D], ACT.Copy)
            ins.then_inc(wt_ready, 1)
            with act.Fori(0, CHUNKS) as c:
                n.scalar(act, K, c)
                n.scalar_turned(act, c)

        @block.tensor
        def _(pe):
            pe.wait_ge(loaded, 128)
            for k in range(4):
                for f in range(2):
                    for a in range(2):
                        ins = pe.transpose(n.pt[:, k, f * D + a * P:f * D + (a + 1) * P],
                                           w[:, k, a, f * P:(f + 1) * P], K["ident"][:, :])
            ins.then_inc(w_turned, 1)
            pe.wait_ge(wt_ready, 1)
            with pe.Fori(0, CHUNKS) as c:
                n.tensor(pe, K, c)
                pe.wait_ge(n.xt_ready, c + 1)
                for t in range(TPC):
                    g = TPC * c + t
                    pe.wait_ge(biased, g if t < 2 else g - 1)
                    for h in range(2):
                        for f in range(2):
                            ins = pe.matmul(pq[:, t % 2, h * 512:(h + 1) * 512], n.xt[:, f, t * P:(t + 1) * P],
                                            wt[:, f, h * 512:(h + 1) * 512], start=(f == 0), stop=(f == 1))
                    ins.then_inc(projected, 1)


def stage_dot(nc, T, K, L):
    H = 4
    STOPS = DEPTH * U // 2
    with ExitStack() as ctx:
        s = Scope(nc, ctx, "d")
        keys = s.sb("keys", [P, NODE_TILES, D])
        src = s.sb("src", [P, L.steps], I32)
        i_row = s.sb("i_row", [1, L.stops], I32)
        spread = s.sb("spread", [P, DEPTH, U * P])
        apart = s.sb("apart", [P, DEPTH, U * P])
        hot = s.sb("hot", [P, DEPTH, U * P])
        idx = s.sb("idx", [P, DEPTH, U], I32)
        q = s.sb("q", [P, DEPTH, U, D])
        prod = s.sb("prod", [P, DEPTH, U * D])
        score = s.sb("score", [P, L.steps, H])
        pk = s.ps("pk", [P, DEPTH, U * D])
        loaded = s.sem("loaded")
        spread_in = [s.sem(f"spread_in{h}") for h in range(DEPTH)]
        q_in = [s.gather_sem(f"q_in{h}") for h in range(DEPTH)]
        idx_ready = s.sem("idx_ready")
        apart_ready = s.sem("apart_ready")
        hot_ready = s.sem("hot_ready")
        keys_out = s.sem("keys_out")
        multiplied = s.sem("multiplied")
        scored = s.sem("scored")
        stored = s.sem("stored")
        block = ctx.enter_context(nc.Block())
        rel_flat = T[L.name + "_rel_rows"].rearrange("s e -> (s e)")

        @block.sync
        def _(sp):
            sp.dma_start(src[:, :], T[L.name + "_src_t"]).then_inc(loaded, 16)
            sp.dma_start(i_row[:, :], T[L.name + "_i_row"][0:L.stops].rearrange("(a s) -> a s", a=1)).then_inc(loaded, 16)
            sp.dma_start(keys[:, :, :], rows_of(T["l0_k"])).then_inc(loaded, 16)
            with sp.Fori(0, L.turns) as i:
                for h in range(DEPTH):
                    g = i * DEPTH + h
                    sp.wait_ge(apart_ready, g + 1)
                    sp.dma_start(spread[:, h, :], rel_flat[bass.ds(g * U * P, U * P)].partition_broadcast(P)
                                 ).then_inc(spread_in[h], 16)
            sp.wait_ge(scored, L.turns * DEPTH)
            sp.dma_start(T["score"][:, 0:L.steps * H], score[:, :, :].rearrange("p s h -> p (s h)")).then_inc(stored, 16)
            sp.wait_ge(stored, 16)

        @block.gpsimd
        def _(pool):
            with pool.Fori(0, L.turns) as i:
                for h in range(DEPTH):
                    g = i * DEPTH + h
                    pool.wait_ge(idx_ready, g + 1)
                    pool.wait_ge(multiplied, g + 1)
                    pool.nop(nofuse=True)
                    for u in range(U):
                        pool.indirect_dma_start(out=q[:, h, u, :], out_offset=None, in_=T["l0_q"],
                                                in_offset=bass.IndirectOffsetOnAxis(ap=idx[:, h, u:u + 1], axis=0)
                                                ).then_inc(q_in[h], 16)

        @block.scalar
        def _(act):
            act.sem_inc(apart_ready, DEPTH)
            act.sem_inc(hot_ready, DEPTH)
            with act.Fori(0, L.turns) as i:
                for h in range(DEPTH):
                    g = i * DEPTH + h
                    act.wait_ge(spread_in[h], 16 * (i + 1))
                    act.activation(apart[:, h, :], spread[:, h, :], ACT.Abs, bias=K["minus_col"][:, 0:1]).then_inc(apart_ready, 1)
                    act.wait_ge(apart_ready, DEPTH + g + 1)
                    act.wait_ge(keys_out, g + 1)
                    act.activation(hot[:, h, :], apart[:, h, :], ACT.Relu, scale=-1.0, bias=K["ones"][:, 0:1]).then_inc(hot_ready, 1)

        @block.vector
        def _(dve):
            dve.sem_inc(multiplied, DEPTH)
            dve.wait_ge(loaded, 48)
            dve.tensor_copy(idx[:, :, :], src[:, 0:DEPTH * U].rearrange("p (d u) -> p d u", u=U)).then_inc(idx_ready, DEPTH)
            with dve.Fori(0, L.turns) as i:
                for h in range(DEPTH):
                    g = i * DEPTH + h
                    dve.wait_ge(q_in[h], 16 * U * (i + 1))
                    dve.tensor_copy(idx[:, h, :], src[:, bass.ds((g + DEPTH) % (L.turns * DEPTH) * U, U)]).then_inc(idx_ready, 1)
                    dve.wait_ge(keys_out, DEPTH + g + 1)
                    dve.tensor_tensor(prod[:, h, :], pk[:, h, :], q[:, h, :, :].rearrange("p u d -> p (u d)"),
                                      ALU.mult).then_inc(multiplied, 1)
                    dve.wait_ge(multiplied, DEPTH + g + 1)
                    dve.tensor_reduce(score[:, bass.ds(g * U, U), :].rearrange("p u h -> p (u h)"),
                                      prod[:, h, :].rearrange("p (a c) -> p a c", c=D // H), AX, ALU.add).then_inc(scored, 1)

        @block.tensor
        def _(pe):
            pe.sem_inc(keys_out, DEPTH)
            pe.wait_ge(loaded, 48)
            with pe.Fori(0, L.turns) as i:
                _, tile = nc.values_load_multi_w_load_instructions(
                    i_row[0:1, bass.ds(i * STOPS, STOPS)], engines=[mybir.EngineType.PE], min_val=0, max_val=NODE_TILES - 1)
                for h in range(DEPTH):
                    g = i * DEPTH + h
                    pe.wait_ge(hot_ready, DEPTH + g + 1)
                    pe.wait_ge(multiplied, g + 1)
                    for u in range(U):
                        mm = pe.matmul(pk[:, h, u * D:(u + 1) * D], hot[:, h, u * P:(u + 1) * P],
                                       keys[:, bass.ds(tile[(h * U + u) // 2], 1), :], start=True, stop=True)
                    mm.then_inc(keys_out, 1)


def stage_softmax(nc, T, K, L, H, scale):
    B, S = L.blocks, L.steps
    W = B * P
    last = S - (B - 1) * P
    with ExitStack() as ctx:
        s = Scope(nc, ctx, "x" + L.name + str(H))
        score = s.sb("score", [P, S, H])
        one = s.sb("one", [P, W])
        rows = s.sb("rows", [P, B, P])
        lane = s.sb("lane", [P, S])
        key = s.sb("key", [P, S + 2])
        rel = s.sb("rel", [P, S])
        off = s.sb("off", [P, S])
        from_left = s.sb("from_left", [P, S])
        from_right = s.sb("from_right", [P, S])
        in_first = s.sb("in_first", [P, S])
        in_last = s.sb("in_last", [P, S])
        val = s.sb("val", [P, S])
        fwd = s.sb("fwd", [P, S])
        bwd = s.sb("bwd", [P, S])
        edge = s.sb("edge", [P, 2])
        spread = s.sb("spread", [P, 2, P])
        match = s.sb("match", [P, 2, 2, P])
        cand = s.sb("cand", [P, 2, 2, P])
        top = s.sb("top", [P, 2])
        weight = s.sb("weight", [P, S, H])
        pt = s.ps("pt", [P, 2, 512])
        pb = s.ps("pb", [P, 2, 512])
        pw = s.ps("pw", [P, 2, 512])
        loaded = s.sem("loaded")
        one_ready = s.sem("one_ready")
        turned = s.sem("turned")
        rows_ready = s.sem("rows_ready")
        rows_out = s.sem("rows_out")
        lane_in = s.sem("lane_in")
        spread_ready = s.sem("spread_ready")
        spread_out = s.sem("spread_out")
        diff_ready = s.sem("diff_ready")
        exp_ready = s.sem("exp_ready")
        back_out = s.sem("back_out")
        back_in = s.sem("back_in")
        back_turned = s.sem("back_turned")
        weighted = s.sem("weighted")
        stored = s.sem("stored")
        block = ctx.enter_context(nc.Block())
        flat = T["lanes"]
        by_lane = flat[0:P * S].rearrange("(p s) -> p s", p=P)
        head_rows = flat[0:(B - 1) * P * P].rearrange("(b s e) -> s b e", s=P, e=P)
        tail_rows = flat[(B - 1) * P * P:S * P].rearrange("(s e) -> s e", e=P)

        @block.sync
        def _(sp):
            sp.dma_start(score[:, :, :].rearrange("p s h -> p (s h)"), T["score"][:, 0:S * H]).then_inc(loaded, 16)
            for to, of in ((key[:, 1:S + 1], "_key_rows"), (rel[:, :], "_rel_rows")):
                sp.dma_start(to, T[L.name + of].rearrange("s e -> (s e)")[0:P * S].rearrange("(p s) -> p s", p=P)
                             ).then_inc(loaded, 16)
            with sp.Fori(0, H) as h:
                sp.wait_ge(rows_ready, h + 1)
                sp.dma_start(head_rows, rows[:, 0:B - 1, :]).then_inc(rows_out, 16)
                sp.dma_start(tail_rows, rows[0:last, B - 1, :]).then_inc(rows_out, 16)
                sp.wait_ge(rows_out, 32 * (h + 1))
                sp.dma_start(lane[:, :], by_lane).then_inc(lane_in, 16)
                sp.wait_ge(exp_ready, h + 1)
                sp.dma_start(by_lane, val[:, :]).then_inc(back_out, 16)
                sp.wait_ge(back_out, 16 * (h + 1))
                sp.dma_start(rows[:, 0:B - 1, :], head_rows).then_inc(back_in, 16)
                sp.dma_start(rows[0:last, B - 1, :], tail_rows).then_inc(back_in, 16)
            sp.wait_ge(weighted, H)
            sp.dma_start(T["weight"][:, 0:S * H], weight[:, :, :].rearrange("p s h -> p (s h)")).then_inc(stored, 16)
            sp.wait_ge(stored, 16)

        @block.vector
        def _(dve):
            link = Tally(dve, s.sem("dve"))
            dve.memset(one[:, :], 0.0)
            dve.memset(rows[:, :, :], 0.0)
            dve.wait_ge(loaded, 48)
            dve.tensor_scalar(off[:, :], rel[:, :], 0.0, -BIG, ALU.is_lt, ALU.mult)
            link.done(dve.tensor_scalar(lane[:, :], rel[:, :], float(P - 1), -BIG, ALU.is_gt, ALU.mult))
            link.done(dve.tensor_tensor(off[:, :], off[:, :], lane[:, :], ALU.add))
            dve.memset(key[:, 0:1], -1.0)
            link.done(dve.memset(key[:, S + 1:S + 2], -1.0))
            link.done(dve.tensor_tensor(from_left[:, :], key[:, 1:S + 1], key[:, 0:S], ALU.not_equal))
            link.done(dve.tensor_tensor(from_right[:, :], key[:, 1:S + 1], key[:, 2:S + 2], ALU.not_equal))
            dve.tensor_scalar(from_left[:, :], from_left[:, :], -BIG, None, ALU.mult)
            dve.tensor_scalar(from_right[:, :], from_right[:, :], -BIG, None, ALU.mult)
            dve.tensor_scalar(in_first[:, :], key[:, 1:S + 1], key[:, 1:2], -BIG, ALU.not_equal, ALU.mult)
            link.done(dve.tensor_scalar(in_last[:, :], key[:, 1:S + 1], key[:, S:S + 1], -BIG, ALU.not_equal, ALU.mult))
            ends = (key[:, 1:2], key[:, S:S + 1])
            for k in range(2):
                dve.tensor_copy(spread[:, k, :], ends[k].broadcast_to((P, P))).then_inc(spread_ready, 1)
            dve.wait_ge(spread_out, 1)
            for a in range(2):
                for k in range(2):
                    ins = dve.tensor_scalar(match[:, a, k, :], pb[:, k, 0:P], ends[a], -BIG, ALU.not_equal, ALU.mult)
            link.done(ins)
            with dve.Fori(0, H) as h:
                link.loop(h, 11)
                dve.tensor_copy(one[:, 0:S], score[:, :, bass.ds(h, 1)].rearrange("p s a -> p (s a)")).then_inc(one_ready, 1)
                dve.wait_ge(turned, h + 1)
                dve.wait_ge(weighted, h)
                full = min(B - 1, 4)
                dve.tensor_copy(rows[:, 0:full, :], pt[:, 0, 0:full * P].rearrange("p (b e) -> p b e", e=P))
                if B - 1 > 4:
                    dve.tensor_copy(rows[:, 4:B - 1, :], pt[:, 1, 0:(B - 5) * P].rearrange("p (b e) -> p b e", e=P))
                dve.tensor_copy(rows[0:last, B - 1, :], pt[0:last, (B - 1) // 4, (B - 1) % 4 * P:((B - 1) % 4 + 1) * P]
                                ).then_inc(rows_ready, 1)
                dve.wait_ge(lane_in, 16 * (h + 1))
                link.done(dve.tensor_tensor(val[:, :], lane[:, :], off[:, :], ALU.add))
                dve.tensor_tensor_scan(fwd[:, :], from_left[:, :], val[:, :], -BIG, ALU.add, ALU.max)
                link.done(dve.tensor_tensor_scan(bwd[:, ::-1], from_right[:, ::-1], val[:, ::-1], -BIG, ALU.add, ALU.max))
                dve.tensor_copy(spread[:, 0, :], bwd[:, 0:1].broadcast_to((P, P))).then_inc(spread_ready, 1)
                dve.tensor_copy(spread[:, 1, :], fwd[:, S - 1:S].broadcast_to((P, P))).then_inc(spread_ready, 1)
                link.done(dve.tensor_tensor(val[:, :], fwd[:, :], bwd[:, :], ALU.max))
                dve.wait_ge(spread_out, h + 2)
                for a in range(2):
                    ins = dve.tensor_tensor(cand[:, a, :, :], pb[:, :, 0:P], match[:, a, :, :], ALU.add)
                link.done(ins)
                link.done(dve.tensor_reduce(top[:, :], cand[:, :, :, :].rearrange("p a k c -> p a (k c)"), AX, ALU.max))
                link.done(dve.scalar_tensor_tensor(val[:, :], in_first[:, :], top[:, 0:1], val[:, :], ALU.add, ALU.max))
                link.done(dve.scalar_tensor_tensor(val[:, :], in_last[:, :], top[:, 1:2], val[:, :], ALU.add, ALU.max))
                link.done(dve.tensor_tensor(val[:, :], lane[:, :], val[:, :], ALU.subtract))
                link.done(dve.tensor_scalar(val[:, :], val[:, :], 0.0, None, ALU.min))
                dve.sem_inc(diff_ready, 1)
                dve.wait_ge(back_turned, h + 1)
                for b in range(0, B, 4):
                    w = min(512, S - b * P)
                    ins = dve.tensor_copy(weight[:, b * P:b * P + w, bass.ds(h, 1)].rearrange("p s a -> p (s a)"),
                                          pw[:, b // 4, 0:w])
                    link.done(ins)
                dve.sem_inc(weighted, 1)
            link.leave(H)

        @block.scalar
        def _(act):
            with act.Fori(0, H) as h:
                act.wait_ge(diff_ready, h + 1)
                act.activation(val[:, :], val[:, :], ACT.Exp, scale=scale).then_inc(exp_ready, 1)

        @block.tensor
        def _(pe):
            pe.wait_ge(spread_ready, 2)
            for k in range(2):
                mm = pe.transpose(pb[:, k, 0:P], spread[:, k, :], K["ident"][:, :])
            mm.then_inc(spread_out, 1)
            with pe.Fori(0, H) as h:
                pe.wait_ge(one_ready, h + 1)
                for b in range(B):
                    mm = pe.transpose(pt[:, b // 4, (b % 4) * P:(b % 4 + 1) * P], one[:, b * P:(b + 1) * P], K["ident"][:, :])
                mm.then_inc(turned, 1)
                pe.wait_ge(spread_ready, 2 * h + 4)
                for k in range(2):
                    mm = pe.transpose(pb[:, k, 0:P], spread[:, k, :], K["ident"][:, :])
                mm.then_inc(spread_out, 1)
                pe.wait_ge(back_in, 32 * (h + 1))
                for b in range(B):
                    mm = pe.transpose(pw[:, b // 4, (b % 4) * P:(b % 4 + 1) * P], rows[:, b, :], K["ident"][:, :])
                mm.then_inc(back_turned, 1)


def stage_sum(nc, T, K, L, H, W, table=None):
    STOPS = DEPTH * U // 2
    PER = U // 2
    LAST = L.turns * DEPTH - 1
    C = W // H
    with ExitStack() as ctx:
        s = Scope(nc, ctx, "a" + L.name + str(H))
        acc = s.sb("acc", [P, NODE_TILES, W + H])
        weight = s.sb("weight", [P, L.steps, H])
        rel = s.sb("rel", [P, L.steps])
        i_row = s.sb("i_row", [1, L.stops], I32)
        apart = s.sb("apart", [P, DEPTH, U, P])
        hot = s.sb("hot", [P, DEPTH, U, P])
        rhs = s.sb("rhs", [P, DEPTH, U, W + H])
        pa = s.ps("pa", [P, DEPTH, PER, 512])
        loaded = s.sem("loaded")
        cleared = s.sem("cleared")
        turned_round = s.sem("turned_round")
        apart_ready = s.sem("apart_ready")
        hot_ready = s.sem("hot_ready")
        rhs_ready = s.sem("rhs_ready")
        summed = s.sem("summed")
        added = s.sem("added")
        stored = s.sem("stored")
        if table is not None:
            src = s.sb("src", [P, L.steps], I32)
            idx = s.sb("idx", [P, DEPTH, U], I32)
            got = s.sb("got", [P, DEPTH, U, W])
            idx_ready = s.sem("idx_ready")
            got_in = [s.gather_sem(f"got_in{h}") for h in range(DEPTH)]
        else:
            every = s.sb("every", [P, L.steps, W])
        block = ctx.enter_context(nc.Block())

        @block.sync
        def _(sp):
            if table is not None:
                sp.dma_start(src[:, :], T[L.name + "_src_t"]).then_inc(loaded, 16)
            else:
                sp.dma_start(every[:, :, :], T["f_rows"]).then_inc(loaded, 16)
            sp.dma_start(i_row[:, :], T[L.name + "_i_row"][0:L.stops].rearrange("(a s) -> a s", a=1)).then_inc(loaded, 16)
            sp.dma_start(rel[:, :], T[L.name + "_rel_t"]).then_inc(loaded, 16)
            sp.dma_start(weight[:, :, :].rearrange("p s h -> p (s h)"), T["weight"][:, 0:L.steps * H]).then_inc(loaded, 16)
            sp.wait_ge(added, PER * DEPTH + L.stops)
            sp.dma_start(T["acc"][:, 0:NODE_TILES * (W + H)], acc[:, :, :].rearrange("p t w -> p (t w)")).then_inc(stored, 16)
            sp.wait_ge(stored, 16)

        if table is not None:
            @block.gpsimd
            def _(pool):
                with pool.Fori(0, L.turns) as i:
                    for h in range(DEPTH):
                        g = i * DEPTH + h
                        pool.wait_ge(idx_ready, g + 1)
                        pool.wait_ge(rhs_ready, g + 1)
                        pool.nop(nofuse=True)
                        for u in range(U):
                            pool.indirect_dma_start(out=got[:, h, u, :], out_offset=None, in_=table,
                                                    in_offset=bass.IndirectOffsetOnAxis(ap=idx[:, h, u:u + 1], axis=0)
                                                    ).then_inc(got_in[h], 16)

        @block.scalar
        def _(act):
            act.sem_inc(apart_ready, DEPTH * U)
            act.sem_inc(hot_ready, DEPTH)
            act.wait_ge(turned_round, 1)
            with act.Fori(0, L.turns) as i:
                for h in range(DEPTH):
                    g = i * DEPTH + h
                    act.wait_ge(hot_ready, g + 1)
                    for u in range(U):
                        act.activation(apart[:, h, u, :], K["frow"][:, :], ACT.Abs, bias=rel[:, bass.ds(g * U + u, 1)]
                                       ).then_inc(apart_ready, 1)
                    act.wait_ge(apart_ready, U * (DEPTH + g + 1))
                    act.wait_ge(summed, g + 1)
                    act.activation(hot[:, h, :, :], apart[:, h, :, :], ACT.Relu, scale=-1.0, bias=K["ones"][:, 0:1]
                                   ).then_inc(hot_ready, 1)

        @block.vector
        def _(dve):
            def weigh(i, h):
                g = i * DEPTH + h
                if table is not None:
                    dve.wait_ge(got_in[h], 16 * U * (i + 1))
                    dve.tensor_copy(idx[:, h, :], src[:, bass.ds((g + DEPTH) % (LAST + 1) * U, U)]).then_inc(idx_ready, 1)
                    rows = got[:, h, :, :]
                else:
                    rows = every[:, bass.ds(g * U, U), :]
                dve.wait_ge(summed, g + 1)
                w = weight[:, bass.ds(g * U, U), :]
                dve.tensor_copy(rhs[:, h, :, W:W + H], w)
                dve.tensor_tensor(rhs[:, h, :, 0:W].rearrange("p u (h c) -> p u h c", h=H),
                                  rows.rearrange("p u (h c) -> p u h c", h=H),
                                  w.unsqueeze(3).broadcast_to((P, U, H, C)), ALU.mult).then_inc(rhs_ready, 1)

            def tiles_of(i):
                return nc.values_load_multi_w_load_instructions(i_row[0:1, bass.ds(i * STOPS, STOPS)],
                                                                engines=[mybir.EngineType.DVE],
                                                                min_val=0, max_val=NODE_TILES - 1)[1]

            def add(i, h, k, tile):
                g = i * DEPTH + h
                dve.wait_ge(summed, DEPTH + g + 1)
                dve.wait_ge(added, PER * (DEPTH + g) + k)
                to = acc[:, bass.ds(tile[h * PER + k], 1), :].rearrange("p a w -> p (a w)")
                dve.tensor_tensor(to, to, pa[:, h, k, 0:W + H], ALU.add).then_inc(added, 1)

            dve.sem_inc(rhs_ready, DEPTH)
            dve.sem_inc(added, PER * DEPTH)
            dve.memset(acc[:, :, :], 0.0).then_inc(cleared, 1)
            dve.wait_ge(loaded, 64)
            dve.tensor_scalar(rel[:, :], rel[:, :], -1.0, None, ALU.mult).then_inc(turned_round, 1)
            dve.wait_ge(cleared, 1)
            if table is not None:
                dve.tensor_copy(idx[:, :, :], src[:, 0:DEPTH * U].rearrange("p (d u) -> p d u", u=U)).then_inc(idx_ready, DEPTH)
            weigh(0, 0)
            weigh(0, 1)
            with dve.Fori(0, L.turns - 1) as i:
                tile = tiles_of(i)
                for h in range(DEPTH):
                    add(i, h, 0, tile)
                    weigh(i + (h + 2) // DEPTH, (h + 2) % DEPTH)
                    add(i, h, 1, tile)
            tile = tiles_of(L.turns - 1)
            for h in range(DEPTH):
                add(L.turns - 1, h, 0, tile)
                if h + 2 < DEPTH:
                    weigh(L.turns - 1, h + 2)
                add(L.turns - 1, h, 1, tile)

        @block.tensor
        def _(pe):
            pe.sem_inc(summed, DEPTH)
            with pe.Fori(0, L.turns) as i:
                for h in range(DEPTH):
                    g = i * DEPTH + h
                    pe.wait_ge(hot_ready, DEPTH + g + 1)
                    pe.wait_ge(rhs_ready, DEPTH + g + 1)
                    pe.wait_ge(added, PER * (g + 1))
                    for u in range(U):
                        mm = pe.matmul(pa[:, h, u // 2, 0:W + H], hot[:, h, u, :], rhs[:, h, u, :],
                                       start=(u % 2 == 0), stop=(u % 2 == 1))
                    mm.then_inc(summed, 1)


PAIRS = -(-TPC // 2)


def chunk_of(ap, c):
    return ap[bass.ds(c * ROWS, ROWS), :].rearrange("(t p) f -> p t f", p=P)


def over_tiles(ap, tiles=TPC):
    return ap.unsqueeze(1).broadcast_to((P, tiles, ap.shape[1]))


def stage_l0_finish(nc, T, K):
    H, W = 4, D
    with ExitStack() as ctx:
        s = Scope(nc, ctx, "e")
        n = Norm(s, turn=False)
        acc = s.sb("acc", [P, TPC, W + H])
        skip = s.sb("skip", [P, TPC, D])
        x0 = s.sb("x0", [P, TPC, D])
        gates = s.sb("gates", [P, 3, D])
        w_skip = s.sb("w_skip", [P, D])
        w_rst = s.sb("w_rst", [P, D])
        gain = s.sb("gain", [P, D])
        shift = s.sb("shift", [P, D])
        slope = s.sb("slope", [P, 1])
        g_bias = s.sb("g_bias", [P, 1])
        rden = s.sb("rden", [P, TPC, H])
        rst = s.sb("rst", [P, TPC, D])
        t1 = s.sb("t1", [P, TPC, D])
        t2 = s.sb("t2", [P, TPC, D])
        z = s.sb("z", [P, TPC])
        gate = s.sb("gate", [P, TPC])
        out = s.sb("out", [P, TPC, D])
        params = s.sem("params")
        loaded = s.sem("loaded")
        z_ready = s.sem("z_ready")
        gate_ready = s.sem("gate_ready")
        out_ready = s.sem("out_ready")
        stored = s.sem("stored")
        block = ctx.enter_context(nc.Block())
        acc_all = T["acc"][:, 0:NODE_TILES * (W + H)]

        @block.sync
        def _(sp):
            sp.dma_start(gates[:, :, :].rearrange("p a d -> p (a d)"), bcast_rows(T["L0_gnn_Wgate"].rearrange("a n -> (a n)"), P)
                         ).then_inc(params, 16)
            sp.dma_start(gain[:, :], bcast_rows(T["L0_gnn_ln_w"], P)).then_inc(params, 16)
            sp.dma_start(shift[:, :], bcast_rows(T["L0_gnn_ln_b"], P)).then_inc(params, 16)
            sp.dma_start(slope[:, :], bcast_rows(T["L0_gnn_prelu_a"], P)).then_inc(params, 16)
            sp.dma_start(g_bias[:, :], bcast_rows(T["L0_gnn_bgate"], P)).then_inc(params, 16)
            with sp.Fori(0, CHUNKS) as c:
                sp.wait_ge(out_ready, c)
                sp.dma_start(acc[:, :, :].rearrange("p t w -> p (t w)"),
                             acc_all[:, bass.ds(c * (TPC * (W + H)), TPC * (W + H))]).then_inc(loaded, 16)
                sp.dma_start(skip[:, :, :], chunk_of(T["l0_skip"], c)).then_inc(loaded, 16)
                sp.dma_start(x0[:, :, :], chunk_of(T["x0"], c)).then_inc(loaded, 16)
                sp.wait_ge(out_ready, c + 1)
                sp.dma_start(chunk_of(T["x1"], c), out[:, :, :]).then_inc(stored, 16)
            sp.wait_ge(stored, 16 * CHUNKS)

        @block.vector
        def _(dve):
            link = Tally(dve, s.sem("dve"))
            dve.wait_ge(params, 80)
            dve.tensor_tensor(w_skip[:, :], gates[:, 0, :], gates[:, 2, :], ALU.add)
            link.done(dve.tensor_tensor(w_rst[:, :], gates[:, 1, :], gates[:, 2, :], ALU.subtract))
            with dve.Fori(0, CHUNKS) as c:
                link.loop(c, 13)
                dve.wait_ge(loaded, 48 * c + 48)
                link.done(dve.tensor_scalar(rden[:, :, :], acc[:, :, W:W + H], 1e-16, 0.5, ALU.add, ALU.max))
                link.done(dve.reciprocal(rden[:, :, :], rden[:, :, :]))
                dve.tensor_tensor(t1[:, :, :], skip[:, :, :], over_tiles(w_skip[:, :]), ALU.mult)
                link.done(dve.tensor_tensor(rst[:, :, :].rearrange("p t (h c) -> p t h c", h=H),
                                            acc[:, :, 0:W].rearrange("p t (h c) -> p t h c", h=H),
                                            rden[:, :, :].unsqueeze(3).broadcast_to((P, TPC, H, W // H)), ALU.mult))
                link.done(dve.tensor_tensor(t2[:, :, :], rst[:, :, :], over_tiles(w_rst[:, :]), ALU.mult))
                link.done(dve.tensor_tensor(t1[:, :, :], t1[:, :, :], t2[:, :, :], ALU.add))
                dve.tensor_reduce(z[:, :], t1[:, :, :], AX, ALU.add).then_inc(z_ready, 1)
                link.done(dve.tensor_tensor(t2[:, :, :], skip[:, :, :], rst[:, :, :], ALU.subtract))
                dve.wait_ge(gate_ready, c + 1)
                for t in range(TPC):
                    ins = dve.scalar_tensor_tensor(rst[:, t, :], t2[:, t, :], gate[:, t:t + 1], rst[:, t, :],
                                                   ALU.mult, ALU.add)
                link.done(ins)
                link.done(n.vector(dve, link, c, x=rst, out=t1))
                link.done(dve.tensor_tensor(t1[:, :, :], t1[:, :, :], over_tiles(gain[:, :]), ALU.mult))
                link.done(dve.tensor_tensor(t1[:, :, :], t1[:, :, :], over_tiles(shift[:, :]), ALU.add))
                dve.tensor_scalar(t2[:, :, :], t1[:, :, :], 0.0, slope[:, 0:1], ALU.min, ALU.mult)
                link.done(dve.scalar_tensor_tensor(rst[:, :, :].rearrange("p t d -> p (t d)"),
                                                   t1[:, :, :].rearrange("p t d -> p (t d)"), 0.0,
                                                   x0[:, :, :].rearrange("p t d -> p (t d)"), ALU.max, ALU.add))
                dve.wait_ge(stored, 16 * c)
                dve.tensor_tensor(out[:, :, :], rst[:, :, :], t2[:, :, :], ALU.add).then_inc(out_ready, 1)
            link.leave(CHUNKS)

        @block.scalar
        def _(act):
            with act.Fori(0, CHUNKS) as c:
                act.wait_ge(params, 80)
                act.wait_ge(z_ready, c + 1)
                act.activation(gate[:, :], z[:, :], ACT.Sigmoid, bias=g_bias[:, 0:1]).then_inc(gate_ready, 1)
                n.scalar(act, K, c)


def stage_hop_project(nc, T, K):
    H, E = 4, 4
    W = H * E
    with ExitStack() as ctx:
        s = Scope(nc, ctx, "h")
        n = Norm(s)
        w = s.sb("w", [P, 2, W])
        att = s.sb("att", [P, 2, W])
        row = s.sb("row", [P, TPC, W + H])
        t1 = s.sb("t1", [P, 2, TPC * H, E])
        to_dst = s.sb("to_dst", [P, NODE_TILES, H])
        ph = s.ps("ph", [P, 512])
        loaded = s.sem("loaded")
        projected = s.sem("projected")
        row_ready = s.sem("row_ready")
        dst_ready = s.sem("dst_ready")
        stored = s.sem("stored")
        block = ctx.enter_context(nc.Block())

        @block.sync
        def _(sp):
            n.load(sp, T["x1"], 0)
            sp.dma_start(w[:, :, :], T["L0_ffn_W_gat"].rearrange("(a p) n -> p a n", p=P)).then_inc(loaded, 16)
            for k, m in enumerate(("src", "dst")):
                sp.dma_start(att[:, k, :], bcast_rows(T["L0_ffn_att_" + m].rearrange("h e -> (h e)"), P)).then_inc(loaded, 16)
            with sp.Fori(0, CHUNKS) as c:
                sp.wait_ge(n.xn_ready, c + 1)
                n.load(sp, T["x1"], (c + 1) % CHUNKS)
                sp.wait_ge(row_ready, c + 1)
                sp.dma_start(chunk_of(T["f_table"], c), row[:, :, :]).then_inc(stored, 16)
            sp.wait_ge(dst_ready, CHUNKS)
            sp.dma_start(T["f_adst"], to_dst[:, :, :]).then_inc(stored, 16)
            sp.wait_ge(stored, 16 * (CHUNKS + 1))
            sp.wait_ge(n.x_loaded, 16 * (CHUNKS + 1))

        @block.vector
        def _(dve):
            link = Tally(dve, s.sem("dve"))
            dve.wait_ge(loaded, 48)
            with dve.Fori(0, CHUNKS) as c:
                link.loop(c, 4)
                dve.wait_ge(n.x_loaded, 16 * c + 16)
                n.vector(dve, link, c).then_inc(n.xn_ready, 1)
                dve.wait_ge(stored, 16 * c)
                dve.wait_ge(projected, c + 1)
                link.done(dve.tensor_copy(row[:, :, 0:W], ph[:, 0:TPC * W].rearrange("p (t w) -> p t w", w=W)))
                for k in range(2):
                    ins = dve.tensor_tensor(t1[:, k, :, :].rearrange("p (t h) e -> p t (h e)", t=TPC), row[:, :, 0:W],
                                            over_tiles(att[:, k, :]), ALU.mult)
                link.done(ins)
                dve.tensor_reduce(to_dst[:, bass.ds(c * TPC, TPC), :].rearrange("p t h -> p (t h)"), t1[:, 1, :, :],
                                  AX, ALU.add).then_inc(dst_ready, 1)
                dve.tensor_reduce(row[:, :, W:W + H], t1[:, 0, :, :].rearrange("p (t h) e -> p t h e", t=TPC), AX, ALU.add
                                  ).then_inc(row_ready, 1)
            link.leave(CHUNKS)

        @block.scalar
        def _(act):
            with act.Fori(0, CHUNKS) as c:
                n.scalar(act, K, c)
                n.scalar_turned(act, c)

        @block.tensor
        def _(pe):
            pe.wait_ge(loaded, 48)
            with pe.Fori(0, CHUNKS) as c:
                n.tensor(pe, K, c)
                pe.wait_ge(n.xt_ready, c + 1)
                pe.wait_ge(row_ready, c)
                for t in range(TPC):
                    for f in range(2):
                        mm = pe.matmul(ph[:, t * W:(t + 1) * W], n.xt[:, f, t * P:(t + 1) * P], w[:, f, :],
                                       start=(f == 0), stop=(f == 1))
                mm.then_inc(projected, 1)


def stage_pair(nc, T, K, L, H, table, W, at, dst_name, edge_name=None, keep=0):
    STOPS = DEPTH * U // 2
    with ExitStack() as ctx:
        s = Scope(nc, ctx, "w" + L.name)
        src = s.sb("src", [P, L.steps], I32)
        idx = s.sb("idx", [P, DEPTH, U], I32)
        got = s.sb("got", [P, DEPTH, U, W])
        apart = s.sb("apart", [P, DEPTH, U * P])
        hot = s.sb("hot", [P, DEPTH, U * P])
        to_dst = s.sb("to_dst", [P, NODE_TILES, H])
        i_row = s.sb("i_row", [1, L.stops], I32)
        j_row = s.sb("j_row", [1, L.stops], I32)
        spread = s.sb("spread", [P, DEPTH, U * P])
        sums = s.sb("sums", [P, DEPTH, U * H])
        score = s.sb("score", [P, L.steps, H])
        pd = s.ps("pd", [P, DEPTH, 512])
        loaded = s.sem("loaded")
        spread_in = [s.sem(f"spread_in{h}") for h in range(DEPTH)]
        got_in = [s.gather_sem(f"got_in{h}") for h in range(DEPTH)]
        idx_ready = s.sem("idx_ready")
        apart_ready = s.sem("apart_ready")
        hot_ready = s.sem("hot_ready")
        dst_out = s.sem("dst_out")
        summed = s.sem("summed")
        edge_added = s.sem("edge_added")
        scored = s.sem("scored")
        stored = s.sem("stored")
        loads = 4
        if keep:
            kept = s.sb("kept", [P, L.steps, keep])
        if edge_name:
            edge = s.sb("edge", [P, L.pairs, 2 * H])
            loads += 1
        block = ctx.enter_context(nc.Block())
        rel_flat = T[L.name + "_rel_rows"].rearrange("s e -> (s e)")

        @block.sync
        def _(sp):
            sp.dma_start(src[:, :], T[L.name + "_src_t"]).then_inc(loaded, 16)
            for row, name in ((i_row, "_i_row"), (j_row, "_j_row")):
                sp.dma_start(row[:, :], T[L.name + name][0:L.stops].rearrange("(a s) -> a s", a=1)).then_inc(loaded, 16)
            sp.dma_start(to_dst[:, :, :], T[dst_name]).then_inc(loaded, 16)
            if edge_name:
                sp.dma_start(edge[:, :, :].rearrange("p j (k h) -> p (j k) h", k=2), T[edge_name]).then_inc(loaded, 16)
            with sp.Fori(0, L.turns) as i:
                for h in range(DEPTH):
                    g = i * DEPTH + h
                    sp.wait_ge(apart_ready, g + 1)
                    sp.dma_start(spread[:, h, :], rel_flat[bass.ds(g * U * P, U * P)].partition_broadcast(P)
                                 ).then_inc(spread_in[h], 16)
            sp.wait_ge(scored, L.turns * DEPTH)
            sp.dma_start(T["score"][:, 0:L.steps * H], score[:, :, :].rearrange("p s h -> p (s h)")).then_inc(stored, 16)
            if keep:
                sp.dma_start(T["f_rows"], kept[:, :, :]).then_inc(stored, 16)
            sp.wait_ge(stored, 32 if keep else 16)

        @block.gpsimd
        def _(pool):
            with pool.Fori(0, L.turns) as i:
                for h in range(DEPTH):
                    g = i * DEPTH + h
                    pool.wait_ge(idx_ready, g + 1)
                    pool.wait_ge(summed, g + 1)
                    pool.nop(nofuse=True)
                    for u in range(U):
                        pool.indirect_dma_start(out=got[:, h, u, :], out_offset=None, in_=table,
                                                in_offset=bass.IndirectOffsetOnAxis(ap=idx[:, h, u:u + 1], axis=0)
                                                ).then_inc(got_in[h], 16)

        @block.scalar
        def _(act):
            act.sem_inc(apart_ready, DEPTH)
            act.sem_inc(hot_ready, DEPTH)
            with act.Fori(0, L.turns) as i:
                for h in range(DEPTH):
                    g = i * DEPTH + h
                    act.wait_ge(spread_in[h], 16 * (i + 1))
                    act.activation(apart[:, h, :], spread[:, h, :], ACT.Abs, bias=K["minus_col"][:, 0:1]).then_inc(apart_ready, 1)
                    act.wait_ge(apart_ready, DEPTH + g + 1)
                    act.wait_ge(dst_out, g + 1)
                    act.activation(hot[:, h, :], apart[:, h, :], ACT.Relu, scale=-1.0, bias=K["ones"][:, 0:1]).then_inc(hot_ready, 1)

        @block.vector
        def _(dve):
            dve.sem_inc(summed, DEPTH)
            dve.wait_ge(loaded, 16 * loads)
            dve.tensor_copy(idx[:, :, :], src[:, 0:DEPTH * U].rearrange("p (d u) -> p d u", u=U)).then_inc(idx_ready, DEPTH)
            with dve.Fori(0, L.turns) as i:
                if edge_name:
                    _, pair = nc.values_load_multi_w_load_instructions(
                        j_row[0:1, bass.ds(i * STOPS, STOPS)], engines=[mybir.EngineType.DVE], min_val=0, max_val=L.pairs - 1)
                for h in range(DEPTH):
                    g = i * DEPTH + h
                    dve.wait_ge(got_in[h], 16 * U * (i + 1))
                    dve.tensor_copy(idx[:, h, :], src[:, bass.ds((g + DEPTH) % (L.turns * DEPTH) * U, U)]).then_inc(idx_ready, 1)
                    dve.wait_ge(dst_out, DEPTH + g + 1)
                    if keep:
                        dve.tensor_copy(kept[:, bass.ds(g * U, U), :], got[:, h, :, 0:keep])
                    dve.tensor_tensor(sums[:, h, :].rearrange("p (u h) -> p u h", h=H), got[:, h, :, at:at + H],
                                      pd[:, h, 0:U * H].rearrange("p (u h) -> p u h", h=H), ALU.add).then_inc(summed, 1)
                    dve.wait_ge(summed, DEPTH + g + 1)
                    if edge_name:
                        for k in range(U // 2):
                            to = sums[:, h, k * 2 * H:(k + 1) * 2 * H]
                            dve.tensor_tensor(to, to, edge[:, bass.ds(pair[h * U // 2 + k], 1), :].rearrange("p a h -> p (a h)"),
                                              ALU.add).then_inc(edge_added, 1)
                        dve.wait_ge(edge_added, U // 2 * (g + 1))
                    dve.scalar_tensor_tensor(score[:, bass.ds(g * U, U), :].rearrange("p u h -> p (u h)"), sums[:, h, :], 0.2,
                                             sums[:, h, :], ALU.mult, ALU.max).then_inc(scored, 1)

        @block.tensor
        def _(pe):
            pe.sem_inc(dst_out, DEPTH)
            pe.wait_ge(loaded, 16 * loads)
            with pe.Fori(0, L.turns) as i:
                _, tile = nc.values_load_multi_w_load_instructions(
                    i_row[0:1, bass.ds(i * STOPS, STOPS)], engines=[mybir.EngineType.PE], min_val=0, max_val=NODE_TILES - 1)
                for h in range(DEPTH):
                    g = i * DEPTH + h
                    pe.wait_ge(hot_ready, DEPTH + g + 1)
                    pe.wait_ge(summed, g + 1)
                    for u in range(U):
                        mm = pe.matmul(pd[:, h, u * H:(u + 1) * H], hot[:, h, u * P:(u + 1) * P],
                                       to_dst[:, bass.ds(tile[(h * U + u) // 2], 1), :], start=True, stop=True)
                    mm.then_inc(dst_out, 1)


def stage_hop_gate(nc, T, K):
    H, E, NT = 4, 4, NODE_TILES
    W = H * E
    with ExitStack() as ctx:
        s = Scope(nc, ctx, "r")
        acc = s.sb("acc", [P, NT, W + H])
        rows = s.sb("rows", [P, 3, W])
        rden = s.sb("rden", [P, NT, H])
        a = s.sb("a", [P, NT, W])
        b = s.sb("b", [P, NT, W])
        m = s.sb("m", [P, NT])
        v = s.sb("v", [P, NT])
        sd = s.sb("sd", [P, NT])
        rs = s.sb("rs", [P, NT])
        sc = s.sb("sc", [P, NT, E])
        order = s.sb("order", [P, E])
        best = s.sb("best", [P, 2, NT])
        at = s.sb("at", [P, NT, E])
        first = s.sb("first", [P, NT])
        one = s.sb("one", [P, 2, NT, E])
        ex = s.sb("ex", [P, NT])
        ws = s.sb("ws", [P, 2, NT])
        gate = s.sb("gate", [P, NT, E])
        loaded = s.sem("loaded")
        var_ready = s.sem("var_ready")
        sd_ready = s.sem("sd_ready")
        diff_ready = s.sem("diff_ready")
        ex_ready = s.sem("ex_ready")
        gate_ready = s.sem("gate_ready")
        stored = s.sem("stored")
        block = ctx.enter_context(nc.Block())

        def per_tile(ap, n):
            return ap.unsqueeze(2).broadcast_to((P, NT, n))

        @block.sync
        def _(sp):
            sp.dma_start(acc[:, :, :].rearrange("p t w -> p (t w)"), T["acc"][:, 0:NT * (W + H)]).then_inc(loaded, 16)
            for k, name in enumerate(("b_gat", "ln_gamma", "ln_beta")):
                sp.dma_start(rows[:, k, :], bcast_rows(T["L0_ffn_" + name], P)).then_inc(loaded, 16)
            sp.wait_ge(gate_ready, 1)
            sp.dma_start(T["f_gate"], gate[:, :, :]).then_inc(stored, 16)
            sp.wait_ge(stored, 16)

        @block.vector
        def _(dve):
            link = Tally(dve, s.sem("dve"))
            dve.wait_ge(loaded, 64)
            link.done(dve.tensor_scalar(rden[:, :, :], acc[:, :, W:W + H], 1e-16, 0.5, ALU.add, ALU.max))
            link.done(dve.reciprocal(rden[:, :, :], rden[:, :, :]))
            link.done(dve.tensor_tensor(a[:, :, :].rearrange("p t (h c) -> p t h c", h=H),
                                        acc[:, :, 0:W].rearrange("p t (h c) -> p t h c", h=H),
                                        rden[:, :, :].unsqueeze(3).broadcast_to((P, NT, H, E)), ALU.mult))
            link.done(dve.tensor_tensor(a[:, :, :], a[:, :, :], over_tiles(rows[:, 0, :], NT), ALU.add))
            link.done(dve.tensor_reduce(m[:, :], a[:, :, :], AX, ALU.add))
            link.done(dve.tensor_scalar(m[:, :], m[:, :], 1.0 / W, None, ALU.mult))
            link.done(dve.tensor_tensor(a[:, :, :], a[:, :, :], per_tile(m[:, :], W), ALU.subtract))
            link.done(dve.tensor_tensor(b[:, :, :], a[:, :, :], a[:, :, :], ALU.mult))
            link.done(dve.tensor_reduce(v[:, :], b[:, :, :], AX, ALU.add))
            link.done(dve.tensor_scalar(v[:, :], v[:, :], 1.0 / W, EPS, ALU.mult, ALU.add))
            dve.sem_inc(var_ready, 1)
            dve.wait_ge(sd_ready, 1)
            link.done(dve.reciprocal(rs[:, :], sd[:, :]))
            link.done(dve.tensor_tensor(a[:, :, :], a[:, :, :], per_tile(rs[:, :], W), ALU.mult))
            link.done(dve.tensor_tensor(a[:, :, :], a[:, :, :], over_tiles(rows[:, 1, :], NT), ALU.mult))
            link.done(dve.tensor_tensor(a[:, :, :], a[:, :, :], over_tiles(rows[:, 2, :], NT), ALU.add))
            link.done(dve.tensor_reduce(sc[:, :, :], a[:, :, :].rearrange("p t (h e) -> p t e h", h=H), AX, ALU.add))
            link.done(dve.tensor_scalar(sc[:, :, :], sc[:, :, :], 1.0 / H, None, ALU.mult))
            dve.tensor_copy(order[:, :], K["frow"][:, 0:E])
            for k in range(2):
                link.done(dve.tensor_reduce(best[:, k, :], sc[:, :, :], AX, ALU.max))
                link.done(dve.tensor_tensor(at[:, :, :], sc[:, :, :], per_tile(best[:, k, :], E), ALU.is_lt))
                link.done(dve.scalar_tensor_tensor(at[:, :, :], at[:, :, :], float(E), over_tiles(order[:, :], NT),
                                                   ALU.mult, ALU.add))
                link.done(dve.tensor_reduce(first[:, :], at[:, :, :], AX, ALU.min))
                link.done(dve.tensor_tensor(one[:, k, :, :], over_tiles(order[:, :], NT), per_tile(first[:, :], E),
                                            ALU.is_equal))
                if k == 0:
                    link.done(dve.scalar_tensor_tensor(sc[:, :, :], one[:, 0, :, :], -BIG, sc[:, :, :], ALU.mult, ALU.add))
            link.done(dve.tensor_tensor(m[:, :], best[:, 1, :], best[:, 0, :], ALU.subtract))
            dve.sem_inc(diff_ready, 1)
            dve.wait_ge(ex_ready, 1)
            link.done(dve.tensor_scalar(v[:, :], ex[:, :], 1.0, None, ALU.add))
            link.done(dve.reciprocal(ws[:, 0, :], v[:, :]))
            link.done(dve.tensor_tensor(ws[:, 1, :], ws[:, 0, :], ex[:, :], ALU.mult))
            for k in range(2):
                ins = dve.tensor_tensor(one[:, k, :, :], one[:, k, :, :], per_tile(ws[:, k, :], E), ALU.mult)
            link.done(ins)
            dve.tensor_tensor(gate[:, :, :], one[:, 0, :, :], one[:, 1, :, :], ALU.add).then_inc(gate_ready, 1)

        @block.scalar
        def _(act):
            act.wait_ge(var_ready, 1)
            act.activation(sd[:, :], v[:, :], ACT.Sqrt).then_inc(sd_ready, 1)
            act.wait_ge(diff_ready, 1)
            act.activation(ex[:, :], m[:, :], ACT.Exp).then_inc(ex_ready, 1)


def stage_experts2(nc, T, K):
    E, F = 4, 2 * D
    FC = F // P
    with ExitStack() as ctx:
        s = Scope(nc, ctx, "t")
        n = Norm(s, turn=False)
        n.xt = s.sb("xt", [P, 2, ROWS])
        n.turned = s.sem("turned")
        n.xt_ready = s.sem("xt_ready")
        w1 = s.sb("w1", [P, E, 2, F])
        w2 = s.sb("w2", [P, E, FC, D])
        b1r = s.sb("b1r", [E * FC, P])
        b1 = s.sb("b1", [P, E * FC])
        b2 = s.sb("b2", [P, E, D])
        gate = s.sb("gate", [P, NODE_TILES, E])
        gc = s.sb("gc", [P, TPC, E])
        hid = s.sb("hid", [P, 2, FC, ROWS])
        acc = s.sb("acc", [P, TPC, D])
        ph = s.ps("ph", [P, 2, 2, 512])
        po = s.ps("po", [P, 4, 512])
        n.pt = po
        loaded = s.sem("loaded")
        b1_turned = s.sem("b1_turned")
        b1_ready = s.sem("b1_ready")
        up = s.sem("up")
        act_done = s.sem("act_done")
        down = s.sem("down")
        acc_done = s.sem("acc_done")
        stored = s.sem("stored")
        block = ctx.enter_context(nc.Block())

        def slot(t):
            return po[:, t // 2, t % 2 * D:(t % 2 + 1) * D]

        @block.sync
        def _(sp):
            n.load(sp, T["x1"], 0)
            sp.dma_start(b1r[:, :], T["L0_ffn_b1"].rearrange("e (a p) -> (e a) p", p=P)).then_inc(loaded, 16)
            sp.dma_start(gate[:, :, :], T["f_gate"]).then_inc(loaded, 16)
            for e in range(E):
                sp.dma_start(w1[:, e, :, :], T["L0_ffn_W1"][e].rearrange("(a p) f -> p a f", p=P)).then_inc(loaded, 16)
                sp.dma_start(w2[:, e, :, :], T["L0_ffn_W2"][e].rearrange("(a p) d -> p a d", p=P)).then_inc(loaded, 16)
                sp.dma_start(b2[:, e, :], bcast_rows(T["L0_ffn_b2"][e], P)).then_inc(loaded, 16)
            with sp.Fori(0, CHUNKS) as c:
                sp.wait_ge(acc_done, PAIRS * E * (c + 1))
                sp.dma_start(chunk_of(T["x2"], c), acc[:, :, :]).then_inc(stored, 16)
                n.load(sp, T["x1"], (c + 1) % CHUNKS)
            sp.wait_ge(stored, 16 * CHUNKS)
            sp.wait_ge(n.x_loaded, 16 * (CHUNKS + 1))

        @block.vector
        def _(dve):
            link = Tally(dve, s.sem("dve"))
            dve.wait_ge(loaded, 16 * (2 + 3 * E))
            with dve.Fori(0, CHUNKS) as c:
                link.loop(c, 2 + 1 + E)
                dve.wait_ge(n.x_loaded, 16 * c + 16)
                n.vector(dve, link, c).then_inc(n.xn_ready, 1)
                link.done(dve.tensor_copy(gc[:, :, :], gate[:, bass.ds(c * TPC, TPC), :]))
                dve.wait_ge(stored, 16 * c)
                for e in range(E):
                    for t in range(TPC):
                        ins = dve.scalar_tensor_tensor(acc[:, t, :], b2[:, e, :], gc[:, t, e:e + 1],
                                                       n.x[:, t, :] if e == 0 else acc[:, t, :], ALU.mult, ALU.add)
                    link.done(ins)
                for e in range(E):
                    for b in range(PAIRS):
                        g = (c * E + e) * PAIRS + b
                        dve.wait_ge(down, g + 1)
                        if e:
                            dve.wait_ge(acc_done, g - PAIRS + 1)
                        for t in range(2 * b, min(2 * b + 2, TPC)):
                            ins = dve.scalar_tensor_tensor(acc[:, t, :], slot(t), gc[:, t, e:e + 1], acc[:, t, :],
                                                           ALU.mult, ALU.add)
                        ins.then_inc(acc_done, 1)
            link.leave(CHUNKS)

        @block.scalar
        def _(act):
            act.wait_ge(b1_turned, 1)
            act.activation(b1[:, :], ph[:, 0, 0, 0:E * FC], ACT.Copy).then_inc(b1_ready, 1)
            act.wait_ge(b1_ready, 1)
            with act.Fori(0, CHUNKS) as c:
                n.scalar(act, K, c)
                n.scalar_turned(act, c)
                for e in range(E):
                    for f in range(FC):
                        g = (c * E + e) * FC + f
                        act.wait_ge(up, g + 1)
                        act.activation(hid[:, e % 2, f, :].rearrange("p (h r) -> p h r", h=2), ph[:, f % 2, :, 0:HALF], ACT.Gelu,
                                       bias=b1[:, e * FC + f:e * FC + f + 1]).then_inc(act_done, 1)

        @block.tensor
        def _(pe):
            def layer1(c, e):
                for f in range(FC):
                    g = (c * E + e) * FC + f
                    pe.wait_ge(act_done, g - 1 if (e or f) else g)
                    for a in range(2):
                        for h in range(2):
                            mm = pe.matmul(ph[:, f % 2, h, 0:HALF], w1[:, e, a, f * P:(f + 1) * P],
                                           n.xt[:, a, h * HALF:(h + 1) * HALF], start=(a == 0), stop=(a == 1))
                    mm.then_inc(up, 1)

            def layer2(c, e):
                pe.wait_ge(act_done, (c * E + e + 1) * FC)
                for b in range(PAIRS):
                    g = (c * E + e) * PAIRS + b
                    pe.wait_ge(acc_done, g - PAIRS + 1 if e else g - b)
                    for t in range(2 * b, min(2 * b + 2, TPC)):
                        for f in range(FC):
                            mm = pe.matmul(slot(t), hid[:, e % 2, f, t * P:(t + 1) * P], w2[:, e, f, :],
                                           start=(f == 0), stop=(f == FC - 1))
                    mm.then_inc(down, 1)

            pe.wait_ge(loaded, 16 * (2 + 3 * E))
            pe.transpose(ph[:, 0, 0, 0:E * FC], b1r[:, :], K["ident"][0:E * FC, 0:E * FC]).then_inc(b1_turned, 1)
            pe.wait_ge(b1_ready, 1)
            with pe.Fori(0, CHUNKS) as c:
                n.tensor(pe, K, c)
                pe.wait_ge(n.xt_ready, c + 1)
                layer1(c, 0)
                for e in range(1, E):
                    layer1(c, e)
                    layer2(c, e - 1)
                layer2(c, E - 1)


def stage_edge_scores(nc, T, K):
    H, A, U = 8, 64, 8
    TURNS = GRAPH.edge_tiles // (2 * U)
    rest = GRAPH.edge_tiles - TURNS * 2 * U - U
    odd = GRAPH.edges - (GRAPH.edge_tiles - 1) * P
    with ExitStack() as ctx:
        s = Scope(nc, ctx, "g")
        we = s.sb("we", [P, D])
        att = s.sb("att", [P, D])
        ve = s.sb("ve", [P, 2 * H])
        attr = s.sb("attr", [P, 2, U, A])
        attr_t = s.sb("attr_t", [P, 2, U // 2, P])
        out = s.sb("out", [P, GRAPH.tiles, H])
        pt = s.ps("pt", [P, 2, 512])
        pv = s.ps("pv", [P, 2, 512])
        params = s.sem("params")
        ve_ready = s.sem("ve_ready")
        cleared = s.sem("cleared")
        attr_in = [s.sem(f"attr_in{h}") for h in range(2)]
        turned = s.sem("turned")
        turned_sb = s.sem("turned_sb")
        scored = s.sem("scored")
        kept = s.sem("kept")
        stored = s.sem("stored")
        block = ctx.enter_context(nc.Block())
        src = T["edge_attr_64"]

        @block.sync
        def _(sp):
            for k in range(2):
                sp.dma_start(we[k * A:(k + 1) * A, :], T["L1_gnn_W_e"]).then_inc(params, 16)
            sp.dma_start(att[:, :], bcast_rows(T["L1_gnn_att_edge"].rearrange("h c -> (h c)"), P)).then_inc(params, 16)
            with sp.Fori(0, TURNS) as i:
                for h in range(2):
                    sp.wait_ge(turned, 2 * i)
                    sp.dma_start(attr[:, h, :, :], src[bass.ds((2 * i + h) * U * P, U * P), :].rearrange("(u p) a -> p u a", p=P)
                                 ).then_inc(attr_in[h], 16)
            sp.wait_ge(turned, 2 * TURNS)
            at = TURNS * 2 * U * P
            sp.dma_start(attr[:, 0, :, :], src[at:at + U * P, :].rearrange("(u p) a -> p u a", p=P)).then_inc(attr_in[0], 16)
            at += U * P
            sp.wait_ge(cleared, 2)
            sp.dma_start(attr[:, 1, 0:rest - 1, :], src[at:at + (rest - 1) * P, :].rearrange("(u p) a -> p u a", p=P)
                         ).then_inc(attr_in[1], 16)
            at += (rest - 1) * P
            sp.dma_start(attr[0:odd, 1, rest - 1, :], src[at:at + odd, :]).then_inc(attr_in[1], 16)
            sp.wait_ge(kept, 2 * TURNS + 2)
            sp.dma_start(T["l1_aedge"], out[:, :, :]).then_inc(stored, 16)
            sp.wait_ge(stored, 16)

        @block.vector
        def _(dve):
            link = Tally(dve, s.sem("dve"))
            dve.memset(out[:, GRAPH.edge_tiles:GRAPH.tiles, :], 0.0).then_inc(cleared, 1)
            link.done(dve.memset(ve[:, :], 0.0))
            dve.wait_ge(params, 48)
            link.done(dve.tensor_tensor(we[:, :], we[:, :], att[:, :], ALU.mult))
            for k in range(2):
                dve.tensor_reduce(ve[k * A:(k + 1) * A, k * H:(k + 1) * H],
                                  we[k * A:(k + 1) * A, :].rearrange("p (h c) -> p h c", h=H), AX, ALU.add).then_inc(ve_ready, 1)

            def keep(g, h, n):
                dve.wait_ge(scored, g + 1)
                dve.tensor_copy(out[:, bass.ds(g * U, n), :] if not isinstance(g, int) else out[:, g * U:g * U + n, :],
                                pv[:, h, 0:n * H].rearrange("p (u h) -> p u h", h=H)).then_inc(kept, 1)

            with dve.Fori(0, TURNS) as i:
                for h in range(2):
                    keep(2 * i + h, h, U)
            dve.wait_ge(turned, 2 * TURNS)
            dve.memset(attr[:, 1, :, :], 0.0).then_inc(cleared, 1)
            keep(2 * TURNS, 0, U)
            keep(2 * TURNS + 1, 1, rest)

        @block.scalar
        def _(act):
            def copy(g, h):
                act.wait_ge(turned, g + 1)
                act.activation(attr_t[:, h, :, :], pt[:, h, :].rearrange("p (u e) -> p u e", e=P), ACT.Copy
                               ).then_inc(turned_sb, 1)

            with act.Fori(0, TURNS) as i:
                for h in range(2):
                    copy(2 * i + h, h)
            for h in range(2):
                copy(2 * TURNS + h, h)

        @block.tensor
        def _(pe):
            def turn(g, h, landed):
                pe.wait_ge(attr_in[h], landed)
                for u in range(U // 2):
                    mm = pe.transpose(pt[:, h, u * P:(u + 1) * P], attr[:, h, 2 * u:2 * u + 2, :].rearrange("p u a -> p (u a)"),
                                      K["ident"][:, :])
                mm.then_inc(turned, 1)

            def score(g, h):
                pe.wait_ge(turned_sb, g + 1)
                for u in range(U // 2):
                    mm = pe.matmul(pv[:, h, u * 2 * H:(u + 1) * 2 * H], attr_t[:, h, u, :], ve[:, :], start=True, stop=True)
                mm.then_inc(scored, 1)

            pe.wait_ge(ve_ready, 2)
            with pe.Fori(0, TURNS) as i:
                pe.wait_ge(kept, 2 * i)
                for h in range(2):
                    turn(2 * i + h, h, 16 * (i + 1))
                for h in range(2):
                    score(2 * i + h, h)
            pe.wait_ge(kept, 2 * TURNS)
            turn(2 * TURNS, 0, 16 * (TURNS + 1))
            turn(2 * TURNS + 1, 1, 16 * (TURNS + 2))
            score(2 * TURNS, 0)
            score(2 * TURNS + 1, 1)


def stage_l1_project(nc, T, K):
    H = 8
    with ExitStack() as ctx:
        s = Scope(nc, ctx, "y")
        n = Norm(s)
        w = s.sb("w", [P, 2, D])
        att = s.sb("att", [P, 2, D])
        row = s.sb("row", [P, TPC, D])
        t1 = s.sb("t1", [P, 2, TPC, D])
        to_src = s.sb("to_src", [P, TPC, H])
        to_dst = s.sb("to_dst", [P, NODE_TILES, H])
        pq = s.ps("pq", [P, 4, 512])
        loaded = s.sem("loaded")
        projected = s.sem("projected")
        row_ready = s.sem("row_ready")
        src_ready = s.sem("src_ready")
        dst_ready = s.sem("dst_ready")
        stored = s.sem("stored")
        block = ctx.enter_context(nc.Block())

        @block.sync
        def _(sp):
            n.load(sp, T["x2"], 0)
            sp.dma_start(w[:, :, :], T["L1_gnn_W"].rearrange("(a p) n -> p a n", p=P)).then_inc(loaded, 16)
            for k, m in enumerate(("src", "dst")):
                sp.dma_start(att[:, k, :], bcast_rows(T["L1_gnn_att_" + m].rearrange("h c -> (h c)"), P)).then_inc(loaded, 16)
            with sp.Fori(0, CHUNKS) as c:
                sp.wait_ge(n.xn_ready, c + 1)
                n.load(sp, T["x2"], (c + 1) % CHUNKS)
                sp.dma_start(chunk_of(T["l1_xn"], c), n.xn[:, :, :]).then_inc(stored, 16)
                sp.wait_ge(row_ready, c + 1)
                sp.dma_start(chunk_of(T["l1_table"], c), row[:, :, :]).then_inc(stored, 16)
                sp.wait_ge(src_ready, c + 1)
                sp.dma_start(chunk_of(T["l1_asrc"], c), to_src[:, :, :]).then_inc(stored, 16)
            sp.wait_ge(dst_ready, CHUNKS)
            sp.dma_start(T["l1_adst"], to_dst[:, :, :]).then_inc(stored, 16)
            sp.wait_ge(stored, 48 * CHUNKS + 16)
            sp.wait_ge(n.x_loaded, 16 * (CHUNKS + 1))

        @block.vector
        def _(dve):
            link = Tally(dve, s.sem("dve"))
            dve.wait_ge(loaded, 48)
            with dve.Fori(0, CHUNKS) as c:
                link.loop(c, 4)
                dve.wait_ge(n.x_loaded, 16 * c + 16)
                dve.wait_ge(stored, 48 * c)
                n.vector(dve, link, c).then_inc(n.xn_ready, 1)
                dve.wait_ge(projected, c + 1)
                for t in range(TPC):
                    ins = dve.tensor_copy(row[:, t, :], pq[:, t // 2, t % 2 * D:(t % 2 + 1) * D])
                ins.then_inc(row_ready, 1)
                dve.wait_ge(row_ready, c + 1)
                for k in range(2):
                    link.done(dve.tensor_tensor(t1[:, k, :, :], row[:, :, :], over_tiles(att[:, k, :]), ALU.mult))
                dve.tensor_reduce(to_src[:, :, :].rearrange("p t h -> p (t h)"),
                                  t1[:, 0, :, :].rearrange("p t (h c) -> p (t h) c", h=H), AX, ALU.add).then_inc(src_ready, 1)
                dve.tensor_reduce(to_dst[:, bass.ds(c * TPC, TPC), :].rearrange("p t h -> p (t h)"),
                                  t1[:, 1, :, :].rearrange("p t (h c) -> p (t h) c", h=H), AX, ALU.add).then_inc(dst_ready, 1)
            link.leave(CHUNKS)

        @block.scalar
        def _(act):
            with act.Fori(0, CHUNKS) as c:
                n.scalar(act, K, c)
                n.scalar_turned(act, c)

        @block.tensor
        def _(pe):
            pe.wait_ge(loaded, 48)
            with pe.Fori(0, CHUNKS) as c:
                n.tensor(pe, K, c)
                pe.wait_ge(n.xt_ready, c + 1)
                pe.wait_ge(row_ready, c)
                for t in range(TPC):
                    for f in range(2):
                        mm = pe.matmul(pq[:, t // 2, t % 2 * D:(t % 2 + 1) * D], n.xt[:, f, t * P:(t + 1) * P], w[:, f, :],
                                       start=(f == 0), stop=(f == 1))
                mm.then_inc(projected, 1)


def stage_l1_finish(nc, T, K):
    H, W = 8, D
    with ExitStack() as ctx:
        s = Scope(nc, ctx, "z")
        n = Norm(s, turn=False)
        acc = s.sb("acc", [P, TPC, W + H])
        xn = s.sb("xn1", [P, TPC, D])
        x2 = s.sb("x2", [P, TPC, D])
        bias = s.sb("bias", [P, D])
        gain = s.sb("gain", [P, D])
        shift = s.sb("shift", [P, D])
        rden = s.sb("rden", [P, TPC, H])
        t1 = s.sb("t1", [P, TPC, D])
        t2 = s.sb("t2", [P, TPC, D])
        out = s.sb("out", [P, TPC, D])
        params = s.sem("params")
        loaded = s.sem("loaded")
        out_ready = s.sem("out_ready")
        stored = s.sem("stored")
        block = ctx.enter_context(nc.Block())
        acc_all = T["acc"][:, 0:NODE_TILES * (W + H)]

        @block.sync
        def _(sp):
            for to, name in ((bias, "bias"), (gain, "gamma"), (shift, "beta")):
                sp.dma_start(to[:, :], bcast_rows(T["L1_gnn_" + name], P)).then_inc(params, 16)
            with sp.Fori(0, CHUNKS) as c:
                sp.wait_ge(out_ready, c)
                sp.dma_start(acc[:, :, :].rearrange("p t w -> p (t w)"),
                             acc_all[:, bass.ds(c * (TPC * (W + H)), TPC * (W + H))]).then_inc(loaded, 16)
                sp.dma_start(xn[:, :, :], chunk_of(T["l1_xn"], c)).then_inc(loaded, 16)
                sp.dma_start(x2[:, :, :], chunk_of(T["x2"], c)).then_inc(loaded, 16)
                sp.wait_ge(out_ready, c + 1)
                sp.dma_start(chunk_of(T["x3"], c), out[:, :, :]).then_inc(stored, 16)
            sp.wait_ge(stored, 16 * CHUNKS)

        @block.vector
        def _(dve):
            link = Tally(dve, s.sem("dve"))
            dve.wait_ge(params, 48)
            with dve.Fori(0, CHUNKS) as c:
                link.loop(c, 10)
                dve.wait_ge(loaded, 48 * c + 48)
                link.done(dve.tensor_scalar(rden[:, :, :], acc[:, :, W:W + H], 1e-16, 0.5, ALU.add, ALU.max))
                link.done(dve.reciprocal(rden[:, :, :], rden[:, :, :]))
                link.done(dve.tensor_tensor(t1[:, :, :].rearrange("p t (h c) -> p t h c", h=H),
                                            acc[:, :, 0:W].rearrange("p t (h c) -> p t h c", h=H),
                                            rden[:, :, :].unsqueeze(3).broadcast_to((P, TPC, H, W // H)), ALU.mult))
                link.done(dve.tensor_tensor(t1[:, :, :], t1[:, :, :], over_tiles(bias[:, :]), ALU.add))
                link.done(dve.tensor_tensor(t1[:, :, :], t1[:, :, :], xn[:, :, :], ALU.add))
                link.done(n.vector(dve, link, c, x=t1, out=t2))
                link.done(dve.tensor_tensor(t2[:, :, :], t2[:, :, :], over_tiles(gain[:, :]), ALU.mult))
                link.done(dve.tensor_tensor(t2[:, :, :], t2[:, :, :], over_tiles(shift[:, :]), ALU.add))
                dve.wait_ge(stored, 16 * c)
                dve.tensor_tensor(out[:, :, :], t2[:, :, :], x2[:, :, :], ALU.add).then_inc(out_ready, 1)
            link.leave(CHUNKS)

        @block.scalar
        def _(act):
            with act.Fori(0, CHUNKS) as c:
                n.scalar(act, K, c)


def stage_experts3(nc, T, K):
    E = 8
    BN_EPS = 0.001
    with ExitStack() as ctx:
        s = Scope(nc, ctx, "l")
        n = Norm(s, turn=False)
        n.xt = s.sb("xt", [P, 2, ROWS])
        n.turned = s.sem("turned")
        n.xt_ready = s.sem("xt_ready")
        wm = [s.sb(f"wm{k}", [P, E, 2, D]) for k in range(3)]
        wr = s.sb("wr", [P, 2, E])
        br = s.sb("br", [P, E])
        raw = s.sb("raw", [5 * 2 * E, 2, P])
        par = s.sb("par", [P, 2, 5, 2 * E])
        bn = s.sb("bn", [P, 2, 2, 2 * E])
        bn_eps = s.sb("bn_eps", [P, 1])
        sdv = s.sb("sdv", [P, 2, 2 * E])
        bo = s.sb("bo", [P, E, D])
        logit = s.sb("logit", [P, TPC, E])
        mx = s.sb("mx", [P, TPC])
        prob = s.sb("prob", [P, TPC, E])
        den = s.sb("den", [P, TPC])
        h1 = s.sb("h1", [P, 2, 2, ROWS])
        h2 = s.sb("h2", [P, 2, 2, ROWS])
        acc = s.sb("acc", [P, TPC, D])
        ph = s.ps("ph", [P, 2, 2, 512])
        po = s.ps("po", [P, 4, 512])
        n.pt = po
        loaded = s.sem("loaded")
        par_turned = s.sem("par_turned")
        var_ready = s.sem("bn_var")
        bn_sd = s.sem("bn_sd")
        bn_ready = s.sem("bn_ready")
        routed = s.sem("routed")
        route_read = s.sem("route_read")
        diff_ready = s.sem("diff_ready")
        exp_ready = s.sem("exp_ready")
        up = s.sem("up")
        act_done = s.sem("act_done")
        down = s.sem("down")
        acc_done = s.sem("acc_done")
        stored = s.sem("stored")
        block = ctx.enter_context(nc.Block())
        n_loads = 3 * E + 2 + 10 + 1
        order = []
        for e in range(E + 1):
            order += [(0, e)] * (e < E) + [(1, e - 1)] * (e > 0)
        place = {what: k for k, what in enumerate(order)}
        PER = 2 * len(order)

        def slot(t):
            return po[:, t // 2, t % 2 * D:(t % 2 + 1) * D]

        @block.sync
        def _(sp):
            n.load(sp, T["x3"], 0)
            for k in range(2):
                for a, name in enumerate(("b", "g", "be", "m", "v")):
                    sp.dma_start(raw[a * 2 * E:(a + 1) * 2 * E, k, :],
                                 T[f"L1_ffn_{name}{k + 1}"].rearrange("e (a p) -> (e a) p", p=P)).then_inc(loaded, 16)
            sp.dma_start(wr[:, :, :], T["L1_ffn_Wr"].rearrange("(a p) e -> p a e", p=P)).then_inc(loaded, 16)
            sp.dma_start(br[:, :], bcast_rows(T["L1_ffn_br"], P)).then_inc(loaded, 16)
            sp.dma_start(bo[:, :, :].rearrange("p e d -> p (e d)"), bcast_rows(T["L1_ffn_bo"].rearrange("e d -> (e d)"), P)
                         ).then_inc(loaded, 16)
            for e in range(E):
                for k, name in enumerate(("W1", "W2", "Wo")):
                    sp.dma_start(wm[k][:, e, :, :], T["L1_ffn_" + name][e].rearrange("(a p) f -> p a f", p=P)).then_inc(loaded, 16)
            with sp.Fori(0, CHUNKS - 1) as c:
                sp.wait_ge(acc_done, PAIRS * E * (c + 1))
                sp.dma_start(T["out"][bass.ds(c * ROWS, ROWS), :].rearrange("(t p) f -> p t f", p=P), acc[:, :, :]
                             ).then_inc(stored, 16)
                n.load(sp, T["x3"], c + 1)
            sp.wait_ge(acc_done, PAIRS * E * CHUNKS)
            at = (CHUNKS - 1) * ROWS
            full = (N - at) // P
            sp.dma_start(T["out"][at:at + full * P, :].rearrange("(t p) f -> p t f", p=P), acc[:, 0:full, :]).then_inc(stored, 16)
            at += full * P
            sp.dma_start(T["out"][at:N, :], acc[0:N - at, full, :]).then_inc(stored, 16)
            sp.wait_ge(stored, 16 * (CHUNKS + 1))

        @block.vector
        def _(dve):
            link = Tally(dve, s.sem("dve"))
            dve.memset(bn_eps[:, :], BN_EPS)
            dve.wait_ge(par_turned, 1)
            for k in range(2):
                ins = dve.tensor_copy(par[:, k, :, :], po[:, k, 0:5 * 2 * E].rearrange("p (a n) -> p a n", a=5))
            link.done(ins)
            dve.sem_inc(var_ready, 1)
            dve.wait_ge(bn_sd, 1)
            link.done(dve.reciprocal(sdv[:, :, :], sdv[:, :, :]))
            link.done(dve.tensor_tensor(bn[:, :, 0, :], sdv[:, :, :], par[:, :, 1, :], ALU.mult))
            link.done(dve.tensor_tensor(sdv[:, :, :], par[:, :, 0, :], par[:, :, 3, :], ALU.subtract))
            link.done(dve.tensor_tensor(sdv[:, :, :], sdv[:, :, :], bn[:, :, 0, :], ALU.mult))
            dve.tensor_tensor(bn[:, :, 1, :], sdv[:, :, :], par[:, :, 2, :], ALU.add).then_inc(bn_ready, 1)
            dve.wait_ge(loaded, 16 * n_loads)
            with dve.Fori(0, CHUNKS) as c:
                link.loop(c, 2 + 4 + E)
                dve.wait_ge(n.x_loaded, 16 * c + 16)
                n.vector(dve, link, c).then_inc(n.xn_ready, 1)
                dve.wait_ge(routed, c + 1)
                dve.tensor_tensor(logit[:, :, :], po[:, 0, 0:TPC * E].rearrange("p (t e) -> p t e", e=E), over_tiles(br[:, :]),
                                  ALU.add).then_inc(route_read, 1)
                dve.wait_ge(route_read, c + 1)
                link.done(dve.tensor_reduce(mx[:, :], logit[:, :, :], AX, ALU.max))
                dve.tensor_tensor(logit[:, :, :], logit[:, :, :], mx[:, :].unsqueeze(2).broadcast_to((P, TPC, E)), ALU.subtract
                                  ).then_inc(diff_ready, 1)
                dve.wait_ge(exp_ready, c + 1)
                link.done(dve.tensor_reduce(den[:, :], prob[:, :, :], AX, ALU.add))
                link.done(dve.reciprocal(den[:, :], den[:, :]))
                link.done(dve.tensor_tensor(prob[:, :, :], prob[:, :, :], den[:, :].unsqueeze(2).broadcast_to((P, TPC, E)), ALU.mult))
                dve.wait_ge(stored, 16 * c)
                for e in range(E):
                    for t in range(TPC):
                        ins = dve.scalar_tensor_tensor(acc[:, t, :], bo[:, e, :], prob[:, t, e:e + 1],
                                                       n.x[:, t, :] if e == 0 else acc[:, t, :], ALU.mult, ALU.add)
                    link.done(ins)
                for e in range(E):
                    for b in range(PAIRS):
                        g = (c * E + e) * PAIRS + b
                        dve.wait_ge(down, g + 1)
                        if e:
                            dve.wait_ge(acc_done, g - PAIRS + 1)
                        for t in range(2 * b, min(2 * b + 2, TPC)):
                            ins = dve.scalar_tensor_tensor(acc[:, t, :], slot(t), prob[:, t, e:e + 1], acc[:, t, :],
                                                           ALU.mult, ALU.add)
                        ins.then_inc(acc_done, 1)
            link.leave(CHUNKS)

        @block.scalar
        def _(act):
            act.wait_ge(var_ready, 1)
            act.activation(sdv[:, :, :], par[:, :, 4, :], ACT.Sqrt, bias=bn_eps[:, 0:1]).then_inc(bn_sd, 1)
            act.wait_ge(bn_ready, 1)
            with act.Fori(0, CHUNKS) as c:
                n.scalar(act, K, c)
                n.scalar_turned(act, c)
                act.wait_ge(diff_ready, c + 1)
                act.activation(prob[:, :, :], logit[:, :, :], ACT.Exp).then_inc(exp_ready, 1)
                for k, (layer, e) in enumerate(order):
                    to = (h1, h2)[layer]
                    for f in range(2):
                        act.wait_ge(up, c * PER + 2 * k + f + 1)
                        act.activation(to[:, e % 2, f, :].rearrange("p (h r) -> p h r", h=2), ph[:, f, :, 0:HALF], ACT.Relu,
                                       scale=bn[:, layer, 0, 2 * e + f:2 * e + f + 1],
                                       bias=bn[:, layer, 1, 2 * e + f:2 * e + f + 1]).then_inc(act_done, 1)

        @block.tensor
        def _(pe):
            def layer(c, which, e):
                k = place[which, e]
                if which:
                    pe.wait_ge(act_done, c * PER + 2 * place[0, e] + 2)
                of = (n.xt[:, :, :], h1[:, e % 2, :, :])[which]
                for f in range(2):
                    pe.wait_ge(act_done, c * PER + 2 * k + f - (1 if k else f))
                    for a in range(2):
                        for h in range(2):
                            mm = pe.matmul(ph[:, f, h, 0:HALF], wm[which][:, e, a, f * P:(f + 1) * P],
                                           of[:, a, h * HALF:(h + 1) * HALF], start=(a == 0), stop=(a == 1))
                    mm.then_inc(up, 1)

            def last(c, e):
                pe.wait_ge(act_done, c * PER + 2 * place[1, e] + 2)
                for b in range(PAIRS):
                    g = (c * E + e) * PAIRS + b
                    pe.wait_ge(acc_done, g - PAIRS + 1 if e else g - b)
                    for t in range(2 * b, min(2 * b + 2, TPC)):
                        for f in range(2):
                            mm = pe.matmul(slot(t), h2[:, e % 2, f, t * P:(t + 1) * P], wm[2][:, e, f, :],
                                           start=(f == 0), stop=(f == 1))
                    mm.then_inc(down, 1)

            pe.wait_ge(loaded, 16 * n_loads)
            for k in range(2):
                mm = pe.transpose(po[:, k, 0:5 * 2 * E], raw[:, k, :], K["ident"][0:5 * 2 * E, 0:5 * 2 * E])
            mm.then_inc(par_turned, 1)
            pe.wait_ge(bn_ready, 1)
            with pe.Fori(0, CHUNKS) as c:
                n.tensor(pe, K, c)
                pe.wait_ge(n.xt_ready, c + 1)
                for t in range(TPC):
                    for f in range(2):
                        mm = pe.matmul(po[:, 0, t * E:(t + 1) * E], n.xt[:, f, t * P:(t + 1) * P], wr[:, f, :],
                                       start=(f == 0), stop=(f == 1))
                mm.then_inc(routed, 1)
                for e in range(E + 2):
                    if e < E:
                        layer(c, 0, e)
                    if 0 < e <= E:
                        layer(c, 1, e - 1)
                    if e > 1:
                        if e == 2:
                            pe.wait_ge(route_read, c + 1)
                        last(c, e - 2)


def scratch_shapes():
    shapes = {"x0": ([NP, D], F32)}
    for L in (GRAPH, HOP):
        n = L.name
        shapes.update({
            n + "_src": ([L.tiles * P], I32), n + "_dst": ([L.tiles * P], I32),
            n + "_rel_rows": ([L.blocks * P, P], F32), n + "_key_rows": ([L.blocks * P, P], F32),
            n + "_i_row": ([L.blocks * P // 2], I32), n + "_j_row": ([L.blocks * P // 2], I32),
            n + "_src_t": ([P, L.steps], I32), n + "_rel_t": ([P, L.steps], F32),
        })
    shapes["f_pairs"] = ([HOP.edges, 2], I32)
    for k in ("q", "k", "v", "skip"):
        shapes["l0_" + k] = ([NP, D], F32)
    shapes.update({
        "score": ([P, GRAPH.steps * 8], F32), "weight": ([P, GRAPH.steps * 8], F32), "lanes": ([P * GRAPH.steps], F32),
        "acc": ([P, NODE_TILES * (D + 8)], F32), "x1": ([NP, D], F32), "x2": ([NP, D], F32), "x3": ([NP, D], F32),
        "f_table": ([NP, 20], F32), "f_rows": ([P, HOP.steps, 16], F32), "f_gate": ([P, NODE_TILES, 4], F32),
        "f_adst": ([P, NODE_TILES, 4], F32),
        "l1_table": ([NP, D], F32), "l1_asrc": ([NP, 8], F32), "l1_adst": ([P, NODE_TILES, 8], F32),
        "l1_aedge": ([P, GRAPH.tiles, 8], F32), "l1_xn": ([NP, D], F32),
    })
    return shapes


def two_layers(nc, T):
    for name, (shape, dt) in scratch_shapes().items():
        T[name] = nc.dram_tensor("tmp_" + name, shape, dt).ap()
    with ExitStack() as ctx:
        K = {name: ctx.enter_context(nc.sbuf_tensor("const_" + name, shape, F32)) for name, shape in
             (("frow", [P, P]), ("pcol", [P, 1]), ("minus_col", [P, 1]), ("ident", [P, P]), ("below", [P, P]), ("ones", [P, P]), ("eps", [P, 1]))}
        stage_constants(nc, T, K)
        stage_sort(nc, T, K)
        stage_split(nc, T, K)
        for edges in (GRAPH, HOP):
            stage_schedule(nc, T, K, edges)
        stage_l0_project(nc, T, K)
        stage_dot(nc, T, K, GRAPH)
        stage_softmax(nc, T, K, GRAPH, 4, 64 ** -0.5)
        stage_sum(nc, T, K, GRAPH, 4, D, T["l0_v"])
        stage_l0_finish(nc, T, K)
        stage_hop_project(nc, T, K)
        stage_pair(nc, T, K, HOP, 4, T["f_table"], 20, 16, "f_adst", keep=16)
        stage_softmax(nc, T, K, HOP, 4, 1.0)
        stage_sum(nc, T, K, HOP, 4, 16)
        stage_hop_gate(nc, T, K)
        stage_experts2(nc, T, K)
        stage_edge_scores(nc, T, K)
        stage_l1_project(nc, T, K)
        stage_pair(nc, T, K, GRAPH, 8, T["l1_asrc"], 8, 0, "l1_adst", edge_name="l1_aedge")
        stage_softmax(nc, T, K, GRAPH, 8, 1.0)
        stage_sum(nc, T, K, GRAPH, 8, D, T["l1_table"])
        stage_l1_finish(nc, T, K)
        stage_experts3(nc, T, K)


def kernel(**inputs):
    import numpy as _np
    import concourse.bacc as _bacc
    from concourse import mybir as _mybir
    from concourse.bass_utils import run_bass_kernel_spmd as _run

    nc = _bacc.Bacc("TRN2", target_bir_lowering=False, num_devices=1)
    arrays, tables = {}, {}
    for name in inputs:
        a = _np.ascontiguousarray(inputs[name])
        a = a.reshape(a.shape or (1,))
        arrays["in_" + name] = a
        tables[name] = nc.dram_tensor("in_" + name, a.shape, _mybir.dt.from_np(a.dtype), kind="ExternalInput").ap()
    tables["out"] = nc.dram_tensor("out", (N, D), _mybir.dt.float32, kind="ExternalOutput").ap()
    two_layers(nc, tables)
    return _run(nc, [arrays], core_ids=[0]).results[0]["out"]
```

```python
from contextlib import ExitStack

import numpy as np

import concourse.bass as bass
from concourse import mybir

F32 = mybir.dt.float32
BF16 = mybir.dt.bfloat16
I32 = mybir.dt.int32
ALU = mybir.AluOpType
ACT = mybir.ActivationFunctionType
AX = mybir.AxisListType.X

P = 128
N = 6250
D = 256
NODE_TILES = -(-N // P)
NP = NODE_TILES * P
CHUNKS = 7
TPC = NODE_TILES // CHUNKS
ROWS = TPC * P
HALF = ROWS // 2
BIG = 1.0e30
FAR = 1.0e6
EPS = 1e-5
HOPS = 65536
HOP_TILES = HOPS // P
U = 4
DEPTH = 4


class EdgeList:

    def __init__(self, name, edges):
        self.name = name
        self.edges = edges
        self.edge_tiles = -(-edges // P)
        self.pairs = -(-self.edge_tiles // 2)
        self.tiles = 2 * self.pairs
        self.real_stops = self.pairs + NODE_TILES - 1
        self.stops = -(-self.real_stops // 8) * 8
        self.steps = 2 * self.stops
        self.blocks = -(-self.steps // P)
        self.pair_blocks = -(-self.pairs // P)
        self.turns = self.steps // (U * DEPTH)
        self.pad = self.tiles * P - edges


GRAPH = EdgeList("g", 106250)
HOP = EdgeList("f", HOPS + NP)


class Tally:

    def __init__(self, eng, sem):
        self.eng, self.sem = eng, sem
        self.before, self.per, self.turn, self.here = 0, 0, 0, 0

    def loop(self, turn, per):
        self.before += self.here
        self.turn, self.per, self.here = turn, per, 0

    def leave(self, turns):
        assert self.here == self.per, (self.here, self.per)
        self.before += turns * self.per
        self.turn, self.per, self.here = 0, 0, 0

    def done(self, ins):
        self.here += 1
        ins.then_inc(self.sem, 1)
        self.eng.wait_ge(self.sem, self.before + self.per * self.turn + self.here)


class Scope:

    def __init__(self, nc, ctx, name):
        self.nc, self.ctx, self.name, self.sems = nc, ctx, name, []
        ctx.callback(self.release)

    def release(self):
        for sem in self.sems:
            self.nc.gpsimd.sem_clear(sem)
            self.nc.release_semaphore(sem)

    def sb(self, name, shape, dt=F32):
        return self.ctx.enter_context(self.nc.sbuf_tensor(f"{self.name}_{name}", shape, dt))

    def ps(self, name, shape, dt=F32):
        return self.ctx.enter_context(self.nc.psum_tensor(f"{self.name}_{name}", shape, dt))

    def gather_sem(self, name):
        return self.nc.alloc_semaphore(f"{self.name}_{name}")

    def sem(self, name):
        self.sems.append(self.nc.alloc_semaphore(f"{self.name}_{name}"))
        return self.sems[-1]


def bcast_rows(ap, n):
    return ap.partition_broadcast(n)


def stage_constants(nc, T, K):
    with ExitStack() as ctx:
        s = Scope(nc, ctx, "c")
        frow_i = s.sb("frow_i", [P, P], I32)
        pcol_i = s.sb("pcol_i", [P, 1], I32)
        zero = s.sb("zero", [P, D])
        pad_dst = s.sb("pad_dst", [P, 2], I32)
        made = s.sem("made")
        filled = s.sem("filled")
        moved = s.sem("moved")
        block = ctx.enter_context(nc.Block())
        tail = NP - N

        @block.gpsimd
        def _(pool):
            pool.iota(frow_i[:, :], pattern=[[1, P]], base=0, channel_multiplier=0).then_inc(made, 1)
            pool.iota(pcol_i[:, :], pattern=[[1, 1]], base=0, channel_multiplier=1).then_inc(made, 1)

        @block.vector
        def _(dve):
            link = Tally(dve, s.sem("dve"))
            dve.memset(zero[:, :], 0.0).then_inc(filled, 1)
            dve.memset(pad_dst[:, :], NP - 1).then_inc(filled, 1)
            dve.wait_ge(made, 2)
            dve.tensor_copy(K["frow"][:, :], frow_i[:, :]).then_inc(link.sem, 1)
            link.here += 1
            link.done(dve.tensor_copy(K["pcol"][:, :], pcol_i[:, :]))
            dve.tensor_scalar(K["ident"][:, :], K["frow"][:, :], K["pcol"][:, 0:1], None, ALU.is_equal)
            dve.tensor_scalar(K["below"][:, :], K["frow"][:, :], K["pcol"][:, 0:1], None, ALU.is_gt)
            dve.tensor_scalar(K["minus_col"][:, :], K["pcol"][:, :], -1.0, None, ALU.mult)
            dve.memset(K["ones"][:, :], 1.0)
            dve.memset(K["eps"][:, :], EPS)

        @block.sync
        def _(sp):
            sp.dma_start(T["x0"][0:N, :], T["x"]).then_inc(moved, 16)
            sp.dma_start(T["g_src"][0:GRAPH.edges].rearrange("(a n) -> a n", a=50),
                         T["src"].rearrange("(a n) -> a n", a=50)).then_inc(moved, 16)
            sp.dma_start(T["g_dst"][0:GRAPH.edges].rearrange("(a n) -> a n", a=50),
                         T["dst"].rearrange("(a n) -> a n", a=50)).then_inc(moved, 16)
            sp.wait_ge(filled, 2)
            sp.dma_start(T["x0"][N:NP, :], zero[0:tail, :]).then_inc(moved, 16)
            for L in (GRAPH, HOP):
                for end in ("_src", "_dst"):
                    sp.dma_start(T[L.name + end][L.edges:].rearrange("(p a) -> p a", a=2),
                                 pad_dst[0:L.pad // 2, :]).then_inc(moved, 16)
            sp.wait_ge(moved, 128)


def stage_sort(nc, T, K, places):
    B = 8
    RING = 4
    TURNS = HOP_TILES // B
    NT = NODE_TILES
    with ExitStack() as ctx:
        s = Scope(nc, ctx, "s")
        ends = s.sb("ends", [P, 2, HOP_TILES], I32)
        hi_i = s.sb("hi_i", [P, HOP_TILES], I32)
        lo_i = s.sb("lo_i", [P, HOP_TILES], I32)
        hi = s.sb("hi", [P, HOP_TILES])
        lo = s.sb("lo", [P, HOP_TILES])
        ident = s.sb("ident", [P, P], BF16)
        zeros = s.sb("zeros", [P, P], BF16)
        one_lo = s.sb("one_lo", [P, RING, B, P], BF16)
        one_hi = s.sb("one_hi", [P, RING, B, NT], BF16)
        total = s.sb("total", [P, NT])
        below = s.sb("below", [P, NT])
        upto = s.sb("upto", [P, NT])
        none = s.sb("none", [P, NT])
        loop_i = s.sb("loop_i", [P, NT], I32)
        taken = s.sb("taken", [P, NT])
        taken_by_tile = s.sb("taken_by_tile", [P, 2, B, NT])
        lo_t = s.sb("lo_t", [P, 2, B, P])
        lo_t16 = s.sb("lo_t16", [P, 2, B, P], BF16)
        earlier = s.sb("earlier", [P, B, P], BF16)
        picked = s.sb("picked", [P, B, NT])
        pos = s.sb("pos", [P, B])
        pt = s.ps("pt", [P, B, P])
        pc = s.ps("pc", [P, 2, 512])
        pq = s.ps("pq", [P, B, P])
        pr = s.ps("pr", [P, 512])
        loaded = s.sem("loaded")
        made = s.sem("made")
        hot = s.sem("hot")
        counted = s.sem("counted")
        all_counted = s.sem("all_counted")
        total_ready = s.sem("total_ready")
        total_summed = s.sem("total_summed")
        hot2 = s.sem("hot2")
        turned = s.sem("turned")
        lo_t_ready = s.sem("lo_t_ready")
        taken_ready = s.sem("taken_ready")
        same_ready = s.sem("same_ready")
        masked = s.sem("masked")
        ranked = s.sem("ranked")
        placed = s.sem("placed")
        iota_done = s.sem("iota_done")
        scatter = Scatter(s, places, 0, places.early, loops=True, placed=placed)
        block = ctx.enter_context(nc.Block())

        def by_tile(ap):
            return ap[:, 0:B * NT].rearrange("p (u c) -> p u c", u=B)

        @block.sync
        def _(sp):
            for k in range(2):
                sp.dma_start(ends[:, k, :], T["L0_ffn_edge_index"][k].rearrange("(p t) -> p t", p=P)).then_inc(loaded, 16)

        @block.vector
        def _(dve):
            link = Tally(dve, s.sem("dve"))

            def build(h, t0):
                dve.tensor_tensor(one_lo[:, h, :, :], K["frow"][:, :].unsqueeze(1).broadcast_to((P, B, P)),
                                  lo[:, bass.ds(t0, B)].unsqueeze(2).broadcast_to((P, B, P)), ALU.is_equal)
                return dve.tensor_tensor(one_hi[:, h, :, :], K["frow"][:, 0:NT].unsqueeze(1).broadcast_to((P, B, NT)),
                                         hi[:, bass.ds(t0, B)].unsqueeze(2).broadcast_to((P, B, NT)), ALU.is_equal)

            dve.tensor_copy(ident[:, :], K["ident"][:, :]).then_inc(made, 1)
            dve.memset(zeros[:, :], 0.0).then_inc(made, 1)
            dve.memset(none[:, :], 0.0)
            dve.wait_ge(loaded, 32)
            dve.tensor_scalar(hi_i[:, :], ends[:, 1, :], 7, None, ALU.arith_shift_right)
            link.done(dve.tensor_scalar(lo_i[:, :], ends[:, 1, :], P - 1, None, ALU.bitwise_and))
            dve.tensor_copy(hi[:, :], hi_i[:, :])
            link.done(dve.tensor_copy(lo[:, :], lo_i[:, :]))
            with dve.Fori(0, TURNS // 2) as i:
                for h in range(2):
                    g = 2 * i + h
                    dve.wait_ge(counted, g + 1)
                    build(h, g * B).then_inc(hot, 1)
            dve.wait_ge(all_counted, 1)
            dve.tensor_scalar(total[:, :], pr[:, 0:NT], 1.0, None, ALU.add).then_inc(total_ready, 1)
            dve.wait_ge(total_summed, 1)
            link.done(dve.tensor_copy(below[:, :], pc[:, 0, 0:NT]))
            link.done(dve.tensor_tensor_scan(upto[:, :], none[:, :], below[:, :], 0.0, ALU.add, ALU.add))
            link.done(dve.tensor_tensor(upto[:, :], upto[:, :], below[:, :], ALU.subtract))
            link.done(dve.tensor_tensor(upto[:, :], upto[:, :], pc[:, 1, 0:NT], ALU.add))
            dve.tensor_copy(places.loop_pos[:, :], upto[:, :])
            link.done(dve.tensor_scalar(taken[:, :], upto[:, :], 1.0, None, ALU.add))
            dve.wait_ge(iota_done, 1)
            for k in range(2):
                dve.tensor_copy(places.loop_pair[:, :, k], loop_i[:, :])
                ins = dve.tensor_copy(places.pair[:, :, k], ends[:, k, :])
            link.done(ins)

            def take(k, g):
                dve.wait_ge(turned, g + 1)
                link.done(dve.tensor_tensor(taken_by_tile[:, k, :, :], by_tile(pc[:, k, :]),
                                            taken[:, :].unsqueeze(1).broadcast_to((P, B, NT)), ALU.add))
                link.done(dve.tensor_tensor(taken[:, :], taken[:, :], pc[:, k, B * NT:(B + 1) * NT], ALU.add))
                dve.sem_inc(taken_ready, 1)

            for g in range(2):
                build(g, g * B).then_inc(hot2, 1)
            take(0, 0)
            with dve.Fori(0, TURNS // RING) as i:
                link.loop(i, RING * 4)
                for r in range(RING):
                    g = RING * i + r
                    dve.wait_ge(same_ready, g + 1)
                    dve.tensor_tensor(earlier[:, :, :], pq[:, :, :], K["below"][:, :].unsqueeze(1).broadcast_to((P, B, P)),
                                      ALU.mult).then_inc(masked, 1)
                    build((r + 2) % RING, (g + 2) % TURNS * B).then_inc(hot2, 1)
                    take((r + 1) % 2, g + 1)
                    dve.wait_ge(hot2, g + 1)
                    dve.wait_ge(ranked, g + 1)
                    link.done(dve.tensor_tensor(picked[:, :, :], by_tile(pr[:, :]), one_hi[:, r, :, :], ALU.mult))
                    dve.wait_ge(placed, g)
                    link.done(dve.tensor_reduce(pos[:, :], picked[:, :, :], AX, ALU.add))
                    dve.tensor_copy(places.pos[:, bass.ds(g * B, B)], pos[:, :]).then_inc(placed, 1)
            link.leave(TURNS // RING)
            dve.wait_ge(placed, TURNS)

        @block.tensor
        def _(pe):
            def turn(h, k):
                for u in range(B):
                    pe.matmul(pt[:, u, :], one_lo[:, h, u, :], ident[:, :], start=True, stop=True)
                pe.matmul(pc[:, k, 0:NT], zeros[:, :], zeros[:, 0:NT], start=True, stop=True)
                for u in range(1, B + 1):
                    for v in range(u):
                        mm = pe.matmul(pc[:, k, u * NT:(u + 1) * NT], one_lo[:, h, v, :], one_hi[:, h, v, :],
                                       start=(v == 0), stop=(v == u - 1))
                return mm

            pe.wait_ge(made, 2)
            pe.sem_inc(counted, 2)
            pe.matmul(pr[:, 0:NT], zeros[:, :], zeros[:, 0:NT], start=True, stop=False)
            with pe.Fori(0, TURNS // 2) as i:
                for h in range(2):
                    pe.wait_ge(hot, 2 * i + h + 1)
                    for u in range(B):
                        mm = pe.matmul(pr[:, 0:NT], one_lo[:, h, u, :], one_hi[:, h, u, :], start=False, stop=False)
                    mm.then_inc(counted, 1)
            pe.matmul(pr[:, 0:NT], zeros[:, :], zeros[:, 0:NT], start=False, stop=True).then_inc(all_counted, 1)
            pe.wait_ge(total_ready, 1)
            pe.matmul(pc[:, 0, 0:NT], K["ones"][:, :], total[:, :], start=True, stop=True)
            pe.matmul(pc[:, 1, 0:NT], K["below"][:, :], total[:, :], start=True, stop=True).then_inc(total_summed, 1)
            pe.wait_ge(hot2, 1)
            turn(0, 0).then_inc(turned, 1)
            with pe.Fori(0, TURNS // RING) as i:
                for r in range(RING):
                    g = RING * i + r
                    k = r % 2
                    pe.wait_ge(lo_t_ready, g + 1)
                    for u in range(B):
                        mm = pe.matmul(pq[:, u, :], lo_t16[:, k, u, :], lo_t16[:, k, u, :], start=True, stop=True)
                    mm.then_inc(same_ready, 1)
                    pe.wait_ge(hot2, g + 2)
                    turn((r + 1) % RING, 1 - k).then_inc(turned, 1)
                    pe.wait_ge(taken_ready, g + 1)
                    pe.wait_ge(masked, g + 1)
                    for u in range(B):
                        rank = pr[:, u * NT:(u + 1) * NT]
                        pe.matmul(rank, lo_t[:, k, u, :], taken_by_tile[:, k, u, :], start=True, stop=False)
                        mm = pe.matmul(rank, earlier[:, u, :], one_hi[:, r, u, :], start=False, stop=True)
                    mm.then_inc(ranked, 1)

        @block.scalar
        def _(act):
            def copy(h):
                act.activation(lo_t[:, h, :, :], pt[:, :, :], ACT.Copy)
                return act.activation(lo_t16[:, h, :, :], pt[:, :, :], ACT.Copy)

            act.wait_ge(turned, 1)
            copy(0).then_inc(lo_t_ready, 1)
            with act.Fori(0, TURNS // 2) as i:
                for h in range(2):
                    g = 2 * i + h
                    act.wait_ge(turned, g + 2)
                    act.wait_ge(ranked, g)
                    copy(1 - h).then_inc(lo_t_ready, 1)

        @block.gpsimd
        def _(pool):
            pool.iota(loop_i[:, :], pattern=[[P, NT]], base=0, channel_multiplier=1).then_inc(iota_done, 1)
            pool.wait_ge(hot2, 1)
            scatter.pool(pool, T)


class Places:

    def __init__(self, nc, ctx):
        def held(name, shape):
            return ctx.enter_context(nc.sbuf_tensor("places_" + name, shape, I32))

        self.loop_pos = held("loop_pos", [P, NODE_TILES])
        self.loop_pair = held("loop_pair", [P, NODE_TILES, 2])
        self.pos = held("pos", [P, HOP_TILES])
        self.early = 16 * 16
        self.pair = held("pair", [P, HOP_TILES, 2])


class Scatter:

    B = 8

    def __init__(self, s, places, first, last, loops=False, placed=None):
        self.places, self.loops, self.placed = places, loops, placed
        self.first, self.turns = first, (last - first) // (2 * self.B)
        assert self.turns * 2 * self.B == last - first
        self.pos = s.sb("scatter_pos", [P, 2, self.B], I32)
        self.pair = s.sb("scatter_pair", [P, 2, self.B, 2], I32)
        self.staged = s.sem("scatter_staged")
        self.put = [s.gather_sem("put0"), s.gather_sem("put1")]

    def pool(self, pool, T):
        of, B = self.places, self.B
        loops = NODE_TILES if self.loops else 0
        for c in range(loops):
            pool.indirect_dma_start(out=T["f_pairs"], out_offset=bass.IndirectOffsetOnAxis(ap=of.loop_pos[:, c:c + 1], axis=0),
                                    in_=of.loop_pair[:, c, :], in_offset=None).then_inc(self.put[0], 16)
        with pool.Fori(0, self.turns) as i:
            for h in range(2):
                at = self.first + (2 * i + h) * B
                if self.placed:
                    pool.wait_ge(self.placed, 2 * i + h + 1)
                pool.wait_ge(self.put[h], 16 * (B * i + loops * (1 - h)))
                pool.tensor_copy(self.pair[:, h, :, :], of.pair[:, bass.ds(at, B), :])
                pool.tensor_copy(self.pos[:, h, :], of.pos[:, bass.ds(at, B)]).then_inc(self.staged, 1)
                pool.wait_ge(self.staged, 2 * i + h + 1)
                pool.nop(nofuse=True)
                for u in range(B):
                    pool.indirect_dma_start(out=T["f_pairs"],
                                            out_offset=bass.IndirectOffsetOnAxis(ap=self.pos[:, h, u:u + 1], axis=0),
                                            in_=self.pair[:, h, u, :], in_offset=None).then_inc(self.put[h], 16)
        for h in range(2):
            pool.wait_ge(self.put[h], 16 * (B * self.turns + loops * (1 - h)))


def stage_split(nc, T, K):
    n = HOP.edge_tiles
    with ExitStack() as ctx:
        s = Scope(nc, ctx, "p")
        pairs = s.sb("pairs", [P, n, 2], I32)
        ends = s.sb("ends", [P, 2, n], I32)
        loaded = s.sem("loaded")
        split = s.sem("split")
        stored = s.sem("stored")
        block = ctx.enter_context(nc.Block())

        @block.sync
        def _(sp):
            sp.dma_start(pairs[:, :, :], T["f_pairs"].rearrange("(p n) c -> p n c", p=P)).then_inc(loaded, 16)
            sp.wait_ge(split, 2)
            sp.dma_start(T["f_src"][0:HOP.edges].rearrange("(p n) -> p n", p=P), ends[:, 0, :]).then_inc(stored, 16)
            sp.dma_start(T["f_dst"][0:HOP.edges].rearrange("(p n) -> p n", p=P), ends[:, 1, :]).then_inc(stored, 16)
            sp.wait_ge(stored, 32)

        @block.vector
        def _(dve):
            dve.wait_ge(loaded, 16)
            for k in range(2):
                dve.tensor_copy(ends[:, k, :], pairs[:, :, k]).then_inc(split, 1)


def stage_schedule(nc, T, K, L):
    B, W = L.blocks, L.blocks * P
    with ExitStack() as ctx:
        s = Scope(nc, ctx, "m" + L.name)
        last_i = s.sb("last_i", [P, L.pair_blocks], I32)
        last = s.sb("last", [P, L.pair_blocks])
        num_i = s.sb("num_i", [P, max(B, L.pair_blocks)], I32)
        num = s.sb("num", [P, max(B, L.pair_blocks)])
        stop_i = s.sb("stop_i", [P, B], I32)
        stop = s.sb("stop", [P, B])
        second_i = s.sb("second_i", [P, B], I32)
        second = s.sb("second", [P, B])
        srow_i = s.sb("srow_i", [P, W], I32)
        srow = s.sb("srow", [P, W])
        left = s.sb("left", [P, L.pair_blocks, W], BF16)
        ones = s.sb("ones", [P, 1], BF16)
        j_of = s.sb("j_of", [P, B])
        i_of = s.sb("i_of", [P, B])
        far = s.sb("far", [P, B])
        j_idx = s.sb("j_idx", [P, B], I32)
        i_row = s.sb("i_row", [1, W])
        j_row = s.sb("j_row", [1, W // 2])
        i_row_i = s.sb("i_row_i", [1, W // 2], I32)
        j_row_i = s.sb("j_row_i", [1, W // 2], I32)
        got = s.sb("got", [P, 2, B, P], I32)
        val = s.sb("val", [P, 2, B, P])
        rel = s.sb("rel", [P, B, P])
        src_t = s.sb("src_t", [P, W], I32)
        rel_t = s.sb("rel_t", [P, W])
        pj = s.ps("pj", [P, 512])
        prow = s.ps("prow", [1, 2, 512])
        pt = s.ps("pt", [P, 4, 512])
        loaded = s.sem("loaded")
        iotas = s.sem("iotas")
        filled = s.sem("filled")
        marked = s.sem("marked")
        placed = s.sem("placed")
        j_ready = s.sem("j_ready")
        got_rows = s.gather_sem("got_rows")
        rel_ready = s.sem("rel_ready")
        turned = s.sem("turned")
        stored = s.sem("stored")
        t_ready = s.sem("t_ready")
        block = ctx.enter_context(nc.Block())
        full = L.pairs // P * P
        rest = L.pairs - full
        pair_rows = T[L.name + "_dst"].rearrange("(j e) -> j e", e=2 * P)
        dst_rows = T[L.name + "_dst"].rearrange("(j e) -> j e", e=P)
        src_rows = T[L.name + "_src"].rearrange("(j e) -> j e", e=P)
        HW = W // 2

        @block.gpsimd
        def _(pool):
            pool.iota(num_i[:, :], pattern=[[P, num_i.shape[1]]], base=0, channel_multiplier=1).then_inc(iotas, 1)
            pool.iota(srow_i[:, :].rearrange("p (r k) -> p r k", k=2), pattern=[[1, W // 2], [0, 2]], base=0, channel_multiplier=0).then_inc(iotas, 1)
            pool.wait_ge(j_ready, 1)
            for b in range(B):
                for k, rows in enumerate((src_rows, dst_rows)):
                    pool.indirect_dma_start(out=got[:, k, b, :], out_offset=None, in_=rows,
                                            in_offset=bass.IndirectOffsetOnAxis(ap=j_idx[:, b:b + 1], axis=0)
                                            ).then_inc(got_rows, 16)

        @block.sync
        def _(sp):
            sp.wait_ge(filled, 1)
            with nc.allow_non_contiguous_dma(reason="one destination of each pair of tiles"):
                sp.dma_start(last_i[:, 0:full // P], pair_rows[0:full, 2 * P - 1:2 * P].rearrange("(b p) a -> p (b a)", p=P)
                             ).then_inc(loaded, 16)
                sp.dma_start(last_i[0:rest, full // P:full // P + 1], pair_rows[full:L.pairs, 2 * P - 1:2 * P]).then_inc(loaded, 16)
            sp.wait_ge(rel_ready, 1)
            sp.dma_start(T[L.name + "_rel_rows"].rearrange("(b s) e -> s b e", s=P), rel[:, :, :]).then_inc(stored, 16)
            sp.dma_start(T[L.name + "_key_rows"].rearrange("(b s) e -> s b e", s=P), val[:, 1, :, :]).then_inc(stored, 16)
            sp.dma_start(T[L.name + "_i_row"].rearrange("(a s) -> a s", a=1), i_row_i[:, :]).then_inc(stored, 16)
            sp.dma_start(T[L.name + "_j_row"].rearrange("(a s) -> a s", a=1), j_row_i[:, :]).then_inc(stored, 16)
            sp.wait_ge(t_ready, 1)
            sp.dma_start(T[L.name + "_src_t"], src_t[:, 0:L.steps]).then_inc(stored, 16)
            sp.dma_start(T[L.name + "_rel_t"], rel_t[:, 0:L.steps]).then_inc(stored, 16)
            sp.wait_ge(stored, 96)

        @block.vector
        def _(dve):
            link = Tally(dve, s.sem("dve"))
            dve.memset(ones[:, :], 1.0)
            dve.memset(last_i[:, :], 1 << 28).then_inc(filled, 1)
            dve.wait_ge(iotas, 2)
            dve.tensor_copy(num[:, :], num_i[:, :])
            dve.tensor_copy(srow[:, :], srow_i[:, :])
            dve.tensor_scalar(stop_i[:, :], num_i[:, 0:B], 1, None, ALU.arith_shift_right)
            link.done(dve.tensor_scalar(second_i[:, :], num_i[:, 0:B], 1, None, ALU.bitwise_and))
            dve.tensor_copy(stop[:, :], stop_i[:, :])
            link.done(dve.tensor_copy(second[:, :], second_i[:, :]))
            dve.wait_ge(loaded, 32)
            link.done(dve.tensor_scalar(last_i[:, :], last_i[:, :], 7, None, ALU.arith_shift_right))
            link.done(dve.tensor_copy(last[:, :], last_i[:, :]))
            link.done(dve.tensor_tensor(last[:, :], last[:, :], num[:, 0:L.pair_blocks], ALU.add))
            for b in range(L.pair_blocks):
                link.done(dve.tensor_scalar(left[:, b, :], srow[:, :], last[:, b:b + 1], None, ALU.is_gt))
            dve.sem_inc(marked, 1)
            dve.wait_ge(placed, 1)
            link.done(dve.tensor_copy(j_of[:, :], pj[:, 0:B]))
            for h in range(2):
                link.done(dve.tensor_tensor(i_row[:, h * HW:(h + 1) * HW], srow[0:1, h * HW:(h + 1) * HW],
                                            prow[:, h, 0:HW], ALU.subtract))
            link.done(dve.tensor_scalar(i_row[:, :], i_row[:, :], float(NODE_TILES - 1), None, ALU.min))
            dve.tensor_copy(i_row_i[:, :], i_row[:, 0:W:2])
            link.done(dve.tensor_tensor(j_row[:, :], srow[0:1, 0:W:2], i_row[:, 0:W:2], ALU.subtract))
            dve.tensor_scalar(j_row_i[:, :], j_row[:, :], float(L.pairs - 1), None, ALU.min)
            link.done(dve.tensor_tensor(i_of[:, :], stop[:, :], j_of[:, :], ALU.subtract))
            link.done(dve.tensor_scalar(j_of[:, :], j_of[:, :], float(L.pairs - 1), 2.0, ALU.min, ALU.mult))
            link.done(dve.tensor_tensor(j_of[:, :], j_of[:, :], second[:, :], ALU.add))
            link.done(dve.tensor_copy(j_idx[:, :], j_of[:, :]))
            dve.sem_inc(j_ready, 1)
            dve.tensor_scalar(far[:, :], stop[:, :], float(L.real_stops) - 0.5, FAR, ALU.is_gt, ALU.mult)
            link.done(dve.tensor_scalar(i_of[:, :], i_of[:, :], float(P), None, ALU.mult))
            link.done(dve.tensor_tensor(i_of[:, :], i_of[:, :], far[:, :], ALU.add))
            dve.wait_ge(got_rows, 32 * B)
            link.done(dve.tensor_copy(val[:, :, :, :], got[:, :, :, :]))
            link.done(dve.tensor_tensor(rel[:, :, :], val[:, 1, :, :], i_of[:, :].unsqueeze(2).broadcast_to((P, B, P)),
                                        ALU.subtract))
            dve.sem_inc(rel_ready, 1)
            dve.wait_ge(turned, 1)
            for k, to in enumerate((src_t, rel_t)):
                for h in range(2):
                    w = min(512, W - h * 512)
                    link.done(dve.tensor_copy(to[:, h * 512:h * 512 + w], pt[:, 2 * k + h, 0:w]))
            dve.sem_inc(t_ready, 1)

        @block.tensor
        def _(pe):
            pe.wait_ge(marked, 1)
            for b in range(B):
                for c in range(L.pair_blocks):
                    pe.matmul(pj[:, b:b + 1], left[:, c, b * P:(b + 1) * P], ones[:, :],
                              start=(c == 0), stop=(c == L.pair_blocks - 1))
            for h in range(2):
                for c in range(L.pair_blocks):
                    mm = pe.matmul(prow[:, h, 0:HW], ones[:, :], left[:, c, h * HW:(h + 1) * HW],
                                   start=(c == 0), stop=(c == L.pair_blocks - 1))
            mm.then_inc(placed, 1)
            pe.wait_ge(rel_ready, 1)
            for k in range(2):
                for b in range(B):
                    of = val[:, 0, b, :] if k == 0 else rel[:, b, :]
                    mm = pe.transpose(pt[:, 2 * k + b // 4, (b % 4) * P:(b % 4 + 1) * P], of, K["ident"][:, :])
            mm.then_inc(turned, 1)


def rows_of(ap):
    return ap.rearrange("(t p) f -> p t f", p=P)


class Norm:

    def __init__(self, s, turn=True):
        self.x = s.sb("x", [P, TPC, D])
        self.xn = s.sb("xn", [P, TPC, D])
        self.stat = s.sb("stat", [P, TPC, 6])
        self.mv = s.sb("mv", [P, TPC, 2])
        self.sd = s.sb("sd", [P, TPC])
        self.rstd = s.sb("rstd", [P, TPC])
        self.x_loaded = s.sem("x_loaded")
        self.var_ready = s.sem("var_ready")
        self.sd_ready = s.sem("sd_ready")
        self.xn_ready = s.sem("xn_ready")
        if turn:
            self.xt = s.sb("xt", [P, 2, ROWS])
            self.pt = s.ps("pt", [P, 4, 512])
            self.turned = s.sem("turned")
            self.xt_ready = s.sem("xt_ready")

    def load(self, sp, table, c):
        sp.dma_start(self.x[:, :, :], table[bass.ds(c * ROWS, ROWS), :].rearrange("(t p) f -> p t f", p=P)
                     ).then_inc(self.x_loaded, 16)

    def vector(self, dve, link, c, x=None, out=None):
        x = self.x if x is None else x
        out = self.xn if out is None else out
        for t in range(TPC):
            ins = dve.bn_stats(self.stat[:, t, :], x[:, t, :])
        link.done(ins)
        dve.nop(nofuse=True)
        for t in range(TPC):
            ins = dve.bn_aggr(self.mv[:, t, :], self.stat[:, t, :])
        ins.then_inc(self.var_ready, 1)
        dve.wait_ge(self.sd_ready, c + 1)
        link.done(dve.reciprocal(self.rstd[:, :], self.sd[:, :]))
        for t in range(TPC):
            ins = dve.tensor_scalar(out[:, t, :], x[:, t, :], self.mv[:, t, 0:1], self.rstd[:, t:t + 1],
                                    ALU.subtract, ALU.mult)
        return ins

    def scalar(self, act, K, c):
        act.wait_ge(self.var_ready, c + 1)
        act.activation(self.sd[:, :], self.mv[:, :, 1], ACT.Sqrt, bias=K["eps"][:, 0:1]).then_inc(self.sd_ready, 1)

    def tensor(self, pe, K, c):
        pe.wait_ge(self.xn_ready, c + 1)
        for f in range(2):
            for t in range(TPC):
                ins = pe.transpose(self.pt[:, 2 * f + t // 4, (t % 4) * P:(t % 4 + 1) * P],
                                   self.xn[:, t, f * P:(f + 1) * P], K["ident"][:, :])
        ins.then_inc(self.turned, 1)

    def scalar_turned(self, act, c):
        act.wait_ge(self.turned, c + 1)
        for f in range(2):
            for h in range(2):
                w = min(512, ROWS - h * 512)
                ins = act.activation(self.xt[:, f, h * 512:h * 512 + w], self.pt[:, 2 * f + h, 0:w], ACT.Copy)
        ins.then_inc(self.xt_ready, 1)


def stage_l0_project(nc, T, K, places):
    with ExitStack() as ctx:
        s = Scope(nc, ctx, "q")
        n = Norm(s)
        w = s.sb("w", [P, 4, 2, D])
        wt = s.sb("wt", [P, 2, 4 * D])
        bias = s.sb("bias", [P, 4 * D])
        out = s.sb("out", [P, 2 * TPC, 4 * D])
        pq = s.ps("pq", [P, 2, 2 * 512])
        loaded = s.sem("loaded")
        w_turned = s.sem("w_turned")
        wt_ready = s.sem("wt_ready")
        projected = s.sem("projected")
        biased = s.sem("biased")
        stored = s.sem("stored")
        scatter = Scatter(s, places, places.early, places.early + 5 * 16)
        block = ctx.enter_context(nc.Block())
        names = ("q", "k", "v", "skip")

        @block.sync
        def _(sp):
            sp.sem_inc(stored, 64)
            n.load(sp, T["x0"], 0)
            for k, m in enumerate(names):
                sp.dma_start(w[:, k, :, :], T["L0_gnn_W" + m].rearrange("(a p) f -> p a f", p=P)).then_inc(loaded, 16)
                sp.dma_start(bias[:, k * D:(k + 1) * D], bcast_rows(T["L0_gnn_b" + m], P)).then_inc(loaded, 16)
            with sp.Fori(0, CHUNKS) as c:
                sp.wait_ge(n.xn_ready, c + 1)
                n.load(sp, T["x0"], (c + 1) % CHUNKS)
                sp.wait_ge(biased, TPC * (c + 1))
                sp.nop(nofuse=True)
                sp.wait_ge(stored, 64 * (c + 1))
                sp.nop(nofuse=True)
                for k, m in enumerate(names):
                    sp.dma_start(T["l0_" + m][bass.ds(c * ROWS, ROWS), :].rearrange("(t p) f -> p t f", p=P),
                                 out[:, bass.ds(c % 2 * TPC, TPC), k * D:(k + 1) * D]).then_inc(stored, 16)
            sp.wait_ge(stored, 64 * (CHUNKS + 1))
            sp.wait_ge(n.x_loaded, 16 * (CHUNKS + 1))

        @block.gpsimd
        def _(pool):
            scatter.pool(pool, T)

        @block.vector
        def _(dve):
            link = Tally(dve, s.sem("dve"))

            def norm(c):
                dve.wait_ge(n.x_loaded, 16 * c + 16)
                dve.wait_ge(n.turned, c)
                n.vector(dve, link, c).then_inc(n.xn_ready, 1)

            def add_bias(c, tiles):
                for t in tiles:
                    dve.wait_ge(projected, TPC * c + t + 1)
                    to = out[:, bass.ds(c % 2 * TPC + t, 1), :].rearrange("p a w -> p (a w)")
                    dve.tensor_tensor(to, pq[:, t % 2, :], bias[:, :], ALU.add).then_inc(biased, 1)

            norm(0)
            dve.wait_ge(loaded, 128)
            with dve.Fori(0, CHUNKS - 1) as c:
                link.loop(c, 2)
                dve.wait_ge(stored, 64 * c)
                add_bias(c, range(TPC // 2))
                norm(c + 1)
                add_bias(c, range(TPC // 2, TPC))
            link.leave(CHUNKS - 1)
            dve.wait_ge(stored, 64 * (CHUNKS - 1))
            add_bias(CHUNKS - 1, range(TPC))

        @block.scalar
        def _(act):
            act.wait_ge(w_turned, 1)
            for k in range(4):
                for f in range(2):
                    ins = act.activation(wt[:, f, k * D:(k + 1) * D], n.pt[:, k, f * D:(f + 1) * D], ACT.Copy)
            ins.then_inc(wt_ready, 1)
            with act.Fori(0, CHUNKS) as c:
                n.scalar(act, K, c)
                n.scalar_turned(act, c)

        @block.tensor
        def _(pe):
            pe.wait_ge(loaded, 128)
            for k in range(4):
                for f in range(2):
                    for a in range(2):
                        ins = pe.transpose(n.pt[:, k, f * D + a * P:f * D + (a + 1) * P],
                                           w[:, k, a, f * P:(f + 1) * P], K["ident"][:, :])
            ins.then_inc(w_turned, 1)
            pe.wait_ge(wt_ready, 1)
            with pe.Fori(0, CHUNKS) as c:
                n.tensor(pe, K, c)
                pe.wait_ge(n.xt_ready, c + 1)
                for t in range(TPC):
                    g = TPC * c + t
                    pe.wait_ge(biased, g if t < 2 else g - 1)
                    for h in range(2):
                        for f in range(2):
                            ins = pe.matmul(pq[:, t % 2, h * 512:(h + 1) * 512], n.xt[:, f, t * P:(t + 1) * P],
                                            wt[:, f, h * 512:(h + 1) * 512], start=(f == 0), stop=(f == 1))
                    ins.then_inc(projected, 1)


def stage_dot(nc, T, K, L, score):
    H = 4
    STOPS = DEPTH * U // 2
    with ExitStack() as ctx:
        s = Scope(nc, ctx, "d")
        keys = s.sb("keys", [P, NODE_TILES, D])
        src = s.sb("src", [P, L.steps], I32)
        i_row = s.sb("i_row", [1, L.stops], I32)
        spread = s.sb("spread", [P, DEPTH, U * P])
        apart = s.sb("apart", [P, DEPTH, U * P])
        hot = s.sb("hot", [P, DEPTH, U * P])
        idx = s.sb("idx", [P, DEPTH, U], I32)
        q = s.sb("q", [P, DEPTH, U, D])
        prod = s.sb("prod", [P, DEPTH, U * D])
        pk = s.ps("pk", [P, DEPTH, U * D])
        loaded = s.sem("loaded")
        spread_in = [s.sem(f"spread_in{h}") for h in range(DEPTH)]
        q_in = [s.gather_sem(f"q_in{h}") for h in range(DEPTH)]
        idx_ready = s.sem("idx_ready")
        apart_ready = s.sem("apart_ready")
        hot_ready = s.sem("hot_ready")
        keys_out = s.sem("keys_out")
        multiplied = s.sem("multiplied")
        scored = s.sem("scored")
        block = ctx.enter_context(nc.Block())
        rel_flat = T[L.name + "_rel_rows"].rearrange("s e -> (s e)")

        @block.sync
        def _(sp):
            sp.dma_start(src[:, :], T[L.name + "_src_t"]).then_inc(loaded, 16)
            sp.dma_start(i_row[:, :], T[L.name + "_i_row"][0:L.stops].rearrange("(a s) -> a s", a=1)).then_inc(loaded, 16)
            sp.dma_start(keys[:, :, :], rows_of(T["l0_k"])).then_inc(loaded, 16)
            with sp.Fori(0, L.turns) as i:
                for h in range(DEPTH):
                    g = i * DEPTH + h
                    sp.wait_ge(apart_ready, g + 1)
                    sp.dma_start(spread[:, h, :], rel_flat[bass.ds(g * U * P, U * P)].partition_broadcast(P)
                                 ).then_inc(spread_in[h], 16)

        @block.gpsimd
        def _(pool):
            with pool.Fori(0, L.turns) as i:
                for h in range(DEPTH):
                    g = i * DEPTH + h
                    pool.wait_ge(idx_ready, g + 1)
                    pool.wait_ge(multiplied, g + 1)
                    pool.nop(nofuse=True)
                    for u in range(U):
                        pool.indirect_dma_start(out=q[:, h, u, :], out_offset=None, in_=T["l0_q"],
                                                in_offset=bass.IndirectOffsetOnAxis(ap=idx[:, h, u:u + 1], axis=0)
                                                ).then_inc(q_in[h], 16)

        @block.scalar
        def _(act):
            act.sem_inc(apart_ready, DEPTH)
            act.sem_inc(hot_ready, DEPTH)
            with act.Fori(0, L.turns) as i:
                for h in range(DEPTH):
                    g = i * DEPTH + h
                    act.wait_ge(spread_in[h], 16 * (i + 1))
                    act.activation(apart[:, h, :], spread[:, h, :], ACT.Abs, bias=K["minus_col"][:, 0:1]).then_inc(apart_ready, 1)
                    act.wait_ge(apart_ready, DEPTH + g + 1)
                    act.wait_ge(keys_out, g + 1)
                    act.activation(hot[:, h, :], apart[:, h, :], ACT.Relu, scale=-1.0, bias=K["ones"][:, 0:1]).then_inc(hot_ready, 1)

        @block.vector
        def _(dve):
            dve.sem_inc(multiplied, DEPTH)
            dve.wait_ge(loaded, 48)
            dve.tensor_copy(idx[:, :, :], src[:, 0:DEPTH * U].rearrange("p (d u) -> p d u", u=U)).then_inc(idx_ready, DEPTH)
            with dve.Fori(0, L.turns) as i:
                for h in range(DEPTH):
                    g = i * DEPTH + h
                    dve.wait_ge(q_in[h], 16 * U * (i + 1))
                    dve.tensor_copy(idx[:, h, :], src[:, bass.ds((g + DEPTH) % (L.turns * DEPTH) * U, U)]).then_inc(idx_ready, 1)
                    dve.wait_ge(keys_out, DEPTH + g + 1)
                    dve.tensor_tensor(prod[:, h, :], pk[:, h, :], q[:, h, :, :].rearrange("p u d -> p (u d)"),
                                      ALU.mult).then_inc(multiplied, 1)
                    dve.wait_ge(multiplied, DEPTH + g + 1)
                    dve.tensor_reduce(score[:, bass.ds(g * U, U), :].rearrange("p u h -> p (u h)"),
                                      prod[:, h, :].rearrange("p (a c) -> p a c", c=D // H), AX, ALU.add).then_inc(scored, 1)

        @block.tensor
        def _(pe):
            pe.sem_inc(keys_out, DEPTH)
            pe.wait_ge(loaded, 48)
            with pe.Fori(0, L.turns) as i:
                _, tile = nc.values_load_multi_w_load_instructions(
                    i_row[0:1, bass.ds(i * STOPS, STOPS)], engines=[mybir.EngineType.PE], min_val=0, max_val=NODE_TILES - 1)
                for h in range(DEPTH):
                    g = i * DEPTH + h
                    pe.wait_ge(hot_ready, DEPTH + g + 1)
                    pe.wait_ge(multiplied, g + 1)
                    for u in range(U):
                        mm = pe.matmul(pk[:, h, u * D:(u + 1) * D], hot[:, h, u * P:(u + 1) * P],
                                       keys[:, bass.ds(tile[(h * U + u) // 2], 1), :], start=True, stop=True)
                    mm.then_inc(keys_out, 1)


def stage_softmax(nc, T, K, L, H, scale, score, places=None):
    B, S = L.blocks, L.steps
    W = B * P
    with ExitStack() as ctx:
        s = Scope(nc, ctx, "x" + L.name + str(H))
        one = s.sb("one", [P, 2, W])
        key = s.sb("key", [P, B, P])
        rel = s.sb("rel", [P, B, P])
        off = s.sb("off", [P, B, P])
        from_left = s.sb("from_left", [P, B, P])
        from_right = s.sb("from_right", [P, B, P])
        not_first = s.sb("not_first", [P, B, P])
        not_last = s.sb("not_last", [P, B, P])
        val = s.sb("val", [P, H, W])
        seg = s.sb("seg", [P, H, W])
        now = s.sb("now", [P, 2, W])
        bwd = s.sb("bwd", [P, B, P])
        ends = s.sb("ends", [P, B, 2, H])
        chain = s.sb("chain", [H, W, 2])
        chain_left = s.sb("chain_left", [H, 2 * W])
        chain_right = s.sb("chain_right", [H, 2 * W])
        top = s.sb("top", [P, B, 2, H])
        mine = s.sb("mine", [P, 2, B, 2])
        exps = s.sb("exps", [P, 2, W])
        pt = s.ps("pt", [P, 2, 8, P])[:, :, 0:B, :]
        pl = s.ps("pl", [P, 2, 8, P])[:, :, 0:B, :]
        loaded = s.sem("loaded")
        tail_ready = s.sem("tail_ready")
        one_ready = s.sem("one_ready")
        turned = s.sem("turned")
        masked = s.sem("masked")
        kept = s.sem("kept")
        ends_ready = s.sem("ends_ready")
        ends_turned = s.sem("ends_turned")
        tops_ready = s.sem("tops_ready")
        tops_turned = s.sem("tops_turned")
        diff_ready = s.sem("diff_ready")
        exp_ready = s.sem("exp_ready")
        back_turned = s.sem("back_turned")
        weighted = s.sem("weighted")
        if places:
            scatter = Scatter(s, places, places.early + 5 * 16, places.early + 10 * 16)
        block = ctx.enter_context(nc.Block())
        chain_flat = chain[:, :, :].rearrange("h s k -> h (s k)")

        @block.sync
        def _(sp):
            for to, of in ((key, "_key_rows"), (rel, "_rel_rows")):
                sp.dma_start(to[:, :, :], T[L.name + of].rearrange("(b s) e -> s b e", s=P)).then_inc(loaded, 16)

        if places:
            @block.gpsimd
            def _(pool):
                scatter.pool(pool, T)

        @block.vector
        def _(dve):
            link = Tally(dve, s.sem("dve"))

            def flat(ap):
                return ap.rearrange("p b e -> p (b e)")

            def restarts(left, right, keys):
                n = keys.shape[-1]
                dve.memset(left[:, :, 0:1], -BIG)
                dve.memset(right[:, :, n - 1:n], -BIG)
                link.done(dve.tensor_tensor(left[:, :, 1:n], keys[:, :, 1:n], keys[:, :, 0:n - 1], ALU.not_equal))
                link.done(dve.tensor_scalar(left[:, :, 1:n], left[:, :, 1:n], -BIG, None, ALU.mult))
                return dve.tensor_copy(right[:, :, 0:n - 1], left[:, :, 1:n])

            dve.memset(one[:, :, S:W], 0.0).then_inc(tail_ready, 1)
            dve.wait_ge(loaded, 32)
            dve.tensor_scalar(not_first[:, :, :], rel[:, :, :], 0.0, -BIG, ALU.is_lt, ALU.mult)
            link.done(dve.tensor_scalar(not_last[:, :, :], rel[:, :, :], float(P - 1), -BIG, ALU.is_gt, ALU.mult))
            link.done(dve.tensor_tensor(off[:, :, :], not_first[:, :, :], not_last[:, :, :], ALU.add))
            link.done(restarts(from_left[:, :, :], from_right[:, :, :], key[:, :, :]))
            for k, at in enumerate((0, P - 1)):
                ins = dve.tensor_copy(ends[:, :, k, :], key[:, :, at:at + 1].broadcast_to((P, B, H)))
            link.done(ins)
            dve.sem_inc(ends_ready, 1)
            for to, at in ((not_first, 0), (not_last, P - 1)):
                dve.tensor_tensor(to[:, :, :], key[:, :, :], key[:, :, at:at + 1].broadcast_to((P, B, P)), ALU.not_equal)
            dve.wait_ge(ends_turned, 1)
            link.done(dve.tensor_copy(chain[:, :, :].rearrange("h s k -> h k s"), pl[0:H, :, :, :].rearrange("h k b e -> h k (b e)")))
            link.done(restarts(chain_left[:, :].unsqueeze(1), chain_right[:, :].unsqueeze(1), chain_flat.unsqueeze(1)))
            for to in (not_first, not_last):
                ins = dve.tensor_scalar(to[:, :, :], to[:, :, :], -BIG, None, ALU.mult)
            link.done(ins)
            with dve.Fori(0, H // 2) as i:
                link.loop(i, 8)
                for k in range(2):
                    h = 2 * i + k
                    mine_val = now[:, k, :]
                    mine_seg = seg[:, bass.ds(h, 1), :].rearrange("p a w -> p (a w)")
                    dve.wait_ge(turned, h + 1)
                    dve.wait_ge(kept, 2 * i)
                    link.done(dve.tensor_tensor(mine_val, flat(pt[:, k, :, :]), flat(off[:, :, :]), ALU.add))
                    dve.sem_inc(masked, 1)
                    dve.tensor_tensor_scan(mine_seg, flat(from_left[:, :, :]), mine_val, -BIG, ALU.add, ALU.max)
                    link.done(dve.tensor_tensor_scan(flat(bwd[:, :, :])[:, ::-1], flat(from_right[:, :, :])[:, ::-1],
                                                     mine_val[:, ::-1], -BIG, ALU.add, ALU.max))
                    dve.tensor_copy(ends[:, :, 0, bass.ds(h, 1)], bwd[:, :, 0:1])
                    link.done(dve.tensor_copy(ends[:, :, 1, bass.ds(h, 1)], mine_seg.rearrange("p (b e) -> p b e", b=B)[:, :, P - 1:P]))
                    link.done(dve.tensor_tensor(mine_seg, mine_seg, flat(bwd[:, :, :]), ALU.max))
            link.leave(H // 2)
            dve.sem_inc(ends_ready, 1)
            dve.wait_ge(ends_turned, 2)
            link.done(dve.tensor_copy(chain[:, :, :].rearrange("h s k -> h k s"), pl[0:H, :, :, :].rearrange("h k b e -> h k (b e)")))
            left = exps[0:H, :, :].rearrange("h k w -> h (k w)")
            right = one[0:H, :, :].rearrange("h k w -> h (k w)")
            dve.wait_ge(turned, H)
            dve.tensor_tensor_scan(left, chain_left[:, :], chain_flat, -BIG, ALU.add, ALU.max)
            link.done(dve.tensor_tensor_scan(right[:, ::-1], chain_right[:, ::-1], chain_flat[:, ::-1], -BIG, ALU.add, ALU.max))
            link.done(dve.tensor_tensor(chain_flat, left, right, ALU.max))
            dve.sem_inc(tops_ready, 1)
            dve.wait_ge(tops_turned, 1)
            dve.wait_ge(kept, H)
            link.done(dve.tensor_copy(top[:, :, :, :].rearrange("p b k h -> p (b k h)"), flat(pl[:, 0, :, :])[:, 0:B * 2 * H]))
            with dve.Fori(0, H // 2) as i:
                link.loop(i, 8)
                for k in range(2):
                    h = 2 * i + k
                    link.done(dve.tensor_copy(mine[:, k, :, :], top[:, :, :, bass.ds(h, 1)].rearrange("p b k a -> p b (k a)")))
                    mine_seg = seg[:, bass.ds(h, 1), :].rearrange("p a (b e) -> p (a b) e", b=B)
                    for e, out_of in enumerate((not_first, not_last)):
                        for b in range(B):
                            ins = dve.scalar_tensor_tensor(mine_seg[:, b, :], out_of[:, b, :], mine[:, k, b, e:e + 1], mine_seg[:, b, :],
                                                           ALU.add, ALU.max)
                        link.done(ins)
                    mine_val = val[:, bass.ds(h, 1), :].rearrange("p a (b e) -> p (a b) e", b=B)
                    link.done(dve.tensor_tensor(mine_val, mine_val, mine_seg, ALU.subtract))
                    dve.sem_inc(diff_ready, 1)
            link.leave(H // 2)

        @block.scalar
        def _(act):
            act.wait_ge(tail_ready, 1)
            with act.Fori(0, H // 2) as i:
                for k in range(2):
                    h = 2 * i + k
                    act.wait_ge(turned, 2 * i)
                    act.activation(one[:, k, 0:S], score[:, :, bass.ds(h, 1)].rearrange("p s a -> p (s a)"), ACT.Copy
                                   ).then_inc(one_ready, 1)
                for k in range(2):
                    h = 2 * i + k
                    act.wait_ge(masked, h + 1)
                    act.activation(val[:, bass.ds(h, 1), :].rearrange("p a w -> p (a w)"), now[:, k, :], ACT.Copy).then_inc(kept, 1)

            def take(h, k):
                act.wait_ge(back_turned, h + 1)
                act.activation(score[:, :, bass.ds(h, 1)].rearrange("p s a -> p (s a)"),
                               pt[:, k, :, :].rearrange("p b e -> p (b e)")[:, 0:S], ACT.Copy).then_inc(weighted, 1)

            act.wait_ge(tops_turned, 1)
            with act.Fori(0, H // 2) as i:
                for k in range(2):
                    h = 2 * i + k
                    act.wait_ge(diff_ready, h + 1)
                    act.wait_ge(back_turned, 2 * i)
                    act.activation(exps[:, k, :], val[:, bass.ds(h, 1), :].rearrange("p a w -> p (a w)"), ACT.Exp, scale=scale
                                   ).then_inc(exp_ready, 1)
                for k in range(2):
                    take(2 * i + k, k)

        @block.tensor
        def _(pe):
            def turn_ends():
                for k in range(2):
                    for b in range(B):
                        mm = pe.transpose(pl[0:H, k, b, :], ends[:, b, k, :], K["ident"][:, :])
                mm.then_inc(ends_turned, 1)

            pe.wait_ge(ends_ready, 1)
            turn_ends()
            with pe.Fori(0, H // 2) as i:
                for k in range(2):
                    h = 2 * i + k
                    pe.wait_ge(one_ready, h + 1)
                    pe.wait_ge(masked, 2 * i)
                    for b in range(B):
                        mm = pe.transpose(pt[:, k, b, :], one[:, k, b * P:(b + 1) * P], K["ident"][:, :])
                    mm.then_inc(turned, 1)
            pe.wait_ge(ends_ready, 2)
            turn_ends()
            pe.wait_ge(tops_ready, 1)
            tops = pl[:, 0, :, :].rearrange("p b e -> p (b e)")
            for b in range(B):
                for k in range(2):
                    at = (b * 2 + k) * H
                    mm = pe.transpose(tops[:, at:at + H], chain[:, b * P:(b + 1) * P, k], K["ident"][0:H, 0:H])
            mm.then_inc(tops_turned, 1)
            with pe.Fori(0, H // 2) as i:
                for k in range(2):
                    h = 2 * i + k
                    pe.wait_ge(exp_ready, h + 1)
                    pe.wait_ge(weighted, 2 * i)
                    for b in range(B):
                        mm = pe.transpose(pt[:, k, b, :], exps[:, k, b * P:(b + 1) * P], K["ident"][:, :])
                    mm.then_inc(back_turned, 1)


def stage_sum(nc, T, K, L, H, W, weight, acc, table):
    STOPS = DEPTH * U // 2
    PER = U // 2
    LAST = L.turns * DEPTH - 1
    C = W // H
    with ExitStack() as ctx:
        s = Scope(nc, ctx, "a" + L.name + str(H))
        rel = s.sb("rel", [P, L.steps])
        i_row = s.sb("i_row", [1, L.stops], I32)
        apart = s.sb("apart", [P, DEPTH, U, P])
        hot = s.sb("hot", [P, DEPTH, U, P])
        rhs = s.sb("rhs", [P, DEPTH, U, W + H])
        pa = s.ps("pa", [P, DEPTH, PER, 512])
        loaded = s.sem("loaded")
        cleared = s.sem("cleared")
        turned_round = s.sem("turned_round")
        apart_ready = s.sem("apart_ready")
        hot_ready = s.sem("hot_ready")
        rhs_ready = s.sem("rhs_ready")
        summed = s.sem("summed")
        added = s.sem("added")
        src = s.sb("src", [P, L.steps], I32)
        idx = s.sb("idx", [P, DEPTH, U], I32)
        got = s.sb("got", [P, DEPTH, U, W])
        idx_ready = s.sem("idx_ready")
        got_in = [s.gather_sem(f"got_in{h}") for h in range(DEPTH)]
        block = ctx.enter_context(nc.Block())

        @block.sync
        def _(sp):
            sp.dma_start(src[:, :], T[L.name + "_src_t"]).then_inc(loaded, 16)
            sp.dma_start(i_row[:, :], T[L.name + "_i_row"][0:L.stops].rearrange("(a s) -> a s", a=1)).then_inc(loaded, 16)
            sp.dma_start(rel[:, :], T[L.name + "_rel_t"]).then_inc(loaded, 16)

        @block.gpsimd
        def _(pool):
            with pool.Fori(0, L.turns) as i:
                for h in range(DEPTH):
                    g = i * DEPTH + h
                    pool.wait_ge(idx_ready, g + 1)
                    pool.wait_ge(rhs_ready, g + 1)
                    pool.nop(nofuse=True)
                    for u in range(U):
                        pool.indirect_dma_start(out=got[:, h, u, :], out_offset=None, in_=table,
                                                in_offset=bass.IndirectOffsetOnAxis(ap=idx[:, h, u:u + 1], axis=0)
                                                ).then_inc(got_in[h], 16)

        @block.scalar
        def _(act):
            act.sem_inc(apart_ready, DEPTH * U)
            act.sem_inc(hot_ready, DEPTH)
            act.wait_ge(turned_round, 1)
            with act.Fori(0, L.turns) as i:
                for h in range(DEPTH):
                    g = i * DEPTH + h
                    act.wait_ge(hot_ready, g + 1)
                    for u in range(U):
                        act.activation(apart[:, h, u, :], K["frow"][:, :], ACT.Abs, bias=rel[:, bass.ds(g * U + u, 1)]
                                       ).then_inc(apart_ready, 1)
                    act.wait_ge(apart_ready, U * (DEPTH + g + 1))
                    act.wait_ge(summed, g + 1)
                    act.activation(hot[:, h, :, :], apart[:, h, :, :], ACT.Relu, scale=-1.0, bias=K["ones"][:, 0:1]
                                   ).then_inc(hot_ready, 1)

        @block.vector
        def _(dve):
            def weigh(i, h):
                g = i * DEPTH + h
                dve.wait_ge(got_in[h], 16 * U * (i + 1))
                dve.tensor_copy(idx[:, h, :], src[:, bass.ds((g + DEPTH) % (LAST + 1) * U, U)]).then_inc(idx_ready, 1)
                dve.wait_ge(summed, g + 1)
                w = weight[:, bass.ds(g * U, U), :]
                dve.tensor_copy(rhs[:, h, :, W:W + H], w)
                dve.tensor_tensor(rhs[:, h, :, 0:W].rearrange("p u (h c) -> p u h c", h=H),
                                  got[:, h, :, :].rearrange("p u (h c) -> p u h c", h=H),
                                  w.unsqueeze(3).broadcast_to((P, U, H, C)), ALU.mult).then_inc(rhs_ready, 1)

            def tiles_of(i):
                return nc.values_load_multi_w_load_instructions(i_row[0:1, bass.ds(i * STOPS, STOPS)],
                                                                engines=[mybir.EngineType.DVE],
                                                                min_val=0, max_val=NODE_TILES - 1)[1]

            def add(i, h, k, tile):
                g = i * DEPTH + h
                dve.wait_ge(summed, DEPTH + g + 1)
                dve.wait_ge(added, PER * (DEPTH + g) + k)
                to = acc[:, bass.ds(tile[h * PER + k], 1), :].rearrange("p a w -> p (a w)")
                dve.tensor_tensor(to, to, pa[:, h, k, 0:W + H], ALU.add).then_inc(added, 1)

            dve.sem_inc(rhs_ready, DEPTH)
            dve.sem_inc(added, PER * DEPTH)
            dve.memset(acc[:, :, :], 0.0).then_inc(cleared, 1)
            dve.wait_ge(loaded, 48)
            dve.wait_ge(cleared, 1)
            dve.tensor_scalar(rel[:, :], rel[:, :], -1.0, None, ALU.mult).then_inc(turned_round, 1)
            dve.tensor_copy(idx[:, :, :], src[:, 0:DEPTH * U].rearrange("p (d u) -> p d u", u=U)).then_inc(idx_ready, DEPTH)
            weigh(0, 0)
            weigh(0, 1)
            with dve.Fori(0, L.turns - 1) as i:
                tile = tiles_of(i)
                for h in range(DEPTH):
                    add(i, h, 0, tile)
                    weigh(i + (h + 2) // DEPTH, (h + 2) % DEPTH)
                    add(i, h, 1, tile)
            tile = tiles_of(L.turns - 1)
            for h in range(DEPTH):
                add(L.turns - 1, h, 0, tile)
                if h + 2 < DEPTH:
                    weigh(L.turns - 1, h + 2)
                add(L.turns - 1, h, 1, tile)

        @block.tensor
        def _(pe):
            pe.sem_inc(summed, DEPTH)
            with pe.Fori(0, L.turns) as i:
                for h in range(DEPTH):
                    g = i * DEPTH + h
                    pe.wait_ge(hot_ready, DEPTH + g + 1)
                    pe.wait_ge(rhs_ready, DEPTH + g + 1)
                    pe.wait_ge(added, PER * (g + 1))
                    for u in range(U):
                        mm = pe.matmul(pa[:, h, u // 2, 0:W + H], hot[:, h, u, :], rhs[:, h, u, :],
                                       start=(u % 2 == 0), stop=(u % 2 == 1))
                    mm.then_inc(summed, 1)


PAIRS = -(-TPC // 2)


def chunk_of(ap, c):
    return ap[bass.ds(c * ROWS, ROWS), :].rearrange("(t p) f -> p t f", p=P)


def over_tiles(ap, tiles=TPC):
    return ap.unsqueeze(1).broadcast_to((P, tiles, ap.shape[1]))


def split_in_three(dve, link, whole, parts):
    for k in range(2):
        link.done(dve.tensor_copy(parts[k], whole))
        link.done(dve.tensor_tensor(whole, whole, parts[k], ALU.subtract))
    return dve.tensor_copy(parts[2], whole)


def stage_l0_finish(nc, T, K, sums, places):
    H, W = 4, D
    with ExitStack() as ctx:
        s = Scope(nc, ctx, "e")
        n = Norm(s, turn=False)
        skips = s.sb("skips", [P, 2 * TPC, D])
        x0s = s.sb("x0s", [P, 2 * TPC, D])
        gates = s.sb("gates", [P, 3, D])
        w_skip = s.sb("w_skip", [P, D])
        w_rst = s.sb("w_rst", [P, D])
        gain = s.sb("gain", [P, D])
        shift = s.sb("shift", [P, D])
        slope = s.sb("slope", [P, 1])
        g_bias = s.sb("g_bias", [P, 1])
        rden = s.sb("rden", [P, TPC, H])
        rst = s.sb("rst", [P, TPC, D])
        t1 = s.sb("t1", [P, TPC, D])
        t2 = s.sb("t2", [P, TPC, D])
        z = s.sb("z", [P, TPC])
        gate = s.sb("gate", [P, TPC])
        outs = s.sb("outs", [P, 2 * TPC, D])
        params = s.sem("params")
        loaded = [s.sem("loaded0"), s.sem("loaded1")]
        z_ready = s.sem("z_ready")
        gate_ready = s.sem("gate_ready")
        out_ready = s.sem("out_ready")
        stored = s.sem("stored")
        scatter = Scatter(s, places, places.early + 10 * 16, HOP_TILES)
        block = ctx.enter_context(nc.Block())

        def slot(buffers, c):
            return buffers[:, bass.ds(c % 2 * TPC, TPC), :]

        @block.sync
        def _(sp):
            sp.dma_start(gates[:, :, :].rearrange("p a d -> p (a d)"), bcast_rows(T["L0_gnn_Wgate"].rearrange("a n -> (a n)"), P)
                         ).then_inc(params, 16)
            sp.dma_start(gain[:, :], bcast_rows(T["L0_gnn_ln_w"], P)).then_inc(params, 16)
            sp.dma_start(shift[:, :], bcast_rows(T["L0_gnn_ln_b"], P)).then_inc(params, 16)
            sp.dma_start(slope[:, :], bcast_rows(T["L0_gnn_prelu_a"], P)).then_inc(params, 16)
            sp.dma_start(g_bias[:, :], bcast_rows(T["L0_gnn_bgate"], P)).then_inc(params, 16)
            sp.sem_inc(out_ready, 1)
            sp.sem_inc(stored, 16)
            sp.dma_start(slot(skips, 0), chunk_of(T["l0_skip"], 0)).then_inc(loaded[0], 16)
            sp.dma_start(slot(x0s, 0), chunk_of(T["x0"], 0)).then_inc(loaded[0], 16)
            with sp.Fori(0, CHUNKS // 2) as i:
                for h in range(2):
                    c = 2 * i + h
                    sp.wait_ge(out_ready, c + 1)
                    sp.dma_start(slot(skips, c + 1), chunk_of(T["l0_skip"], c + 1)).then_inc(loaded[1 - h], 16)
                    sp.dma_start(slot(x0s, c + 1), chunk_of(T["x0"], c + 1)).then_inc(loaded[1 - h], 16)
                    sp.wait_ge(out_ready, c + 2)
                    sp.dma_start(chunk_of(T["x1"], c), slot(outs, c)).then_inc(stored, 16)
            sp.wait_ge(out_ready, CHUNKS + 1)
            sp.dma_start(chunk_of(T["x1"], CHUNKS - 1), slot(outs, CHUNKS - 1)).then_inc(stored, 16)
            sp.wait_ge(stored, 16 * (CHUNKS + 1))

        @block.gpsimd
        def _(pool):
            scatter.pool(pool, T)

        @block.vector
        def _(dve):
            link = Tally(dve, s.sem("dve"))
            dve.wait_ge(params, 80)
            dve.tensor_tensor(w_skip[:, :], gates[:, 0, :], gates[:, 2, :], ALU.add)
            link.done(dve.tensor_tensor(w_rst[:, :], gates[:, 1, :], gates[:, 2, :], ALU.subtract))
            def finish(c, h, turn):
                skip, x0, out = slot(skips, c), slot(x0s, c), slot(outs, c)
                acc = sums[:, bass.ds(c * TPC, TPC), :]
                dve.wait_ge(loaded[h], 32 * (turn + 1))
                link.done(dve.tensor_scalar(rden[:, :, :], acc[:, :, W:W + H], 1e-16, 0.5, ALU.add, ALU.max))
                link.done(dve.reciprocal(rden[:, :, :], rden[:, :, :]))
                dve.tensor_tensor(t1[:, :, :], skip, over_tiles(w_skip[:, :]), ALU.mult)
                link.done(dve.tensor_tensor(rst[:, :, :].rearrange("p t (h c) -> p t h c", h=H),
                                            acc[:, :, 0:W].rearrange("p t (h c) -> p t h c", h=H),
                                            rden[:, :, :].unsqueeze(3).broadcast_to((P, TPC, H, W // H)), ALU.mult))
                link.done(dve.tensor_tensor(t2[:, :, :], rst[:, :, :], over_tiles(w_rst[:, :]), ALU.mult))
                link.done(dve.tensor_tensor(t1[:, :, :], t1[:, :, :], t2[:, :, :], ALU.add))
                dve.tensor_reduce(z[:, :], t1[:, :, :], AX, ALU.add).then_inc(z_ready, 1)
                link.done(dve.tensor_tensor(t2[:, :, :], skip, rst[:, :, :], ALU.subtract))
                dve.wait_ge(gate_ready, c + 1)
                for t in range(TPC):
                    ins = dve.scalar_tensor_tensor(rst[:, t, :], t2[:, t, :], gate[:, t:t + 1], rst[:, t, :],
                                                   ALU.mult, ALU.add)
                link.done(ins)
                link.done(n.vector(dve, link, c, x=rst, out=t1))
                link.done(dve.tensor_tensor(t1[:, :, :], t1[:, :, :], over_tiles(gain[:, :]), ALU.mult))
                link.done(dve.tensor_tensor(t1[:, :, :], t1[:, :, :], over_tiles(shift[:, :]), ALU.add))
                dve.tensor_scalar(t2[:, :, :], t1[:, :, :], 0.0, slope[:, 0:1], ALU.min, ALU.mult)
                link.done(dve.scalar_tensor_tensor(rst[:, :, :].rearrange("p t d -> p (t d)"),
                                                   t1[:, :, :].rearrange("p t d -> p (t d)"), 0.0,
                                                   x0.rearrange("p t d -> p (t d)"), ALU.max, ALU.add))
                dve.wait_ge(stored, 16 * c)
                dve.tensor_tensor(out, rst[:, :, :], t2[:, :, :], ALU.add).then_inc(out_ready, 1)

            with dve.Fori(0, CHUNKS // 2) as i:
                link.loop(i, 2 * 13)
                for h in range(2):
                    finish(2 * i + h, h, i)
            link.leave(CHUNKS // 2)
            finish(CHUNKS - 1, 0, CHUNKS // 2)

        @block.scalar
        def _(act):
            with act.Fori(0, CHUNKS) as c:
                act.wait_ge(params, 80)
                act.wait_ge(z_ready, c + 1)
                act.activation(gate[:, :], z[:, :], ACT.Sigmoid, bias=g_bias[:, 0:1]).then_inc(gate_ready, 1)
                n.scalar(act, K, c)


def stage_hop_project(nc, T, K):
    H, E = 4, 4
    W = H * E
    with ExitStack() as ctx:
        s = Scope(nc, ctx, "h")
        n = Norm(s)
        w = s.sb("w", [P, 2, W])
        att = s.sb("att", [P, 2, W])
        row = s.sb("row", [P, TPC, W + H])
        t1 = s.sb("t1", [P, 2, TPC * H, E])
        to_dst = s.sb("to_dst", [P, NODE_TILES, H])
        ph = s.ps("ph", [P, 512])
        loaded = s.sem("loaded")
        projected = s.sem("projected")
        row_ready = s.sem("row_ready")
        dst_ready = s.sem("dst_ready")
        stored = s.sem("stored")
        block = ctx.enter_context(nc.Block())

        @block.sync
        def _(sp):
            n.load(sp, T["x1"], 0)
            sp.dma_start(w[:, :, :], T["L0_ffn_W_gat"].rearrange("(a p) n -> p a n", p=P)).then_inc(loaded, 16)
            for k, m in enumerate(("src", "dst")):
                sp.dma_start(att[:, k, :], bcast_rows(T["L0_ffn_att_" + m].rearrange("h e -> (h e)"), P)).then_inc(loaded, 16)
            with sp.Fori(0, CHUNKS) as c:
                sp.wait_ge(n.xn_ready, c + 1)
                n.load(sp, T["x1"], (c + 1) % CHUNKS)
                sp.wait_ge(row_ready, c + 1)
                sp.dma_start(chunk_of(T["f_table"], c), row[:, :, :]).then_inc(stored, 16)
            sp.wait_ge(dst_ready, CHUNKS)
            sp.dma_start(T["f_adst"], to_dst[:, :, :]).then_inc(stored, 16)
            sp.wait_ge(stored, 16 * (CHUNKS + 1))
            sp.wait_ge(n.x_loaded, 16 * (CHUNKS + 1))

        @block.vector
        def _(dve):
            link = Tally(dve, s.sem("dve"))
            dve.wait_ge(loaded, 48)

            def norm(c):
                dve.wait_ge(n.x_loaded, 16 * c + 16)
                dve.wait_ge(n.turned, c)
                n.vector(dve, link, c).then_inc(n.xn_ready, 1)

            def rows(c):
                dve.wait_ge(stored, 16 * c)
                dve.wait_ge(projected, c + 1)
                link.done(dve.tensor_copy(row[:, :, 0:W], ph[:, 0:TPC * W].rearrange("p (t w) -> p t w", w=W)))
                for k in range(2):
                    ins = dve.tensor_tensor(t1[:, k, :, :].rearrange("p (t h) e -> p t (h e)", t=TPC), row[:, :, 0:W],
                                            over_tiles(att[:, k, :]), ALU.mult)
                link.done(ins)
                dve.tensor_reduce(to_dst[:, bass.ds(c * TPC, TPC), :].rearrange("p t h -> p (t h)"), t1[:, 1, :, :],
                                  AX, ALU.add).then_inc(dst_ready, 1)
                dve.tensor_reduce(row[:, :, W:W + H], t1[:, 0, :, :].rearrange("p (t h) e -> p t h e", t=TPC), AX, ALU.add
                                  ).then_inc(row_ready, 1)

            norm(0)
            with dve.Fori(0, CHUNKS - 1) as c:
                link.loop(c, 4)
                norm(c + 1)
                rows(c)
            link.leave(CHUNKS - 1)
            rows(CHUNKS - 1)

        @block.scalar
        def _(act):
            with act.Fori(0, CHUNKS) as c:
                n.scalar(act, K, c)
                n.scalar_turned(act, c)

        @block.tensor
        def _(pe):
            pe.wait_ge(loaded, 48)
            with pe.Fori(0, CHUNKS) as c:
                n.tensor(pe, K, c)
                pe.wait_ge(n.xt_ready, c + 1)
                pe.wait_ge(row_ready, c)
                for t in range(TPC):
                    for f in range(2):
                        mm = pe.matmul(ph[:, t * W:(t + 1) * W], n.xt[:, f, t * P:(t + 1) * P], w[:, f, :],
                                       start=(f == 0), stop=(f == 1))
                mm.then_inc(projected, 1)


def stage_sources(nc, T, K, L):
    B = -(-L.tiles // P)
    FULL, REST = divmod(L.tiles, P)
    PER = L.tiles
    with ExitStack() as ctx:
        s = Scope(nc, ctx, "o")
        rows = s.sb("rows", [P, B, P], I32)
        rows_f = s.sb("rows_f", [P, B, P])
        flat = s.sb("flat", [P, PER], I32)
        lo = s.sb("lo", [P, PER])
        by_edge = s.sb("by_edge", [P, B * P], I32)
        hi_i = s.sb("hi_i", [P, B * P], I32)
        hi = s.sb("hi", [P, B * P])
        pt = s.ps("pt", [P, 2, 512])
        loaded = s.sem("loaded")
        cleared = s.sem("cleared")
        rows_ready = s.sem("rows_ready")
        turned = s.sem("turned")
        lo_ready = s.sem("lo_ready")
        by_edge_ready = s.sem("by_edge_ready")
        hi_ready = s.sem("hi_ready")
        stored = s.sem("stored")
        block = ctx.enter_context(nc.Block())
        by_tile = T[L.name + "_src"].rearrange("(t e) -> t e", e=P)

        @block.sync
        def _(sp):
            sp.dma_start(flat[:, :], T[L.name + "_src"].rearrange("(p n) -> p n", p=P)).then_inc(loaded, 16)
            sp.wait_ge(cleared, 1)
            sp.dma_start(rows[:, 0:FULL, :], by_tile[0:FULL * P, :].rearrange("(b t) e -> t b e", t=P)).then_inc(loaded, 16)
            sp.dma_start(rows[0:REST, FULL, :], by_tile[FULL * P:L.tiles, :]).then_inc(loaded, 16)
            sp.wait_ge(lo_ready, 1)
            sp.dma_start(T[L.name + "_lo_flat"].rearrange("(p n) -> p n", p=P), lo[:, :]).then_inc(stored, 16)
            sp.wait_ge(by_edge_ready, 1)
            sp.dma_start(T[L.name + "_src_by_edge"], by_edge[:, 0:L.tiles]).then_inc(stored, 16)
            sp.wait_ge(hi_ready, 1)
            sp.dma_start(T[L.name + "_hi_by_edge"], hi[:, 0:L.tiles]).then_inc(stored, 16)
            sp.wait_ge(stored, 48)

        @block.vector
        def _(dve):
            link = Tally(dve, s.sem("dve"))
            dve.memset(rows[:, FULL, :], 0).then_inc(cleared, 1)
            dve.wait_ge(loaded, 48)
            dve.tensor_copy(rows_f[:, :, :], rows[:, :, :]).then_inc(rows_ready, 1)
            link.done(dve.tensor_scalar(flat[:, :], flat[:, :], P - 1, None, ALU.bitwise_and))
            dve.tensor_copy(lo[:, :], flat[:, :]).then_inc(lo_ready, 1)
            dve.wait_ge(turned, 1)
            for k in range(2):
                w = min(512, B * P - k * 512)
                link.done(dve.tensor_copy(by_edge[:, k * 512:k * 512 + w], pt[:, k, 0:w]))
            dve.sem_inc(by_edge_ready, 1)
            link.done(dve.tensor_scalar(hi_i[:, :], by_edge[:, :], 7, None, ALU.arith_shift_right))
            dve.tensor_copy(hi[:, :], hi_i[:, :]).then_inc(hi_ready, 1)

        @block.tensor
        def _(pe):
            pe.wait_ge(rows_ready, 1)
            for b in range(B):
                mm = pe.transpose(pt[:, b // 4, (b % 4) * P:(b % 4 + 1) * P], rows_f[:, b, :], K["ident"][:, :])
            mm.then_inc(turned, 1)


def stage_l1_scores(nc, T, K, score):
    L, H, A = GRAPH, 8, 64
    G = 1
    M = U - G
    NT = NODE_TILES
    EDGE_TURNS = L.tiles // (U * DEPTH)
    assert EDGE_TURNS * U * DEPTH == L.tiles and EDGE_TURNS < L.turns
    BATCHES = EDGE_TURNS * DEPTH
    LAST_AT = (L.tiles - U) * P
    LAST_FULL, LAST_ODD = divmod(L.edges - LAST_AT, P)
    STOPS = DEPTH * U // 2
    REL, LO = U * P, G * P
    with ExitStack() as ctx:
        s = Scope(nc, ctx, "w" + L.name)
        src = s.sb("src", [P, L.tiles], I32)
        hi = s.sb("hi", [P, L.tiles])
        idx = s.sb("idx", [P, DEPTH, M], I32)
        got = s.sb("got", [P, DEPTH, M, H])
        spread = s.sb("spread", [P, DEPTH, REL + LO])
        apart = s.sb("apart", [P, DEPTH, REL + LO])
        hot = s.sb("hot", [P, DEPTH, REL + LO], BF16)
        hot_hi = s.sb("hot_hi", [P, 2, G, NT])
        by_hi = s.sb("by_hi", [P, G, H, NT])
        picked = s.sb("picked", [P, G, H])
        to_src = s.sb("to_src", [P, NT, H])
        src_parts = s.sb("src_parts", [P, 3, H, NT], BF16)
        to_dst = s.sb("to_dst", [P, NT, H])
        dst_parts = s.sb("dst_parts", [P, 3, NT, H], BF16)
        i_row = s.sb("i_row", [1, L.stops], I32)
        j_row = s.sb("j_row", [1, L.stops], I32)
        sums = s.sb("sums", [P, DEPTH, U * H])
        edge = s.sb("edge", [P, L.tiles, H])
        we = s.sb("we", [P, D])
        att = s.sb("att", [P, D])
        ve = s.sb("ve", [P, 2 * H])
        attr = s.sb("attr", [P, DEPTH, U, A])
        attr_t = s.sb("attr_t", [P, 2, U // 2, P])
        pt = s.ps("pt", [P, 2, 512])
        pd = s.ps("pd", [P, DEPTH, 512])
        ph = s.ps("ph", [P, 2, G, 512])
        loaded = s.sem("loaded")
        params = s.sem("params")
        spread_in = [s.sem(f"spread_in{h}") for h in range(DEPTH)]
        attr_in = [s.sem(f"attr_in{h}") for h in range(DEPTH)]
        got_in = [s.gather_sem(f"got_in{h}") for h in range(DEPTH)]
        idx_ready = s.sem("idx_ready")
        parts_ready = s.sem("parts_ready")
        apart_ready = s.sem("apart_ready")
        hot_ready = s.sem("hot_ready")
        hot_hi_ready = s.sem("hot_hi_ready")
        rows_out = s.sem("rows_out")
        masked = s.sem("masked")
        reduced = s.sem("reduced")
        edge_ready = s.sem("edge_ready")
        gathered = s.sem("gathered")
        steps_out = s.sem("steps_out")
        summed = s.sem("summed")
        scored = s.sem("scored")
        ve_ready = s.sem("ve_ready")
        cleared = s.sem("cleared")
        turned = s.sem("turned")
        turned_sb = s.sem("turned_sb")
        block = ctx.enter_context(nc.Block())
        rel_flat = T[L.name + "_rel_rows"].rearrange("s e -> (s e)")
        lo_rows = T[L.name + "_lo_flat"].rearrange("(g e) -> g e", e=REL)[:, M * P:REL]

        @block.sync
        def _(sp):
            sp.dma_start(src[:, :], T[L.name + "_src_by_edge"]).then_inc(loaded, 16)
            sp.dma_start(hi[:, :], T[L.name + "_hi_by_edge"]).then_inc(loaded, 16)
            for row, name in ((i_row, "_i_row"), (j_row, "_j_row")):
                sp.dma_start(row[:, :], T[L.name + name][0:L.stops].rearrange("(a s) -> a s", a=1)).then_inc(loaded, 16)
            sp.dma_start(to_dst[:, :, :], T["l1_adst"]).then_inc(loaded, 16)
            sp.dma_start(to_src[:, :, :], rows_of(T["l1_asrc"])).then_inc(loaded, 16)
            for k in range(2):
                sp.dma_start(we[k * A:(k + 1) * A, :], T["L1_gnn_W_e"]).then_inc(params, 16)
            sp.dma_start(att[:, :], bcast_rows(T["L1_gnn_att_edge"].rearrange("h c -> (h c)"), P)).then_inc(params, 16)

            def steps(g, h):
                sp.wait_ge(apart_ready, g + 1)
                sp.nop(nofuse=True)
                sp.dma_start(spread[:, h, 0:REL], rel_flat[bass.ds(g * REL, REL)].partition_broadcast(P)).then_inc(spread_in[h], 16)

            def batch(g, h):
                steps(g, h)
                sp.dma_start(spread[:, h, REL:REL + LO], lo_rows[bass.ds(g, 1), :].rearrange("a e -> (a e)").partition_broadcast(P)
                             ).then_inc(spread_in[h], 16)

            def attributes(at, n):
                return T["edge_attr_64"][bass.ds(at, n * P), :].rearrange("(u p) a -> p u a", p=P)

            def edges(g, h):
                sp.wait_ge(turned, g + 1)
                sp.dma_start(attr[:, h, :, :], attributes(g * (U * P), U)).then_inc(attr_in[h], 16)

            with sp.Fori(0, EDGE_TURNS - 1) as i:
                for h in range(DEPTH):
                    edges(i * DEPTH + h, h)
                    batch(i * DEPTH + h, h)
            for h in range(DEPTH - 1):
                edges(BATCHES - DEPTH + h, h)
                batch(BATCHES - DEPTH + h, h)
            sp.wait_ge(cleared, 1)
            if LAST_FULL:
                sp.dma_start(attr[:, DEPTH - 1, 0:LAST_FULL, :], attributes(LAST_AT, LAST_FULL)).then_inc(attr_in[DEPTH - 1], 16)
            if LAST_ODD:
                sp.dma_start(attr[0:LAST_ODD, DEPTH - 1, LAST_FULL, :], T["edge_attr_64"][L.edges - LAST_ODD:L.edges, :]
                             ).then_inc(attr_in[DEPTH - 1], 16)
            batch(BATCHES - 1, DEPTH - 1)
            with sp.Fori(EDGE_TURNS, L.turns) as i:
                for h in range(DEPTH):
                    steps(i * DEPTH + h, h)

        @block.gpsimd
        def _(pool):
            with pool.Fori(0, EDGE_TURNS) as i:
                for h in range(DEPTH):
                    g = i * DEPTH + h
                    pool.wait_ge(idx_ready, g + 1)
                    pool.wait_ge(gathered, g + 1)
                    pool.nop(nofuse=True)
                    for u in range(M):
                        pool.indirect_dma_start(out=got[:, h, u, :], out_offset=None, in_=T["l1_asrc"],
                                                in_offset=bass.IndirectOffsetOnAxis(ap=idx[:, h, u:u + 1], axis=0)
                                                ).then_inc(got_in[h], 16)

        @block.scalar
        def _(act):
            act.sem_inc(apart_ready, DEPTH)
            act.sem_inc(hot_ready, DEPTH)
            act.sem_inc(turned_sb, 2)

            def batch(g, h, spreads, edges):
                n = REL + LO if edges else REL
                act.wait_ge(spread_in[h], 16 * spreads)
                act.activation(apart[:, h, 0:n], spread[:, h, 0:n], ACT.Abs, bias=K["minus_col"][:, 0:1]).then_inc(apart_ready, 1)
                act.wait_ge(apart_ready, DEPTH + g + 1)
                act.wait_ge(steps_out, g + 1)
                act.activation(hot[:, h, 0:n], apart[:, h, 0:n], ACT.Relu, scale=-1.0, bias=K["ones"][:, 0:1]).then_inc(hot_ready, 1)
                if edges:
                    act.wait_ge(turned, DEPTH + g + 1)
                    act.activation(attr_t[:, h % 2, :, :], pt[:, h % 2, 0:U // 2 * P].rearrange("p (u e) -> p u e", e=P), ACT.Copy
                                   ).then_inc(turned_sb, 1)

            with act.Fori(0, EDGE_TURNS) as i:
                for h in range(DEPTH):
                    batch(i * DEPTH + h, h, 2 * (i + 1), True)
            with act.Fori(EDGE_TURNS, L.turns) as i:
                for h in range(DEPTH):
                    batch(i * DEPTH + h, h, i + 1 + EDGE_TURNS, False)

        @block.vector
        def _(dve):
            link = Tally(dve, s.sem("dve"))
            dve.sem_inc(gathered, DEPTH)
            dve.sem_inc(masked, 2)
            dve.sem_inc(scored, DEPTH)
            dve.wait_ge(loaded, 96)
            dve.tensor_copy(idx[:, :, :], src[:, 0:DEPTH * U].rearrange("p (d u) -> p d u", u=U)[:, :, 0:M]).then_inc(idx_ready, DEPTH)
            link.done(split_in_three(dve, link, to_src[:, :, :].rearrange("p t h -> p h t"), [src_parts[:, k, :, :] for k in range(3)]))
            link.done(split_in_three(dve, link, to_dst[:, :, :], [dst_parts[:, k, :, :] for k in range(3)]))
            dve.sem_inc(parts_ready, 1)
            link.done(dve.memset(ve[:, :], 0.0))
            dve.wait_ge(params, 48)
            link.done(dve.tensor_tensor(we[:, :], we[:, :], att[:, :], ALU.mult))
            for k in range(2):
                dve.tensor_reduce(ve[k * A:(k + 1) * A, k * H:(k + 1) * H],
                                  we[k * A:(k + 1) * A, :].rearrange("p (h c) -> p h c", h=H), AX, ALU.add).then_inc(ve_ready, 1)

            def mark(k, g):
                dve.tensor_tensor(hot_hi[:, k, :, :], K["frow"][:, 0:NT].unsqueeze(1).broadcast_to((P, G, NT)),
                                  hi[:, bass.ds(g * U + M, G)].unsqueeze(2).broadcast_to((P, G, NT)), ALU.is_equal
                                  ).then_inc(hot_hi_ready, 1)

            def pairs_of(i):
                return nc.values_load_multi_w_load_instructions(j_row[0:1, bass.ds(i * STOPS, STOPS)],
                                                                engines=[mybir.EngineType.DVE],
                                                                min_val=0, max_val=L.pairs - 1)[1]

            def of_edge(h):
                return pd[:, h, U * H:2 * U * H].rearrange("p (u h) -> p u h", h=H)

            def mask(g, h):
                dve.wait_ge(rows_out, g + 1)
                dve.wait_ge(hot_hi_ready, g + 1)
                dve.wait_ge(reduced, g)
                dve.tensor_tensor(by_hi[:, :, :, :], ph[:, h % 2, :, 0:H * NT].rearrange("p u (h c) -> p u h c", h=H),
                                  hot_hi[:, h % 2, :, :].unsqueeze(2).broadcast_to((P, G, H, NT)), ALU.mult).then_inc(masked, 1)
                mark((h + 1) % 2, (g + 1) % BATCHES)

            def take(i, h):
                g = i * DEPTH + h
                dve.wait_ge(got_in[h], 16 * M * (i + 1))
                dve.tensor_copy(idx[:, h, :], src[:, bass.ds((g + DEPTH) % BATCHES * U, M)]).then_inc(idx_ready, 1)
                dve.wait_ge(steps_out, 2 + g + 1)
                dve.tensor_tensor(edge[:, bass.ds(g * U, M), :], got[:, h, :, :], of_edge(h)[:, 0:M, :], ALU.add).then_inc(gathered, 1)
                dve.wait_ge(masked, 2 + g + 1)
                dve.wait_ge(edge_ready, g)
                dve.tensor_reduce(picked[:, :, :].rearrange("p u h -> p (u h)"),
                                  by_hi[:, :, :, :].rearrange("p u h c -> p (u h) c"), AX, ALU.add).then_inc(reduced, 1)

            def finish(g, h):
                dve.wait_ge(reduced, g + 1)
                dve.tensor_tensor(edge[:, bass.ds(g * U + M, G), :], picked[:, :, :], of_edge(h)[:, M:U, :], ALU.add
                                  ).then_inc(edge_ready, 1)

            def add(g, h, pair, tiles_done):
                dve.wait_ge(edge_ready, tiles_done)
                dve.wait_ge(steps_out, 2 + g + 1)
                for k in range(U // 2):
                    dve.tensor_tensor(sums[:, h, k * 2 * H:(k + 1) * 2 * H], pd[:, h, k * 2 * H:(k + 1) * 2 * H],
                                      edge[:, bass.ds(pair[h * U // 2 + k] * 2, 2), :].rearrange("p a h -> p (a h)"),
                                      ALU.add).then_inc(summed, 1)

            def relu(g, h):
                dve.wait_ge(summed, U // 2 * (g + 1))
                dve.scalar_tensor_tensor(score[:, bass.ds(g * U, U), :].rearrange("p u h -> p (u h)"), sums[:, h, :], 0.2,
                                         sums[:, h, :], ALU.mult, ALU.max).then_inc(scored, 1)

            def batch(i, h, pair, more=True):
                g, ahead = i * DEPTH + h, (h + 1) % DEPTH
                add(g, h, pair, g + 1)
                take(i + (h + 1) // DEPTH, ahead)
                relu(g, h)
                finish(g + 1, ahead)
                if more:
                    mask(g + 2, (h + 2) % DEPTH)

            mark(0, 0)
            mask(0, 0)
            take(0, 0)
            finish(0, 0)
            mask(1, 1)
            with dve.Fori(0, EDGE_TURNS - 1) as i:
                pair = pairs_of(i)
                for h in range(DEPTH):
                    batch(i, h, pair)
            dve.wait_ge(turned, BATCHES)
            dve.memset(attr[:, DEPTH - 1, :, :], 0.0).then_inc(cleared, 1)
            pair = pairs_of(EDGE_TURNS - 1)
            for h in range(DEPTH - 1):
                batch(EDGE_TURNS - 1, h, pair, h + 2 < DEPTH)
            add(BATCHES - 1, DEPTH - 1, pair, BATCHES)
            relu(BATCHES - 1, DEPTH - 1)
            with dve.Fori(EDGE_TURNS, L.turns) as i:
                pair = pairs_of(i)
                for h in range(DEPTH):
                    g = i * DEPTH + h
                    add(g, h, pair, BATCHES)
                    relu(g, h)

        @block.tensor
        def _(pe):
            pe.sem_inc(turned, DEPTH)
            pe.sem_inc(steps_out, 2)
            pe.wait_ge(loaded, 96)
            pe.wait_ge(parts_ready, 1)
            pe.wait_ge(ve_ready, 2)

            def tiles_of(i):
                return nc.values_load_multi_w_load_instructions(i_row[0:1, bass.ds(i * STOPS, STOPS)], engines=[mybir.EngineType.PE],
                                                                min_val=0, max_val=NODE_TILES - 1)[1]

            def turn(g, h, attributes_in):
                pe.wait_ge(attr_in[h], attributes_in)
                pe.wait_ge(turned_sb, g + 1)
                for k in range(U // 2):
                    mm = pe.transpose(pt[:, h % 2, k * P:(k + 1) * P], attr[:, h, 2 * k:2 * k + 2, :].rearrange("p u a -> p (u a)"),
                                      K["ident"][:, :])
                mm.then_inc(turned, 1)

            def rows(g, h):
                pe.wait_ge(hot_ready, DEPTH + g + 1)
                pe.wait_ge(masked, g + 1)
                for u in range(G):
                    for k in range(3):
                        mm = pe.matmul(ph[:, h % 2, u, 0:H * NT], hot[:, h, REL + u * P:REL + (u + 1) * P],
                                       src_parts[:, k, :, :].rearrange("p h t -> p (h t)"), start=(k == 0), stop=(k == 2))
                mm.then_inc(rows_out, 1)

            def steps(g, h, tile, edges):
                pe.wait_ge(hot_ready, DEPTH + g + 1)
                pe.wait_ge(scored, g + 1)
                for u in range(U):
                    for k in range(3):
                        mm = pe.matmul(pd[:, h, u * H:(u + 1) * H], hot[:, h, u * P:(u + 1) * P],
                                       dst_parts[:, k, bass.ds(tile[(h * U + u) // 2], 1), :], start=(k == 0), stop=(k == 2))
                if edges:
                    pe.wait_ge(turned_sb, 2 + g + 1)
                    for k in range(U // 2):
                        at = U * H + k * 2 * H
                        mm = pe.matmul(pd[:, h, at:at + 2 * H], attr_t[:, h % 2, k, :], ve[:, :], start=True, stop=True)
                mm.then_inc(steps_out, 1)

            turn(0, 0, 16)
            with pe.Fori(0, EDGE_TURNS - 1) as i:
                for h in range(DEPTH):
                    g = i * DEPTH + h
                    rows(g, h)
                    turn(g + 1, (h + 1) % DEPTH, 16 * (i + 1 + (h + 1) // DEPTH))
                    if h == 0:
                        tile = tiles_of(i)
                    steps(g, h, tile, True)
            tile = tiles_of(EDGE_TURNS - 1)
            for h in range(DEPTH):
                g = BATCHES - DEPTH + h
                rows(g, h)
                if h < DEPTH - 1:
                    loads = (1, (LAST_FULL > 0) + (LAST_ODD > 0))[h == DEPTH - 2]
                    turn(g + 1, h + 1, 16 * (EDGE_TURNS - 1 + loads))
                steps(g, h, tile, True)
            with pe.Fori(EDGE_TURNS, L.turns) as i:
                tile = tiles_of(i)
                for h in range(DEPTH):
                    steps(i * DEPTH + h, h, tile, False)


def stage_hop_sum(nc, T, K, weight, rows, acc):
    L, H, W = HOP, 4, 16
    C = W // H
    Q = W + H
    PER = U // 2
    STOPS = DEPTH * PER
    with ExitStack() as ctx:
        s = Scope(nc, ctx, "af")
        rel = s.sb("rel", [P, L.steps])
        minus_rel = s.sb("minus_rel", [P, L.steps])
        apart = s.sb("apart", [P, DEPTH // 2, U, P])
        i_row = s.sb("i_row", [1, L.stops], I32)
        parts = s.sb("parts", [P, L.steps, 3, Q], BF16)
        hot = s.sb("hot", [P, DEPTH, U, P], BF16)
        acc3 = s.sb("acc3", [P, NODE_TILES, 3 * Q])
        pa = s.ps("pa", [P, DEPTH, 512])
        loaded = s.sem("loaded")
        parts_ready = s.sem("parts_ready")
        rel_ready = s.sem("rel_ready")
        apart_ready = s.sem("apart_ready")
        hot_ready = [s.sem("hot_ready0"), s.sem("hot_ready1")]
        summed = s.sem("summed")
        added = s.sem("added")
        block = ctx.enter_context(nc.Block())

        @block.sync
        def _(sp):
            sp.dma_start(rel[:, :], T[L.name + "_rel_t"]).then_inc(loaded, 16)
            sp.dma_start(i_row[:, :], T[L.name + "_i_row"][0:L.stops].rearrange("(a s) -> a s", a=1)).then_inc(loaded, 16)

        @block.scalar
        def _(act):
            act.wait_ge(rel_ready, 1)
            with act.Fori(0, L.turns) as i:
                for h in range(1, DEPTH, 2):
                    g = i * DEPTH + h
                    b = h // 2
                    act.wait_ge(summed, g + 1)
                    for u in range(U):
                        act.activation(apart[:, b, u, :], K["frow"][:, :], ACT.Abs, bias=minus_rel[:, bass.ds(g * U + u, 1)]
                                       ).then_inc(apart_ready, 1)
                    act.wait_ge(apart_ready, U * (i * DEPTH // 2 + b + 1))
                    act.activation(hot[:, h, :, :], apart[:, b, :, :], ACT.Relu, scale=-1.0, bias=K["ones"][:, 0:1]
                                   ).then_inc(hot_ready[1], 1)

        @block.vector
        def _(dve):
            link = Tally(dve, s.sem("dve"))
            dve.sem_inc(added, PER * DEPTH)
            dve.wait_ge(loaded, 32)
            dve.tensor_scalar(minus_rel[:, :], rel[:, :], -1.0, None, ALU.mult).then_inc(rel_ready, 1)
            link.done(dve.memset(acc3[:, :, :], 0.0))
            link.done(dve.tensor_tensor(rows[:, :, :].rearrange("p s (h c) -> p s h c", h=H),
                                        rows[:, :, :].rearrange("p s (h c) -> p s h c", h=H),
                                        weight[:, :, :].unsqueeze(3).broadcast_to((P, L.steps, H, C)), ALU.mult))
            link.done(split_in_three(dve, link, rows[:, :, :], [parts[:, :, k, 0:W] for k in range(3)]))
            split_in_three(dve, link, weight[:, :, :], [parts[:, :, k, W:Q] for k in range(3)]).then_inc(parts_ready, 1)

            def make_hot(i, h):
                g = i * DEPTH + h
                dve.wait_ge(summed, g + 1)
                dve.tensor_tensor(hot[:, h, :, :], K["frow"][:, :].unsqueeze(1).broadcast_to((P, U, P)),
                                  rel[:, bass.ds(g * U, U)].unsqueeze(2).broadcast_to((P, U, P)), ALU.is_equal
                                  ).then_inc(hot_ready[0], 1)

            make_hot(0, 0)
            make_hot(0, 2)
            with dve.Fori(0, L.turns) as i:
                _, tile = nc.values_load_multi_w_load_instructions(i_row[0:1, bass.ds(i * STOPS, STOPS)],
                                                                   engines=[mybir.EngineType.DVE], min_val=0, max_val=NODE_TILES - 1)
                for h in range(DEPTH):
                    g = i * DEPTH + h
                    dve.wait_ge(summed, DEPTH + g + 1)
                    for k in range(PER):
                        dve.wait_ge(added, PER * (DEPTH + g) + k)
                        to = acc3[:, bass.ds(tile[h * PER + k], 1), :].rearrange("p a w -> p (a w)")
                        dve.tensor_tensor(to, to, pa[:, h, k * 3 * Q:(k + 1) * 3 * Q], ALU.add).then_inc(added, 1)
                        if k == 0 and h % 2 == 1:
                            make_hot((i + 1) % L.turns, h - 1)
            dve.wait_ge(added, PER * (DEPTH + L.turns * DEPTH))
            dve.tensor_reduce(acc[:, :, :], acc3[:, :, :].rearrange("p t (k q) -> p t q k", k=3), AX, ALU.add)

        @block.tensor
        def _(pe):
            pe.sem_inc(summed, DEPTH)
            pe.wait_ge(parts_ready, 1)
            with pe.Fori(0, L.turns) as i:
                for h in range(DEPTH):
                    g = i * DEPTH + h
                    pe.wait_ge(hot_ready[h % 2], i * DEPTH // 2 + h // 2 + 1)
                    pe.wait_ge(added, PER * (g + 1))
                    for u in range(U):
                        k = u // 2
                        mm = pe.matmul(pa[:, h, k * 3 * Q:(k + 1) * 3 * Q], hot[:, h, u, :],
                                       parts[:, bass.ds(g * U + u, 1), :, :].rearrange("p a k q -> p (a k q)"),
                                       start=(u % 2 == 0), stop=(u % 2 == 1))
                    mm.then_inc(summed, 1)


def stage_hop_gate(nc, T, K, acc):
    H, E, NT = 4, 4, NODE_TILES
    W = H * E
    with ExitStack() as ctx:
        s = Scope(nc, ctx, "r")
        rows = s.sb("rows", [P, 3, W])
        rden = s.sb("rden", [P, NT, H])
        a = s.sb("a", [P, NT, W])
        b = s.sb("b", [P, NT, W])
        m = s.sb("m", [P, NT])
        v = s.sb("v", [P, NT])
        sd = s.sb("sd", [P, NT])
        rs = s.sb("rs", [P, NT])
        sc = s.sb("sc", [P, NT, E])
        order = s.sb("order", [P, E])
        best = s.sb("best", [P, 2, NT])
        at = s.sb("at", [P, NT, E])
        first = s.sb("first", [P, NT])
        one = s.sb("one", [P, 2, NT, E])
        ex = s.sb("ex", [P, NT])
        ws = s.sb("ws", [P, 2, NT])
        gate = s.sb("gate", [P, NT, E])
        loaded = s.sem("loaded")
        var_ready = s.sem("var_ready")
        sd_ready = s.sem("sd_ready")
        diff_ready = s.sem("diff_ready")
        ex_ready = s.sem("ex_ready")
        gate_ready = s.sem("gate_ready")
        stored = s.sem("stored")
        block = ctx.enter_context(nc.Block())

        def per_tile(ap, n):
            return ap.unsqueeze(2).broadcast_to((P, NT, n))

        @block.sync
        def _(sp):
            for k, name in enumerate(("b_gat", "ln_gamma", "ln_beta")):
                sp.dma_start(rows[:, k, :], bcast_rows(T["L0_ffn_" + name], P)).then_inc(loaded, 16)
            sp.wait_ge(gate_ready, 1)
            sp.dma_start(T["f_gate"], gate[:, :, :]).then_inc(stored, 16)
            sp.wait_ge(stored, 16)

        @block.vector
        def _(dve):
            link = Tally(dve, s.sem("dve"))
            dve.wait_ge(loaded, 48)
            link.done(dve.tensor_scalar(rden[:, :, :], acc[:, :, W:W + H], 1e-16, 0.5, ALU.add, ALU.max))
            link.done(dve.reciprocal(rden[:, :, :], rden[:, :, :]))
            link.done(dve.tensor_tensor(a[:, :, :].rearrange("p t (h c) -> p t h c", h=H),
                                        acc[:, :, 0:W].rearrange("p t (h c) -> p t h c", h=H),
                                        rden[:, :, :].unsqueeze(3).broadcast_to((P, NT, H, E)), ALU.mult))
            link.done(dve.tensor_tensor(a[:, :, :], a[:, :, :], over_tiles(rows[:, 0, :], NT), ALU.add))
            link.done(dve.tensor_reduce(m[:, :], a[:, :, :], AX, ALU.add))
            link.done(dve.tensor_scalar(m[:, :], m[:, :], 1.0 / W, None, ALU.mult))
            link.done(dve.tensor_tensor(a[:, :, :], a[:, :, :], per_tile(m[:, :], W), ALU.subtract))
            link.done(dve.tensor_tensor(b[:, :, :], a[:, :, :], a[:, :, :], ALU.mult))
            link.done(dve.tensor_reduce(v[:, :], b[:, :, :], AX, ALU.add))
            link.done(dve.tensor_scalar(v[:, :], v[:, :], 1.0 / W, EPS, ALU.mult, ALU.add))
            dve.sem_inc(var_ready, 1)
            dve.wait_ge(sd_ready, 1)
            link.done(dve.reciprocal(rs[:, :], sd[:, :]))
            link.done(dve.tensor_tensor(a[:, :, :], a[:, :, :], per_tile(rs[:, :], W), ALU.mult))
            link.done(dve.tensor_tensor(a[:, :, :], a[:, :, :], over_tiles(rows[:, 1, :], NT), ALU.mult))
            link.done(dve.tensor_tensor(a[:, :, :], a[:, :, :], over_tiles(rows[:, 2, :], NT), ALU.add))
            link.done(dve.tensor_reduce(sc[:, :, :], a[:, :, :].rearrange("p t (h e) -> p t e h", h=H), AX, ALU.add))
            link.done(dve.tensor_scalar(sc[:, :, :], sc[:, :, :], 1.0 / H, None, ALU.mult))
            dve.tensor_copy(order[:, :], K["frow"][:, 0:E])
            for k in range(2):
                link.done(dve.tensor_reduce(best[:, k, :], sc[:, :, :], AX, ALU.max))
                link.done(dve.tensor_tensor(at[:, :, :], sc[:, :, :], per_tile(best[:, k, :], E), ALU.is_lt))
                link.done(dve.scalar_tensor_tensor(at[:, :, :], at[:, :, :], float(E), over_tiles(order[:, :], NT),
                                                   ALU.mult, ALU.add))
                link.done(dve.tensor_reduce(first[:, :], at[:, :, :], AX, ALU.min))
                link.done(dve.tensor_tensor(one[:, k, :, :], over_tiles(order[:, :], NT), per_tile(first[:, :], E),
                                            ALU.is_equal))
                if k == 0:
                    link.done(dve.scalar_tensor_tensor(sc[:, :, :], one[:, 0, :, :], -BIG, sc[:, :, :], ALU.mult, ALU.add))
            link.done(dve.tensor_tensor(m[:, :], best[:, 1, :], best[:, 0, :], ALU.subtract))
            dve.sem_inc(diff_ready, 1)
            dve.wait_ge(ex_ready, 1)
            link.done(dve.tensor_scalar(v[:, :], ex[:, :], 1.0, None, ALU.add))
            link.done(dve.reciprocal(ws[:, 0, :], v[:, :]))
            link.done(dve.tensor_tensor(ws[:, 1, :], ws[:, 0, :], ex[:, :], ALU.mult))
            for k in range(2):
                ins = dve.tensor_tensor(one[:, k, :, :], one[:, k, :, :], per_tile(ws[:, k, :], E), ALU.mult)
            link.done(ins)
            dve.tensor_tensor(gate[:, :, :], one[:, 0, :, :], one[:, 1, :, :], ALU.add).then_inc(gate_ready, 1)

        @block.scalar
        def _(act):
            act.wait_ge(var_ready, 1)
            act.activation(sd[:, :], v[:, :], ACT.Sqrt).then_inc(sd_ready, 1)
            act.wait_ge(diff_ready, 1)
            act.activation(ex[:, :], m[:, :], ACT.Exp).then_inc(ex_ready, 1)


def stage_hop_scores_and_experts(nc, T, K, score, kept):
    L, H, W, KEEP = HOP, 4, 20, 16
    E, F = 4, 2 * D
    FC = F // P
    STOPS = DEPTH * U // 2
    SLOTS = L.turns * DEPTH // CHUNKS
    assert SLOTS * CHUNKS == L.turns * DEPTH and SLOTS % DEPTH == 0
    order = [("up", 0, f) for f in range(FC)]
    for e in range(1, E):
        for f in range(FC):
            order += [("up", e, f), ("down", e - 1, f)]
    order += [("norm", 0, 0)] + [("down", E - 1, b) for b in range(PAIRS)]
    pieces = [[] for _ in range(SLOTS)]
    for i, piece in enumerate(order):
        pieces[i * SLOTS // len(order)].append(piece)
    with ExitStack() as ctx:
        s = Scope(nc, ctx, "t")
        src = s.sb("src", [P, L.steps], I32)
        idx = s.sb("idx", [P, DEPTH, U], I32)
        got = s.sb("got", [P, DEPTH, U, W])
        spread = s.sb("spread", [P, DEPTH, U * P])
        hot = s.sb("hot", [P, DEPTH, U * P], BF16)
        to_dst = s.sb("to_dst", [P, NODE_TILES, H])
        dst_parts = s.sb("dst_parts", [P, NODE_TILES, 3 * H], BF16)
        from_dst = s.sb("from_dst", [P, DEPTH, U * H])
        i_row = s.sb("i_row", [1, L.stops], I32)
        sums = s.sb("sums", [P, DEPTH, U * H])
        n = Norm(s, turn=False)
        xt = s.sb("xt", [P, 2, ROWS])
        w1 = s.sb("w1", [P, E, 2, F])
        w2 = s.sb("w2", [P, E, FC, D])
        b1r = s.sb("b1r", [E * FC, P])
        b1 = s.sb("b1", [P, E * FC])
        b2 = s.sb("b2", [P, E, D])
        hid = s.sb("hid", [P, 2, FC, ROWS])
        y = s.sb("y", [P, 2, TPC, D])
        ph = s.ps("ph", [P, 2, 2, 512])
        po = s.ps("po", [P, 2, 2, D])
        pd = s.ps("pd", [P, 2, 512])
        loaded = s.sem("loaded")
        spread_in = [s.sem(f"spread_in{h}") for h in range(DEPTH)]
        got_in = [s.gather_sem(f"got_in{h}") for h in range(DEPTH)]
        idx_ready = s.sem("idx_ready")
        apart_ready = s.sem("apart_ready")
        hot_ready = s.sem("hot_ready")
        parts_ready = s.sem("parts_ready")
        dst_out = s.sem("dst_out")
        dst_taken = s.sem("dst_taken")
        summed = s.sem("summed")
        scored = s.sem("scored")
        turned = s.sem("turned")
        xt_ready = s.sem("xt_ready")
        b1_turned = s.sem("b1_turned")
        b1_ready = s.sem("b1_ready")
        up = s.sem("up")
        hid_ready = s.sem("hid_ready")
        down = s.sem("down")
        y_taken = s.sem("y_taken")
        y_stored = [s.sem("y_stored0"), s.sem("y_stored1")]
        block = ctx.enter_context(nc.Block())
        rel_flat = T[L.name + "_rel_rows"].rearrange("s e -> (s e)")

        @block.sync
        def _(sp):
            n.load(sp, T["x1"], 0)
            sp.dma_start(b1r[:, :], T["L0_ffn_b1"].rearrange("e (a p) -> (e a) p", p=P)).then_inc(loaded, 16)
            sp.dma_start(src[:, :], T[L.name + "_src_t"]).then_inc(loaded, 16)
            sp.dma_start(i_row[:, :], T[L.name + "_i_row"][0:L.stops].rearrange("(a s) -> a s", a=1)).then_inc(loaded, 16)
            sp.dma_start(to_dst[:, :, :], T["f_adst"]).then_inc(loaded, 16)
            for e in range(E):
                sp.dma_start(w1[:, e, :, :], T["L0_ffn_W1"][e].rearrange("(a p) f -> p a f", p=P)).then_inc(loaded, 16)
                sp.dma_start(w2[:, e, :, :], T["L0_ffn_W2"][e].rearrange("(a p) d -> p a d", p=P)).then_inc(loaded, 16)
                sp.dma_start(b2[:, e, :], bcast_rows(T["L0_ffn_b2"][e], P)).then_inc(loaded, 16)
            with sp.Fori(0, CHUNKS) as c:
                for k in range(SLOTS):
                    g, h = c * SLOTS + k, k % DEPTH
                    sp.wait_ge(hot_ready, g + 1)
                    sp.dma_start(spread[:, h, :], rel_flat[bass.ds(g * U * P, U * P)].partition_broadcast(P)
                                 ).then_inc(spread_in[h], 16)
                    if k == 1:
                        sp.wait_ge(n.xn_ready, c + 1)
                        n.load(sp, T["x1"], (c + 1) % CHUNKS)
                    for kind, e, b in (pieces[k - 1] if k else []):
                        if kind == "down" and b == PAIRS - 1:
                            sp.wait_ge(y_taken, 2 + (c * E + e + 1) * PAIRS)
                            sp.dma_start(chunk_of(T["f_experts"][e], c), y[:, e % 2, :, :]).then_inc(y_stored[e % 2], 16)
                sp.wait_ge(y_taken, 2 + (c + 1) * E * PAIRS)
                sp.dma_start(chunk_of(T["f_experts"][E - 1], c), y[:, (E - 1) % 2, :, :]).then_inc(y_stored[(E - 1) % 2], 16)
            for h in range(2):
                sp.wait_ge(y_stored[h], 16 * CHUNKS * E // 2)
            sp.wait_ge(n.x_loaded, 16 * (CHUNKS + 1))

        @block.gpsimd
        def _(pool):
            with pool.Fori(0, L.turns) as i:
                for h in range(DEPTH):
                    g = i * DEPTH + h
                    pool.wait_ge(idx_ready, g + 1)
                    pool.wait_ge(summed, g + 1)
                    pool.nop(nofuse=True)
                    for u in range(U):
                        pool.indirect_dma_start(out=got[:, h, u, :], out_offset=None, in_=T["f_table"],
                                                in_offset=bass.IndirectOffsetOnAxis(ap=idx[:, h, u:u + 1], axis=0)
                                                ).then_inc(got_in[h], 16)

        @block.scalar
        def _(act):
            def turn(c):
                act.wait_ge(turned, c + 1)
                for f in range(2):
                    for h in range(2):
                        w = min(512, ROWS - h * 512)
                        ins = act.activation(xt[:, f, h * 512:h * 512 + w], ph[:, f, h, 0:w], ACT.Copy)
                ins.then_inc(xt_ready, 1)

            act.sem_inc(apart_ready, DEPTH)
            act.sem_inc(hot_ready, DEPTH)
            act.wait_ge(b1_turned, 1)
            act.activation(b1[:, :], ph[:, 0, 0, 0:E * FC], ACT.Copy).then_inc(b1_ready, 1)
            act.wait_ge(b1_ready, 1)
            act.sem_inc(hid_ready, 2)
            n.scalar(act, K, 0)
            turn(0)
            with act.Fori(0, CHUNKS) as c:
                for k in range(SLOTS):
                    g, h = c * SLOTS + k, k % DEPTH
                    act.wait_ge(spread_in[h], 16 * (c * (SLOTS // DEPTH) + k // DEPTH + 1))
                    act.activation(spread[:, h, :], spread[:, h, :], ACT.Abs, bias=K["minus_col"][:, 0:1]).then_inc(apart_ready, 1)
                    act.wait_ge(apart_ready, DEPTH + g + 1)
                    act.wait_ge(dst_out, g + 1)
                    act.activation(hot[:, h, :], spread[:, h, :], ACT.Relu, scale=-1.0, bias=K["ones"][:, 0:1]).then_inc(hot_ready, 1)
                    if k == SLOTS // 2:
                        n.scalar(act, K, c + 1)
                    for kind, e, f in pieces[k]:
                        if kind == "up":
                            act.wait_ge(up, (c * E + e) * FC + f + 1)
                            act.activation(hid[:, e % 2, f, :].rearrange("p (h r) -> p h r", h=2), ph[:, f % 2, :, 0:HALF], ACT.Gelu,
                                           bias=b1[:, e * FC + f:e * FC + f + 1]).then_inc(hid_ready, 1)
                        elif kind == "norm":
                            turn(c + 1)

        @block.vector
        def _(dve):
            link = Tally(dve, s.sem("dve"))
            dve.sem_inc(summed, DEPTH)
            dve.sem_inc(y_taken, 2)
            dve.wait_ge(n.x_loaded, 16)
            n.vector(dve, link, 0).then_inc(n.xn_ready, 1)
            dve.wait_ge(loaded, 16 * (4 + 3 * E))
            link.done(split_in_three(dve, link, to_dst[:, :, :], [dst_parts[:, :, k * H:(k + 1) * H] for k in range(3)]))
            dve.sem_inc(parts_ready, 1)
            dve.sem_inc(dst_taken, 2)
            dve.tensor_copy(idx[:, :, :], src[:, 0:DEPTH * U].rearrange("p (d u) -> p d u", u=U)).then_inc(idx_ready, DEPTH)
            with dve.Fori(0, CHUNKS) as c:
                link.loop(c, 2)
                for k in range(SLOTS):
                    g, h = c * SLOTS + k, k % DEPTH
                    if k == SLOTS // 2:
                        dve.wait_ge(n.x_loaded, 16 * (c + 2))
                        dve.wait_ge(turned, c + 1)
                        n.vector(dve, link, c + 1).then_inc(n.xn_ready, 1)
                    for kind, e, b in pieces[k]:
                        if kind == "down":
                            if b == 0:
                                dve.wait_ge(y_stored[e % 2], 16 * (c * E // 2 + e // 2))
                            dve.wait_ge(down, (c * E + e) * PAIRS + b + 1)
                            m = min(2, TPC - 2 * b)
                            dve.tensor_tensor(y[:, e % 2, 2 * b:2 * b + m, :], po[:, b % 2, 0:m, :], over_tiles(b2[:, e, :], m),
                                              ALU.add).then_inc(y_taken, 1)
                    dve.wait_ge(got_in[h], 16 * U * (c * (SLOTS // DEPTH) + k // DEPTH + 1))
                    dve.tensor_copy(idx[:, h, :], src[:, bass.ds((g + DEPTH) % (L.turns * DEPTH) * U, U)]).then_inc(idx_ready, 1)
                    dve.wait_ge(dst_out, DEPTH + g + 1)
                    dve.tensor_copy(kept[:, bass.ds(g * U, U), :], got[:, h, :, 0:KEEP])
                    dve.tensor_reduce(from_dst[:, h, :], pd[:, h % 2, 0:U * 3 * H].rearrange("p (u k h) -> p u h k", k=3, h=H), AX,
                                      ALU.add).then_inc(dst_taken, 1)
                    dve.wait_ge(dst_taken, 2 + g + 1)
                    dve.tensor_tensor(sums[:, h, :].rearrange("p (u h) -> p u h", h=H), got[:, h, :, KEEP:W],
                                      from_dst[:, h, :].rearrange("p (u h) -> p u h", h=H), ALU.add).then_inc(summed, 1)
                    dve.wait_ge(summed, DEPTH + g + 1)
                    dve.scalar_tensor_tensor(score[:, bass.ds(g * U, U), :].rearrange("p u h -> p (u h)"), sums[:, h, :], 0.2,
                                             sums[:, h, :], ALU.mult, ALU.max).then_inc(scored, 1)
            link.leave(CHUNKS)

        @block.tensor
        def _(pe):
            def turn(c):
                pe.wait_ge(n.xn_ready, c + 1)
                for f in range(2):
                    for t in range(TPC):
                        mm = pe.transpose(ph[:, f, t // 4, (t % 4) * P:(t % 4 + 1) * P], n.xn[:, t, f * P:(f + 1) * P], K["ident"][:, :])
                mm.then_inc(turned, 1)

            pe.sem_inc(dst_out, DEPTH)
            pe.wait_ge(loaded, 16 * (4 + 3 * E))
            pe.transpose(ph[:, 0, 0, 0:E * FC], b1r[:, :], K["ident"][0:E * FC, 0:E * FC]).then_inc(b1_turned, 1)
            pe.wait_ge(b1_ready, 1)
            turn(0)
            pe.wait_ge(parts_ready, 1)
            with pe.Fori(0, CHUNKS) as c:
                pe.wait_ge(xt_ready, c + 1)
                for k in range(SLOTS):
                    g, h = c * SLOTS + k, k % DEPTH
                    if h == 0:
                        _, tile = nc.values_load_multi_w_load_instructions(
                            i_row[0:1, bass.ds((c * (SLOTS // DEPTH) + k // DEPTH) * STOPS, STOPS)],
                            engines=[mybir.EngineType.PE], min_val=0, max_val=NODE_TILES - 1)
                    for kind, e, f in pieces[k]:
                        if kind == "up":
                            pe.wait_ge(hid_ready, (c * E + e) * FC + f + 1)
                            for a in range(2):
                                for half in range(2):
                                    mm = pe.matmul(ph[:, f % 2, half, 0:HALF], w1[:, e, a, f * P:(f + 1) * P],
                                                   xt[:, a, half * HALF:(half + 1) * HALF], start=(a == 0), stop=(a == 1))
                            mm.then_inc(up, 1)
                        elif kind == "down":
                            pe.wait_ge(hid_ready, 2 + (c * E + e + 1) * FC)
                            pe.wait_ge(y_taken, (c * E + e) * PAIRS + f + 1)
                            for t in range(2 * f, min(2 * f + 2, TPC)):
                                for a in range(FC):
                                    mm = pe.matmul(po[:, f % 2, t % 2, :], hid[:, e % 2, a, t * P:(t + 1) * P], w2[:, e, a, :],
                                                   start=(a == 0), stop=(a == FC - 1))
                            mm.then_inc(down, 1)
                        else:
                            pe.wait_ge(hid_ready, 2 + (c + 1) * E * FC)
                            turn(c + 1)
                    pe.wait_ge(hot_ready, DEPTH + g + 1)
                    pe.wait_ge(dst_taken, g + 1)
                    for u in range(U):
                        mm = pe.matmul(pd[:, h % 2, u * 3 * H:(u + 1) * 3 * H], hot[:, h, u * P:(u + 1) * P],
                                       dst_parts[:, bass.ds(tile[(h * U + u) // 2], 1), :], start=True, stop=True)
                    mm.then_inc(dst_out, 1)


def stage_l1_project(nc, T, K):
    H, E = 8, 4
    with ExitStack() as ctx:
        s = Scope(nc, ctx, "y")
        n = Norm(s)
        w = s.sb("w", [P, 2, D])
        att = s.sb("att", [P, 2, D])
        gate = s.sb("gate", [P, NODE_TILES, E])
        mine = s.sb("mine", [P, TPC, E])
        x1 = s.sb("x1", [P, 2, TPC, D])
        y = s.sb("y", [P, 2, E, TPC, D])
        row = s.sb("row", [P, TPC, D])
        t1 = s.sb("t1", [P, TPC, D])
        t2 = s.sb("t2", [P, TPC, D])
        to_src = s.sb("to_src", [P, TPC, H])
        to_dst = s.sb("to_dst", [P, NODE_TILES, H])
        pq = s.ps("pq", [P, 4, 512])
        loaded = s.sem("loaded")
        chunk_in = [s.sem("chunk_in0"), s.sem("chunk_in1")]
        gated = s.sem("gated")
        x2_ready = s.sem("x2_ready")
        projected = s.sem("projected")
        row_ready = s.sem("row_ready")
        t2_ready = s.sem("t2_ready")
        src_ready = s.sem("src_ready")
        dst_ready = s.sem("dst_ready")
        x2_stored = s.sem("x2_stored")
        xn_stored = s.sem("xn_stored")
        row_stored = s.sem("row_stored")
        src_stored = s.sem("src_stored")
        stored = s.sem("stored")
        block = ctx.enter_context(nc.Block())

        @block.sync
        def _(sp):
            def load(c, h):
                sp.dma_start(x1[:, h, :, :], chunk_of(T["x1"], c)).then_inc(chunk_in[h], 16)
                for e in range(E):
                    sp.dma_start(y[:, h, e, :, :], chunk_of(T["f_experts"][e], c)).then_inc(chunk_in[h], 16)

            def front(c, h=None):
                sp.wait_ge(x2_ready, c + 1)
                sp.dma_start(chunk_of(T["x2"], c), n.x[:, :, :]).then_inc(x2_stored, 16)
                if h is not None:
                    load(c + 2, h)
                sp.wait_ge(n.xn_ready, c + 1)
                sp.dma_start(chunk_of(T["l1_xn"], c), n.xn[:, :, :]).then_inc(xn_stored, 16)

            def back(c):
                sp.wait_ge(row_ready, c + 1)
                sp.dma_start(chunk_of(T["l1_table"], c), row[:, :, :]).then_inc(row_stored, 16)
                sp.wait_ge(src_ready, c + 1)
                sp.dma_start(chunk_of(T["l1_asrc"], c), to_src[:, :, :]).then_inc(src_stored, 16)

            sp.dma_start(gate[:, :, :], T["f_gate"]).then_inc(loaded, 16)
            load(0, 0)
            sp.dma_start(w[:, :, :], T["L1_gnn_W"].rearrange("(a p) n -> p a n", p=P)).then_inc(loaded, 16)
            for k, m in enumerate(("src", "dst")):
                sp.dma_start(att[:, k, :], bcast_rows(T["L1_gnn_att_" + m].rearrange("h c -> (h c)"), P)).then_inc(loaded, 16)
            load(1, 1)
            front(0, 0)
            with sp.Fori(0, CHUNKS // 2 - 1) as i:
                for h in range(2):
                    front(2 * i + h + 1, 1 - h)
                    back(2 * i + h)
            for c in (CHUNKS - 3, CHUNKS - 2):
                front(c + 1)
                back(c)
            back(CHUNKS - 1)
            sp.wait_ge(dst_ready, CHUNKS)
            sp.dma_start(T["l1_adst"], to_dst[:, :, :]).then_inc(stored, 16)
            sp.wait_ge(stored, 16)
            for sem in (x2_stored, xn_stored, row_stored, src_stored):
                sp.wait_ge(sem, 16 * CHUNKS)

        @block.vector
        def _(dve):
            link = Tally(dve, s.sem("dve"))
            dve.wait_ge(loaded, 64)

            def front(c, h, turn):
                dve.wait_ge(chunk_in[h], 16 * (1 + E) * (turn + 1))
                link.done(dve.tensor_copy(mine[:, :, :], gate[:, bass.ds(c * TPC, TPC), :]))
                dve.wait_ge(x2_stored, 16 * c)
                for e in range(E):
                    for t in range(TPC):
                        ins = dve.scalar_tensor_tensor(n.x[:, t, :], y[:, h, e, t, :], mine[:, t, e:e + 1],
                                                       x1[:, h, t, :] if e == 0 else n.x[:, t, :], ALU.mult, ALU.add)
                    link.done(ins)
                dve.sem_inc(x2_ready, 1)
                dve.wait_ge(xn_stored, 16 * c)
                dve.wait_ge(n.turned, c)
                n.vector(dve, link, c).then_inc(n.xn_ready, 1)

            def back(c):
                dve.wait_ge(row_ready, c + 1)
                link.done(dve.tensor_tensor(t1[:, :, :], row[:, :, :], over_tiles(att[:, 0, :]), ALU.mult))
                dve.wait_ge(src_stored, 16 * c)
                dve.tensor_reduce(to_src[:, :, :].rearrange("p t h -> p (t h)"),
                                  t1[:, :, :].rearrange("p t (h c) -> p (t h) c", h=H), AX, ALU.add).then_inc(src_ready, 1)
                dve.wait_ge(t2_ready, c + 1)
                dve.tensor_reduce(to_dst[:, bass.ds(c * TPC, TPC), :].rearrange("p t h -> p (t h)"),
                                  t2[:, :, :].rearrange("p t (h c) -> p (t h) c", h=H), AX, ALU.add).then_inc(dst_ready, 1)

            front(0, 0, 0)
            with dve.Fori(0, CHUNKS // 2) as i:
                link.loop(i, 2 * (1 + E + 3))
                for h in range(2):
                    front(2 * i + h + 1, 1 - h, i + h)
                    back(2 * i + h)
            link.leave(CHUNKS // 2)
            back(CHUNKS - 1)

        @block.gpsimd
        def _(pool):
            pool.wait_ge(loaded, 64)
            with pool.Fori(0, CHUNKS) as c:
                pool.wait_ge(row_ready, c + 1)
                pool.wait_ge(dst_ready, c)
                pool.tensor_tensor(t2[:, :, :], row[:, :, :], over_tiles(att[:, 1, :]), ALU.mult).then_inc(t2_ready, 1)

        @block.scalar
        def _(act):
            with act.Fori(0, CHUNKS) as c:
                n.scalar(act, K, c)
                n.scalar_turned(act, c)
                act.wait_ge(projected, c + 1)
                act.wait_ge(row_stored, 16 * c)
                act.wait_ge(dst_ready, c)
                for t in range(0, TPC, 2):
                    m = min(2, TPC - t)
                    ins = act.activation(row[:, t:t + m, :], pq[:, t // 2, 0:m * D].rearrange("p (t d) -> p t d", d=D), ACT.Copy)
                ins.then_inc(row_ready, 1)

        @block.tensor
        def _(pe):
            pe.wait_ge(loaded, 64)
            with pe.Fori(0, CHUNKS) as c:
                n.tensor(pe, K, c)
                pe.wait_ge(n.xt_ready, c + 1)
                pe.wait_ge(row_ready, c)
                for t in range(TPC):
                    for f in range(2):
                        mm = pe.matmul(pq[:, t // 2, t % 2 * D:(t % 2 + 1) * D], n.xt[:, f, t * P:(t + 1) * P], w[:, f, :],
                                       start=(f == 0), stop=(f == 1))
                mm.then_inc(projected, 1)


def stage_l1_finish(nc, T, K, sums):
    H, W = 8, D
    with ExitStack() as ctx:
        s = Scope(nc, ctx, "z")
        n = Norm(s, turn=False)
        xns = s.sb("xns", [P, 2 * TPC, D])
        x2s = s.sb("x2s", [P, 2 * TPC, D])
        bias = s.sb("bias", [P, D])
        gain = s.sb("gain", [P, D])
        shift = s.sb("shift", [P, D])
        rden = s.sb("rden", [P, TPC, H])
        t1 = s.sb("t1", [P, TPC, D])
        t2 = s.sb("t2", [P, TPC, D])
        outs = s.sb("outs", [P, 2 * TPC, D])
        params = s.sem("params")
        loaded = [s.sem("loaded0"), s.sem("loaded1")]
        out_ready = s.sem("out_ready")
        stored = s.sem("stored")
        block = ctx.enter_context(nc.Block())

        def slot(buffers, c):
            return buffers[:, bass.ds(c % 2 * TPC, TPC), :]

        @block.sync
        def _(sp):
            for to, name in ((bias, "bias"), (gain, "gamma"), (shift, "beta")):
                sp.dma_start(to[:, :], bcast_rows(T["L1_gnn_" + name], P)).then_inc(params, 16)
            sp.sem_inc(out_ready, 1)
            sp.sem_inc(stored, 16)
            sp.dma_start(slot(xns, 0), chunk_of(T["l1_xn"], 0)).then_inc(loaded[0], 16)
            sp.dma_start(slot(x2s, 0), chunk_of(T["x2"], 0)).then_inc(loaded[0], 16)
            with sp.Fori(0, CHUNKS // 2) as i:
                for h in range(2):
                    c = 2 * i + h
                    sp.wait_ge(out_ready, c + 1)
                    sp.dma_start(slot(xns, c + 1), chunk_of(T["l1_xn"], c + 1)).then_inc(loaded[1 - h], 16)
                    sp.dma_start(slot(x2s, c + 1), chunk_of(T["x2"], c + 1)).then_inc(loaded[1 - h], 16)
                    sp.wait_ge(out_ready, c + 2)
                    sp.dma_start(chunk_of(T["x3"], c), slot(outs, c)).then_inc(stored, 16)
            sp.wait_ge(out_ready, CHUNKS + 1)
            sp.dma_start(chunk_of(T["x3"], CHUNKS - 1), slot(outs, CHUNKS - 1)).then_inc(stored, 16)
            sp.wait_ge(stored, 16 * (CHUNKS + 1))

        @block.vector
        def _(dve):
            link = Tally(dve, s.sem("dve"))
            dve.wait_ge(params, 48)
            def finish(c, h, turn):
                xn, x2, out = slot(xns, c), slot(x2s, c), slot(outs, c)
                acc = sums[:, bass.ds(c * TPC, TPC), :]
                dve.wait_ge(loaded[h], 32 * (turn + 1))
                link.done(dve.tensor_scalar(rden[:, :, :], acc[:, :, W:W + H], 1e-16, 0.5, ALU.add, ALU.max))
                link.done(dve.reciprocal(rden[:, :, :], rden[:, :, :]))
                link.done(dve.tensor_tensor(t1[:, :, :].rearrange("p t (h c) -> p t h c", h=H),
                                            acc[:, :, 0:W].rearrange("p t (h c) -> p t h c", h=H),
                                            rden[:, :, :].unsqueeze(3).broadcast_to((P, TPC, H, W // H)), ALU.mult))
                link.done(dve.tensor_tensor(t1[:, :, :], t1[:, :, :], over_tiles(bias[:, :]), ALU.add))
                link.done(dve.tensor_tensor(t1[:, :, :], t1[:, :, :], xn, ALU.add))
                link.done(n.vector(dve, link, c, x=t1, out=t2))
                link.done(dve.tensor_tensor(t2[:, :, :], t2[:, :, :], over_tiles(gain[:, :]), ALU.mult))
                link.done(dve.tensor_tensor(t2[:, :, :], t2[:, :, :], over_tiles(shift[:, :]), ALU.add))
                dve.wait_ge(stored, 16 * c)
                dve.tensor_tensor(out, t2[:, :, :], x2, ALU.add).then_inc(out_ready, 1)

            with dve.Fori(0, CHUNKS // 2) as i:
                link.loop(i, 2 * 10)
                for h in range(2):
                    finish(2 * i + h, h, i)
            link.leave(CHUNKS // 2)
            finish(CHUNKS - 1, 0, CHUNKS // 2)

        @block.scalar
        def _(act):
            with act.Fori(0, CHUNKS) as c:
                n.scalar(act, K, c)


def stage_experts3(nc, T, K):
    E = 8
    BN_EPS = 0.001
    with ExitStack() as ctx:
        s = Scope(nc, ctx, "l")
        n = Norm(s, turn=False)
        xt = s.sb("xt", [P, 2, ROWS])
        turned = s.sem("turned")
        xt_ready = s.sem("xt_ready")
        wm = [s.sb(f"wm{k}", [P, E, 2, D]) for k in range(3)]
        wr = s.sb("wr", [P, 2, E])
        br = s.sb("br", [P, E])
        raw = s.sb("raw", [5 * 2 * E, 2, P])
        par = s.sb("par", [P, 2, 5, 2 * E])
        bn = s.sb("bn", [P, 2, 2, 2 * E])
        bn_eps = s.sb("bn_eps", [P, 1])
        sdv = s.sb("sdv", [P, 2, 2 * E])
        bo = s.sb("bo", [P, E, D])
        logit = s.sb("logit", [P, TPC, E])
        mx = s.sb("mx", [P, TPC])
        prob = s.sb("prob", [P, TPC, E])
        den = s.sb("den", [P, TPC])
        h1 = s.sb("h1", [P, 2, 2, ROWS])
        h2 = s.sb("h2", [P, 2, 2, ROWS])
        prob_next = s.sb("prob_next", [P, TPC, E])
        accs = s.sb("accs", [P, 2 * TPC, D])
        ph = s.ps("ph", [P, 2, 2, 512])
        po = s.ps("po", [P, 4, 512])
        loaded = s.sem("loaded")
        par_turned = s.sem("par_turned")
        var_ready = s.sem("bn_var")
        bn_sd = s.sem("bn_sd")
        bn_ready = s.sem("bn_ready")
        routed = s.sem("routed")
        route_read = s.sem("route_read")
        diff_ready = s.sem("diff_ready")
        exp_ready = s.sem("exp_ready")
        up = s.sem("up")
        act_done = s.sem("act_done")
        down = s.sem("down")
        acc_done = s.sem("acc_done")
        started = s.sem("started")
        stored = s.sem("stored")
        block = ctx.enter_context(nc.Block())
        n_loads = 3 * E + 2 + 10 + 1
        order = []
        for e in range(E + 1):
            order += [(0, e)] * (e < E) + [(1, e - 1)] * (e > 0)
        place = {what: k for k, what in enumerate(order)}
        PER = 2 * len(order)

        def acc_of(c):
            return accs[:, bass.ds(c % 2 * TPC, TPC), :]

        def slot(t):
            return po[:, t // 2, t % 2 * D:(t % 2 + 1) * D]

        @block.sync
        def _(sp):
            n.load(sp, T["x3"], 0)
            for k in range(2):
                for a, name in enumerate(("b", "g", "be", "m", "v")):
                    sp.dma_start(raw[a * 2 * E:(a + 1) * 2 * E, k, :],
                                 T[f"L1_ffn_{name}{k + 1}"].rearrange("e (a p) -> (e a) p", p=P)).then_inc(loaded, 16)
            sp.dma_start(wr[:, :, :], T["L1_ffn_Wr"].rearrange("(a p) e -> p a e", p=P)).then_inc(loaded, 16)
            sp.dma_start(br[:, :], bcast_rows(T["L1_ffn_br"], P)).then_inc(loaded, 16)
            sp.dma_start(bo[:, :, :].rearrange("p e d -> p (e d)"), bcast_rows(T["L1_ffn_bo"].rearrange("e d -> (e d)"), P)
                         ).then_inc(loaded, 16)
            for e in range(E):
                for k, name in enumerate(("W1", "W2", "Wo")):
                    sp.dma_start(wm[k][:, e, :, :], T["L1_ffn_" + name][e].rearrange("(a p) f -> p a f", p=P)).then_inc(loaded, 16)
            sp.sem_inc(stored, 16)
            with sp.Fori(0, CHUNKS - 1) as c:
                sp.wait_ge(started, c + 1)
                n.load(sp, T["x3"], c + 1)
                sp.wait_ge(acc_done, PAIRS + PAIRS * E * (c + 1))
                sp.dma_start(T["out"][bass.ds(c * ROWS, ROWS), :].rearrange("(t p) f -> p t f", p=P), acc_of(c)).then_inc(stored, 16)
            sp.wait_ge(acc_done, PAIRS + PAIRS * E * CHUNKS)
            at = (CHUNKS - 1) * ROWS
            full = (N - at) // P
            acc = acc_of(CHUNKS - 1)
            sp.dma_start(T["out"][at:at + full * P, :].rearrange("(t p) f -> p t f", p=P), acc[:, 0:full, :]).then_inc(stored, 16)
            at += full * P
            sp.dma_start(T["out"][at:N, :], acc[0:N - at, full, :]).then_inc(stored, 16)
            sp.wait_ge(stored, 16 * (CHUNKS + 2))

        @block.vector
        def _(dve):
            link = Tally(dve, s.sem("dve"))
            dve.memset(bn_eps[:, :], BN_EPS)
            dve.wait_ge(par_turned, 1)
            for k in range(2):
                ins = dve.tensor_copy(par[:, k, :, :], po[:, k, 0:5 * 2 * E].rearrange("p (a n) -> p a n", a=5))
            link.done(ins)
            dve.sem_inc(var_ready, 1)
            dve.wait_ge(bn_sd, 1)
            link.done(dve.reciprocal(sdv[:, :, :], sdv[:, :, :]))
            link.done(dve.tensor_tensor(bn[:, :, 0, :], sdv[:, :, :], par[:, :, 1, :], ALU.mult))
            link.done(dve.tensor_tensor(sdv[:, :, :], par[:, :, 0, :], par[:, :, 3, :], ALU.subtract))
            link.done(dve.tensor_tensor(sdv[:, :, :], sdv[:, :, :], bn[:, :, 0, :], ALU.mult))
            dve.tensor_tensor(bn[:, :, 1, :], sdv[:, :, :], par[:, :, 2, :], ALU.add).then_inc(bn_ready, 1)
            dve.wait_ge(loaded, 16 * n_loads)
            def norm(c):
                dve.wait_ge(n.x_loaded, 16 * c + 16)
                n.vector(dve, link, c).then_inc(n.xn_ready, 1)

            def route(c):
                dve.wait_ge(routed, c + 1)
                dve.tensor_tensor(logit[:, :, :], ph[:, 1, 1, 0:TPC * E].rearrange("p (t e) -> p t e", e=E), over_tiles(br[:, :]),
                                  ALU.add).then_inc(route_read, 1)
                dve.wait_ge(route_read, c + 1)
                link.done(dve.tensor_reduce(mx[:, :], logit[:, :, :], AX, ALU.max))
                dve.tensor_tensor(logit[:, :, :], logit[:, :, :], mx[:, :].unsqueeze(2).broadcast_to((P, TPC, E)), ALU.subtract
                                  ).then_inc(diff_ready, 1)
                dve.wait_ge(exp_ready, c + 1)
                link.done(dve.tensor_reduce(den[:, :], prob_next[:, :, :], AX, ALU.add))
                link.done(dve.reciprocal(den[:, :], den[:, :]))
                link.done(dve.tensor_tensor(prob_next[:, :, :], prob_next[:, :, :], den[:, :].unsqueeze(2).broadcast_to((P, TPC, E)),
                                            ALU.mult))

            def start(c):
                acc = acc_of(c)
                dve.wait_ge(acc_done, (c * E + 1) * PAIRS)
                link.done(dve.tensor_copy(prob[:, :, :], prob_next[:, :, :]))
                dve.wait_ge(stored, 16 * c)
                for e in range(E):
                    for t in range(TPC):
                        ins = dve.scalar_tensor_tensor(acc[:, t, :], bo[:, e, :], prob[:, t, e:e + 1],
                                                       n.x[:, t, :] if e == 0 else acc[:, t, :], ALU.mult, ALU.add)
                    link.done(ins)
                dve.sem_inc(started, 1)

            def add(c, e):
                acc = acc_of(c)
                for b in range(PAIRS):
                    g = (c * E + e) * PAIRS + b
                    dve.wait_ge(down, g + 1)
                    dve.wait_ge(acc_done, g + 1)
                    for t in range(2 * b, min(2 * b + 2, TPC)):
                        ins = dve.scalar_tensor_tensor(acc[:, t, :], slot(t), prob[:, t, e:e + 1], acc[:, t, :], ALU.mult, ALU.add)
                    ins.then_inc(acc_done, 1)

            dve.sem_inc(acc_done, PAIRS)
            norm(0)
            route(0)
            start(0)
            with dve.Fori(0, CHUNKS - 1) as c:
                link.loop(c, 2 + 4 + 1 + E)
                for e in range(E):
                    add(c, e)
                    if e == E // 2:
                        norm(c + 1)
                    if e == E - 2:
                        route(c + 1)
                start(c + 1)
            link.leave(CHUNKS - 1)
            for e in range(E):
                add(CHUNKS - 1, e)

        @block.scalar
        def _(act):
            act.wait_ge(var_ready, 1)
            act.activation(sdv[:, :, :], par[:, :, 4, :], ACT.Sqrt, bias=bn_eps[:, 0:1]).then_inc(bn_sd, 1)
            act.wait_ge(bn_ready, 1)
            act.sem_inc(act_done, 2)

            def turn(c):
                act.wait_ge(turned, c + 1)
                for f in range(2):
                    for h in range(2):
                        w = min(512, ROWS - h * 512)
                        ins = act.activation(xt[:, f, h * 512:h * 512 + w], ph[:, f, h, 0:w], ACT.Copy)
                ins.then_inc(xt_ready, 1)

            def exps(c):
                act.wait_ge(diff_ready, c + 1)
                act.activation(prob_next[:, :, :], logit[:, :, :], ACT.Exp).then_inc(exp_ready, 1)

            def chunk(c, more):
                for k, (layer, e) in enumerate(order):
                    to = (h1, h2)[layer]
                    for f in range(2):
                        act.wait_ge(up, c * PER + 2 * k + f + 1)
                        act.activation(to[:, e % 2, f, :].rearrange("p (h r) -> p h r", h=2), ph[:, f, :, 0:HALF], ACT.Relu,
                                       scale=bn[:, layer, 0, 2 * e + f:2 * e + f + 1],
                                       bias=bn[:, layer, 1, 2 * e + f:2 * e + f + 1]).then_inc(act_done, 1)
                    if more and (layer, e) == (0, E // 2 + 2):
                        n.scalar(act, K, c + 1)
                    if more and (layer, e) == (1, E - 2):
                        turn(c + 1)
                        exps(c + 1)

            n.scalar(act, K, 0)
            turn(0)
            exps(0)
            with act.Fori(0, CHUNKS - 1) as c:
                chunk(c, True)
            chunk(CHUNKS - 1, False)

        @block.tensor
        def _(pe):
            def turn(c):
                pe.wait_ge(n.xn_ready, c + 1)
                for f in range(2):
                    for t in range(TPC):
                        mm = pe.transpose(ph[:, f, t // 4, (t % 4) * P:(t % 4 + 1) * P], n.xn[:, t, f * P:(f + 1) * P], K["ident"][:, :])
                mm.then_inc(turned, 1)

            def route(c):
                pe.wait_ge(xt_ready, c + 1)
                for t in range(TPC):
                    for f in range(2):
                        mm = pe.matmul(ph[:, 1, 1, t * E:(t + 1) * E], xt[:, f, t * P:(t + 1) * P], wr[:, f, :],
                                       start=(f == 0), stop=(f == 1))
                mm.then_inc(routed, 1)

            def layer(c, which, e):
                k = place[which, e]
                if which:
                    pe.wait_ge(act_done, 2 + c * PER + 2 * place[0, e] + 2)
                of = (xt[:, :, :], h1[:, e % 2, :, :])[which]
                for f in range(2):
                    pe.wait_ge(act_done, c * PER + 2 * k + f + 1)
                    for a in range(2):
                        for h in range(2):
                            mm = pe.matmul(ph[:, f, h, 0:HALF], wm[which][:, e, a, f * P:(f + 1) * P],
                                           of[:, a, h * HALF:(h + 1) * HALF], start=(a == 0), stop=(a == 1))
                    mm.then_inc(up, 1)

            def last(c, e):
                pe.wait_ge(act_done, 2 + c * PER + 2 * place[1, e] + 2)
                for b in range(PAIRS):
                    pe.wait_ge(acc_done, (c * E + e) * PAIRS + b + 1)
                    for t in range(2 * b, min(2 * b + 2, TPC)):
                        for f in range(2):
                            mm = pe.matmul(slot(t), h2[:, e % 2, f, t * P:(t + 1) * P], wm[2][:, e, f, :],
                                           start=(f == 0), stop=(f == 1))
                    mm.then_inc(down, 1)

            def chunk(c, more):
                pe.wait_ge(route_read, c + 1)
                for e in range(E):
                    layer(c, 0, e)
                    if e > 0:
                        layer(c, 1, e - 1)
                    if e > 1:
                        last(c, e - 2)
                if more:
                    pe.wait_ge(act_done, 2 + c * PER + 2 * place[1, E - 2] + 2)
                    turn(c + 1)
                last(c, E - 2)
                if more:
                    route(c + 1)
                    pe.wait_ge(route_read, c + 2)
                layer(c, 1, E - 1)
                last(c, E - 1)

            pe.wait_ge(loaded, 16 * n_loads)
            for k in range(2):
                mm = pe.transpose(po[:, k, 0:5 * 2 * E], raw[:, k, :], K["ident"][0:5 * 2 * E, 0:5 * 2 * E])
            mm.then_inc(par_turned, 1)
            pe.wait_ge(bn_ready, 1)
            turn(0)
            route(0)
            with pe.Fori(0, CHUNKS - 1) as c:
                chunk(c, True)
            chunk(CHUNKS - 1, False)


def scratch_shapes():
    shapes = {"x0": ([NP, D], F32)}
    for L in (GRAPH, HOP):
        n = L.name
        shapes.update({
            n + "_src": ([L.tiles * P], I32), n + "_dst": ([L.tiles * P], I32),
            n + "_rel_rows": ([L.blocks * P, P], F32), n + "_key_rows": ([L.blocks * P, P], F32),
            n + "_i_row": ([L.blocks * P // 2], I32), n + "_j_row": ([L.blocks * P // 2], I32),
            n + "_src_t": ([P, L.steps], I32), n + "_rel_t": ([P, L.steps], F32),
        })
    shapes.update({"g_src_by_edge": ([P, GRAPH.tiles], I32), "g_hi_by_edge": ([P, GRAPH.tiles], F32),
                   "g_lo_flat": ([GRAPH.tiles * P], F32)})
    shapes["f_pairs"] = ([HOP.edges, 2], I32)
    for k in ("q", "k", "v", "skip"):
        shapes["l0_" + k] = ([NP, D], F32)
    shapes.update({
        "x1": ([NP, D], F32), "x2": ([NP, D], F32), "x3": ([NP, D], F32),
        "f_table": ([NP, 20], F32), "f_experts": ([4, NP, D], F32), "f_gate": ([P, NODE_TILES, 4], F32),
        "f_adst": ([P, NODE_TILES, 4], F32),
        "l1_table": ([NP, D], F32), "l1_asrc": ([NP, 8], F32), "l1_adst": ([P, NODE_TILES, 8], F32),
        "l1_xn": ([NP, D], F32),
    })
    return shapes


def two_layers(nc, T):
    for name, (shape, dt) in scratch_shapes().items():
        T[name] = nc.dram_tensor("tmp_" + name, shape, dt).ap()
    with ExitStack() as ctx:
        K = {name: ctx.enter_context(nc.sbuf_tensor("const_" + name, shape, F32)) for name, shape in
             (("frow", [P, P]), ("pcol", [P, 1]), ("minus_col", [P, 1]), ("ident", [P, P]), ("below", [P, P]), ("ones", [P, P]), ("eps", [P, 1]))}

        def held(name, shape):
            return nc.sbuf_tensor(name, shape, F32)

        stage_constants(nc, T, K)
        stage_schedule(nc, T, K, GRAPH)
        stage_sources(nc, T, K, GRAPH)
        places = Places(nc, ctx)
        stage_sort(nc, T, K, places)
        stage_l0_project(nc, T, K, places)
        with held("l0_score", [P, GRAPH.steps, 4]) as score, held("l0_sums", [P, NODE_TILES, D + 4]) as sums:
            stage_dot(nc, T, K, GRAPH, score)
            stage_softmax(nc, T, K, GRAPH, 4, 64 ** -0.5, score, places)
            stage_sum(nc, T, K, GRAPH, 4, D, score, sums, T["l0_v"])
            stage_l0_finish(nc, T, K, sums, places)
        stage_split(nc, T, K)
        stage_schedule(nc, T, K, HOP)
        stage_hop_project(nc, T, K)
        with held("hop_score", [P, HOP.steps, 4]) as score, held("hop_rows", [P, HOP.steps, 16]) as rows:
            stage_hop_scores_and_experts(nc, T, K, score, rows)
            stage_softmax(nc, T, K, HOP, 4, 1.0, score)
            with held("hop_sums", [P, NODE_TILES, 16 + 4]) as sums:
                stage_hop_sum(nc, T, K, score, rows, sums)
                stage_hop_gate(nc, T, K, sums)
        stage_l1_project(nc, T, K)
        with held("l1_score", [P, GRAPH.steps, 8]) as score:
            stage_l1_scores(nc, T, K, score)
            stage_softmax(nc, T, K, GRAPH, 8, 1.0, score)
            with held("l1_sums", [P, NODE_TILES, D + 8]) as sums:
                stage_sum(nc, T, K, GRAPH, 8, D, score, sums, T["l1_table"])
                stage_l1_finish(nc, T, K, sums)
        stage_experts3(nc, T, K)


def kernel(**inputs):
    import numpy as _np
    import concourse.bacc as _bacc
    from concourse import mybir as _mybir
    from concourse.bass_utils import run_bass_kernel_spmd as _run

    nc = _bacc.Bacc("TRN2", target_bir_lowering=False, num_devices=1)
    arrays, tables = {}, {}
    for name in inputs:
        a = _np.ascontiguousarray(inputs[name])
        a = a.reshape(a.shape or (1,))
        arrays["in_" + name] = a
        tables[name] = nc.dram_tensor("in_" + name, a.shape, _mybir.dt.from_np(a.dtype), kind="ExternalInput").ap()
    tables["out"] = nc.dram_tensor("out", (N, D), _mybir.dt.float32, kind="ExternalOutput").ap()
    two_layers(nc, tables)
    return _run(nc, [arrays], core_ids=[0]).results[0]["out"]
```
